# Optimizing a Trainium2 kernel written in Bass

```python
import numpy as np
import jax
import jax.numpy as jnp

def _softmax(x, axis=-1):
    return jax.nn.softmax(x, axis=axis)

def _gelu(x):
    return jax.nn.gelu(x, approximate=True)

def _silu(x):
    return jax.nn.silu(x)

def _sigmoid(x):
    return jax.nn.sigmoid(x)

def _layernorm(x, axis=-1, eps=1e-05):
    m = jnp.mean(x, axis=axis, keepdims=True)
    v = jnp.var(x, axis=axis, keepdims=True)
    return (x - m) / jnp.sqrt(v + eps)

def _scatter_add(tgt, idx, src, axis=0):
    return tgt.at[idx].add(src)

def _segment_sum(src, seg, n):
    return jax.ops.segment_sum(src, seg, n)
kernel_name = 'mk_early_fusion_d2_tok_img768_r4_7cb0d3'

def setup_inputs(seed: int=0):
    np.random.seed(seed)
    _w = jnp.asarray

    def _rec_inputs():
        import jax
        import jax.numpy as jnp
        _rk = jax.random.key(seed)
        x = 7.57192e-06 + 1.00007 * jax.random.normal(jax.random.fold_in(_rk, 1), (16, 224, 224, 3), jnp.float32)
        txt = -0.000241419 + 1.20654 * jax.random.normal(jax.random.fold_in(_rk, 2), (16, 512, 192), jnp.float32)
        return (x, txt)
    x, txt = _rec_inputs()

    def _L0_tok_setup():
        import jax, jax.numpy as jnp
        import numpy as np
        IMG = 224
        P = 16
        HP = P // 2
        D = 192
        C_IN = 3
        B = 64

        def _crop_shift_pad(images, oh, ow):
            th = IMG - HP
            tw = IMG - HP
            out = jnp.zeros_like(images)
            return out.at[:, oh:oh + th, ow:ow + tw, :].set(images[:, oh:oh + th, ow:ow + tw, :])
        key = jax.random.key(seed)
        k1, k2 = jax.random.split(key, 2)
        images = jax.random.normal(k1, (B, IMG, IMG, C_IN), dtype=jnp.float32)
        pvs = P * P * C_IN * 5
        W = jax.random.normal(k2, (pvs, D), dtype=jnp.float32) * 0.02
        b = jnp.zeros((D,), dtype=jnp.float32)
        return {'images': images, 'W': W, 'b': b}
    _L0_tok_all = _L0_tok_setup()
    _L0_tok_in = {k: v for k, v in _L0_tok_all.items() if k in ('W', 'b')}
    del _L0_tok_all

    def _L0_attn_setup():
        import jax, jax.numpy as jnp
        import numpy as np
        DIM = 192
        HEADS = 12
        HEAD_DIM = DIM // HEADS
        EPS = 1e-12

        def _l1_normalize(t):
            denom = jnp.maximum(jnp.sum(jnp.abs(t), axis=-2, keepdims=True), EPS)
            return t / denom
        key = jax.random.key(seed)
        k1, k2, k3 = jax.random.split(key, 3)
        x = jax.random.normal(k1, (8, 1024, DIM), dtype=jnp.float32)
        s = 1.0 / np.sqrt(DIM)
        w_qkv = jax.random.uniform(k2, (3 * DIM, DIM), dtype=jnp.float32, minval=-s, maxval=s)
        w_proj = jax.random.uniform(k3, (DIM, DIM), dtype=jnp.float32, minval=-s, maxval=s)
        b_proj = jnp.zeros((DIM,), dtype=jnp.float32)
        return {'x': x, 'w_qkv': w_qkv, 'w_proj': w_proj, 'b_proj': b_proj}
    _L0_attn_all = _L0_attn_setup()
    _L0_attn_in = {k: v for k, v in _L0_attn_all.items() if k in ('w_qkv', 'w_proj', 'b_proj')}
    del _L0_attn_all

    def _L0_ffn_setup():
        import jax, jax.numpy as jnp
        import numpy as np
        import math
        B, S, D = (4, 1024, 192)
        E = 8
        TOP_K = 2
        H = 512
        CAP_F = 1.25
        EPS = 1e-06
        ALPHA = 1.0
        key = jax.random.key(seed)
        k0, k1, k2, k3 = jax.random.split(key, 4)
        x = jax.random.normal(k0, (B, S, D), jnp.float32)
        gate_w = jax.random.normal(k1, (E, D), jnp.float32) * 0.02
        w13 = jax.random.normal(k2, (E, 2 * H, D), jnp.float32) * 0.02
        w2 = jax.random.normal(k3, (E, D, H), jnp.float32) * 0.02
        norm_w = jnp.ones((E, D), jnp.float32)
        return {'x': x, 'gate_w': gate_w, 'w13': w13, 'w2': w2, 'norm_w': norm_w}
    _L0_ffn_all = _L0_ffn_setup()
    _L0_ffn_in = {k: v for k, v in _L0_ffn_all.items() if k in ('gate_w', 'w13', 'w2', 'norm_w')}
    del _L0_ffn_all

    def _L1_attn_setup():
        import jax, jax.numpy as jnp
        import numpy as np
        BETA, ALPHA, NS_STEPS = (0.9, 1.0, 1)
        D_MODEL, D_STATE, D_CONV, EXPAND = (192, 16, 4, 2)
        D_INNER = EXPAND * D_MODEL
        DT_RANK = -(-D_MODEL // 16)
        B, L = (2, 256)

        def _newton_schulz(G, steps):
            a, b, c = (3.4445, -4.775, 2.0315)
            X = G / (jnp.linalg.norm(G, axis=(-2, -1), keepdims=True) + 1e-07)
            X = X.swapaxes(-2, -1)
            for _ in range(steps):
                A = X @ X.swapaxes(-2, -1)
                Bm = b * A + c * (A @ A)
                X = a * X + Bm @ X
            return X.swapaxes(-2, -1)
        key = jax.random.key(seed)
        ks = jax.random.split(key, 8)
        s = lambda k, shape, sc=0.02: jax.random.normal(k, shape, jnp.float32) * sc
        return {'hidden_states': jax.random.normal(ks[0], (B, L, D_MODEL), jnp.float32), 'in_proj_w': s(ks[1], (2 * D_INNER, D_MODEL)), 'conv_w': s(ks[2], (D_INNER, 1, D_CONV), 0.2), 'conv_b': jnp.zeros((D_INNER,), jnp.float32), 'x_proj_w': s(ks[3], (DT_RANK + 2 * D_STATE, D_INNER)), 'dt_head_w': s(ks[4], (D_INNER, DT_RANK)), 'dt_head_b': s(ks[5], (D_INNER,), 0.1), 'out_proj_w': s(ks[6], (D_MODEL, D_INNER)), 'D': jnp.ones((D_INNER,), jnp.float32)}
    _L1_attn_all = _L1_attn_setup()
    _L1_attn_in = {k: v for k, v in _L1_attn_all.items() if k in ('in_proj_w', 'conv_w', 'conv_b', 'x_proj_w', 'dt_head_w', 'dt_head_b', 'out_proj_w', 'D')}
    del _L1_attn_all

    def _L1_ffn_setup():
        import jax, jax.numpy as jnp
        import numpy as np
        H = 12
        ALPHA = (1, 2, 3)
        DEPTH = 5
        BLOCK_DEPTH = 3
        TOTAL_DEPTH_M1 = 14 - 1
        SMALL_ACTIVE = BLOCK_DEPTH <= DEPTH <= TOTAL_DEPTH_M1 - BLOCK_DEPTH

        def _ln(x, g, b, eps=1e-05):
            m = jnp.mean(x, axis=-1, keepdims=True)
            v = jnp.mean((x - m) ** 2, axis=-1, keepdims=True)
            return (x - m) * jax.lax.rsqrt(v + eps) * g + b

        def _attn_branch(xp, w_qkv, w_proj, b_proj, keep_heads, keep_ch):
            B2, N, C = xp.shape
            hd = C // H
            scale = hd ** (-0.5)
            qkv = (xp @ w_qkv).reshape(B2, N, 3, H, hd).transpose(2, 0, 3, 1, 4)
            hmask = (jnp.arange(H) < keep_heads).astype(xp.dtype)[None, :, None, None]
            q, k, v = (qkv[0] * hmask, qkv[1] * hmask, qkv[2] * hmask)
            a = jax.nn.softmax(jnp.einsum('bhnd,bhmd->bhnm', q, k) * scale, axis=-1)
            o = jnp.einsum('bhnm,bhmd->bhnd', a, v).transpose(0, 2, 1, 3).reshape(B2, N, C)
            o = o @ w_proj + b_proj
            cmask = (jnp.arange(C) < keep_ch).astype(xp.dtype)
            return o * cmask

        def _mlp_branch(xp, w1, b1, w2, b2, keep_ch):
            C = xp.shape[-1]
            cmask = (jnp.arange(C) < keep_ch).astype(xp.dtype)
            h = jax.nn.gelu(xp * cmask @ w1 + b1, approximate=False)
            return (h @ w2 + b2) * cmask
        key = jax.random.key(seed)
        ks = jax.random.split(key, 8)
        B, N, C = (64, 257, 192)
        HID = 4 * C

        def w(k, shape):
            return jax.random.normal(k, shape, jnp.float32) * 0.02
        return {'x': jax.random.normal(ks[0], (B, N, C), jnp.float32), 'gumbel_weights': jax.random.uniform(ks[1], (3,), jnp.float32), 'n1l_g': jnp.ones((C,), jnp.float32), 'n1l_b': jnp.zeros((C,), jnp.float32), 'n1s_g': jnp.ones((C,), jnp.float32), 'n1s_b': jnp.zeros((C,), jnp.float32), 'w_qkv': w(ks[2], (C, 3 * C)), 'w_proj': w(ks[3], (C, C)), 'b_proj': jnp.zeros((C,), jnp.float32), 'n2l_g': jnp.ones((C,), jnp.float32), 'n2l_b': jnp.zeros((C,), jnp.float32), 'n2s_g': jnp.ones((C,), jnp.float32), 'n2s_b': jnp.zeros((C,), jnp.float32), 'w_fc1': w(ks[4], (C, HID)), 'b_fc1': jnp.zeros((HID,), jnp.float32), 'w_fc2': w(ks[5], (HID, C)), 'b_fc2': jnp.zeros((C,), jnp.float32)}
    _L1_ffn_all = _L1_ffn_setup()
    _L1_ffn_in = {k: v for k, v in _L1_ffn_all.items() if k in ('gumbel_weights', 'n1l_g', 'n1l_b', 'n1s_g', 'n1s_b', 'w_qkv', 'w_proj', 'b_proj', 'n2l_g', 'n2l_b', 'n2s_g', 'n2s_b', 'w_fc1', 'b_fc1', 'w_fc2', 'b_fc2')}
    del _L1_ffn_all
    return {'x': x, 'txt': txt, 'L0_tok_W': _L0_tok_in['W'], 'L0_tok_b': _L0_tok_in['b'], 'L0_attn_w_qkv': _L0_attn_in['w_qkv'], 'L0_attn_w_proj': _L0_attn_in['w_proj'], 'L0_attn_b_proj': _L0_attn_in['b_proj'], 'L0_ffn_gate_w': _L0_ffn_in['gate_w'], 'L0_ffn_w13': _L0_ffn_in['w13'], 'L0_ffn_w2': _L0_ffn_in['w2'], 'L0_ffn_norm_w': _L0_ffn_in['norm_w'], 'L1_attn_in_proj_w': _L1_attn_in['in_proj_w'], 'L1_attn_conv_w': _L1_attn_in['conv_w'], 'L1_attn_conv_b': _L1_attn_in['conv_b'], 'L1_attn_x_proj_w': _L1_attn_in['x_proj_w'], 'L1_attn_dt_head_w': _L1_attn_in['dt_head_w'], 'L1_attn_dt_head_b': _L1_attn_in['dt_head_b'], 'L1_attn_out_proj_w': _L1_attn_in['out_proj_w'], 'L1_attn_D': _L1_attn_in['D'], 'L1_ffn_gumbel_weights': _L1_ffn_in['gumbel_weights'], 'L1_ffn_n1l_g': _L1_ffn_in['n1l_g'], 'L1_ffn_n1l_b': _L1_ffn_in['n1l_b'], 'L1_ffn_n1s_g': _L1_ffn_in['n1s_g'], 'L1_ffn_n1s_b': _L1_ffn_in['n1s_b'], 'L1_ffn_w_qkv': _L1_ffn_in['w_qkv'], 'L1_ffn_w_proj': _L1_ffn_in['w_proj'], 'L1_ffn_b_proj': _L1_ffn_in['b_proj'], 'L1_ffn_n2l_g': _L1_ffn_in['n2l_g'], 'L1_ffn_n2l_b': _L1_ffn_in['n2l_b'], 'L1_ffn_n2s_g': _L1_ffn_in['n2s_g'], 'L1_ffn_n2s_b': _L1_ffn_in['n2s_b'], 'L1_ffn_w_fc1': _L1_ffn_in['w_fc1'], 'L1_ffn_b_fc1': _L1_ffn_in['b_fc1'], 'L1_ffn_w_fc2': _L1_ffn_in['w_fc2'], 'L1_ffn_b_fc2': _L1_ffn_in['b_fc2']}

def reference(x, txt, L0_tok_W, L0_tok_b, L0_attn_w_qkv, L0_attn_w_proj, L0_attn_b_proj, L0_ffn_gate_w, L0_ffn_w13, L0_ffn_w2, L0_ffn_norm_w, L1_attn_in_proj_w, L1_attn_conv_w, L1_attn_conv_b, L1_attn_x_proj_w, L1_attn_dt_head_w, L1_attn_dt_head_b, L1_attn_out_proj_w, L1_attn_D, L1_ffn_gumbel_weights, L1_ffn_n1l_g, L1_ffn_n1l_b, L1_ffn_n1s_g, L1_ffn_n1s_b, L1_ffn_w_qkv, L1_ffn_w_proj, L1_ffn_b_proj, L1_ffn_n2l_g, L1_ffn_n2l_b, L1_ffn_n2s_g, L1_ffn_n2s_b, L1_ffn_w_fc1, L1_ffn_b_fc1, L1_ffn_w_fc2, L1_ffn_b_fc2):
    import jax
    import jax.numpy as jnp

    def _L0_tok_ref(images, W, b):
        import jax, jax.numpy as jnp
        import numpy as np
        IMG = 224
        P = 16
        HP = P // 2
        D = 192
        C_IN = 3
        B = 64

        def _crop_shift_pad(images, oh, ow):
            th = IMG - HP
            tw = IMG - HP
            out = jnp.zeros_like(images)
            return out.at[:, oh:oh + th, ow:ow + tw, :].set(images[:, oh:oh + th, ow:ow + tw, :])
        offsets = [(0, 0), (HP, 0), (0, HP), (HP, HP)]
        concat = jnp.concatenate([images] + [_crop_shift_pad(images, oh, ow) for oh, ow in offsets], axis=-1)
        Bn, _, _, C = concat.shape
        g = IMG // P
        x = concat.reshape(Bn, g, P, g, P, C)
        x = x.transpose(0, 1, 3, 2, 4, 5).reshape(Bn, g * g, P * P * C)
        return x @ W + b

    def _L0_attn_ref(x, w_qkv, w_proj, b_proj):
        import jax, jax.numpy as jnp
        import numpy as np
        DIM = 192
        HEADS = 12
        HEAD_DIM = DIM // HEADS
        EPS = 1e-12

        def _l1_normalize(t):
            denom = jnp.maximum(jnp.sum(jnp.abs(t), axis=-2, keepdims=True), EPS)
            return t / denom
        B, N, C = x.shape
        hd = C // HEADS
        qkv = x @ w_qkv.T
        qkv = qkv.reshape(B, N, 3, HEADS, hd).transpose(2, 0, 3, 1, 4)
        q, k, v = (qkv[0], qkv[1], qkv[2])
        q = _l1_normalize(q)
        k = _l1_normalize(k)
        if N < hd:
            out = jnp.einsum('bhnd,bhmd,bhme->bhne', q, k, v)
        else:
            kv = jnp.einsum('bhnd,bhne->bhde', k, v)
            out = jnp.einsum('bhnd,bhde->bhne', q, kv)
        out = out.transpose(0, 2, 1, 3).reshape(B, N, C)
        return out @ w_proj.T + b_proj

    def _L0_ffn_ref(x, gate_w, w13, w2, norm_w):
        import jax, jax.numpy as jnp
        import numpy as np
        import math
        B, S, D = (4, 1024, 192)
        E = 8
        TOP_K = 2
        H = 512
        CAP_F = 1.25
        EPS = 1e-06
        ALPHA = 1.0
        Bx, Sx, Dx = x.shape
        N = Bx * Sx
        cap = int(math.ceil(CAP_F * TOP_K * N / E))
        xf = x.reshape(N, Dx)
        logits = xf.astype(jnp.float32) @ gate_w.T
        probs = jax.nn.softmax(logits, axis=-1)
        top_p, top_i = jax.lax.top_k(probs, TOP_K)
        w = top_p / jnp.sum(top_p, axis=-1, keepdims=True)
        flat_e = top_i.reshape(-1)
        onehot = jax.nn.one_hot(flat_e, E, dtype=jnp.int32)
        pos = jnp.take_along_axis(jnp.cumsum(onehot, axis=0) - 1, flat_e[:, None], axis=1)[:, 0]
        keep = pos < cap
        didx = flat_e * cap + jnp.minimum(pos, cap - 1)
        safe = jnp.where(keep, didx, E * cap)
        x_rep = jnp.repeat(xf, TOP_K, axis=0)
        buf = jnp.zeros((E * cap + 1, Dx), x.dtype).at[safe].set(x_rep)
        buf = buf[:-1].reshape(E, cap, Dx)
        z = 2.0 * buf
        z = z * jax.lax.rsqrt(jnp.mean(z * z, axis=-1, keepdims=True) + EPS)
        z = z * norm_w[:, None, :]
        gu = jnp.einsum('ecd,ehd->ech', z, w13)
        g, u = jnp.split(gu, 2, axis=-1)
        y = buf + ALPHA * jnp.einsum('ech,edh->ecd', jax.nn.silu(g) * u, w2)
        y_tok = y.reshape(E * cap, Dx)[didx]
        cw = (w.reshape(-1) * keep.astype(w.dtype)).astype(x.dtype)
        out = (cw[:, None] * y_tok).reshape(N, TOP_K, Dx).sum(axis=1)
        return out.reshape(Bx, Sx, Dx)

    def _L1_attn_ref(hidden_states, in_proj_w, conv_w, conv_b, x_proj_w, dt_head_w, dt_head_b, out_proj_w, D):
        import jax, jax.numpy as jnp
        import numpy as np
        BETA, ALPHA, NS_STEPS = (0.9, 1.0, 1)
        D_MODEL, D_STATE, D_CONV, EXPAND = (192, 16, 4, 2)
        D_INNER = EXPAND * D_MODEL
        DT_RANK = -(-D_MODEL // 16)
        B, L = (2, 256)

        def _newton_schulz(G, steps):
            a, b, c = (3.4445, -4.775, 2.0315)
            X = G / (jnp.linalg.norm(G, axis=(-2, -1), keepdims=True) + 1e-07)
            X = X.swapaxes(-2, -1)
            for _ in range(steps):
                A = X @ X.swapaxes(-2, -1)
                Bm = b * A + c * (A @ A)
                X = a * X + Bm @ X
            return X.swapaxes(-2, -1)
        Bz, Lz, _ = hidden_states.shape
        dtype = hidden_states.dtype
        xz = jnp.einsum('bld,ed->ble', hidden_states, in_proj_w)
        x, z = jnp.split(xz, 2, axis=-1)
        xc = jax.lax.conv_general_dilated(x.swapaxes(1, 2), conv_w, (1,), [(D_CONV - 1, 0)], dimension_numbers=('NCH', 'OIH', 'NCH'), feature_group_count=D_INNER)
        x = jax.nn.silu(xc.swapaxes(1, 2) + conv_b)
        x_dbl = jnp.einsum('bld,ed->ble', x, x_proj_w)
        dt_low, k, q = jnp.split(x_dbl, [DT_RANK, DT_RANK + D_STATE], axis=-1)
        dt = jnp.einsum('blr,dr->bld', dt_low, dt_head_w)

        def step(carry, inp):
            v, h = carry
            x_t, dt_t, k_t, q_t = inp
            dt_t = jax.nn.sigmoid(dt_t + dt_head_b)
            dt_t = dt_t / (1.0 + dt_t * jnp.sum(k_t * k_t, axis=-1, keepdims=True))
            dA = 1.0 - dt_t[:, :, None] * (k_t * k_t)[:, None, :]
            G = (dt_t * x_t)[:, :, None] * k_t[:, None, :]
            v = BETA * v + ALPHA * _newton_schulz(G, NS_STEPS)
            h = dA * h + v
            y_t = jnp.einsum('bdn,bn->bd', h, q_t) + D * x_t
            return ((v, h), y_t)
        init = (jnp.zeros((Bz, D_INNER, D_STATE), dtype), jnp.zeros((Bz, D_INNER, D_STATE), dtype))
        xs = (x.swapaxes(0, 1), dt.swapaxes(0, 1), k.swapaxes(0, 1), q.swapaxes(0, 1))
        _, y = jax.lax.scan(step, init, xs)
        y = y.swapaxes(0, 1) * jax.nn.silu(z)
        return jnp.einsum('bld,od->blo', y, out_proj_w)

    def _L1_ffn_ref(x, gumbel_weights, n1l_g, n1l_b, n1s_g, n1s_b, w_qkv, w_proj, b_proj, n2l_g, n2l_b, n2s_g, n2s_b, w_fc1, b_fc1, w_fc2, b_fc2):
        import jax, jax.numpy as jnp
        import numpy as np
        H = 12
        ALPHA = (1, 2, 3)
        DEPTH = 5
        BLOCK_DEPTH = 3
        TOTAL_DEPTH_M1 = 14 - 1
        SMALL_ACTIVE = BLOCK_DEPTH <= DEPTH <= TOTAL_DEPTH_M1 - BLOCK_DEPTH

        def _ln(x, g, b, eps=1e-05):
            m = jnp.mean(x, axis=-1, keepdims=True)
            v = jnp.mean((x - m) ** 2, axis=-1, keepdims=True)
            return (x - m) * jax.lax.rsqrt(v + eps) * g + b

        def _attn_branch(xp, w_qkv, w_proj, b_proj, keep_heads, keep_ch):
            B2, N, C = xp.shape
            hd = C // H
            scale = hd ** (-0.5)
            qkv = (xp @ w_qkv).reshape(B2, N, 3, H, hd).transpose(2, 0, 3, 1, 4)
            hmask = (jnp.arange(H) < keep_heads).astype(xp.dtype)[None, :, None, None]
            q, k, v = (qkv[0] * hmask, qkv[1] * hmask, qkv[2] * hmask)
            a = jax.nn.softmax(jnp.einsum('bhnd,bhmd->bhnm', q, k) * scale, axis=-1)
            o = jnp.einsum('bhnm,bhmd->bhnd', a, v).transpose(0, 2, 1, 3).reshape(B2, N, C)
            o = o @ w_proj + b_proj
            cmask = (jnp.arange(C) < keep_ch).astype(xp.dtype)
            return o * cmask

        def _mlp_branch(xp, w1, b1, w2, b2, keep_ch):
            C = xp.shape[-1]
            cmask = (jnp.arange(C) < keep_ch).astype(xp.dtype)
            h = jax.nn.gelu(xp * cmask @ w1 + b1, approximate=False)
            return (h @ w2 + b2) * cmask
        B, N, C = x.shape
        B2 = B // 2
        nl = _ln(x[:B2], n1l_g, n1l_b)
        ns = _ln(x[B2:], n1s_g, n1s_b)
        a_large = _attn_branch(nl, w_qkv, w_proj, b_proj, H, C)
        if SMALL_ACTIVE:
            a_small = sum((gumbel_weights[i] * _attn_branch(ns, w_qkv, w_proj, b_proj, H // ALPHA[i], C // ALPHA[i]) for i in range(3)))
            attn_out = jnp.concatenate([a_large, a_small], axis=0)
        else:
            attn_out = jnp.concatenate([a_large, a_large], axis=0)
        x = x + attn_out
        nl2 = _ln(x[:B2], n2l_g, n2l_b)
        ns2 = _ln(x[B2:], n2s_g, n2s_b)
        m_large = _mlp_branch(nl2, w_fc1, b_fc1, w_fc2, b_fc2, C)
        if SMALL_ACTIVE:
            m_small = sum((gumbel_weights[i] * _mlp_branch(ns2, w_fc1, b_fc1, w_fc2, b_fc2, C // ALPHA[i]) for i in range(3)))
            mlp_out = jnp.concatenate([m_large, m_small], axis=0)
        else:
            mlp_out = jnp.concatenate([m_large, m_large], axis=0)
        return x + mlp_out
    h = _L0_tok_ref(x, L0_tok_W, L0_tok_b)
    h = jnp.concatenate([h, txt], axis=1)
    h = h + _L0_attn_ref(_layernorm(h, axis=-1), L0_attn_w_qkv, L0_attn_w_proj, L0_attn_b_proj)
    h = h + _L0_ffn_ref(_layernorm(h, axis=-1), L0_ffn_gate_w, L0_ffn_w13, L0_ffn_w2, L0_ffn_norm_w)
    h = h + _L1_attn_ref(_layernorm(h, axis=-1), L1_attn_in_proj_w, L1_attn_conv_w, L1_attn_conv_b, L1_attn_x_proj_w, L1_attn_dt_head_w, L1_attn_dt_head_b, L1_attn_out_proj_w, L1_attn_D)
    h = h + _L1_ffn_ref(_layernorm(h, axis=-1), L1_ffn_gumbel_weights, L1_ffn_n1l_g, L1_ffn_n1l_b, L1_ffn_n1s_g, L1_ffn_n1s_b, L1_ffn_w_qkv, L1_ffn_w_proj, L1_ffn_b_proj, L1_ffn_n2l_g, L1_ffn_n2l_b, L1_ffn_n2s_g, L1_ffn_n2s_b, L1_ffn_w_fc1, L1_ffn_b_fc1, L1_ffn_w_fc2, L1_ffn_b_fc2)
    return h

_drawn_inputs = setup_inputs


def setup_inputs(seed=0):
    import zlib

    import numpy as np

    out = dict(_drawn_inputs(seed))
    spreads = {'L0_tok_b': (0.0, 0.1),
     'L0_attn_b_proj': (0.0, 0.1),
     'L0_ffn_norm_w': (1.0, 0.6),
     'L1_attn_conv_b': (0.0, 0.8),
     'L1_attn_D': (1.0, 0.6),
     'L1_ffn_n1l_g': (1.0, 0.6),
     'L1_ffn_n1l_b': (0.0, 0.8),
     'L1_ffn_n1s_g': (1.0, 0.6),
     'L1_ffn_n1s_b': (0.0, 0.8),
     'L1_ffn_b_proj': (0.0, 2.0),
     'L1_ffn_n2l_g': (1.0, 0.6),
     'L1_ffn_n2l_b': (0.0, 2.0),
     'L1_ffn_n2s_g': (1.0, 0.6),
     'L1_ffn_n2s_b': (0.0, 2.0),
     'L1_ffn_b_fc1': (0.0, 2.0),
     'L1_ffn_b_fc2': (0.0, 2.0)}
    factors = {'L0_attn_w_qkv': 8.0,
     'L0_attn_w_proj': 8.0,
     'L0_ffn_gate_w': 8.0,
     'L0_ffn_w13': 8.0,
     'L0_ffn_w2': 8.0,
     'L1_attn_dt_head_w': 64.0,
     'L1_attn_dt_head_b': 64.0,
     'L1_ffn_gumbel_weights': 8.0,
     'L1_ffn_w_qkv': 8.0,
     'L1_ffn_w_proj': 8.0,
     'L1_ffn_w_fc1': 9.502,
     'L1_ffn_w_fc2': 2.701,
     'L1_attn_in_proj_w': 8.0,
     'L1_attn_conv_w': 8.0,
     'L1_attn_x_proj_w': 5.661,
     'L1_attn_out_proj_w': 8.0}
    for name, (base, spread) in spreads.items():
        noise = np.random.default_rng([zlib.crc32(name.encode()), seed]).standard_normal(out[name].shape)
        drawn = base * np.exp(spread * noise) if base else spread * noise
        out[name] = jnp.asarray(drawn.astype(out[name].dtype))
    for name, factor in factors.items():
        out[name] = (out[name] * factor).astype(out[name].dtype)
    return out
```

```python
from contextlib import ExitStack

import numpy as np
import concourse.bass as bass
from concourse import mybir

F32 = mybir.dt.float32
I32 = mybir.dt.int32
U32 = mybir.dt.uint32
ALU = mybir.AluOpType
ACT = mybir.ActivationFunctionType
AX_X = mybir.AxisListType.X

D = 192
DH = 96
N_TXT = 512
GRID = 14
N_PATCH = GRID * GRID
SEQ = N_PATCH + N_TXT
T = 118
NT = SEQ // T
G = 3 * T
QUAD_K = 8
E = 8
HID = 512
HEADS = 12
HD = 16
LN_EPS = 1e-5
MOE_EPS = 1e-6
L1_EPS = 1e-12


class Chain:

    def __init__(self, eng, sem, start=0, per=None):
        self.eng, self.sem, self.start, self.per, self.count = eng, sem, start, per, 0

    def link(self, ins):
        self.count += 1
        ins.then_inc(self.sem, 1)
        self.eng.wait_ge(self.sem, self.start + self.count)

    def close(self):
        assert self.count == self.per, (self.count, self.per)


def identity(pool, ident, sem, n):
    pool.memset(ident, 0.0).then_inc(sem, 1)
    pool.wait_ge(sem, n + 1)
    pool.affine_select(out=ident, in_=ident, compare_op=ALU.not_equal, fill=1.0, base=0,
                       pattern=[[-1, ident.shape[1]]], channel_multiplier=1).then_inc(sem, 1)


def region(q, c):
    a, b = q // 2, q % 2
    inner = [slice(1, GRID), slice(0, GRID - 1)]
    edge = [slice(0, 1), slice(GRID - 1, GRID)]
    return (edge if c & 1 else inner)[a], (edge if c & 2 else inner)[b]


DI = 384
M3 = DI // 128
NS = 16
RANK = 12
TAPS = 4
CH = 59
NC = SEQ // CH
CARRY = 64
KR = CARRY + NS
Q4 = 4
NQ = NS // Q4
BETA = 0.9
NS_A, NS_B, NS_C = 3.4445, -4.775, 2.0315
BF16 = mybir.dt.bfloat16

MLP = 768
PRODUCTS = ((0, 0), (0, 1), (1, 0), (1, 1), (0, 2), (2, 0))
QK_ROWS = HD * len(PRODUCTS)


def phase_route(nc, a, n_img, cap, h1_dram, x2_dram, slot_dram, route):
    with ExitStack() as ctx:
        def sb(name, shape, dt=F32):
            return ctx.enter_context(nc.sbuf_tensor("ra_" + name, shape, dt))

        def sem(name):
            return nc.alloc_semaphore("ra_" + name)

        def bank(name):
            return ctx.enter_context(nc.psum_tensor("ra_" + name, [128, 512], F32))

        w_copies = sb("w_copies", [DH, QUAD_K, 5, D])
        w_class = sb("w_class", [DH, QUAD_K, 4, D])
        b_tok = sb("b_tok", [DH, 2])
        wqkvT = sb("wqkvT", [DH, 2, 3 * D])
        wq = sb("wq", [DH, 2, D])
        wprojT = sb("wprojT", [DH, 2, D])
        gateT = sb("gateT", [DH, 2, E])
        b_proj = sb("b_proj", [1, D])
        ident = sb("ident", [128, 128])
        blocks = sb("blocks", [DH, DH])
        before = sb("before", [T, T])
        ones = sb("ones", [T, T])
        zero_rows = sb("zero_rows", [T, E * cap // T], I32)
        iota8 = sb("iota8", [T, E])
        tok_of_p = sb("tok_of_p", [T, NT])
        patches = sb("patches", [DH, 2, QUAD_K, N_PATCH])
        tokT = sb("tokT", [DH, 2, N_PATCH])
        x = sb("x", [T, NT, D])
        stats = sb("stats", [T, NT, 6])
        mv = sb("mv", [T, NT, 2])
        rstd = sb("rstd", [T, NT])
        z = sb("z", [T, NT, D])
        zT = sb("zT", [DH, 2, SEQ])
        scratch = sb("scratch", [DH, 4, G])
        qsum = sb("qsum", [DH, 2, 2])
        dq = sb("dq", [DH, 2])
        dk = sb("dk", [DH, 2])
        kv = sb("kv", [T, NT, 2 * D])
        kabs = sb("kabs", [T, NT, D])
        stT = sb("stT", [DH, 2, DH])
        m1 = sb("m1", [DH, 2, D])
        m2 = sb("m2", [DH, 2, D])
        h1 = sb("h1", [T, NT, D])
        x2 = sb("x2", [T, NT, D + 1])
        squares = sb("squares", [T, NT, D])
        sumsq = sb("sumsq", [T, NT])
        moe_eps = sb("moe_eps", [T, 1])
        lmax = sb("lmax", [T, NT])
        prob = sb("prob", [T, NT, E])
        top = sb("top", [T, NT, E])
        topi = sb("topi", [T, NT, E], U32)
        topf = sb("topf", [T, NT, 2])
        hot = sb("hot", [T, 2, NT, E])
        both = sb("both", [T, NT, E])
        earlier = sb("earlier", [T, NT + 1, E])
        pos = sb("pos", [T, 2, NT])
        keep = sb("keep", [T, 2, NT])
        row = sb("row", [T, 2, NT])
        slot = sb("slot", [T, 2, NT])
        slot_i = sb("slot_i", [T, 2, NT], I32)
        first_token = sb("first_token", [T, 1])
        tokid = sb("tokid", [T, NT])
        tokid_i = sb("tokid_i", [T, NT], I32)
        tmp8 = sb("tmp8", [T, 2, NT, E])
        eps_col = sb("eps_col", [T, 1])

        ps_tok, ps_a, ps_b, ps_c, ps_d, ps_e, ps_f, ps_g = (
            bank(n) for n in ("tok", "a", "b", "c", "d", "e", "f", "g"))

        weights_in = sem("weights_in")
        consts = sem("consts")
        w_chain = sem("w_chain")
        w_summed = sem("w_summed")
        table_clear = sem("table_clear")
        patches_in = [sem("patches_in0"), sem("patches_in1")]
        txt_in = sem("txt_in")
        tok_done = sem("tok_done")
        tok_biased = sem("tok_biased")
        tok_turned = sem("tok_turned")
        z_turned = sem("z_turned")
        zT_ready = sem("zT_ready")
        var_ready = sem("var_ready")
        std_ready = sem("std_ready")
        z_ready = sem("z_ready")
        q_done = sem("q_done")
        q_summed = sem("q_summed")
        kv_done = sem("kv_done")
        kv_ready = sem("kv_ready")
        kabs_ready = sem("kabs_ready")
        st_done = sem("st_done")
        st_ready = sem("st_ready")
        m1_done = sem("m1_done")
        m1_ready = sem("m1_ready")
        m2_done = sem("m2_done")
        m2_ready = sem("m2_ready")
        y_done = sem("y_done")
        h1_ready = sem("h1_ready")
        h1_out = sem("h1_out")
        x2_ready = sem("x2_ready")
        sumsq_ready = sem("sumsq_ready")
        rms_ready = sem("rms_ready")
        norm_ready = sem("norm_ready")
        x2_out = sem("x2_out")
        x2_turned = sem("x2_turned")
        x2T_ready = sem("x2T_ready")
        logits_done = sem("logits_done")
        shifted = sem("shifted")
        exped = sem("exped")
        hot_ready = sem("hot_ready")
        pos_done = sem("pos_done")
        slots_ready = sem("slots_ready")
        scattered = sem("scattered")
        lists_free = sem("lists_free")
        passed = sem("passed")
        chain = sem("chain")

        V_PER = 37
        W_IN = 7 * 16

        block = ctx.enter_context(nc.Block())

        @block.sync
        def _(sp):
            sp.dma_start(w_copies[:], a["tok_w"]).then_inc(weights_in, 16)
            sp.dma_start(b_tok[:], a["tok_b"]).then_inc(weights_in, 16)
            sp.dma_start(wqkvT[:], a["a_wqkvT"]).then_inc(weights_in, 16)
            sp.dma_start(wq[:], a["a_wqkv"][:, 0:2, :]).then_inc(weights_in, 16)
            sp.dma_start(wprojT[:], a["a_wprojT"]).then_inc(weights_in, 16)
            sp.dma_start(gateT[:], a["gateT"]).then_inc(weights_in, 16)
            sp.dma_start(b_proj[:], a["a_bproj"]).then_inc(weights_in, 16)
            sp.wait_ge(consts, 12)
            sp.dma_start(slot_dram.rearrange("(p k) one -> p (k one)", p=T), zero_rows[:]).then_inc(table_clear, 16)
            first = 2 * T - N_PATCH

            def load_patches(b, k):
                sp.dma_start(patches[:, k], a["patches"][b]).then_inc(patches_in[k], 16)

            def load_text(b):
                sp.dma_start(x[N_PATCH - T:T, 1, :], a["txt"][b, 0:first, :]).then_inc(txt_in, 16)
                sp.dma_start(x[:, 2:NT, :], a["txt"][b, first:N_TXT, :].rearrange("(t p) d -> p t d", p=T)
                             ).then_inc(txt_in, 16)

            def step(b, k, ahead):
                if ahead:
                    sp.wait_ge(tok_done, b + 1)
                    load_patches(b + 1, 1 - k)
                sp.wait_ge(h1_ready, b + 1)
                sp.dma_start(h1_dram[b], h1[:]).then_inc(h1_out, 16)
                if ahead:
                    load_text(b + 1)
                sp.wait_ge(norm_ready, b + 1)
                sp.dma_start(x2_dram[b], x2[:]).then_inc(x2_out, 16)

            sp.sem_inc(h1_out, 16)
            sp.sem_inc(x2_out, 16)
            load_patches(0, 0)
            load_text(0)
            if n_img > 2:
                with sp.Fori(0, n_img // 2 - 1) as j:
                    for k in range(2):
                        step(2 * j + k, k, True)
            step(n_img - 2, 0, True)
            step(n_img - 1, 1, False)
            sp.wait_ge(patches_in[0], 16 * (n_img // 2))
            sp.wait_ge(patches_in[1], 16 * (n_img // 2))
            sp.wait_ge(h1_out, 16 * n_img + 16)
            sp.wait_ge(x2_out, 16 * n_img + 16)

        @block.gpsimd
        def _(pool):
            identity(pool, ident[:], consts, 0)
            pool.wait_ge(consts, 2)
            pool.memset(ones[:], 1.0).then_inc(consts, 1)
            pool.memset(blocks[:], 1.0).then_inc(consts, 1)
            pool.memset(zero_rows[:], 0).then_inc(consts, 1)
            pool.memset(eps_col[:], LN_EPS)
            pool.memset(first_token[:], 0.0).then_inc(consts, 1)
            pool.iota(iota8[:], pattern=[[1, E]], base=0, channel_multiplier=0,
                      allow_small_or_imprecise_dtypes=True).then_inc(consts, 1)
            pool.memset(moe_eps[:], MOE_EPS)
            pool.iota(tok_of_p[:], pattern=[[1, NT]], base=0, channel_multiplier=NT,
                      allow_small_or_imprecise_dtypes=True).then_inc(consts, 1)
            pool.wait_ge(consts, 8)
            pool.affine_select(out=before[:], in_=ones[:], compare_op=ALU.is_gt, fill=0.0, base=0,
                               pattern=[[1, T]], channel_multiplier=-1).then_inc(consts, 1)
            heads = blocks[:].rearrange("e (h d) -> e h d", d=HD)
            pool.affine_select(out=heads, in_=heads, compare_op=ALU.is_ge, fill=0.0, base=0,
                               pattern=[[-HD, DH // HD], [0, HD]], channel_multiplier=1).then_inc(consts, 1)
            pool.wait_ge(consts, 10)
            pool.affine_select(out=heads, in_=heads, compare_op=ALU.is_ge, fill=0.0, base=HD - 1,
                               pattern=[[HD, DH // HD], [0, HD]], channel_multiplier=-1).then_inc(consts, 1)
            pool.memset(earlier[:], 0.0).then_inc(consts, 1)
            pool.wait_ge(table_clear, 16)
            pool.sem_inc(lists_free, 1)
            with pool.Fori(0, n_img) as b:
                pool.wait_ge(slots_ready, b + 1)
                pool.sem_inc(passed, 1)
                for k in range(2):
                    for t in range(NT):
                        pool.indirect_dma_start(
                            out=slot_dram, out_offset=bass.IndirectOffsetOnAxis(ap=slot_i[:, k, t:t + 1], axis=0),
                            in_=tokid_i[:, t:t + 1], in_offset=None, bounds_check=E * cap - 1,
                            oob_is_err=False).then_inc(scattered, 16)
                pool.wait_ge(scattered, 16 * 2 * NT * (b + 1))
                pool.sem_inc(lists_free, 1)

        @block.tensor
        def _(pe):
            pe.wait_ge(weights_in, W_IN)
            pe.wait_ge(consts, 12)
            pe.wait_ge(w_summed, 1)

            def tokens(b, k, j):
                pe.wait_ge(patches_in[k], 16 * (j + 1))
                for m in range(2):
                    o = ps_tok[0:DH, m * 256:m * 256 + N_PATCH].rearrange("p (y x) -> p y x", x=GRID)
                    for c in range(4):
                        for kt in range(QUAD_K):
                            ys, xs = region(kt // 2, c)
                            mv_ = patches[:, k, kt, :].rearrange("p (y x) -> p y x", x=GRID)
                            ins = pe.matmul(o[:, ys, xs], w_class[:, kt, c, m * DH:(m + 1) * DH], mv_[:, ys, xs],
                                            start=(m == 0 and c == 0 and kt == 0), stop=(c == 3 and kt == QUAD_K - 1),
                                            skip_group_check=True)
                ins.then_inc(tok_done, 1)

            def turn(src, done):
                for m in range(2):
                    for g in range(2):
                        out = (ps_b, ps_c, ps_d, ps_e)[2 * m + g]
                        for t in range(3):
                            ins = pe.transpose(out[0:DH, t * T:(t + 1) * T],
                                               src[:, 3 * g + t, m * DH:(m + 1) * DH], ident[0:T, 0:T])
                ins.then_inc(done, 1)

            with pe.Fori(0, n_img // 2) as j:
                for k in range(2):
                    b = 2 * j + k
                    tokens(b, k, j)
                    pe.wait_ge(tok_biased, b + 1)
                    for m in range(2):
                        pe.transpose(ps_a[0:T, m * DH:(m + 1) * DH], tokT[:, m, 0:T], ident[0:DH, 0:DH])
                        ins = pe.transpose(ps_a[0:N_PATCH - T, D + m * DH:D + (m + 1) * DH],
                                           tokT[:, m, T:N_PATCH], ident[0:DH, 0:DH])
                    ins.then_inc(tok_turned, 1)
                    pe.wait_ge(z_ready, b + 1)
                    turn(z, z_turned)
                    pe.wait_ge(zT_ready, 2 * b + 2)
                    for m in range(2):
                        for g in range(2):
                            out = (ps_a, ps_tok)[m][0:DH, 0:G] if g == 0 else (ps_f, ps_g)[m][0:DH, 0:G]
                            for c in range(2):
                                ins = pe.matmul(out, wqkvT[:, c, m * DH:(m + 1) * DH], zT[:, c, g * G:(g + 1) * G],
                                                start=(c == 0), stop=(c == 1))
                    ins.then_inc(q_done, 1)
                    for t in range(NT):
                        out = (ps_b, ps_c, ps_d, ps_e)[t % 4]
                        if t >= 4:
                            pe.wait_ge(kv_ready, NT * b + t - 3)
                        for c in range(2):
                            ins = pe.matmul(out[0:T, 0:2 * D], zT[:, c, t * T:(t + 1) * T], wqkvT[:, c, D:3 * D],
                                            start=(c == 0), stop=(c == 1))
                        ins.then_inc(kv_done, 1)
                    pe.wait_ge(q_summed, 4 * b + 4)
                    pe.wait_ge(kabs_ready, NT * b + NT)
                    pe.wait_ge(kv_ready, NT * b + NT)
                    for m in range(2):
                        for t in range(NT):
                            pe.matmul(ps_a[0:DH, m * DH:(m + 1) * DH], kv[:, t, D + m * DH:D + (m + 1) * DH],
                                      kv[:, t, m * DH:(m + 1) * DH], start=(t == 0), stop=(t == NT - 1))
                    for m in range(2):
                        for t in range(NT):
                            ins = pe.matmul(ps_f[0:DH, m:m + 1], kabs[:, t, m * DH:(m + 1) * DH], ones[0:T, 0:1],
                                            start=(t == 0), stop=(t == NT - 1))
                    ins.then_inc(st_done, 1)
                    pe.wait_ge(st_ready, b + 1)
                    for m in range(2):
                        ins = pe.matmul(ps_g[0:DH, m * D:(m + 1) * D], stT[:, m, :], wprojT[:, m, :],
                                        start=True, stop=True)
                    ins.then_inc(m1_done, 1)
                    pe.wait_ge(m1_ready, b + 1)
                    for c in range(2):
                        for m in range(2):
                            ins = pe.matmul(ps_a[0:DH, c * D:(c + 1) * D], wq[:, m, c * DH:(c + 1) * DH], m1[:, m, :],
                                            start=(m == 0), stop=(m == 1))
                    ins.then_inc(m2_done, 1)
                    pe.wait_ge(m2_ready, b + 1)
                    for t in range(NT):
                        out = (ps_b, ps_c, ps_d)[t // 2][0:T, (t % 2) * D:(t % 2 + 1) * D]
                        for c in range(2):
                            pe.matmul(out, zT[:, c, t * T:(t + 1) * T], m2[:, c, :], start=(c == 0), stop=False)
                        ins = pe.matmul(out, ones[0:1, 0:T], b_proj[0:1, :], start=False, stop=True)
                    ins.then_inc(y_done, 1)
                    pe.wait_ge(x2_ready, b + 1)
                    turn(x2, x2_turned)
                    pe.wait_ge(x2T_ready, 2 * b + 2)
                    for t in range(NT):
                        for c in range(2):
                            ins = pe.matmul(ps_f[0:T, t * E:(t + 1) * E], zT[:, c, t * T:(t + 1) * T], gateT[:, c, :],
                                            start=(c == 0), stop=(c == 1))
                    ins.then_inc(logits_done, 1)
                    pe.wait_ge(hot_ready, b + 1)
                    flat = ps_g[0:T, 0:NT * E]
                    pe.matmul(flat, before[:], both[:].rearrange("p t e -> p (t e)"), start=True, stop=False)
                    pe.matmul(flat, ones[:], earlier[:, 0:NT, :].rearrange("p t e -> p (t e)"),
                              start=False, stop=True).then_inc(pos_done, 1)

        @block.scalar
        def _(act):
            act.wait_ge(weights_in, W_IN)
            act.wait_ge(consts, 12)
            with act.Fori(0, n_img) as b:
                act.wait_ge(tok_done, b + 1)
                for m in range(2):
                    ins = act.activation(tokT[:, m, :], ps_tok[0:DH, m * 256:m * 256 + N_PATCH], ACT.Identity,
                                         bias=b_tok[:, m:m + 1])
                    if m == 1:
                        ins.then_inc(tok_biased, 1)
                act.wait_ge(var_ready, 2 * b + 1)
                act.activation(rstd[:], mv[:, :, 1], ACT.Sqrt, bias=eps_col[:, 0:1]).then_inc(std_ready, 1)
                act.wait_ge(z_turned, b + 1)
                act.activation(zT[:, 1, 0:G], ps_d[0:DH, 0:G], ACT.Copy)
                act.activation(zT[:, 1, G:SEQ], ps_e[0:DH, 0:G], ACT.Copy).then_inc(zT_ready, 1)
                act.wait_ge(q_done, b + 1)
                for m in range(2):
                    for g in range(2):
                        src = (ps_a, ps_tok)[m] if g == 0 else (ps_f, ps_g)[m]
                        act.activation(scratch[:, 2 * m + g, :], src[0:DH, 0:G], ACT.Abs,
                                       accum_out=qsum[:, m, g:g + 1]).then_inc(q_summed, 1)
                for t in range(NT):
                    act.wait_ge(kv_ready, NT * b + t + 1)
                    act.activation(kabs[:, t, :], kv[:, t, 0:D], ACT.Abs).then_inc(kabs_ready, 1)
                act.wait_ge(m2_done, b + 1)
                act.activation(m2[:].rearrange("p c d -> p (c d)"), ps_a[0:DH, 0:2 * D], ACT.Copy).then_inc(m2_ready, 1)
                act.wait_ge(var_ready, 2 * b + 2)
                act.activation(rstd[:], mv[:, :, 1], ACT.Sqrt, bias=eps_col[:, 0:1]).then_inc(std_ready, 1)
                act.wait_ge(x2_ready, b + 1)
                for t in range(NT):
                    ins = act.activation(squares[:, t, :], x2[:, t, 0:D], ACT.Square, scale=2.0,
                                         accum_out=sumsq[:, t:t + 1])
                ins.then_inc(sumsq_ready, 1)
                act.wait_ge(sumsq_ready, b + 1)
                act.activation(sumsq[:], sumsq[:], ACT.Sqrt, bias=moe_eps[:, 0:1], scale=1.0 / D).then_inc(rms_ready, 1)
                act.wait_ge(x2_turned, b + 1)
                act.activation(zT[:, 1, 0:G], ps_d[0:DH, 0:G], ACT.Copy)
                act.activation(zT[:, 1, G:SEQ], ps_e[0:DH, 0:G], ACT.Copy).then_inc(x2T_ready, 1)
                act.wait_ge(shifted, b + 1)
                act.activation(prob[:], prob[:], ACT.Exp).then_inc(exped, 1)

        @block.vector
        def _(dve):
            dve.wait_ge(weights_in, W_IN)
            dve.wait_ge(consts, 12)
            w = Chain(dve, w_chain)
            for q in range(4):
                qa, qb = q // 2, q % 2
                ks = slice(2 * q, 2 * q + 2)
                own_y, own_x, other_y, other_x = qa, 2 * qb, 1 - qa, 2 * (1 - qb)
                w.link(dve.tensor_tensor(w_class[:, ks, 3, :], w_copies[:, ks, 0, :],
                                         w_copies[:, ks, 1 + own_y + own_x, :], ALU.add))
                w.link(dve.tensor_tensor(w_class[:, ks, 1, :], w_class[:, ks, 3, :],
                                         w_copies[:, ks, 1 + own_y + other_x, :], ALU.add))
                w.link(dve.tensor_tensor(w_class[:, ks, 2, :], w_class[:, ks, 3, :],
                                         w_copies[:, ks, 1 + other_y + own_x, :], ALU.add))
                w.link(dve.tensor_tensor(w_class[:, ks, 0, :], w_class[:, ks, 1, :],
                                         w_copies[:, ks, 1 + other_y + own_x, :], ALU.add))
                w.link(dve.tensor_tensor(w_class[:, ks, 0, :], w_class[:, ks, 0, :],
                                         w_copies[:, ks, 1 + other_y + other_x, :], ALU.add))
            dve.sem_inc(w_summed, 1)
            with dve.Fori(0, n_img) as b:
                c = Chain(dve, chain, V_PER * b, V_PER)

                def layernorm(src, dst, n, done):
                    for t in range(NT):
                        ins = dve.bn_stats(stats[:, t, :], src[:, t, :])
                    c.link(ins)
                    dve.sem_inc(passed, 1)
                    for t in range(NT):
                        ins = dve.bn_aggr(mv[:, t, :], stats[:, t, :])
                    ins.then_inc(var_ready, 1)
                    dve.wait_ge(std_ready, 2 * b + n + 1)
                    c.link(dve.reciprocal(rstd[:], rstd[:]))
                    for t in range(NT):
                        ins = dve.tensor_scalar(dst[:, t, 0:D], src[:, t, :], mv[:, t, 0:1], rstd[:, t:t + 1],
                                                ALU.subtract, ALU.mult)
                    ins.then_inc(done, 1)

                dve.wait_ge(tok_turned, b + 1)
                dve.wait_ge(txt_in, 32 * b + 32)
                dve.tensor_copy(x[:, 0, :], ps_a[0:T, 0:D])
                c.link(dve.tensor_copy(x[0:N_PATCH - T, 1, :], ps_a[0:N_PATCH - T, D:2 * D]))
                layernorm(x, z, 0, z_ready)
                dve.wait_ge(z_turned, b + 1)
                dve.tensor_copy(zT[:, 0, 0:G], ps_b[0:DH, 0:G])
                dve.tensor_copy(zT[:, 0, G:SEQ], ps_c[0:DH, 0:G]).then_inc(zT_ready, 1)
                for t in range(NT):
                    dve.wait_ge(kv_done, NT * b + t + 1)
                    dve.tensor_copy(kv[:, t, :], (ps_b, ps_c, ps_d, ps_e)[t % 4][0:T, 0:2 * D]).then_inc(kv_ready, 1)
                dve.wait_ge(st_done, b + 1)
                dve.wait_ge(q_summed, 4 * b + 4)
                c.link(dve.tensor_tensor(dq[:], qsum[:, :, 0], qsum[:, :, 1], ALU.add))
                dve.tensor_scalar(dk[:], ps_f[0:DH, 0:2], L1_EPS, None, ALU.max)
                c.link(dve.tensor_scalar(dq[:], dq[:], L1_EPS, None, ALU.max))
                dve.reciprocal(dk[:], dk[:])
                c.link(dve.reciprocal(dq[:], dq[:]))
                for m in range(2):
                    ins = dve.tensor_tensor(stT[:, m, :], ps_a[0:DH, m * DH:(m + 1) * DH], blocks[:], ALU.mult)
                ins.then_inc(st_ready, 1)
                dve.wait_ge(m1_done, b + 1)
                for m in range(2):
                    ins = dve.tensor_scalar(m1[:, m, :], ps_g[0:DH, m * D:(m + 1) * D], dq[:, m:m + 1], dk[:, m:m + 1],
                                            ALU.mult, ALU.mult)
                ins.then_inc(m1_ready, 1)
                dve.wait_ge(y_done, b + 1)
                dve.wait_ge(h1_out, 16 * b + 16)
                for t in range(3):
                    ins = dve.tensor_tensor(h1[:, 2 * t:2 * t + 2, :],
                                            (ps_b, ps_c, ps_d)[t][0:T, 0:2 * D].rearrange("p (t d) -> p t d", d=D),
                                            x[:, 2 * t:2 * t + 2, :], ALU.add)
                ins.then_inc(h1_ready, 1)
                dve.wait_ge(h1_ready, b + 1)
                dve.wait_ge(x2_out, 16 * b + 16)
                layernorm(h1, x2, 1, x2_ready)
                dve.wait_ge(rms_ready, b + 1)
                c.link(dve.reciprocal(sumsq[:], sumsq[:]))
                dve.tensor_scalar(x2[:, :, D], sumsq[:], 2.0, None, ALU.mult).then_inc(norm_ready, 1)
                dve.wait_ge(x2_turned, b + 1)
                dve.tensor_copy(zT[:, 0, 0:G], ps_b[0:DH, 0:G])
                dve.tensor_copy(zT[:, 0, G:SEQ], ps_c[0:DH, 0:G]).then_inc(x2T_ready, 1)
                dve.wait_ge(logits_done, b + 1)
                logits = ps_f[0:T, 0:NT * E].rearrange("p (t e) -> p t e", e=E)
                c.link(dve.tensor_reduce(lmax[:], logits, AX_X, ALU.max))
                dve.tensor_tensor(prob[:], logits, lmax[:].unsqueeze(2).to_broadcast([T, NT, E]), ALU.subtract
                                  ).then_inc(shifted, 1)
                dve.wait_ge(exped, b + 1)
                c.link(dve.tensor_reduce(lmax[:], prob[:], AX_X, ALU.add))
                c.link(dve.reciprocal(lmax[:], lmax[:]))
                c.link(dve.tensor_tensor(prob[:], prob[:], lmax[:].unsqueeze(2).to_broadcast([T, NT, E]), ALU.mult))
                dve.sem_inc(passed, 1)
                for t in range(NT):
                    ins = dve.max(top[:, t, :], prob[:, t, :])
                c.link(ins)
                dve.sem_inc(passed, 1)
                for t in range(NT):
                    ins = dve.max_index(topi[:, t, :], top[:, t, :], prob[:, t, :])
                c.link(ins)
                c.link(dve.tensor_copy(topf[:], topi[:, :, 0:2]))
                for k in range(2):
                    ins = dve.tensor_tensor(hot[:, k], iota8[:].unsqueeze(1).to_broadcast([T, NT, E]),
                                            topf[:, :, k:k + 1].to_broadcast([T, NT, E]), ALU.is_equal)
                c.link(ins)
                c.link(dve.tensor_tensor(both[:], hot[:, 0], hot[:, 1], ALU.add))
                for t in range(NT):
                    ins = dve.tensor_tensor(earlier[:, t + 1, :], earlier[:, t, :], both[:, t, :], ALU.add)
                    if t < NT - 1:
                        c.link(ins)
                ins.then_inc(hot_ready, 1)
                dve.wait_ge(pos_done, b + 1)
                c.link(dve.tensor_copy(earlier[:, 0, :], earlier[:, NT, :]))
                counts = ps_g[0:T, 0:NT * E].rearrange("p (t e) -> p t e", e=E)
                for k in range(2):
                    ins = dve.tensor_tensor(tmp8[:, k], counts, hot[:, k], ALU.mult)
                c.link(ins)
                c.link(dve.tensor_reduce(pos[:], tmp8[:], AX_X, ALU.add))
                c.link(dve.tensor_scalar(keep[:], pos[:], float(cap), None, ALU.is_lt))
                c.link(dve.tensor_scalar(row[:], pos[:], float(cap - 1), None, ALU.min))
                for k in range(2):
                    ins = dve.scalar_tensor_tensor(out=row[:, k], in0=topf[:, :, k], scalar=float(cap), in1=row[:, k],
                                                   op0=ALU.mult, op1=ALU.add)
                c.link(ins)
                c.link(dve.tensor_scalar(slot[:], keep[:], -float(E * cap), float(E * cap), ALU.mult, ALU.add))
                c.link(dve.tensor_tensor(slot[:], slot[:], row[:], ALU.add))
                dve.tensor_scalar(tokid[:], tok_of_p[:], first_token[:, 0:1], None, ALU.add)
                c.link(dve.tensor_tensor(lmax[:], top[:, :, 0], top[:, :, 1], ALU.add))
                c.link(dve.reciprocal(lmax[:], lmax[:]))
                for k in range(2):
                    ins = dve.tensor_tensor(pos[:, k], top[:, :, k], lmax[:], ALU.mult)
                c.link(ins)
                c.link(dve.tensor_tensor(pos[:], pos[:], keep[:], ALU.mult))
                dve.tensor_copy(route[:, b, 0:2, :], row[:])
                c.link(dve.tensor_copy(route[:, b, 2:4, :], pos[:]))
                c.link(dve.tensor_scalar(first_token[:], first_token[:], float(SEQ), None, ALU.add))
                dve.wait_ge(lists_free, b + 1)
                dve.tensor_copy(tokid_i[:], tokid[:])
                dve.tensor_copy(slot_i[:], slot[:]).then_inc(slots_ready, 1)
                c.close()


def phase_experts(nc, a, n_img, cap, x2_dram, slot_dram, y_dram):
    steps = cap // G
    assert steps % 2 == 0 and cap % G == 0
    KT = HID // 128
    with ExitStack() as ctx:
        def sb(name, shape, dt=F32):
            return ctx.enter_context(nc.sbuf_tensor("b_" + name + "_t", shape, dt))

        def sem(name):
            return nc.alloc_semaphore("b_" + name)

        def bank(name):
            return ctx.enter_context(nc.psum_tensor("b_" + name, [128, 512], F32))

        slots = sb("slots", [T, E * 3 * steps + 3], I32)
        rows = sb("rows", [T, 2, 3], I32)
        xg = sb("xg", [T, 2, 3, D + 1])
        z = sb("z", [T, 3, D])
        zT = sb("zT", [DH, 2, G])
        w13 = sb("w13", [DH, 2, 2, 2 * HID])
        w2 = sb("w2", [128, 2, KT, D])
        norm = sb("norm", [DH, E, 2])
        gate = sb("gate", [128, 2, G])
        hidden = sb("hidden", [128, KT, G])
        y = sb("y", [T, 2, 3, D])
        ident = sb("ident", [128, 128])

        ps_z0, ps_z1, ps_g0, ps_g1, ps_u0, ps_u1, ps_y0, ps_y1 = (
            bank(n) for n in ("z0", "z1", "g0", "g1", "u0", "u1", "y0", "y1"))
        ps_g, ps_u = (ps_g0, ps_g1), (ps_u0, ps_u1)

        consts = sem("consts")
        norm_in = sem("norm_in")
        slots_in = sem("slots_in")
        w13_in = [sem("w13_in0"), sem("w13_in1")]
        w2_in = [sem("w2_in0"), sem("w2_in1")]
        w13_ready = sem("w13_ready")
        rows_ready = sem("rows_ready")
        gathered = [sem("gathered0"), sem("gathered1")]
        z_ready = sem("z_ready")
        z_turned = sem("z_turned")
        zT0_ready = sem("zT0_ready")
        zT1_ready = sem("zT1_ready")
        up_done = sem("up_done")
        gate_ready = sem("gate_ready")
        hidden_ready = sem("hidden_ready")
        y_done = sem("y_done")
        y_ready = sem("y_ready")
        y_out = [sem("y_out0"), sem("y_out1")]
        expert_done = sem("expert_done")
        passed = sem("passed")

        x_rows = x2_dram.rearrange("b p t d -> (b p t) d")
        y_steps = y_dram.rearrange("(e p g j) d -> e g p (j d)", e=E, p=T, j=3)

        block = ctx.enter_context(nc.Block())

        @block.sync
        def _(sp):
            def weights(e, k):
                sp.dma_start(w13[:, k], a["w13T"][e]).then_inc(w13_in[k], 16)
                sp.dma_start(w2[:, k], a["w2T"][e]).then_inc(w2_in[k], 16)

            def stores(e):
                with sp.Fori(0, steps // 2) as h:
                    for k in range(2):
                        sp.wait_ge(y_ready, steps * e + 2 * h + k + 2)
                        sp.dma_start(y_steps[e, 2 * h + k], y[:, k].rearrange("p j d -> p (j d)")).then_inc(y_out[k], 16)

            sp.dma_start(norm[:], a["norm_w"]).then_inc(norm_in, 16)
            sp.wait_ge(consts, 3)
            sp.dma_start(slots[:, 0:E * 3 * steps].rearrange("p (e k) -> p e k", e=E),
                         slot_dram.rearrange("(e p k) one -> p e (k one)", e=E, p=T)).then_inc(slots_in, 16)
            weights(0, 0)
            weights(1, 1)
            sp.sem_inc(y_out[0], 16)
            sp.sem_inc(y_out[1], 16)
            with sp.Fori(0, E // 2 - 1) as j:
                for k in range(2):
                    stores(2 * j + k)
                    sp.wait_ge(expert_done, 2 * j + k + 1)
                    weights(2 * j + k + 2, k)
            for k in range(2):
                stores(E - 2 + k)
            for k in range(2):
                sp.wait_ge(y_out[k], 16 * (E * steps // 2 + 1))

        @block.gpsimd
        def _(pool):
            identity(pool, ident[:], consts, 0)
            pool.memset(slots[:, E * 3 * steps:], 0).then_inc(consts, 1)
            pool.wait_ge(slots_in, 16)
            pool.wait_ge(norm_in, 16)

            def gather(s, k):
                pool.tensor_copy(rows[:, k, :], slots[:, bass.ds(3 * s, 3)]).then_inc(rows_ready, 1)
                pool.wait_ge(rows_ready, s + 1)
                pool.sem_inc(passed, 1)
                for i in range(3):
                    pool.indirect_dma_start(out=xg[:, k, i, :], out_offset=None, in_=x_rows,
                                            in_offset=bass.IndirectOffsetOnAxis(ap=rows[:, k, i:i + 1], axis=0),
                                            ).then_inc(gathered[k], 16)

            gather(0, 0)
            with pool.Fori(0, E // 2) as j:
                for ke in range(2):
                    e = 2 * j + ke
                    pool.wait_ge(w13_in[ke], 16 * j + 16)
                    pool.sem_inc(passed, 1)
                    for m in range(2):
                        ins = pool.tensor_tensor(w13[:, ke, m, :], w13[:, ke, m, :],
                                                 norm[:, bass.ds(e, 1), m].to_broadcast([DH, 2 * HID]), ALU.mult)
                    ins.then_inc(w13_ready, 1)
                    with pool.Fori(0, steps // 2) as h:
                        for k in range(2):
                            s = steps * e + 2 * h + k
                            pool.wait_ge(y_ready, s + 1)
                            pool.sem_inc(passed, 1)
                            gather(s + 1, 1 - k)
            pool.wait_ge(gathered[0], 48 * (E * steps // 2 + 1))
            pool.wait_ge(gathered[1], 48 * (E * steps // 2))

        @block.tensor
        def _(pe):
            pe.wait_ge(consts, 2)

            def turn(n):
                pe.wait_ge(z_ready, n)
                for m in range(2):
                    for t in range(3):
                        ins = pe.transpose((ps_z0, ps_z1)[m][0:DH, t * T:(t + 1) * T],
                                           z[:, t, m * DH:(m + 1) * DH], ident[0:T, 0:T])
                ins.then_inc(z_turned, 1)

            turn(1)
            with pe.Fori(0, E // 2) as j:
                for ke in range(2):
                    e = 2 * j + ke
                    pe.wait_ge(w13_ready, e + 1)
                    pe.wait_ge(w2_in[ke], 16 * j + 16)
                    pe.sem_inc(passed, 1)
                    with pe.Fori(0, steps) as h:
                        s = steps * e + h
                        pe.wait_ge(zT0_ready, s + 1)
                        pe.wait_ge(zT1_ready, s + 1)
                        for i in range(KT):
                            pe.wait_ge(hidden_ready, 4 * s + i + 1)
                            for ps, off in ((ps_g, 0), (ps_u, HID)):
                                for c in range(2):
                                    ins = pe.matmul(ps[i % 2][:, 0:G], w13[:, ke, c, off + i * 128:off + (i + 1) * 128],
                                                    zT[:, c, :], start=(c == 0), stop=(c == 1))
                            ins.then_inc(up_done, 1)
                        turn(s + 2)
                        pe.wait_ge(y_ready, s + 1)
                        for i in range(KT):
                            pe.wait_ge(hidden_ready, 4 * s + i + 3)
                            for t in range(3):
                                out = ps_y0[0:T, t * D:(t + 1) * D] if t < 2 else ps_y1[0:T, 0:D]
                                ins = pe.matmul(out, hidden[:, i, t * T:(t + 1) * T], w2[:, ke, i, :],
                                                start=(i == 0 and t != 1), stop=(i == KT - 1), skip_group_check=True)
                        ins.then_inc(y_done, 1)
                    pe.sem_inc(passed, 1)
                    pe.wait_ge(y_done, steps * (e + 1))
                    pe.sem_inc(expert_done, 1)

        @block.scalar
        def _(act):
            act.wait_ge(z_turned, 1)
            act.activation(zT[:, 1, :], ps_z1[0:DH, 0:G], ACT.Copy).then_inc(zT1_ready, 1)
            with act.Fori(0, E * steps) as s:
                for i in range(KT):
                    act.wait_ge(up_done, 4 * s + i + 1)
                    act.wait_ge(hidden_ready, 4 * s + i + 1)
                    act.activation(gate[:, i % 2, :], ps_g[i % 2][:, 0:G], ACT.Silu).then_inc(gate_ready, 1)
                act.wait_ge(z_turned, s + 2)
                act.activation(zT[:, 1, :], ps_z1[0:DH, 0:G], ACT.Copy).then_inc(zT1_ready, 1)

        @block.vector
        def _(dve):
            dve.sem_inc(hidden_ready, 2)
            dve.sem_inc(y_ready, 1)

            def normed(k, count):
                dve.wait_ge(gathered[k], count)
                dve.tensor_tensor(z[:], xg[:, k, :, 0:D], xg[:, k, :, D:D + 1].to_broadcast([T, 3, D]), ALU.mult
                                  ).then_inc(z_ready, 1)

            def turned(s):
                dve.wait_ge(z_turned, s + 1)
                dve.tensor_copy(zT[:, 0, :], ps_z0[0:DH, 0:G]).then_inc(zT0_ready, 1)

            normed(0, 48)
            turned(0)
            with dve.Fori(0, E * steps // 2) as h:
                for k in range(2):
                    s = 2 * h + k
                    for i in range(KT):
                        if i == 2:
                            normed(1 - k, 48 * (h + k) + 48)
                        dve.wait_ge(gate_ready, 4 * s + i + 1)
                        dve.tensor_tensor(hidden[:, i, :], gate[:, i % 2, :], ps_u[i % 2][:, 0:G], ALU.mult
                                          ).then_inc(hidden_ready, 1)
                    turned(s + 1)
                    dve.wait_ge(y_done, s + 1)
                    dve.wait_ge(y_out[k], 16 * h + 16)
                    dve.tensor_tensor(y[:, k, 0:2, :], ps_y0[0:T, 0:2 * D].rearrange("p (t d) -> p t d", d=D),
                                      xg[:, k, 0:2, 0:D], ALU.add)
                    dve.tensor_tensor(y[:, k, 2, :], ps_y1[0:T, 0:D], xg[:, k, 2, 0:D], ALU.add).then_inc(y_ready, 1)


def phase_prepare(nc, a, n_img, h1_dram, y_dram, route, h2_dram, u_dram, ak_dram, delta_dram, kq_dram, dx_dram, zs_dram):
    with ExitStack() as ctx:
        def sb(name, shape, dt=F32):
            return ctx.enter_context(nc.sbuf_tensor("c_" + name + "_t", shape, dt))

        def sem(name):
            return nc.alloc_semaphore("c_" + name)

        inT = sb("inT", [DH, 2, 2 * DI])
        xprojT = sb("xprojT", [128, M3, 80])
        dtheadT = sb("dtheadT", [CARRY + RANK, DI])
        conv_w = sb("conv_w", [128, M3, TAPS])
        conv_b = sb("conv_b", [128, M3])
        dt_b = sb("dt_b", [128, M3])
        d_skip = sb("d_skip", [128, M3])
        decay = sb("decay", [CH, 1])
        ck = sb("ck", [KR, NC, NS])
        ident = sb("ident", [128, 128])
        ones = sb("ones", [NS, 128])
        eps_col = sb("eps_col", [T, 1])
        rows = sb("rows", [T, 2, NT], I32)
        shares = sb("shares", [T, 2, NT])
        yg = sb("yg", [T, 2, NT, D])
        h = sb("h", [T, NT, D])
        h2 = sb("h2", [T, NT, D])
        stats = sb("stats", [T, NT, 6])
        mv = sb("mv", [T, NT, 2])
        rstd = sb("rstd", [T, NT])
        z = sb("z", [T, NT, D])
        zT = sb("zT", [DH, 2, SEQ])
        xpad = sb("xpad", [128, M3, SEQ + TAPS - 1])
        xc = sb("xc", [128, M3, SEQ])
        xs = sb("xs", [128, M3, SEQ])
        zs = sb("zs", [128, M3, SEQ])
        dx = sb("dx", [128, M3, SEQ])
        xd = sb("xd", [80, SEQ])
        dts = sb("dts", [128, M3, SEQ])
        den = sb("den", [128, M3, SEQ])
        delta = sb("delta", [128, M3, SEQ])
        u = sb("u", [128, M3, SEQ])
        kq = sb("kq", [NS, 2, SEQ])
        rest = sb("rest", [NS, 2, SEQ])
        mid = sb("mid", [NS, 2, SEQ], BF16)
        split = sb("split", [80, 2, SEQ], BF16)
        uT = sb("uT", [KR, NC, DI])
        squares = sb("squares", [CH, 2, DI])
        u2 = sb("u2", [CH, NC])
        kT = sb("kT", [CH, NC, NS])
        kTsq = sb("kTsq", [CH, NC, NS])
        k2 = sb("k2", [CH, NC])
        g2 = sb("g2", [CH, NC])
        gn = sb("gn", [CH, NC])
        gr = sb("gr", [CH, NC])
        alpha = sb("alpha", [CH, NC])
        ak = sb("ak", [CH, NC, NS])

        ps = [ctx.enter_context(nc.psum_tensor(f"c_ps{n}", [128, 512], F32)) for n in range(8)]

        weights_in = sem("weights_in")
        consts = sem("consts")
        rows_ready = sem("rows_ready")
        rows_used = sem("rows_used")
        gathered = sem("gathered")
        h1_in = sem("h1_in")
        h1_used = sem("h1_used")
        h2_ready = sem("h2_ready")
        var_ready = sem("var_ready")
        std_ready = sem("std_ready")
        z_ready = sem("z_ready")
        z_turned = sem("z_turned")
        zT0_ready = sem("zT0_ready")
        zT1_ready = sem("zT1_ready")
        in_done = sem("in_done")
        x_copied = sem("x_copied")
        zs_ready = sem("zs_ready")
        conv_ready = sem("conv_ready")
        xs_ready = sem("xs_ready")
        xd_done = sem("xd_done")
        xd_ready = sem("xd_ready")
        dt_done = sem("dt_done")
        dts_ready = sem("dts_ready")
        ksq_ready = sem("ksq_ready")
        ksq_done = sem("ksq_done")
        den_mul = sem("den_mul")
        den_ready = sem("den_ready")
        delta_ready = sem("delta_ready")
        u_ready = sem("u_ready")
        u_turned = sem("u_turned")
        uT_copied = sem("uT_copied")
        u2_ready = sem("u2_ready")
        k_turned = sem("k_turned")
        g2_ready = sem("g2_ready")
        g_ready = sem("g_ready")
        ck_ready = sem("ck_ready")
        carry_done = sem("carry_done")
        carry_ready = sem("carry_ready")
        dx_ready = sem("dx_ready")
        split_ready = sem("split_ready")
        stored = {n: sem("stored_" + n) for n in ("h2", "u", "ak", "delta", "kq", "dx", "zs")}
        chain = sem("chain")
        pchain = sem("pchain")
        passed = sem("passed")
        V_PER = 31
        W_IN = 9 * 16

        y_rows = y_dram
        block = ctx.enter_context(nc.Block())

        @block.sync
        def _(sp):
            for dst, src in ((inT, "inT"), (xprojT, "xprojT"), (conv_w, "conv_w"), (conv_b, "conv_b"), (dt_b, "dt_b"),
                             (d_skip, "d_skip"), (decay, "decay")):
                sp.dma_start(dst[:], a[src]).then_inc(weights_in, 16)
            sp.dma_start(dtheadT[CARRY:, :], a["dtheadT"]).then_inc(weights_in, 16)
            sp.dma_start(ck[CARRY:, :, :], a["carry_decay"]).then_inc(weights_in, 16)
            for s in stored.values():
                sp.sem_inc(s, 16)
            with sp.Fori(0, n_img) as b:
                sp.wait_ge(h1_used, b + 1)
                sp.dma_start(h[:], h1_dram[b]).then_inc(h1_in, 16)
                sp.wait_ge(h2_ready, b + 1)
                sp.dma_start(h2_dram[b], h2[:]).then_inc(stored["h2"], 16)
                sp.wait_ge(zs_ready, 6 * b + 6)
                sp.dma_start(zs_dram[b], zs[:]).then_inc(stored["zs"], 16)
                sp.wait_ge(dx_ready, b + 1)
                sp.dma_start(dx_dram[b], dx[:]).then_inc(stored["dx"], 16)
                sp.wait_ge(delta_ready, b + 1)
                sp.dma_start(delta_dram[b], delta[:]).then_inc(stored["delta"], 16)
                sp.wait_ge(split_ready, 3 * b + 3)
                sp.dma_start(kq_dram[b], split[:]).then_inc(stored["kq"], 16)
                sp.wait_ge(ck_ready, b + 1)
                sp.dma_start(ak_dram[b], ak[:]).then_inc(stored["ak"], 16)
                sp.wait_ge(carry_ready, (NC - 1) * (b + 1))
                sp.dma_start(u_dram[b], uT[:]).then_inc(stored["u"], 16)
            for s in stored.values():
                sp.wait_ge(s, 16 * n_img + 16)

        @block.gpsimd
        def _(pool):
            identity(pool, ident[:], consts, 0)
            pool.memset(ones[:], 1.0)
            pool.memset(eps_col[:], LN_EPS)
            pool.memset(xpad[:], 0.0)
            pool.memset(split[:], 0.0)
            pool.memset(uT[:], 0.0)
            pool.memset(ck[0:CARRY], 0.0).then_inc(consts, 1)
            pool.sem_inc(rows_used, 1)
            with pool.Fori(0, n_img) as b:
                pool.wait_ge(rows_ready, b + 1)
                pool.sem_inc(passed, 1)
                for k in range(2):
                    for t in range(NT):
                        pool.indirect_dma_start(out=yg[:, k, t, :], out_offset=None, in_=y_rows,
                                                in_offset=bass.IndirectOffsetOnAxis(ap=rows[:, k, t:t + 1], axis=0),
                                                ).then_inc(gathered, 16)
                pool.wait_ge(delta_ready, b + 1)
                pool.sem_inc(passed, 1)
                pool.tensor_tensor(u[:], delta[:], xs[:], ALU.mult).then_inc(u_ready, 1)

        @block.tensor
        def _(pe):
            pe.wait_ge(weights_in, W_IN)
            pe.wait_ge(consts, 3)
            with pe.Fori(0, n_img) as b:
                pe.wait_ge(z_ready, b + 1)
                for m in range(2):
                    for g in range(2):
                        for t in range(3):
                            ins = pe.transpose(ps[2 * m + g][0:DH, t * T:(t + 1) * T],
                                               z[:, 3 * g + t, m * DH:(m + 1) * DH], ident[0:T, 0:T])
                ins.then_inc(z_turned, 1)
                pe.wait_ge(zT0_ready, b + 1)
                pe.wait_ge(zT1_ready, b + 1)
                for m in range(2 * M3):
                    for g in range(2):
                        n = 2 * m + g
                        if 4 <= n < 10:
                            pe.wait_ge(x_copied, 6 * b + n - 3)
                        elif n >= 10:
                            pe.wait_ge(zs_ready, 6 * b + n - 9)
                        for c in range(2):
                            ins = pe.matmul(ps[4 + n % 4][:, 0:G], inT[:, c, m * 128:(m + 1) * 128],
                                            zT[:, c, g * G:(g + 1) * G], start=(c == 0), stop=(c == 1))
                        ins.then_inc(in_done, 1)
                pe.wait_ge(xs_ready, M3 * b + M3)
                for g in range(2):
                    for m in range(M3):
                        ins = pe.matmul(ps[g][0:80, 0:G], xprojT[:, m, :], xs[:, m, g * G:(g + 1) * G],
                                        start=(m == 0), stop=(m == M3 - 1))
                    ins.then_inc(xd_done, 1)
                pe.wait_ge(xd_ready, 2 * b + 2)
                for m in range(M3):
                    for g in range(2):
                        n = 2 * m + g
                        if n < 4:
                            pe.wait_ge(zs_ready, 6 * b + 6)
                        else:
                            pe.wait_ge(dts_ready, 6 * b + n - 3)
                        pe.matmul(ps[4 + n % 4][:, 0:G], dtheadT[CARRY:, m * 128:(m + 1) * 128],
                                  xd[CARRY:CARRY + RANK, g * G:(g + 1) * G], start=True, stop=True
                                  ).then_inc(dt_done, 1)
                pe.wait_ge(ksq_ready, b + 1)
                for g in range(2):
                    ins = pe.matmul(ps[2 + g][:, 0:G], ones[:, :], kq[:, 0, g * G:(g + 1) * G], start=True, stop=True)
                ins.then_inc(ksq_done, 1)
                for c in range(NC):
                    ins = pe.transpose(ps[0][0:CH, c * NS:(c + 1) * NS], xd[0:NS, c * CH:(c + 1) * CH], ident[0:NS, 0:NS])
                ins.then_inc(k_turned, 1)
                pe.wait_ge(u_ready, b + 1)
                pe.wait_ge(dts_ready, 6 * b + 6)
                for c in range(NC):
                    if c >= 4:
                        pe.wait_ge(uT_copied, NC * b + c - 3)
                    pe.sem_inc(passed, 1)
                    for m in range(M3):
                        ins = pe.transpose(ps[4 + c % 4][0:CH, m * 128:(m + 1) * 128], u[:, m, c * CH:(c + 1) * CH],
                                           ident[:])
                    ins.then_inc(u_turned, 1)
                pe.wait_ge(ck_ready, b + 1)
                pe.wait_ge(uT_copied, NC * b + NC)
                for c in range(NC - 1):
                    if c:
                        pe.wait_ge(carry_ready, (NC - 1) * b + c)
                    pe.matmul(ps[1][0:NS, 0:DI], ck[:, c, :], uT[:, c, :], start=True, stop=True).then_inc(carry_done, 1)

        @block.scalar
        def _(act):
            act.wait_ge(weights_in, W_IN)
            act.wait_ge(consts, 3)
            with act.Fori(0, n_img) as b:
                act.wait_ge(var_ready, b + 1)
                act.activation(rstd[:], mv[:, :, 1], ACT.Sqrt, bias=eps_col[:, 0:1]).then_inc(std_ready, 1)
                act.wait_ge(z_turned, b + 1)
                act.activation(zT[:, 1, 0:G], ps[2][0:DH, 0:G], ACT.Copy)
                act.activation(zT[:, 1, G:SEQ], ps[3][0:DH, 0:G], ACT.Copy).then_inc(zT1_ready, 1)
                act.wait_ge(stored["zs"], 16 * b + 16)
                for m in range(M3):
                    for g in range(2):
                        n = 2 * m + g
                        act.wait_ge(in_done, 12 * b + 6 + n + 1)
                        act.activation(zs[:, m, g * G:(g + 1) * G], ps[4 + (n + 6) % 4][:, 0:G], ACT.Silu
                                       ).then_inc(zs_ready, 1)
                for m in range(M3):
                    act.wait_ge(conv_ready, M3 * b + m + 1)
                    act.activation(xs[:, m, :], xc[:, m, :], ACT.Silu, bias=conv_b[:, m:m + 1]).then_inc(xs_ready, 1)
                for g in range(2):
                    act.wait_ge(xd_done, 2 * b + g + 1)
                    act.activation(xd[:, g * G:(g + 1) * G], ps[g][0:80, 0:G], ACT.Copy).then_inc(xd_ready, 1)
                for m in range(M3):
                    for g in range(2):
                        n = 2 * m + g
                        act.wait_ge(dt_done, 6 * b + n + 1)
                        act.activation(dts[:, m, g * G:(g + 1) * G], ps[4 + n % 4][:, 0:G], ACT.Sigmoid,
                                       bias=dt_b[:, m:m + 1]).then_inc(dts_ready, 1)
                act.wait_ge(stored["dx"], 16 * b + 16)
                act.wait_ge(xs_ready, M3 * b + M3)
                for m in range(M3):
                    ins = act.activation(dx[:, m, :], xs[:, m, :], ACT.Copy, scale=d_skip[:, m:m + 1])
                ins.then_inc(dx_ready, 1)
                act.wait_ge(den_mul, b + 1)
                act.activation(den[:], den[:], ACT.Copy, bias=1.0).then_inc(den_ready, 1)
                for c in range(NC):
                    act.wait_ge(uT_copied, NC * b + c + 1)
                    if c >= 2:
                        act.wait_ge(u2_ready, NC * b + c - 1)
                    act.activation(squares[:, c % 2, :], uT[0:CH, c, :], ACT.Square, accum_out=u2[:, c:c + 1]
                                   ).then_inc(u2_ready, 1)
                act.wait_ge(g2_ready, b + 1)
                act.activation(gn[:], g2[:], ACT.Sqrt).then_inc(g_ready, 1)

        @block.vector
        def _(dve):
            dve.wait_ge(weights_in, W_IN)
            dve.wait_ge(consts, 3)
            dve.sem_inc(h1_used, 1)
            with dve.Fori(0, n_img) as b:
                c_ = Chain(dve, chain, V_PER * b, V_PER)
                dve.tensor_copy(rows[:], route[:, bass.ds(b, 1), 0:2, :].rearrange("p one k t -> p (one k) t")
                                ).then_inc(rows_ready, 1)
                c_.link(dve.tensor_copy(shares[:], route[:, bass.ds(b, 1), 2:4, :].rearrange("p one k t -> p (one k) t")))
                dve.wait_ge(gathered, 16 * 2 * NT * (b + 1))
                for k in range(2):
                    ins = dve.tensor_tensor(yg[:, k], yg[:, k], shares[:, k, :].unsqueeze(2).to_broadcast([T, NT, D]),
                                            ALU.mult)
                c_.link(ins)
                c_.link(dve.tensor_tensor(yg[:, 0], yg[:, 0], yg[:, 1], ALU.add))
                dve.wait_ge(h1_in, 16 * b + 16)
                dve.wait_ge(stored["h2"], 16 * b + 16)
                dve.tensor_tensor(h2[:], h[:], yg[:, 0], ALU.add).then_inc(h2_ready, 1)
                dve.sem_inc(passed, 1)
                dve.wait_ge(h2_ready, b + 1)
                dve.sem_inc(h1_used, 1)
                for t in range(NT):
                    ins = dve.bn_stats(stats[:, t, :], h2[:, t, :])
                c_.link(ins)
                dve.sem_inc(passed, 1)
                for t in range(NT):
                    ins = dve.bn_aggr(mv[:, t, :], stats[:, t, :])
                ins.then_inc(var_ready, 1)
                dve.wait_ge(std_ready, b + 1)
                c_.link(dve.reciprocal(rstd[:], rstd[:]))
                for t in range(NT):
                    ins = dve.tensor_scalar(z[:, t, :], h2[:, t, :], mv[:, t, 0:1], rstd[:, t:t + 1],
                                            ALU.subtract, ALU.mult)
                ins.then_inc(z_ready, 1)
                dve.wait_ge(z_turned, b + 1)
                dve.tensor_copy(zT[:, 0, 0:G], ps[0][0:DH, 0:G])
                dve.tensor_copy(zT[:, 0, G:SEQ], ps[1][0:DH, 0:G]).then_inc(zT0_ready, 1)
                for m in range(M3):
                    for g in range(2):
                        n = 2 * m + g
                        dve.wait_ge(in_done, 12 * b + n + 1)
                        dve.tensor_copy(xpad[:, m, TAPS - 1 + g * G:TAPS - 1 + (g + 1) * G], ps[4 + n % 4][:, 0:G]
                                        ).then_inc(x_copied, 1)
                    dve.wait_ge(x_copied, 6 * b + 2 * m + 2)
                    c_.link(dve.tensor_scalar(xc[:, m, :], xpad[:, m, 0:SEQ], conv_w[:, m, 0:1], None, ALU.mult))
                    for j in range(1, TAPS):
                        ins = dve.scalar_tensor_tensor(out=xc[:, m, :], in0=xpad[:, m, j:j + SEQ],
                                                       scalar=conv_w[:, m, j:j + 1], in1=xc[:, m, :],
                                                       op0=ALU.mult, op1=ALU.add)
                        if j < TAPS - 1:
                            c_.link(ins)
                    ins.then_inc(conv_ready, 1)
                dve.wait_ge(xd_ready, 2 * b + 2)
                dve.tensor_tensor(kq[:, 0, :], xd[0:NS, :], xd[0:NS, :], ALU.mult).then_inc(ksq_ready, 1)
                c_.link(dve.tensor_copy(kq[:, 1, :], xd[32:32 + NS, :]))
                dve.wait_ge(stored["kq"], 16 * b + 16)
                dve.tensor_copy(split[0:NS], kq[:]).then_inc(split_ready, 1)
                dve.wait_ge(split_ready, 3 * b + 1)
                c_.link(dve.tensor_tensor(rest[:], kq[:], split[0:NS], ALU.subtract))
                c_.link(dve.tensor_copy(mid[:], rest[:]))
                dve.tensor_copy(split[32:32 + NS], mid[:]).then_inc(split_ready, 1)
                c_.link(dve.tensor_tensor(rest[:], rest[:], mid[:], ALU.subtract))
                dve.tensor_copy(split[64:64 + NS], rest[:]).then_inc(split_ready, 1)
                dve.wait_ge(ksq_done, b + 1)
                dve.wait_ge(dts_ready, 6 * b + 6)
                for g in range(2):
                    ins = dve.tensor_tensor(den[:, :, g * G:(g + 1) * G], dts[:, :, g * G:(g + 1) * G],
                                            ps[2 + g][:, 0:G].unsqueeze(1).to_broadcast([128, M3, G]), ALU.mult)
                ins.then_inc(den_mul, 1)
                dve.wait_ge(k_turned, b + 1)
                c_.link(dve.tensor_copy(kT[:].rearrange("p c n -> p (c n)"), ps[0][0:CH, 0:NC * NS]))
                c_.link(dve.tensor_tensor(kTsq[:], kT[:], kT[:], ALU.mult))
                c_.link(dve.tensor_reduce(k2[:], kTsq[:], AX_X, ALU.add))
                dve.wait_ge(den_ready, b + 1)
                c_.link(dve.reciprocal(den[:], den[:]))
                dve.wait_ge(stored["delta"], 16 * b + 16)
                dve.tensor_tensor(delta[:], dts[:], den[:], ALU.mult).then_inc(delta_ready, 1)
                dve.wait_ge(stored["u"], 16 * b + 16)
                for c in range(NC):
                    dve.wait_ge(u_turned, NC * b + c + 1)
                    dve.tensor_copy(uT[0:CH, c, :], ps[4 + c % 4][0:CH, 0:DI]).then_inc(uT_copied, 1)
                dve.wait_ge(u2_ready, NC * b + NC)
                dve.tensor_tensor(g2[:], u2[:], k2[:], ALU.mult).then_inc(g2_ready, 1)
                dve.wait_ge(g_ready, b + 1)
                c_.link(dve.tensor_scalar(gn[:], gn[:], 1e-7, None, ALU.add))
                c_.link(dve.reciprocal(gn[:], gn[:]))
                c_.link(dve.tensor_tensor(gr[:], gn[:], gn[:], ALU.mult))
                c_.link(dve.tensor_tensor(gr[:], gr[:], g2[:], ALU.mult))
                c_.link(dve.tensor_scalar(alpha[:], gr[:], NS_C, NS_B, ALU.mult, ALU.add))
                c_.link(dve.tensor_tensor(alpha[:], alpha[:], gr[:], ALU.mult))
                c_.link(dve.tensor_scalar(alpha[:], alpha[:], NS_A, None, ALU.add))
                c_.link(dve.tensor_tensor(alpha[:], alpha[:], gn[:], ALU.mult))
                dve.wait_ge(stored["ak"], 16 * b + 16)
                c_.link(dve.tensor_tensor(ak[:], kT[:], alpha[:].unsqueeze(2).to_broadcast([CH, NC, NS]), ALU.mult))
                dve.tensor_scalar(ck[0:CH], ak[:], decay[:, 0:1], None, ALU.mult).then_inc(ck_ready, 1)
                for c in range(NC - 1):
                    dve.wait_ge(carry_done, (NC - 1) * b + c + 1)
                    dve.tensor_copy(uT[CARRY:, c + 1, :], ps[1][0:NS, 0:DI]).then_inc(carry_ready, 1)
                c_.close()


def phase_scan(nc, a, n_img, u_dram, ak_dram, delta_dram, kq_dram, dx_dram, zs_dram, h2_dram, h3_dram):
    UNITS = NQ * M3
    PAIRS = NC // 2
    with ExitStack() as ctx:
        def sb(name, shape, dt=F32):
            return ctx.enter_context(nc.sbuf_tensor("d_" + name + "_t", shape, dt))

        def sem(name):
            return nc.alloc_semaphore("d_" + name)

        v = sb("v", [128, M3, Q4, SEQ])
        da = sb("da", [128, 2, Q4, SEQ])
        kb = sb("kb", [128, 2, Q4, SEQ])
        qb = sb("qb", [128, 2, Q4, SEQ])
        lk = sb("lk", [KR, 2, NC, Q4, CH])
        uT = sb("uT", [KR, NC, DI])
        ak = sb("ak", [CH, NC, NS])
        kq = sb("kq", [80, 2, SEQ], BF16)
        delta = sb("delta", [128, M3, SEQ])
        y = sb("y", [128, M3, SEQ])
        zs = sb("zs", [128, M3, SEQ])
        h2 = sb("h2", [T, NT, D])
        h3 = sb("h3", [T, NT, D])
        within = sb("within", [CH, CH])
        select = sb("select", [80, NS, 128], BF16)
        outT = sb("outT", [128, M3, D])
        ident = sb("ident", [128, 128])

        ps_v = [ctx.enter_context(nc.psum_tensor(f"d_v{n}", [128, 512], F32)) for n in range(4)]
        ps_y = ctx.enter_context(nc.psum_tensor("d_y", [128, 2, 512], F32))
        ps_b = ctx.enter_context(nc.psum_tensor("d_b", [128, 2, 512], F32))

        V0 = 36
        W0 = 6
        weights_in = sem("weights_in")
        consts = sem("consts")
        u_in = sem("u_in")
        ak_in = sem("ak_in")
        kq_in = sem("kq_in")
        delta_in = sem("delta_in")
        dx_in = sem("dx_in")
        zs_in = sem("zs_in")
        h2_in = sem("h2_in")
        carried_in = [sem("carried_in0"), sem("carried_in1")]
        lk_ready = sem("lk_ready")
        spread = sem("spread")
        spread_copied = sem("spread_copied")
        v_done = sem("v_done")
        v_ready = sem("v_ready")
        w_ready = sem("w_ready")
        da_ready = sem("da_ready")
        scanned = sem("scanned")
        hq_ready = sem("hq_ready")
        ysum_done = sem("ysum_done")
        y_added = sem("y_added")
        gated = sem("gated")
        out_done = sem("out_done")
        h3_ready = sem("h3_ready")
        h3_out = sem("h3_out")
        passed = sem("passed")

        block = ctx.enter_context(nc.Block())

        @block.sync
        def _(sp):
            sp.dma_start(within[:], a["within"]).then_inc(weights_in, 16)
            sp.dma_start(outT[:], a["outT"]).then_inc(weights_in, 16)
            sp.sem_inc(h3_out, 16)

            def load_first(b):
                sp.wait_ge(v_done, V0 + 12 * PAIRS * b)
                sp.dma_start(uT[:], u_dram[b]).then_inc(u_in, 16)
                sp.wait_ge(lk_ready, NQ * b + 1)
                sp.dma_start(ak[:], ak_dram[b]).then_inc(ak_in, 16)
                sp.wait_ge(spread, 8 * NQ * b + 1)
                sp.dma_start(kq[:], kq_dram[b]).then_inc(kq_in, 16)
                sp.wait_ge(w_ready, W0 + UNITS * b)
                sp.dma_start(delta[:], delta_dram[b]).then_inc(delta_in, 16)

            def image(b, ahead):
                for q in range(NQ):
                    sp.wait_ge(v_done, 12 * PAIRS * b + M3 * PAIRS * (q + 1))
                    sp.dma_start(lk[CARRY:, q % 2].rearrange("p c n t -> p (c n t)"),
                                 a["carried"][q].rearrange("p c n t -> p (c n t)")).then_inc(carried_in[q % 2], 16)
                    if q == 0:
                        sp.wait_ge(out_done, b + 1)
                        sp.dma_start(y[:], dx_dram[b]).then_inc(dx_in, 16)
                        sp.dma_start(zs[:], zs_dram[b]).then_inc(zs_in, 16)
                        sp.wait_ge(h3_ready, b + 1)
                        sp.dma_start(h2[:], h2_dram[b]).then_inc(h2_in, 16)
                if ahead:
                    load_first(b + 1)
                sp.wait_ge(h3_ready, b + 2)
                sp.dma_start(h3_dram[b], h3[:]).then_inc(h3_out, 16)

            load_first(0)
            if n_img > 1:
                with sp.Fori(0, n_img - 1) as b:
                    image(b, True)
            image(n_img - 1, False)
            sp.wait_ge(h3_out, 16 * n_img + 16)

        @block.gpsimd
        def _(pool):
            identity(pool, ident[:], consts, 0)
            pool.memset(select[:], 0.0).then_inc(consts, 1)
            for part in range(3):
                pool.wait_ge(consts, part + 3)
                pool.affine_select(out=select[:], in_=select[:], compare_op=ALU.not_equal, fill=1.0, base=-32 * part,
                                   pattern=[[-1, NS], [0, 128]], channel_multiplier=1).then_inc(consts, 1)
            pool.memset(lk[0:CARRY], 0.0)
            pool.memset(da[:], 0.0).then_inc(consts, 1)
            pool.wait_ge(weights_in, 32)
            pool.wait_ge(consts, 7)
            pool.sem_inc(hq_ready, W0)
            pool.sem_inc(lk_ready, 1)

            def powers(b, q):
                pool.wait_ge(v_done, 12 * PAIRS * b + M3 * PAIRS * (q + 1))
                pool.tensor_tensor(lk[0:CH, q % 2], within[:].unsqueeze(1).unsqueeze(1).to_broadcast([CH, NC, Q4, CH]),
                                   ak[:, :, Q4 * q:Q4 * q + Q4].unsqueeze(3).to_broadcast([CH, NC, Q4, CH]),
                                   ALU.mult).then_inc(lk_ready, 1)

            with pool.Fori(0, n_img) as b:
                pool.wait_ge(ak_in, 16 * b + 16)
                powers(b, 0)
                for u in range(UNITS):
                    q, m = u // M3, u % M3
                    pool.wait_ge(spread_copied, 8 * NQ * b + 8 * q + 9)
                    pool.wait_ge(scanned, UNITS * b + u + 1)
                    pool.tensor_tensor(v[:, m], v[:, m], qb[:, q % 2], ALU.mult).then_inc(hq_ready, 1)
                    if m == 0 and q + 1 < NQ:
                        powers(b, q + 1)

        @block.tensor
        def _(pe):
            pe.wait_ge(weights_in, 32)
            pe.wait_ge(consts, 7)
            pe.sem_inc(ysum_done, 3)
            pe.sem_inc(v_done, V0)
            pe.sem_inc(spread, 1)
            pe.sem_inc(out_done, 1)

            def spread_rows(b, q, first, last):
                for i in range(first, last):
                    pe.wait_ge(spread_copied, 8 * NQ * b + 8 * q + i + 1)
                    for g in range(2):
                        ins = pe.matmul(ps_b[:, g, 0:G], select[:, Q4 * q + i % Q4, :], kq[:, i // Q4, g * G:(g + 1) * G],
                                        start=True, stop=True)
                    ins.then_inc(spread, 1)

            def momentum(b, u):
                q, m = u // M3, u % M3
                if m == 0:
                    pe.wait_ge(lk_ready, NQ * b + q + 2)
                    pe.wait_ge(carried_in[q % 2], 16 * (2 * b + q // 2 + 1))
                for k in range(PAIRS):
                    n = PAIRS * u + k
                    pe.wait_ge(v_ready, UNITS * PAIRS * b + n + 1)
                    for c in range(2):
                        ins = pe.matmul(ps_v[n % 4][:, c * Q4 * CH:(c + 1) * Q4 * CH], uT[:, 2 * k + c, m * 128:(m + 1) * 128],
                                        lk[:, q % 2, 2 * k + c].rearrange("p n t -> p (n t)"), start=True, stop=True)
                    ins.then_inc(v_done, 1)

            def sum_states(b, u):
                m = u % M3
                pe.wait_ge(hq_ready, W0 + UNITS * b + u + 1)
                pe.wait_ge(y_added, UNITS * b + u + 1)
                for g in range(2):
                    for i in range(Q4):
                        ins = pe.matmul(ps_y[:, g, 0:G], ident[:], v[:, m, i, g * G:(g + 1) * G],
                                        start=(i == 0), stop=(i == Q4 - 1))
                ins.then_inc(ysum_done, 1)

            with pe.Fori(0, n_img) as b:
                pe.wait_ge(kq_in, 16 * b + 16)
                pe.wait_ge(h3_ready, b + 1)
                spread_rows(b, 0, 0, 8)
                pe.wait_ge(u_in, 16 * b + 16)
                for u in range(UNITS):
                    q, m = u // M3, u % M3
                    momentum(b, u)
                    if q + 1 < NQ:
                        spread_rows(b, q + 1, (0, 3, 6)[m], (3, 6, 8)[m])
                    if u >= 2:
                        sum_states(b, u - 2)
                sum_states(b, UNITS - 2)
                sum_states(b, UNITS - 1)
                pe.wait_ge(gated, b + 1)
                pe.wait_ge(spread_copied, 8 * NQ * (b + 1) + 1)
                for t in range(NT):
                    out = (ps_b[0:T, 0], ps_b[0:T, 1], ps_y[0:T, 0])[t // 2][:, (t % 2) * D:(t % 2 + 1) * D]
                    for m in range(M3):
                        ins = pe.matmul(out, y[:, m, t * T:(t + 1) * T], outT[:, m, :], start=(m == 0), stop=(m == M3 - 1))
                ins.then_inc(out_done, 1)

        @block.scalar
        def _(act):
            act.wait_ge(consts, 7)
            act.sem_inc(v_ready, 4)
            act.sem_inc(spread_copied, 1)

            def copy_spread(b, q, first, last):
                for i in range(first, last):
                    if i == 0:
                        act.wait_ge(w_ready, UNITS * b + M3 * (q + 1))
                    if i == Q4:
                        act.wait_ge(hq_ready, UNITS * b + M3 * (q + 1))
                    act.wait_ge(spread, 8 * NQ * b + 8 * q + i + 2)
                    act.activation((kb, qb)[i // Q4][:, q % 2, i % Q4, :].rearrange("p (g t) -> p g t", g=2),
                                   ps_b[:, :, 0:G], ACT.Copy).then_inc(spread_copied, 1)

            with act.Fori(0, n_img) as b:
                copy_spread(b, 0, 0, 8)
                for u in range(UNITS):
                    q, m = u // M3, u % M3
                    act.wait_ge(w_ready, W0 + UNITS * b + u + 1)
                    act.activation(da[:, u % 2, :, 1:SEQ], da[:, u % 2, :, 1:SEQ], ACT.Copy, scale=-1.0, bias=1.0
                                   ).then_inc(da_ready, 1)
                    act.wait_ge(ysum_done, UNITS * b + u + 1)
                    for k in range(PAIRS):
                        n = PAIRS * u + k
                        act.wait_ge(v_done, V0 + UNITS * PAIRS * b + n + 1)
                        act.activation(v[:, m, :, k * T:(k + 1) * T].rearrange("p n (c t) -> p n c t", c=2),
                                       ps_v[n % 4][:, 0:2 * Q4 * CH].rearrange("p (c n t) -> p n c t", c=2, n=Q4),
                                       ACT.Copy).then_inc(v_ready, 1)
                    if q + 1 < NQ:
                        copy_spread(b, q + 1, (0, 3, 6)[m], (3, 6, 8)[m])

        @block.vector
        def _(dve):
            dve.wait_ge(consts, 7)
            dve.sem_inc(w_ready, W0)
            dve.sem_inc(y_added, 1)
            dve.sem_inc(h3_ready, 1)

            def decays(b, u):
                q, m = u // M3, u % M3
                dve.wait_ge(spread_copied, 8 * NQ * b + 8 * q + 5)
                if u >= 2:
                    dve.wait_ge(scanned, UNITS * b + u - 1)
                dve.tensor_tensor(da[:, u % 2, :, 1:SEQ], kb[:, q % 2, :, 1:SEQ],
                                  delta[:, m, 1:SEQ].unsqueeze(1).to_broadcast([128, Q4, SEQ - 1]), ALU.mult
                                  ).then_inc(w_ready, 1)

            def add_states(b, u):
                m = u % M3
                dve.wait_ge(ysum_done, UNITS * b + u + 4)
                if u >= M3:
                    dve.wait_ge(y_added, UNITS * b + u - 1)
                dve.tensor_tensor(y[:, m, :].rearrange("p (g t) -> p g t", g=2), ps_y[:, :, 0:G],
                                  y[:, m, :].rearrange("p (g t) -> p g t", g=2), ALU.add).then_inc(y_added, 1)

            with dve.Fori(0, n_img) as b:
                dve.wait_ge(delta_in, 16 * b + 16)
                decays(b, 0)
                dve.wait_ge(dx_in, 16 * b + 16)
                for u in range(UNITS):
                    m = u % M3
                    if u + 1 < UNITS:
                        decays(b, u + 1)
                    dve.wait_ge(da_ready, UNITS * b + u + 1)
                    dve.wait_ge(v_ready, UNITS * PAIRS * b + PAIRS * (u + 1) + 4)
                    flat = v[:, m].rearrange("p n t -> p (n t)")
                    dve.tensor_tensor_scan(flat, da[:, u % 2].rearrange("p n t -> p (n t)"), flat, 0.0, ALU.mult, ALU.add
                                           ).then_inc(scanned, 1)
                    if u >= 2:
                        add_states(b, u - 2)
                add_states(b, UNITS - 2)
                add_states(b, UNITS - 1)
                dve.wait_ge(zs_in, 16 * b + 16)
                dve.wait_ge(y_added, UNITS * (b + 1) + 1)
                dve.tensor_tensor(y[:], y[:], zs[:], ALU.mult).then_inc(gated, 1)
                dve.wait_ge(out_done, b + 2)
                dve.wait_ge(h2_in, 16 * b + 16)
                dve.wait_ge(h3_out, 16 * b + 16)
                for t in range(3):
                    src = (ps_b[0:T, 0], ps_b[0:T, 1], ps_y[0:T, 0])[t][:, 0:2 * D]
                    ins = dve.tensor_tensor(h3[:, 2 * t:2 * t + 2, :], src.rearrange("p (t d) -> p t d", d=D),
                                            h2[:, 2 * t:2 * t + 2, :], ALU.add)
                ins.then_inc(h3_ready, 1)


def phase_project(nc, a, half, n_img, h3_dram, hn_dram, qk_dram, v_dram):
    b0 = half * n_img
    P = "e%d_" % half
    with ExitStack() as ctx:
        def sb(name, shape, dt=F32):
            return ctx.enter_context(nc.sbuf_tensor(P + name + "_t", shape, dt))

        def sem(name):
            return nc.alloc_semaphore(P + name)

        w = sb("w", [DH, 2, 3 * D])
        gain = sb("gain", [DH, 2])
        shift = sb("shift", [DH, 2])
        gumbel = sb("gumbel", [T, 3])
        bias = sb("bias", [T, D])
        ident = sb("ident", [128, 128])
        eps_col = sb("eps_col", [T, 1])
        h = sb("h", [T, NT, D])
        hn = sb("hn", [T, NT, D])
        hb = sb("hb", [T, NT, D])
        z = sb("z", [T, NT, D])
        stats = sb("stats", [T, NT, 6])
        mv = sb("mv", [T, NT, 2])
        rstd = sb("rstd", [T, NT])
        zT = sb("zT", [DH, 2, SEQ])
        parts = sb("parts", [DH, 2, 3, 2, SEQ], BF16)
        rest = sb("rest", [DH, 4, G])
        va = sb("va", [T, NT, HEADS, 32])

        ps = [ctx.enter_context(nc.psum_tensor(f"{P}ps{n}", [128, 512], F32)) for n in range(8)]

        weights_in = sem("weights_in")
        consts = sem("consts")
        h_in = sem("h_in")
        h_used = sem("h_used")
        var_ready = sem("var_ready")
        std_ready = sem("std_ready")
        hn_ready = sem("hn_ready")
        hb_ready = sem("hb_ready")
        hb_out = sem("hb_out")
        z_ready = sem("z_ready")
        z_turned = sem("z_turned")
        zT0_ready = sem("zT0_ready")
        zT1_ready = sem("zT1_ready")
        qk_done = sem("qk_done")
        hi_ready = sem("hi_ready")
        rest_ready = sem("rest_ready")
        mid_ready = sem("mid_ready")
        lo_ready = sem("lo_ready")
        qk_out = sem("qk_out")
        v_done = sem("v_done")
        v_ready = sem("v_ready")
        v_out = sem("v_out")
        chain = sem("chain")
        passed = sem("passed")
        V_PER = 4

        block = ctx.enter_context(nc.Block())

        @block.sync
        def _(sp):
            names = ("n1s_g", "n1s_b") if half else ("n1l_g", "n1l_b")
            sp.dma_start(w[:], a["f_wqkv"]).then_inc(weights_in, 16)
            sp.dma_start(gain[:], a[names[0]]).then_inc(weights_in, 16)
            sp.dma_start(shift[:], a[names[1]]).then_inc(weights_in, 16)
            sp.dma_start(gumbel[:], a["gumbel"].partition_broadcast(T)).then_inc(weights_in, 16)
            sp.dma_start(bias[:], a["f_bproj"].partition_broadcast(T)).then_inc(weights_in, 16)
            sp.sem_inc(hb_out, 16)
            sp.sem_inc(qk_out, 64)
            sp.sem_inc(v_out, 16)
            with sp.Fori(0, n_img) as b:
                sp.wait_ge(h_used, b + 1)
                sp.dma_start(h[:], h3_dram[b + b0]).then_inc(h_in, 16)
                sp.wait_ge(hb_ready, b + 1)
                sp.dma_start(hn_dram[b + b0], hb[:]).then_inc(hb_out, 16)
                sp.wait_ge(v_ready, 3 * b + 3)
                sp.dma_start(v_dram[b + b0], va[:]).then_inc(v_out, 16)
                sp.wait_ge(lo_ready, 8 * b + 12)
                for m in range(2):
                    for x in range(2):
                        sp.dma_start(qk_dram[b + b0, x, :, m * DH:(m + 1) * DH, :].rearrange("p r t -> r p t"),
                                     parts[:, x, :, m, :]).then_inc(qk_out, 16)
            sp.wait_ge(hb_out, 16 * n_img + 16)
            sp.wait_ge(qk_out, 64 * n_img + 64)
            sp.wait_ge(v_out, 16 * n_img + 16)

        @block.gpsimd
        def _(pool):
            identity(pool, ident[:], consts, 0)
            pool.memset(eps_col[:], LN_EPS)
            pool.memset(va[:], 1.0).then_inc(consts, 1)
            pool.wait_ge(weights_in, 80)
            if half:
                pool.tensor_scalar(gumbel[:, 1:2], gumbel[:, 1:2], gumbel[:, 0:1], None, ALU.add).then_inc(consts, 1)
                pool.wait_ge(consts, 4)
                pool.tensor_scalar(gumbel[:, 2:3], gumbel[:, 2:3], gumbel[:, 1:2], None, ALU.add).then_inc(consts, 1)
                pool.wait_ge(consts, 5)
                for n, (lo, hi) in enumerate(((DH, D), (64, DH), (0, 64))):
                    ins = pool.tensor_scalar(bias[:, lo:hi], bias[:, lo:hi], gumbel[:, n:n + 1], None, ALU.mult)
                ins.then_inc(consts, 1)
                pool.wait_ge(consts, 6)
            pool.sem_inc(lo_ready, 4)
            with pool.Fori(0, n_img) as b:
                pool.wait_ge(hn_ready, b + 1)
                pool.wait_ge(hb_out, 16 * b + 16)
                pool.tensor_tensor(hb[:], hn[:], bias[:].unsqueeze(1).to_broadcast([T, NT, D]), ALU.add
                                   ).then_inc(hb_ready, 1)
                for n in range(8):
                    x, m, g = n // 4, n // 2 % 2, n % 2
                    pool.wait_ge(mid_ready, 8 * b + n + 1)
                    pool.tensor_tensor(parts[:, x, 2, m, g * G:(g + 1) * G], rest[:, n % 4, :],
                                       parts[:, x, 1, m, g * G:(g + 1) * G], ALU.subtract).then_inc(lo_ready, 1)

        @block.tensor
        def _(pe):
            pe.wait_ge(weights_in, 80)
            pe.wait_ge(consts, 3)
            with pe.Fori(0, n_img) as b:
                pe.wait_ge(z_ready, b + 1)
                for m in range(2):
                    for g in range(2):
                        for t in range(3):
                            ins = pe.transpose(ps[2 * m + g][0:DH, t * T:(t + 1) * T],
                                               z[:, 3 * g + t, m * DH:(m + 1) * DH], ident[0:T, 0:T])
                ins.then_inc(z_turned, 1)
                pe.wait_ge(zT0_ready, b + 1)
                pe.wait_ge(zT1_ready, b + 1)
                for n in range(8):
                    x, m, g = n // 4, n // 2 % 2, n % 2
                    if n >= 4:
                        pe.wait_ge(rest_ready, 8 * b + n - 3)
                    for c in range(2):
                        ins = pe.matmul(ps[4 + n % 4][0:DH, 0:G], w[:, c, x * D + m * DH:x * D + (m + 1) * DH],
                                        zT[:, c, g * G:(g + 1) * G], start=(c == 0), stop=(c == 1))
                    ins.then_inc(qk_done, 1)
                for t in range(NT):
                    for c in range(2):
                        ins = pe.matmul(ps[t // 2][0:T, (t % 2) * D:(t % 2 + 1) * D], zT[:, c, t * T:(t + 1) * T],
                                        w[:, c, 2 * D:3 * D], start=(c == 0), stop=(c == 1))
                    if t % 2:
                        ins.then_inc(v_done, 1)

        @block.scalar
        def _(act):
            act.wait_ge(weights_in, 80)
            act.wait_ge(consts, 3)
            with act.Fori(0, n_img) as b:
                for n in range(2):
                    act.wait_ge(var_ready, 2 * b + n + 1)
                    act.activation(rstd[:], mv[:, :, 1], ACT.Sqrt, bias=eps_col[:, 0:1]).then_inc(std_ready, 1)
                act.wait_ge(z_turned, b + 1)
                for g in range(2):
                    ins = act.activation(zT[:, 1, g * G:(g + 1) * G], ps[2 + g][0:DH, 0:G], ACT.Identity,
                                         scale=gain[:, 1:2], bias=shift[:, 1:2])
                ins.then_inc(zT1_ready, 1)
                act.wait_ge(qk_out, 64 * b + 64)

                def high(n):
                    x, m, g = n // 4, n // 2 % 2, n % 2
                    act.wait_ge(qk_done, 8 * b + n + 1)
                    act.activation(parts[:, x, 0, m, g * G:(g + 1) * G], ps[4 + n % 4][0:DH, 0:G], ACT.Copy
                                   ).then_inc(hi_ready, 1)

                high(0)
                for n in range(8):
                    x, m, g = n // 4, n // 2 % 2, n % 2
                    if n < 7:
                        high(n + 1)
                    act.wait_ge(rest_ready, 8 * b + n + 1)
                    act.activation(parts[:, x, 1, m, g * G:(g + 1) * G], rest[:, n % 4, :], ACT.Copy
                                   ).then_inc(mid_ready, 1)

        @block.vector
        def _(dve):
            dve.wait_ge(weights_in, 80)
            dve.wait_ge(consts, 3)
            dve.sem_inc(h_used, 1)
            with dve.Fori(0, n_img) as b:
                c_ = Chain(dve, chain, V_PER * b, V_PER)

                def layernorm(src, dst, n, done):
                    for t in range(NT):
                        ins = dve.bn_stats(stats[:, t, :], src[:, t, :])
                    c_.link(ins)
                    dve.sem_inc(passed, 1)
                    for t in range(NT):
                        ins = dve.bn_aggr(mv[:, t, :], stats[:, t, :])
                    ins.then_inc(var_ready, 1)
                    dve.wait_ge(std_ready, 2 * b + n + 1)
                    c_.link(dve.reciprocal(rstd[:], rstd[:]))
                    for t in range(NT):
                        ins = dve.tensor_scalar(dst[:, t, :], src[:, t, :], mv[:, t, 0:1], rstd[:, t:t + 1],
                                                ALU.subtract, ALU.mult)
                    ins.then_inc(done, 1)

                dve.wait_ge(h_in, 16 * b + 16)
                dve.wait_ge(h_used, b + 1)
                layernorm(h, hn, 0, hn_ready)
                dve.wait_ge(hn_ready, b + 1)
                layernorm(hn, z, 1, z_ready)
                dve.wait_ge(hb_ready, b + 1)
                dve.sem_inc(h_used, 1)
                dve.wait_ge(z_turned, b + 1)
                for g in range(2):
                    ins = dve.tensor_scalar(zT[:, 0, g * G:(g + 1) * G], ps[g][0:DH, 0:G], gain[:, 0:1], shift[:, 0:1],
                                            ALU.mult, ALU.add)
                ins.then_inc(zT0_ready, 1)
                for n in range(8):
                    x, m, g = n // 4, n // 2 % 2, n % 2
                    dve.wait_ge(hi_ready, 8 * b + n + 1)
                    dve.wait_ge(lo_ready, 8 * b + n + 1)
                    dve.tensor_tensor(rest[:, n % 4, :], ps[4 + n % 4][0:DH, 0:G], parts[:, x, 0, m, g * G:(g + 1) * G],
                                      ALU.subtract).then_inc(rest_ready, 1)
                dve.wait_ge(v_out, 16 * b + 16)
                for t in range(3):
                    dve.wait_ge(v_done, 3 * b + t + 1)
                    dve.tensor_copy(va[:, 2 * t:2 * t + 2, :, 0:HD],
                                    ps[t][0:T, 0:2 * D].rearrange("p (t h d) -> p t h d", t=2, h=HEADS)
                                    ).then_inc(v_ready, 1)
                c_.close()


def phase_attend(nc, a, n_img, hn_dram, qk_dram, v_dram, x1_dram):
    R = 36
    KR6 = QK_ROWS + 3
    MISC = 11
    SQ = HEADS * NT * 2
    with ExitStack() as ctx:
        def sb(name, shape, dt=F32):
            return ctx.enter_context(nc.sbuf_tensor("f_" + name + "_t", shape, dt))

        def sem(name):
            return nc.alloc_semaphore("f_" + name)

        q6 = sb("q6", [KR6, 2, HEADS, SEQ], BF16)
        k6 = sb("k6", [KR6, 2, HEADS, SEQ], BF16)
        va = sb("va", [T, 2, NT, HEADS, 32])
        p = sb("p", [T, 2, 4, G])
        mx = sb("mx", [T, HEADS, NT, 2])
        nmx = sb("nmx", [T, NT, HEADS])
        nm = sb("nm", [HEADS, SEQ])
        nrest = sb("nrest", [HEADS, SEQ])
        nparts = sb("nparts", [HEADS, 3, SEQ], BF16)
        oraw = sb("oraw", [128, 2, G])
        inv = sb("inv", [128, 2, G])
        oT = sb("oT", [128, 3, SEQ])
        wp = sb("wp", [128, 2, 3, D])
        gumbel = sb("gumbel", [128, 3])
        ident = sb("ident", [128, 128])
        sums_of = sb("sums_of", [128, 4, 32])
        hn = sb("hn", [T, NT, D])
        x1 = sb("x1", [T, NT, D])

        ps_s = [ctx.enter_context(nc.psum_tensor(f"f_s{n}", [128, 2, 512], F32)) for n in range(2)]
        ps_q = [ctx.enter_context(nc.psum_tensor(f"f_q{n}", [128, 512], F32)) for n in range(2)]
        ps_o = ctx.enter_context(nc.psum_tensor("f_o", [128, 512], F32))
        ps_m = ctx.enter_context(nc.psum_tensor("f_m", [128, 512], F32))

        weights_in = sem("weights_in")
        consts = sem("consts")
        w_chain = sem("w_chain")
        qk_in = [[sem(f"qk_in{k}{j}") for j in range(3)] for k in range(2)]
        v_in = [sem("v_in0"), sem("v_in1")]
        hn_in = sem("hn_in")
        q_done = sem("q_done")
        q_used = sem("q_used")
        nmx_ready = sem("nmx_ready")
        misc_done = sem("misc_done")
        misc_used = sem("misc_used")
        nm_ready = sem("nm_ready")
        nparts_ready = sem("nparts_ready")
        max_in = [sem("max_in0"), sem("max_in1")]
        s_done = sem("s_done")
        p_ready = sem("p_ready")
        pv_done = sem("pv_done")
        o_ready = sem("o_ready")
        inv_ready = sem("inv_ready")
        oT_ready = sem("oT_ready")
        x1_ready = sem("x1_ready")
        x1_out = sem("x1_out")
        chain = sem("chain")
        passed = sem("passed")

        block = ctx.enter_context(nc.Block())

        def each_image(eng, body):
            if n_img > 2:
                with eng.Fori(0, n_img // 2 - 1) as j:
                    body(j, 0, True)
                    body(j, 1, True)
            body(n_img // 2 - 1, 0, True)
            body(n_img // 2 - 1, 1, False)

        @block.sync
        def _(sp):
            for half in range(2):
                sp.dma_start(wp[:, half], a["f_wproj"]).then_inc(weights_in, 16)
            sp.dma_start(gumbel[:], a["gumbel"].partition_broadcast(128)).then_inc(weights_in, 16)
            sp.sem_inc(x1_out, 16)

            def load(b, k):
                for j in range(3):
                    for x, dst in enumerate((q6, k6)):
                        for n, pair in enumerate(PRODUCTS):
                            sp.dma_start(dst[HD * n:HD * n + HD, k, 4 * j:4 * j + 4, :],
                                         qk_dram[b, x, pair[x], 4 * HD * j:4 * HD * (j + 1), :].rearrange(
                                             "(i d) t -> d i t", d=HD)).then_inc(qk_in[k][j], 16)
                sp.dma_start(va[:, k], v_dram[b]).then_inc(v_in[k], 16)

            def maxima(b, k):
                sp.wait_ge(nparts_ready, b + 1)
                for n in range(3):
                    sp.dma_start(q6[QK_ROWS + n:QK_ROWS + n + 1, k, :, :], nparts[:, n, :]
                                 ).then_inc(max_in[k], 16)

            def image(j, k, ahead):
                b = 2 * j + k
                sp.wait_ge(x1_ready, b + 1)
                sp.dma_start(hn[:], hn_dram[b]).then_inc(hn_in, 16)
                if ahead:
                    sp.wait_ge(pv_done, R * b + 2)
                    load(b + 1, 1 - k)
                    maxima(b + 1, 1 - k)
                sp.wait_ge(x1_ready, b + 2)
                sp.dma_start(x1_dram[b], x1[:]).then_inc(x1_out, 16)

            load(0, 0)
            maxima(0, 0)
            each_image(sp, image)
            sp.wait_ge(x1_out, 16 * n_img + 16)

        @block.gpsimd
        def _(pool):
            identity(pool, ident[:], consts, 0)
            pool.memset(sums_of[:], 0.0).then_inc(consts, 1)
            pool.wait_ge(consts, 3)
            pool.affine_select(out=sums_of[:], in_=sums_of[:], compare_op=ALU.not_equal, fill=1.0, base=-HD,
                               pattern=[[-32, 4], [0, 32]], channel_multiplier=1).then_inc(consts, 1)
            pool.wait_ge(consts, 4)
            pool.memset(k6[QK_ROWS:], 1.0).then_inc(consts, 1)
            pool.wait_ge(consts, 5)
            pool.wait_ge(weights_in, 48)
            pool.tensor_scalar(gumbel[:, 1:2], gumbel[:, 1:2], gumbel[:, 0:1], None, ALU.add).then_inc(consts, 1)
            pool.wait_ge(consts, 6)
            pool.tensor_scalar(gumbel[:, 2:3], gumbel[:, 2:3], gumbel[:, 1:2], None, ALU.add).then_inc(consts, 1)
            pool.wait_ge(consts, 7)
            scaled = Chain(pool, w_chain)
            for rows, j, cols, n in ((slice(0, 128), 0, slice(0, 64), 3), (slice(0, 128), 0, slice(64, DH), 2),
                                     (slice(0, 128), 0, slice(DH, D), 1), (slice(0, 64), 1, slice(0, DH), 2),
                                     (slice(0, 64), 1, slice(DH, D), 1), (slice(64, 128), 1, slice(0, D), 1),
                                     (slice(0, 128), 2, slice(0, D), 1)):
                scaled.link(pool.tensor_scalar(wp[rows, 1, j, cols], wp[rows, 1, j, cols], gumbel[rows, n - 1:n], None,
                                               ALU.mult))
            pool.sem_inc(consts, 1)

            def split_maxima(b):
                pool.wait_ge(nm_ready, 2 * b + 2)
                pool.sem_inc(passed, 1)
                pool.tensor_copy(nparts[:, 0, :], nm[:]).then_inc(chain, 1)
                pool.wait_ge(chain, 3 * b + 1)
                pool.tensor_tensor(nrest[:], nm[:], nparts[:, 0, :], ALU.subtract).then_inc(chain, 1)
                pool.wait_ge(chain, 3 * b + 2)
                pool.sem_inc(passed, 1)
                pool.tensor_copy(nparts[:, 1, :], nrest[:]).then_inc(chain, 1)
                pool.wait_ge(chain, 3 * b + 3)
                pool.tensor_tensor(nparts[:, 2, :], nrest[:], nparts[:, 1, :], ALU.subtract).then_inc(nparts_ready, 1)

            def image(j_, k, ahead):
                b = 2 * j_ + k
                for n in range(6):
                    j, g = n // 2, n % 2
                    pool.wait_ge(inv_ready, 6 * b + n + 1)
                    pool.tensor_tensor(oT[:, j, g * G:(g + 1) * G], oraw[:, n % 2], inv[:, n % 2], ALU.mult
                                       ).then_inc(oT_ready, 1)
                if ahead:
                    pool.wait_ge(max_in[k], 48 * (j_ + 1))
                    split_maxima(b + 1)

            pool.sem_inc(oT_ready, 2)
            split_maxima(0)
            each_image(pool, image)

        @block.tensor
        def _(pe):
            pe.wait_ge(weights_in, 48)
            pe.wait_ge(consts, 8)
            pe.sem_inc(pv_done, 2)

            def by_queries(b, k, n):
                h, t, g = n // (2 * NT), n // 2 % NT, n % 2
                pe.wait_ge(q_used, SQ * b + n + 1)
                pe.matmul(ps_q[n % 2][0:T, 0:G], q6[0:QK_ROWS, k, h, t * T:(t + 1) * T],
                          k6[0:QK_ROWS, k, h, g * G:(g + 1) * G], start=True, stop=True).then_inc(q_done, 1)

            def turn_maxima(b, first):
                pe.wait_ge(nmx_ready, b + 1)
                for g in range(2):
                    pe.wait_ge(misc_used, first + g + 1)
                    pe.sem_inc(passed, 1)
                    for t in range(3):
                        ins = pe.transpose(ps_m[0:HEADS, t * T:(t + 1) * T], nmx[:, 3 * g + t, :], ident[0:T, 0:T])
                    ins.then_inc(misc_done, 1)

            def image(j_, k, ahead, half):
                b = 2 * j_ + k
                base = MISC * b + 2

                def weigh(r):
                    j, g, t = r // 12, r // 6 % 2, r % 6
                    pe.wait_ge(p_ready, 2 * R * b + 2 * r + 4)
                    if t == 0:
                        pe.wait_ge(o_ready, 6 * b + r // 6 + 1)
                    for i in range(4):
                        ins = pe.matmul(ps_o[32 * i:32 * i + 32, 0:G], va[:, k, t, 4 * j + i, :], p[:, r % 2, i, :],
                                        start=(t == 0), stop=(t == NT - 1))
                    ins.then_inc(pv_done, 1)

                def sums(n):
                    pe.wait_ge(o_ready, 6 * b + n + 2)
                    pe.wait_ge(misc_used, base + n + 1)
                    pe.matmul(ps_m[:, 0:G], sums_of[:].rearrange("p i c -> p (i c)"), oraw[:, n % 2], start=True, stop=True
                              ).then_inc(misc_done, 1)

                pe.wait_ge(max_in[k], 48 * (j_ + 1))
                pe.wait_ge(v_in[k], 16 * (j_ + 1))
                nq = 0
                for r in range(R):
                    j, g, t = r // 12, r // 6 % 2, r % 6
                    for e in range(2):
                        pe.wait_ge(p_ready, 2 * R * b + 2 * r + e + 1)
                        for i in range(2):
                            h = 4 * j + 2 * e + i
                            ins = pe.matmul(ps_s[e][0:T, i, 0:G], k6[:, k, h, t * T:(t + 1) * T],
                                            q6[:, k, h, g * G:(g + 1) * G], start=True, stop=True)
                        ins.then_inc(s_done, 1)
                    if ahead and r >= 6:
                        for n in range(5 * (r - 6), min(5 * (r - 5), SQ)):
                            if n % (8 * NT) == 0:
                                pe.wait_ge(qk_in[1 - k][n // (8 * NT)], 192 * (j_ + k + 1))
                            by_queries(b + 1, 1 - k, n)
                    if r:
                        weigh(r - 1)
                    if r >= 7 and r % 6 == 1:
                        sums(r // 6 - 1)
                weigh(R - 1)
                sums(5)
                pe.wait_ge(oT_ready, 6 * b + 8)
                for n in range(3):
                    pe.wait_ge(misc_used, base + 6 + n + 1)
                    for t in range(2 * n, 2 * n + 2):
                        for j in range(3):
                            ins = pe.matmul(ps_m[0:T, (t % 2) * D:(t % 2 + 1) * D], oT[:, j, t * T:(t + 1) * T],
                                            wp[:, half, j, :], start=(j == 0), stop=(j == 2))
                    ins.then_inc(misc_done, 1)
                if ahead:
                    turn_maxima(b + 1, base + 9)

            for j in range(3):
                pe.wait_ge(qk_in[0][j], 192)
            for n in range(SQ):
                by_queries(0, 0, n)
            turn_maxima(0, 0)
            last = n_img // 2 - 1
            for half, (first, end) in enumerate(((0, n_img // 4), (n_img // 4, last))):
                if end > first:
                    with pe.Fori(first, end) as j:
                        image(j, 0, True, half)
                        image(j, 1, True, half)
            image(last, 0, True, 1)
            image(last, 1, False, 1)

        @block.scalar
        def _(act):
            act.wait_ge(consts, 8)
            act.sem_inc(p_ready, 2)
            act.sem_inc(o_ready, 1)

            def image(j_, k, ahead):
                b = 2 * j_ + k

                def keep(n):
                    act.wait_ge(pv_done, R * b + 6 * n + 8)
                    act.wait_ge(oT_ready, 6 * b + n + 1)
                    act.activation(oraw[:, n % 2], ps_o[:, 0:G], ACT.Copy).then_inc(o_ready, 1)

                for r in range(R):
                    for e in range(2):
                        act.wait_ge(s_done, 2 * R * b + 2 * r + e + 1)
                        if e == 0:
                            act.wait_ge(pv_done, R * b + r + 1)
                        act.activation(p[:, r % 2, 2 * e:2 * e + 2, :], ps_s[e][0:T, :, 0:G], ACT.Exp, scale=HD ** -0.5
                                       ).then_inc(p_ready, 1)
                    if r >= 6 and r % 6 == 0:
                        keep(r // 6 - 1)
                keep(5)

            each_image(act, image)

        @block.vector
        def _(dve):
            dve.wait_ge(consts, 8)
            dve.sem_inc(q_used, 2)
            dve.sem_inc(misc_used, 1)
            dve.sem_inc(x1_ready, 1)

            def maximum(b, n):
                h, t, g = n // (2 * NT), n // 2 % NT, n % 2
                dve.wait_ge(q_done, SQ * b + n + 1)
                dve.tensor_reduce(mx[:, h, t, g:g + 1], ps_q[n % 2][0:T, 0:G], AX_X, ALU.max).then_inc(q_used, 1)

            def negated(b):
                dve.wait_ge(q_used, SQ * (b + 1) + 2)
                dve.tensor_reduce(nmx[:].rearrange("p t h -> p h t"), mx[:], AX_X, ALU.max, negate=True
                                  ).then_inc(nmx_ready, 1)

            def maxima_rows(b, first):
                for g in range(2):
                    dve.wait_ge(misc_done, first + g + 1)
                    dve.tensor_copy(nm[:, g * G:(g + 1) * G], ps_m[0:HEADS, 0:G]).then_inc(nm_ready, 1)
                    dve.wait_ge(nm_ready, 2 * b + g + 1)
                    dve.sem_inc(misc_used, 1)

            def image(j_, k, ahead):
                b = 2 * j_ + k
                base = MISC * b + 2

                def invert(n):
                    dve.wait_ge(misc_done, base + n + 1)
                    dve.wait_ge(oT_ready, 6 * b + n + 1)
                    dve.reciprocal(inv[:, n % 2], ps_m[:, 0:G]).then_inc(inv_ready, 1)
                    dve.wait_ge(inv_ready, 6 * b + n + 1)
                    dve.sem_inc(misc_used, 1)

                for r in range(R):
                    if ahead and r >= 6:
                        for n in range(5 * (r - 6), min(5 * (r - 5), SQ)):
                            maximum(b + 1, n)
                    if r >= 7 and r % 6 == 1:
                        invert(r // 6 - 1)
                if ahead:
                    negated(b + 1)
                invert(5)
                dve.wait_ge(hn_in, 16 * b + 16)
                dve.wait_ge(x1_out, 16 * b + 16)
                for n in range(3):
                    dve.wait_ge(misc_done, base + 6 + n + 1)
                    ins = dve.tensor_tensor(x1[:, 2 * n:2 * n + 2, :],
                                            ps_m[0:T, 0:2 * D].rearrange("p (t d) -> p t d", d=D),
                                            hn[:, 2 * n:2 * n + 2, :], ALU.add)
                    if n < 2:
                        ins.then_inc(misc_used, 1)
                    else:
                        ins.then_inc(x1_ready, 1)
                        dve.wait_ge(x1_ready, b + 2)
                        dve.sem_inc(misc_used, 1)
                if ahead:
                    maxima_rows(b + 1, base + 9)

            for n in range(SQ):
                maximum(0, n)
            negated(0)
            maxima_rows(0, 0)
            each_image(dve, image)


def phase_mlp(nc, a, half, n_img, h3_dram, x1_dram, out_dram):
    b0 = half * n_img
    P = "g%d_" % half
    BR = 3 if half else 1
    KEEP = (D, DH, 64)
    MT = MLP // 128
    U = 2 * BR
    with ExitStack() as ctx:
        def sb(name, shape, dt=F32):
            return ctx.enter_context(nc.sbuf_tensor(P + name + "_t", shape, dt))

        def sem(name):
            return nc.alloc_semaphore(P + name)

        w1 = sb("w1", [DH, 2, MLP])
        w1c = sb("w1c", [DH, MLP])
        b1 = sb("b1", [128, MT])
        w2 = sb("w2", [128, BR, MT, D])
        gain = sb("gain", [DH, 2])
        shift = sb("shift", [DH, 2])
        gumbel = sb("gumbel", [128, 3])
        gsum = sb("gsum", [T, 3])
        bias = sb("bias", [T, D])
        ident = sb("ident", [128, 128])
        eps_col = sb("eps_col", [T, 1])
        x1 = sb("x1", [T, NT, D])
        h = sb("h", [T, NT, D])
        res = sb("res", [T, 2, NT, D])
        z = sb("z", [T, NT, D])
        stats = sb("stats", [T, NT, 6])
        mv = sb("mv", [T, NT, 2])
        rstd = sb("rstd", [T, NT])
        zT = sb("zT", [DH, 2, SEQ])
        hid = sb("hid", [128, 2, MT, G])
        o = sb("o", [T, NT, D])

        ps = [ctx.enter_context(nc.psum_tensor(f"{P}ps{n}", [128, 512], F32)) for n in range(8)]

        weights_in = sem("weights_in")
        consts = sem("consts")
        w_chain = sem("w_chain")
        x1_in = sem("x1_in")
        h_in = sem("h_in")
        var_ready = sem("var_ready")
        std_ready = sem("std_ready")
        z_ready = sem("z_ready")
        res1_ready = sem("res1_ready")
        res_ready = sem("res_ready")
        z_turned = sem("z_turned")
        zT0_ready = sem("zT0_ready")
        zT1_ready = sem("zT1_ready")
        up_done = sem("up_done")
        hid_ready = sem("hid_ready")
        down_done = sem("down_done")
        o_ready = sem("o_ready")
        o_out = sem("o_out")
        chain = sem("chain")
        passed = sem("passed")
        V_PER = 2
        W_IN = 8 * 16

        block = ctx.enter_context(nc.Block())

        def each_image(eng, body):
            if n_img > 2:
                with eng.Fori(0, n_img // 2 - 1) as j:
                    body(j, 0, True)
                    body(j, 1, True)
            body(n_img // 2 - 1, 0, True)
            body(n_img // 2 - 1, 1, False)

        @block.sync
        def _(sp):
            names = ("n2s_g", "n2s_b") if half else ("n2l_g", "n2l_b")
            sp.dma_start(w1[:], a["w_fc1"]).then_inc(weights_in, 16)
            sp.dma_start(w1c[0:64, :], a["w_fc1"][0:64, 0, :]).then_inc(weights_in, 16)
            sp.dma_start(b1[:], a["b_fc1"]).then_inc(weights_in, 16)
            sp.dma_start(w2[:, 0], a["w_fc2"]).then_inc(weights_in, 16)
            sp.dma_start(gain[:], a[names[0]]).then_inc(weights_in, 16)
            sp.dma_start(shift[:], a[names[1]]).then_inc(weights_in, 16)
            sp.dma_start(gumbel[:], a["gumbel"].partition_broadcast(128)).then_inc(weights_in, 16)
            sp.dma_start(bias[:], a["b_fc2"].partition_broadcast(T)).then_inc(weights_in, 16)
            sp.sem_inc(o_out, 16)

            def load(b):
                sp.dma_start(x1[:], x1_dram[b + b0]).then_inc(x1_in, 16)
                sp.dma_start(h[:], h3_dram[b + b0]).then_inc(h_in, 16)

            def image(j, k, ahead):
                b = 2 * j + k
                if ahead:
                    sp.wait_ge(z_ready, b + 1)
                    sp.wait_ge(res_ready, b + 1)
                    load(b + 1)
                sp.wait_ge(o_ready, 2 * b + 3)
                for t in range(NT):
                    sp.dma_start(out_dram[b + b0, t * T:(t + 1) * T, :], o[:, t, :]).then_inc(o_out, 16)

            load(0)
            each_image(sp, image)
            sp.wait_ge(o_out, 16 * NT * n_img + 16)

        @block.gpsimd
        def _(pool):
            identity(pool, ident[:], consts, 0)
            pool.memset(eps_col[:], LN_EPS).then_inc(consts, 1)
            pool.wait_ge(consts, 3)
            pool.memset(w1c[64:DH, :], 0.0).then_inc(consts, 1)
            pool.wait_ge(weights_in, W_IN)
            pool.wait_ge(consts, 4)
            if half:
                scaled = Chain(pool, w_chain)
                scaled.link(pool.tensor_copy(gsum[:, 0:1], gumbel[0:T, 0:1]))
                for n in range(1, 3):
                    scaled.link(pool.tensor_scalar(gsum[:, n:n + 1], gumbel[0:T, n:n + 1], gsum[:, n - 1:n], None, ALU.add))
                for n, (lo, hi) in enumerate(((DH, D), (64, DH), (0, 64))):
                    scaled.link(pool.tensor_scalar(bias[:, lo:hi], bias[:, lo:hi], gsum[:, n:n + 1], None, ALU.mult))
                for n in (2, 1, 0):
                    scaled.link(pool.tensor_scalar(w2[:, n], w2[:, 0], gumbel[:, n:n + 1], None, ALU.mult))
            pool.sem_inc(consts, 1)

            def residual(b, k):
                pool.wait_ge(x1_in, 16 * b + 16)
                pool.wait_ge(h_in, 16 * b + 16)
                pool.tensor_tensor(res[:, k], x1[:], h[:], ALU.add).then_inc(res1_ready, 1)
                pool.wait_ge(res1_ready, b + 1)
                pool.tensor_tensor(res[:, k], res[:, k], bias[:].unsqueeze(1).to_broadcast([T, NT, D]), ALU.add
                                   ).then_inc(res_ready, 1)

            def image(j, k, ahead):
                b = 2 * j + k
                if ahead:
                    pool.wait_ge(o_ready, 2 * b + 1)
                    residual(b + 1, 1 - k)

            residual(0, 0)
            each_image(pool, image)

        @block.tensor
        def _(pe):
            pe.wait_ge(weights_in, W_IN)
            pe.wait_ge(consts, 5)
            pe.sem_inc(down_done, 2)

            def turn(b):
                pe.wait_ge(z_ready, b + 1)
                for m in range(2):
                    for g in range(2):
                        pe.wait_ge((zT0_ready, zT1_ready)[m], 2 * b + g + 1)
                        pe.sem_inc(passed, 1)
                        for t in range(3):
                            ins = pe.transpose(ps[m][0:DH, t * T:(t + 1) * T], z[:, 3 * g + t, m * DH:(m + 1) * DH],
                                               ident[0:T, 0:T])
                        ins.then_inc(z_turned, 1)

            def up(b, u):
                g, br = u // BR, u % BR
                for i in range(MT):
                    n = MT * u + i
                    pe.wait_ge(hid_ready, MT * U * b + n + 1)
                    out = ps[2 + n % 4][:, 0:G]
                    for c in range(2 if br == 0 else 1):
                        w = w1c if br == 2 else w1[:, c, :]
                        ins = pe.matmul(out, w[:, i * 128:(i + 1) * 128], zT[:, c, g * G:(g + 1) * G],
                                        start=(c == 0), stop=(br > 0 or c == 1))
                    ins.then_inc(up_done, 1)

            def down(b, u):
                g, br = u // BR, u % BR
                pe.wait_ge(hid_ready, MT * U * b + MT * (u + 1) + 4)
                if br == 0:
                    pe.wait_ge(o_ready, 2 * b + g + 1)
                for t in range(3):
                    for i in range(MT):
                        out = (ps[6][0:T, t * D:t * D + KEEP[br]] if t < 2 else ps[7][0:T, 0:KEEP[br]])
                        ins = pe.matmul(out, hid[:, u % 2, i, t * T:(t + 1) * T], w2[:, br, i, 0:KEEP[br]],
                                        start=(br == 0 and i == 0 and t != 1), stop=(br == BR - 1 and i == MT - 1),
                                        skip_group_check=True)
                ins.then_inc(down_done, 1)

            def image(j, k, ahead):
                b = 2 * j + k
                pe.wait_ge(zT0_ready, 2 * b + 3)
                pe.wait_ge(zT1_ready, 2 * b + 3)
                for u in range(U):
                    up(b, u)
                    if u:
                        down(b, u - 1)
                if ahead:
                    turn(b + 1)
                down(b, U - 1)

            turn(0)
            each_image(pe, image)

        @block.scalar
        def _(act):
            act.wait_ge(weights_in, W_IN)
            act.wait_ge(consts, 5)
            act.sem_inc(hid_ready, 4)
            act.sem_inc(zT1_ready, 1)

            def root(b):
                act.wait_ge(var_ready, b + 1)
                act.activation(rstd[:], mv[:, :, 1], ACT.Sqrt, bias=eps_col[:, 0:1]).then_inc(std_ready, 1)

            def turned(b):
                for g in range(2):
                    act.wait_ge(z_turned, 4 * b + 3 + g)
                    act.activation(zT[:, 1, g * G:(g + 1) * G], ps[1][0:DH, 0:G], ACT.Identity,
                                   scale=gain[:, 1:2], bias=shift[:, 1:2]).then_inc(zT1_ready, 1)

            def image(j, k, ahead):
                b = 2 * j + k
                for u in range(U):
                    act.wait_ge(down_done, U * b + u + 1)
                    for i in range(MT):
                        n = MT * u + i
                        act.wait_ge(up_done, MT * U * b + n + 1)
                        act.activation(hid[:, u % 2, i, :], ps[2 + n % 4][:, 0:G], ACT.Gelu, bias=b1[:, i:i + 1]
                                       ).then_inc(hid_ready, 1)
                    if u == 0 and ahead:
                        root(b + 1)
                if ahead:
                    turned(b + 1)

            root(0)
            turned(0)
            each_image(act, image)

        @block.vector
        def _(dve):
            dve.wait_ge(weights_in, W_IN)
            dve.wait_ge(consts, 5)
            dve.sem_inc(zT0_ready, 1)
            dve.sem_inc(o_ready, 1)

            def layernorm(b):
                c_ = Chain(dve, chain, V_PER * b, V_PER)
                dve.wait_ge(x1_in, 16 * b + 16)
                for t in range(NT):
                    ins = dve.bn_stats(stats[:, t, :], x1[:, t, :])
                c_.link(ins)
                dve.sem_inc(passed, 1)
                for t in range(NT):
                    ins = dve.bn_aggr(mv[:, t, :], stats[:, t, :])
                ins.then_inc(var_ready, 1)
                dve.wait_ge(std_ready, b + 1)
                c_.link(dve.reciprocal(rstd[:], rstd[:]))
                for t in range(NT):
                    ins = dve.tensor_scalar(z[:, t, :], x1[:, t, :], mv[:, t, 0:1], rstd[:, t:t + 1],
                                            ALU.subtract, ALU.mult)
                ins.then_inc(z_ready, 1)
                c_.close()

            def turned(b):
                for g in range(2):
                    dve.wait_ge(z_turned, 4 * b + 1 + g)
                    dve.tensor_scalar(zT[:, 0, g * G:(g + 1) * G], ps[0][0:DH, 0:G], gain[:, 0:1], shift[:, 0:1],
                                      ALU.mult, ALU.add).then_inc(zT0_ready, 1)

            def image(j, k, ahead):
                b = 2 * j + k
                if ahead:
                    layernorm(b + 1)
                dve.wait_ge(res_ready, b + 1)
                dve.wait_ge(o_out, 16 * NT * b + 16)
                for g in range(2):
                    if g == 1 and ahead:
                        turned(b + 1)
                    dve.wait_ge(down_done, U * b + BR * (g + 1) + 2)
                    dve.tensor_tensor(o[:, 3 * g:3 * g + 2, :], ps[6][0:T, 0:2 * D].rearrange("p (t d) -> p t d", d=D),
                                      res[:, k, 3 * g:3 * g + 2, :], ALU.add)
                    dve.tensor_tensor(o[:, 3 * g + 2, :], ps[7][0:T, 0:D], res[:, k, 3 * g + 2, :], ALU.add
                                      ).then_inc(o_ready, 1)

            layernorm(0)
            turned(0)
            each_image(dve, image)


def build(nc, a, out):
    n_img = a["txt"].shape[0]
    cap = -(-5 * 2 * n_img * SEQ // (4 * E))

    def scratch(name, shape, dt=F32):
        return nc.dram_tensor(name, shape, dt, kind="Internal").ap()

    h1 = scratch("h1_scratch", (n_img, T, NT, D))
    x2 = scratch("x2_scratch", (n_img, T, NT, D + 1))
    slots = scratch("slots_scratch", (E * cap, 1), I32)
    y = scratch("y_scratch", (E * cap, D))
    h2 = scratch("h2_scratch", (n_img, T, NT, D))
    u = scratch("u_scratch", (n_img, KR, NC, DI))
    ak = scratch("ak_scratch", (n_img, CH, NC, NS))
    delta = scratch("delta_scratch", (n_img, 128, M3, SEQ))
    kq = scratch("kq_scratch", (n_img, 80, 2, SEQ), BF16)
    dx = scratch("dx_scratch", (n_img, 128, M3, SEQ))
    zs = scratch("zs_scratch", (n_img, 128, M3, SEQ))
    h3 = scratch("h3_scratch", (n_img, T, NT, D))
    hn = scratch("hn_scratch", (n_img, T, NT, D))
    qk = scratch("qk_scratch", (n_img, 2, 3, 192, SEQ), BF16)
    v = scratch("v_scratch", (n_img, T, NT, HEADS, 32))
    x1 = scratch("x1_scratch", (n_img, T, NT, D))

    with nc.sbuf_tensor("route", [T, n_img, 4, NT], F32) as route:
        with nc.cleanup_on_exit():
            phase_route(nc, a, n_img, cap, h1, x2, slots, route)
        with nc.cleanup_on_exit():
            phase_experts(nc, a, n_img, cap, x2, slots, y)
        with nc.cleanup_on_exit():
            phase_prepare(nc, a, n_img, h1, y, route, h2, u, ak, delta, kq, dx, zs)
    with nc.cleanup_on_exit():
        phase_scan(nc, a, n_img, u, ak, delta, kq, dx, zs, h2, h3)
    for half in range(2):
        with nc.cleanup_on_exit():
            phase_project(nc, a, half, n_img // 2, h3, hn, qk, v)
    with nc.cleanup_on_exit():
        phase_attend(nc, a, n_img, hn, qk, v, x1)
    for half in range(2):
        with nc.cleanup_on_exit():
            phase_mlp(nc, a, half, n_img // 2, h3, x1, out)


def lay_out(i):
    c = np.ascontiguousarray
    i = {k: np.asarray(v) for k, v in i.items()}
    n = i["x"].shape[0]
    o = {}
    p = i["x"].reshape(n, 14, 2, 8, 14, 2, 8, 3).transpose(0, 2, 5, 3, 6, 7, 1, 4).reshape(n, 8, 96, 196)
    o["patches"] = c(p.transpose(0, 2, 1, 3))
    w = i["L0_tok_W"].reshape(2, 8, 2, 8, 5, 3, 192).transpose(0, 2, 1, 3, 5, 4, 6).reshape(8, 96, 5, 192)
    o["tok_w"] = c(w.transpose(1, 0, 2, 3))
    o["tok_b"] = c(i["L0_tok_b"].reshape(2, 96).T)
    o["txt"] = c(i["txt"])
    halves = lambda m: c(m.reshape(2, 96, -1).transpose(1, 0, 2))
    o["a_wqkvT"] = halves(i["L0_attn_w_qkv"].T)
    o["a_wqkv"] = c(i["L0_attn_w_qkv"].reshape(6, 96, 192).transpose(1, 0, 2))
    o["a_wprojT"] = halves(i["L0_attn_w_proj"].T)
    o["a_bproj"] = c(i["L0_attn_b_proj"].reshape(1, 192))
    o["gateT"] = halves(i["L0_ffn_gate_w"].T)
    o["w13T"] = c(i["L0_ffn_w13"].transpose(0, 2, 1).reshape(8, 2, 96, 1024).transpose(0, 2, 1, 3))
    o["w2T"] = c(i["L0_ffn_w2"].transpose(0, 2, 1).reshape(8, 4, 128, 192).transpose(0, 2, 1, 3))
    o["norm_w"] = c(i["L0_ffn_norm_w"].reshape(8, 2, 96).transpose(2, 0, 1))
    thirds = lambda m: c(m.reshape(3, 128, -1).transpose(1, 0, 2))
    o["inT"] = halves(i["L1_attn_in_proj_w"].T)
    xp = i["L1_attn_x_proj_w"].T
    pad = np.zeros((384, 16), xp.dtype)
    o["xprojT"] = thirds(np.concatenate([xp[:, 12:28], pad, xp[:, 28:44], pad, xp[:, 0:12], pad[:, :4]], 1))
    o["dtheadT"] = c(i["L1_attn_dt_head_w"].T)
    o["conv_w"] = thirds(i["L1_attn_conv_w"][:, 0, :])
    o["conv_b"] = c(i["L1_attn_conv_b"].reshape(3, 128).T)
    o["dt_b"] = c(i["L1_attn_dt_head_b"].reshape(3, 128).T)
    o["d_skip"] = c(i["L1_attn_D"].reshape(3, 128).T)
    o["outT"] = thirds(i["L1_attn_out_proj_w"].T)
    s = np.arange(59)
    p = np.float64(0.9) ** np.arange(60)
    o["decay"] = p[58 - s].astype(np.float32)[:, None]
    o["carry_decay"] = c(np.broadcast_to((p[59] * np.eye(16))[:, None, :], (16, 12, 16)).astype(np.float32))
    o["within"] = np.where(s[None, :] >= s[:, None], p[np.maximum(s[None, :] - s[:, None], 0)], 0).astype(np.float32)
    e = np.eye(16).reshape(16, 4, 1, 4, 1) * p[1:60]
    o["carried"] = c(np.broadcast_to(e, (16, 4, 12, 4, 59)).transpose(1, 0, 2, 3, 4).astype(np.float32))
    o["f_wqkv"] = halves(i["L1_ffn_w_qkv"])
    for n in ("n1l_g", "n1l_b", "n1s_g", "n1s_b", "n2l_g", "n2l_b", "n2s_g", "n2s_b"):
        o[n] = c(i["L1_ffn_" + n].reshape(2, 96).T)
    o["gumbel"] = c(i["L1_ffn_gumbel_weights"])
    o["w_fc1"] = halves(i["L1_ffn_w_fc1"])
    o["b_fc1"] = c(i["L1_ffn_b_fc1"].reshape(6, 128).T)
    o["w_fc2"] = c(i["L1_ffn_w_fc2"].reshape(6, 128, 192).transpose(1, 0, 2))
    o["b_fc2"] = c(i["L1_ffn_b_fc2"])
    o["f_bproj"] = c(i["L1_ffn_b_proj"])
    wp = np.zeros((4, 32, 3, 192), np.float32)
    wp[:, :16] = i["L1_ffn_w_proj"].reshape(3, 4, 16, 192).transpose(1, 2, 0, 3)
    o["f_wproj"] = c(wp.reshape(128, 3, 192))
    return o


def kernel(**inputs):
    import concourse.bacc as bacc
    from concourse.bass_utils import run_bass_kernel_spmd

    arrays = lay_out(inputs)
    nc = bacc.Bacc("TRN2", target_bir_lowering=False, num_devices=1)
    a = {name: nc.dram_tensor(name, v.shape, mybir.dt.from_np(v.dtype), kind="ExternalInput").ap()
         for name, v in arrays.items()}
    n_img = inputs["txt"].shape[0]
    out = nc.dram_tensor("out", (n_img, SEQ, D), F32, kind="ExternalOutput").ap()
    build(nc, a, out)
    r = run_bass_kernel_spmd(nc, [arrays], core_ids=[0])
    return r.results[0]["out"]
```

```python
from contextlib import ExitStack

import numpy as np
import concourse.bass as bass
from concourse import mybir

F32 = mybir.dt.float32
I32 = mybir.dt.int32
U32 = mybir.dt.uint32
ALU = mybir.AluOpType
ACT = mybir.ActivationFunctionType
AX_X = mybir.AxisListType.X

D = 192
DH = 96
N_TXT = 512
GRID = 14
N_PATCH = GRID * GRID
SEQ = N_PATCH + N_TXT
T = 118
NT = SEQ // T
G = 3 * T
QUAD_K = 8
E = 8
HID = 512
HEADS = 12
HD = 16
LN_EPS = 1e-5
MOE_EPS = 1e-6
L1_EPS = 1e-12


class Chain:

    def __init__(self, eng, sem, start=0, per=None):
        self.eng, self.sem, self.start, self.per, self.count = eng, sem, start, per, 0

    def link(self, ins):
        self.count += 1
        ins.then_inc(self.sem, 1)
        self.eng.wait_ge(self.sem, self.start + self.count)

    def close(self):
        assert self.count == self.per, (self.count, self.per)


def identity(pool, ident, sem, n):
    pool.memset(ident, 0.0).then_inc(sem, 1)
    pool.wait_ge(sem, n + 1)
    pool.affine_select(out=ident, in_=ident, compare_op=ALU.not_equal, fill=1.0, base=0,
                       pattern=[[-1, ident.shape[1]]], channel_multiplier=1).then_inc(sem, 1)


def region(q, c):
    a, b = q // 2, q % 2
    inner = [slice(1, GRID), slice(0, GRID - 1)]
    edge = [slice(0, 1), slice(GRID - 1, GRID)]
    return (edge if c & 1 else inner)[a], (edge if c & 2 else inner)[b]


DI = 384
M3 = DI // 128
NS = 16
RANK = 12
TAPS = 4
CH = 59
NC = SEQ // CH
CARRY = 64
KR = 96
Q4 = 4
NQ = NS // Q4
BETA = 0.9
NS_A, NS_B, NS_C = 3.4445, -4.775, 2.0315
BF16 = mybir.dt.bfloat16

MLP = 768
PRODUCTS = ((0, 0), (0, 1), (1, 0), (1, 1), (0, 2), (2, 0))
QK_ROWS = HD * len(PRODUCTS)


def phase_route(nc, a, n_img, cap, h1_dram, x2_dram, slot_dram, route):
    with ExitStack() as ctx:
        def sb(name, shape, dt=F32):
            return ctx.enter_context(nc.sbuf_tensor("ra_" + name, shape, dt))

        def sem(name):
            return nc.alloc_semaphore("ra_" + name)

        def bank(name):
            return ctx.enter_context(nc.psum_tensor("ra_" + name, [128, 512], F32))

        w_copies = sb("w_copies", [DH, QUAD_K, 5, D])
        w_class = sb("w_class", [DH, QUAD_K, 4, D])
        b_tok = sb("b_tok", [DH, 2])
        wqkvT = sb("wqkvT", [DH, 2, 3 * D])
        wq = sb("wq", [DH, 2, D])
        wprojT = sb("wprojT", [DH, 2, D])
        gateT = sb("gateT", [DH, 2, E])
        b_proj = sb("b_proj", [1, D])
        ident = sb("ident", [128, 128])
        blocks = sb("blocks", [DH, DH])
        before = sb("before", [T, T])
        ones = sb("ones", [T, T])
        zero_rows = sb("zero_rows", [T, E * cap // T], I32)
        iota8 = sb("iota8", [T, E])
        tok_of_p = sb("tok_of_p", [T, NT])
        patches = sb("patches", [DH, 2, QUAD_K, N_PATCH])
        tokT = sb("tokT", [DH, 2, N_PATCH])
        x = sb("x", [T, NT, D])
        stats = sb("stats", [T, NT, 6])
        mv = sb("mv", [T, NT, 2])
        rstd = sb("rstd", [T, NT])
        z = sb("z", [T, NT, D])
        zT = sb("zT", [DH, 2, SEQ])
        scratch = sb("scratch", [DH, 4, G])
        qsum = sb("qsum", [DH, 2, 2])
        dq = sb("dq", [DH, 2])
        dk = sb("dk", [DH, 2])
        kv = sb("kv", [T, NT, 2 * D])
        kabs = sb("kabs", [T, NT, D])
        stT = sb("stT", [DH, 2, DH])
        m1 = sb("m1", [DH, 2, D])
        m2 = sb("m2", [DH, 2, D])
        h1 = sb("h1", [T, NT, D])
        x2 = sb("x2", [T, NT, D + 1])
        squares = sb("squares", [T, NT, D])
        sumsq = sb("sumsq", [T, NT])
        moe_eps = sb("moe_eps", [T, 1])
        lmax = sb("lmax", [T, NT])
        prob = sb("prob", [T, NT, E])
        top = sb("top", [T, NT, E])
        topi = sb("topi", [T, NT, E], U32)
        topf = sb("topf", [T, NT, 2])
        hot = sb("hot", [T, 2, NT, E])
        both = sb("both", [T, NT, E])
        earlier = sb("earlier", [T, NT + 1, E])
        pos = sb("pos", [T, 2, NT])
        keep = sb("keep", [T, 2, NT])
        row = sb("row", [T, 2, NT])
        slot = sb("slot", [T, 2, NT])
        slot_i = sb("slot_i", [T, 2, NT], I32)
        first_token = sb("first_token", [T, 1])
        tokid = sb("tokid", [T, NT])
        tokid_i = sb("tokid_i", [T, NT], I32)
        tmp8 = sb("tmp8", [T, 2, NT, E])
        eps_col = sb("eps_col", [T, 1])

        ps_tok, ps_a, ps_b, ps_c, ps_d, ps_e, ps_f, ps_g = (
            bank(n) for n in ("tok", "a", "b", "c", "d", "e", "f", "g"))

        weights_in = sem("weights_in")
        consts = sem("consts")
        w_chain = sem("w_chain")
        w_summed = sem("w_summed")
        table_clear = sem("table_clear")
        patches_in = [sem("patches_in0"), sem("patches_in1")]
        txt_in = sem("txt_in")
        tok_done = sem("tok_done")
        tok_biased = sem("tok_biased")
        tok_turned = sem("tok_turned")
        z_turned = sem("z_turned")
        zT_ready = sem("zT_ready")
        var_ready = sem("var_ready")
        std_ready = sem("std_ready")
        z_ready = sem("z_ready")
        q_done = sem("q_done")
        q_summed = sem("q_summed")
        kv_done = sem("kv_done")
        kv_ready = sem("kv_ready")
        kabs_ready = sem("kabs_ready")
        st_done = sem("st_done")
        st_ready = sem("st_ready")
        m1_done = sem("m1_done")
        m1_ready = sem("m1_ready")
        m2_done = sem("m2_done")
        m2_ready = sem("m2_ready")
        y_done = sem("y_done")
        h1_ready = sem("h1_ready")
        h1_out = sem("h1_out")
        x2_ready = sem("x2_ready")
        sumsq_ready = sem("sumsq_ready")
        rms_ready = sem("rms_ready")
        norm_ready = sem("norm_ready")
        x2_out = sem("x2_out")
        x2_turned = sem("x2_turned")
        x2T_ready = sem("x2T_ready")
        logits_done = sem("logits_done")
        shifted = sem("shifted")
        exped = sem("exped")
        hot_ready = sem("hot_ready")
        pos_done = sem("pos_done")
        slots_ready = sem("slots_ready")
        scattered = sem("scattered")
        lists_free = sem("lists_free")
        passed = sem("passed")
        chain = sem("chain")

        V_PER = 37
        W_IN = 7 * 16

        block = ctx.enter_context(nc.Block())

        @block.sync
        def _(sp):
            sp.dma_start(w_copies[:], a["tok_w"]).then_inc(weights_in, 16)
            sp.dma_start(b_tok[:], a["tok_b"]).then_inc(weights_in, 16)
            sp.dma_start(wqkvT[:], a["a_wqkvT"]).then_inc(weights_in, 16)
            sp.dma_start(wq[:], a["a_wqkv"][:, 0:2, :]).then_inc(weights_in, 16)
            sp.dma_start(wprojT[:], a["a_wprojT"]).then_inc(weights_in, 16)
            sp.dma_start(gateT[:], a["gateT"]).then_inc(weights_in, 16)
            sp.dma_start(b_proj[:], a["a_bproj"]).then_inc(weights_in, 16)
            sp.wait_ge(consts, 12)
            sp.dma_start(slot_dram.rearrange("(p k) one -> p (k one)", p=T), zero_rows[:]).then_inc(table_clear, 16)
            first = 2 * T - N_PATCH

            def load_patches(b, k):
                sp.dma_start(patches[:, k], a["patches"][b]).then_inc(patches_in[k], 16)

            def load_text(b):
                sp.dma_start(x[N_PATCH - T:T, 1, :], a["txt"][b, 0:first, :]).then_inc(txt_in, 16)
                sp.dma_start(x[:, 2:NT, :], a["txt"][b, first:N_TXT, :].rearrange("(t p) d -> p t d", p=T)
                             ).then_inc(txt_in, 16)

            def step(b, k, ahead):
                if ahead:
                    sp.wait_ge(tok_done, b + 1)
                    load_patches(b + 1, 1 - k)
                sp.wait_ge(h1_ready, b + 1)
                sp.dma_start(h1_dram[b], h1[:]).then_inc(h1_out, 16)
                if ahead:
                    load_text(b + 1)
                sp.wait_ge(norm_ready, b + 1)
                sp.dma_start(x2_dram[b], x2[:]).then_inc(x2_out, 16)

            sp.sem_inc(h1_out, 16)
            sp.sem_inc(x2_out, 16)
            load_patches(0, 0)
            load_text(0)
            if n_img > 2:
                with sp.Fori(0, n_img // 2 - 1) as j:
                    for k in range(2):
                        step(2 * j + k, k, True)
            step(n_img - 2, 0, True)
            step(n_img - 1, 1, False)
            sp.wait_ge(patches_in[0], 16 * (n_img // 2))
            sp.wait_ge(patches_in[1], 16 * (n_img // 2))
            sp.wait_ge(h1_out, 16 * n_img + 16)
            sp.wait_ge(x2_out, 16 * n_img + 16)

        @block.gpsimd
        def _(pool):
            identity(pool, ident[:], consts, 0)
            pool.wait_ge(consts, 2)
            pool.memset(ones[:], 1.0).then_inc(consts, 1)
            pool.memset(blocks[:], 1.0).then_inc(consts, 1)
            pool.memset(zero_rows[:], 0).then_inc(consts, 1)
            pool.memset(eps_col[:], LN_EPS)
            pool.memset(first_token[:], 0.0).then_inc(consts, 1)
            pool.iota(iota8[:], pattern=[[1, E]], base=0, channel_multiplier=0,
                      allow_small_or_imprecise_dtypes=True).then_inc(consts, 1)
            pool.memset(moe_eps[:], MOE_EPS)
            pool.iota(tok_of_p[:], pattern=[[1, NT]], base=0, channel_multiplier=NT,
                      allow_small_or_imprecise_dtypes=True).then_inc(consts, 1)
            pool.wait_ge(consts, 8)
            pool.affine_select(out=before[:], in_=ones[:], compare_op=ALU.is_gt, fill=0.0, base=0,
                               pattern=[[1, T]], channel_multiplier=-1).then_inc(consts, 1)
            heads = blocks[:].rearrange("e (h d) -> e h d", d=HD)
            pool.affine_select(out=heads, in_=heads, compare_op=ALU.is_ge, fill=0.0, base=0,
                               pattern=[[-HD, DH // HD], [0, HD]], channel_multiplier=1).then_inc(consts, 1)
            pool.wait_ge(consts, 10)
            pool.affine_select(out=heads, in_=heads, compare_op=ALU.is_ge, fill=0.0, base=HD - 1,
                               pattern=[[HD, DH // HD], [0, HD]], channel_multiplier=-1).then_inc(consts, 1)
            pool.memset(earlier[:], 0.0).then_inc(consts, 1)
            pool.wait_ge(table_clear, 16)
            pool.sem_inc(lists_free, 1)
            with pool.Fori(0, n_img) as b:
                pool.wait_ge(slots_ready, b + 1)
                pool.sem_inc(passed, 1)
                for k in range(2):
                    for t in range(NT):
                        pool.indirect_dma_start(
                            out=slot_dram, out_offset=bass.IndirectOffsetOnAxis(ap=slot_i[:, k, t:t + 1], axis=0),
                            in_=tokid_i[:, t:t + 1], in_offset=None, bounds_check=E * cap - 1,
                            oob_is_err=False).then_inc(scattered, 16)
                pool.wait_ge(scattered, 16 * 2 * NT * (b + 1))
                pool.sem_inc(lists_free, 1)

        @block.tensor
        def _(pe):
            pe.wait_ge(weights_in, W_IN)
            pe.wait_ge(consts, 12)
            pe.wait_ge(w_summed, 1)

            def tokens(b, k, j):
                pe.wait_ge(patches_in[k], 16 * (j + 1))
                for m in range(2):
                    o = ps_tok[0:DH, m * 256:m * 256 + N_PATCH].rearrange("p (y x) -> p y x", x=GRID)
                    for c in range(4):
                        for kt in range(QUAD_K):
                            ys, xs = region(kt // 2, c)
                            mv_ = patches[:, k, kt, :].rearrange("p (y x) -> p y x", x=GRID)
                            ins = pe.matmul(o[:, ys, xs], w_class[:, kt, c, m * DH:(m + 1) * DH], mv_[:, ys, xs],
                                            start=(m == 0 and c == 0 and kt == 0), stop=(c == 3 and kt == QUAD_K - 1),
                                            skip_group_check=True)
                ins.then_inc(tok_done, 1)

            def turn(src, done):
                for m in range(2):
                    for g in range(2):
                        out = (ps_b, ps_c, ps_d, ps_e)[2 * m + g]
                        for t in range(3):
                            ins = pe.transpose(out[0:DH, t * T:(t + 1) * T],
                                               src[:, 3 * g + t, m * DH:(m + 1) * DH], ident[0:T, 0:T])
                ins.then_inc(done, 1)

            with pe.Fori(0, n_img // 2) as j:
                for k in range(2):
                    b = 2 * j + k
                    tokens(b, k, j)
                    pe.wait_ge(tok_biased, b + 1)
                    for m in range(2):
                        pe.transpose(ps_a[0:T, m * DH:(m + 1) * DH], tokT[:, m, 0:T], ident[0:DH, 0:DH])
                        ins = pe.transpose(ps_a[0:N_PATCH - T, D + m * DH:D + (m + 1) * DH],
                                           tokT[:, m, T:N_PATCH], ident[0:DH, 0:DH])
                    ins.then_inc(tok_turned, 1)
                    pe.wait_ge(z_ready, b + 1)
                    turn(z, z_turned)
                    pe.wait_ge(zT_ready, 2 * b + 2)
                    for m in range(2):
                        for g in range(2):
                            out = (ps_a, ps_tok)[m][0:DH, 0:G] if g == 0 else (ps_f, ps_g)[m][0:DH, 0:G]
                            for c in range(2):
                                ins = pe.matmul(out, wqkvT[:, c, m * DH:(m + 1) * DH], zT[:, c, g * G:(g + 1) * G],
                                                start=(c == 0), stop=(c == 1))
                    ins.then_inc(q_done, 1)
                    for t in range(NT):
                        out = (ps_b, ps_c, ps_d, ps_e)[t % 4]
                        if t >= 4:
                            pe.wait_ge(kv_ready, NT * b + t - 3)
                        for c in range(2):
                            ins = pe.matmul(out[0:T, 0:2 * D], zT[:, c, t * T:(t + 1) * T], wqkvT[:, c, D:3 * D],
                                            start=(c == 0), stop=(c == 1))
                        ins.then_inc(kv_done, 1)
                    pe.wait_ge(q_summed, 4 * b + 4)
                    pe.wait_ge(kabs_ready, NT * b + NT)
                    pe.wait_ge(kv_ready, NT * b + NT)
                    for m in range(2):
                        for t in range(NT):
                            pe.matmul(ps_a[0:DH, m * DH:(m + 1) * DH], kv[:, t, D + m * DH:D + (m + 1) * DH],
                                      kv[:, t, m * DH:(m + 1) * DH], start=(t == 0), stop=(t == NT - 1))
                    for m in range(2):
                        for t in range(NT):
                            ins = pe.matmul(ps_f[0:DH, m:m + 1], kabs[:, t, m * DH:(m + 1) * DH], ones[0:T, 0:1],
                                            start=(t == 0), stop=(t == NT - 1))
                    ins.then_inc(st_done, 1)
                    pe.wait_ge(st_ready, b + 1)
                    for m in range(2):
                        ins = pe.matmul(ps_g[0:DH, m * D:(m + 1) * D], stT[:, m, :], wprojT[:, m, :],
                                        start=True, stop=True)
                    ins.then_inc(m1_done, 1)
                    pe.wait_ge(m1_ready, b + 1)
                    for c in range(2):
                        for m in range(2):
                            ins = pe.matmul(ps_a[0:DH, c * D:(c + 1) * D], wq[:, m, c * DH:(c + 1) * DH], m1[:, m, :],
                                            start=(m == 0), stop=(m == 1))
                    ins.then_inc(m2_done, 1)
                    pe.wait_ge(m2_ready, b + 1)
                    for t in range(NT):
                        out = (ps_b, ps_c, ps_d)[t // 2][0:T, (t % 2) * D:(t % 2 + 1) * D]
                        for c in range(2):
                            pe.matmul(out, zT[:, c, t * T:(t + 1) * T], m2[:, c, :], start=(c == 0), stop=False)
                        ins = pe.matmul(out, ones[0:1, 0:T], b_proj[0:1, :], start=False, stop=True)
                    ins.then_inc(y_done, 1)
                    pe.wait_ge(x2_ready, b + 1)
                    turn(x2, x2_turned)
                    pe.wait_ge(x2T_ready, 2 * b + 2)
                    for t in range(NT):
                        for c in range(2):
                            ins = pe.matmul(ps_f[0:T, t * E:(t + 1) * E], zT[:, c, t * T:(t + 1) * T], gateT[:, c, :],
                                            start=(c == 0), stop=(c == 1))
                    ins.then_inc(logits_done, 1)
                    pe.wait_ge(hot_ready, b + 1)
                    flat = ps_g[0:T, 0:NT * E]
                    pe.matmul(flat, before[:], both[:].rearrange("p t e -> p (t e)"), start=True, stop=False)
                    pe.matmul(flat, ones[:], earlier[:, 0:NT, :].rearrange("p t e -> p (t e)"),
                              start=False, stop=True).then_inc(pos_done, 1)

        @block.scalar
        def _(act):
            act.wait_ge(weights_in, W_IN)
            act.wait_ge(consts, 12)
            with act.Fori(0, n_img) as b:
                act.wait_ge(tok_done, b + 1)
                for m in range(2):
                    ins = act.activation(tokT[:, m, :], ps_tok[0:DH, m * 256:m * 256 + N_PATCH], ACT.Identity,
                                         bias=b_tok[:, m:m + 1])
                    if m == 1:
                        ins.then_inc(tok_biased, 1)
                act.wait_ge(var_ready, 2 * b + 1)
                act.activation(rstd[:], mv[:, :, 1], ACT.Sqrt, bias=eps_col[:, 0:1]).then_inc(std_ready, 1)
                act.wait_ge(z_turned, b + 1)
                act.activation(zT[:, 1, 0:G], ps_d[0:DH, 0:G], ACT.Copy)
                act.activation(zT[:, 1, G:SEQ], ps_e[0:DH, 0:G], ACT.Copy).then_inc(zT_ready, 1)
                act.wait_ge(q_done, b + 1)
                for m in range(2):
                    for g in range(2):
                        src = (ps_a, ps_tok)[m] if g == 0 else (ps_f, ps_g)[m]
                        act.activation(scratch[:, 2 * m + g, :], src[0:DH, 0:G], ACT.Abs,
                                       accum_out=qsum[:, m, g:g + 1]).then_inc(q_summed, 1)
                for t in range(NT):
                    act.wait_ge(kv_ready, NT * b + t + 1)
                    act.activation(kabs[:, t, :], kv[:, t, 0:D], ACT.Abs).then_inc(kabs_ready, 1)
                act.wait_ge(m2_done, b + 1)
                act.activation(m2[:].rearrange("p c d -> p (c d)"), ps_a[0:DH, 0:2 * D], ACT.Copy).then_inc(m2_ready, 1)
                act.wait_ge(var_ready, 2 * b + 2)
                act.activation(rstd[:], mv[:, :, 1], ACT.Sqrt, bias=eps_col[:, 0:1]).then_inc(std_ready, 1)
                act.wait_ge(x2_ready, b + 1)
                for t in range(NT):
                    ins = act.activation(squares[:, t, :], x2[:, t, 0:D], ACT.Square, scale=2.0,
                                         accum_out=sumsq[:, t:t + 1])
                ins.then_inc(sumsq_ready, 1)
                act.wait_ge(sumsq_ready, b + 1)
                act.activation(sumsq[:], sumsq[:], ACT.Sqrt, bias=moe_eps[:, 0:1], scale=1.0 / D).then_inc(rms_ready, 1)
                act.wait_ge(x2_turned, b + 1)
                act.activation(zT[:, 1, 0:G], ps_d[0:DH, 0:G], ACT.Copy)
                act.activation(zT[:, 1, G:SEQ], ps_e[0:DH, 0:G], ACT.Copy).then_inc(x2T_ready, 1)
                act.wait_ge(shifted, b + 1)
                act.activation(prob[:], prob[:], ACT.Exp).then_inc(exped, 1)

        @block.vector
        def _(dve):
            dve.wait_ge(weights_in, W_IN)
            dve.wait_ge(consts, 12)
            w = Chain(dve, w_chain)
            for q in range(4):
                qa, qb = q // 2, q % 2
                ks = slice(2 * q, 2 * q + 2)
                own_y, own_x, other_y, other_x = qa, 2 * qb, 1 - qa, 2 * (1 - qb)
                w.link(dve.tensor_tensor(w_class[:, ks, 3, :], w_copies[:, ks, 0, :],
                                         w_copies[:, ks, 1 + own_y + own_x, :], ALU.add))
                w.link(dve.tensor_tensor(w_class[:, ks, 1, :], w_class[:, ks, 3, :],
                                         w_copies[:, ks, 1 + own_y + other_x, :], ALU.add))
                w.link(dve.tensor_tensor(w_class[:, ks, 2, :], w_class[:, ks, 3, :],
                                         w_copies[:, ks, 1 + other_y + own_x, :], ALU.add))
                w.link(dve.tensor_tensor(w_class[:, ks, 0, :], w_class[:, ks, 1, :],
                                         w_copies[:, ks, 1 + other_y + own_x, :], ALU.add))
                w.link(dve.tensor_tensor(w_class[:, ks, 0, :], w_class[:, ks, 0, :],
                                         w_copies[:, ks, 1 + other_y + other_x, :], ALU.add))
            dve.sem_inc(w_summed, 1)
            with dve.Fori(0, n_img) as b:
                c = Chain(dve, chain, V_PER * b, V_PER)

                def layernorm(src, dst, n, done):
                    for t in range(NT):
                        ins = dve.bn_stats(stats[:, t, :], src[:, t, :])
                    c.link(ins)
                    dve.sem_inc(passed, 1)
                    for t in range(NT):
                        ins = dve.bn_aggr(mv[:, t, :], stats[:, t, :])
                    ins.then_inc(var_ready, 1)
                    dve.wait_ge(std_ready, 2 * b + n + 1)
                    c.link(dve.reciprocal(rstd[:], rstd[:]))
                    for t in range(NT):
                        ins = dve.tensor_scalar(dst[:, t, 0:D], src[:, t, :], mv[:, t, 0:1], rstd[:, t:t + 1],
                                                ALU.subtract, ALU.mult)
                    ins.then_inc(done, 1)

                dve.wait_ge(tok_turned, b + 1)
                dve.wait_ge(txt_in, 32 * b + 32)
                dve.tensor_copy(x[:, 0, :], ps_a[0:T, 0:D])
                c.link(dve.tensor_copy(x[0:N_PATCH - T, 1, :], ps_a[0:N_PATCH - T, D:2 * D]))
                layernorm(x, z, 0, z_ready)
                dve.wait_ge(z_turned, b + 1)
                dve.tensor_copy(zT[:, 0, 0:G], ps_b[0:DH, 0:G])
                dve.tensor_copy(zT[:, 0, G:SEQ], ps_c[0:DH, 0:G]).then_inc(zT_ready, 1)
                for t in range(NT):
                    dve.wait_ge(kv_done, NT * b + t + 1)
                    dve.tensor_copy(kv[:, t, :], (ps_b, ps_c, ps_d, ps_e)[t % 4][0:T, 0:2 * D]).then_inc(kv_ready, 1)
                dve.wait_ge(st_done, b + 1)
                dve.wait_ge(q_summed, 4 * b + 4)
                c.link(dve.tensor_tensor(dq[:], qsum[:, :, 0], qsum[:, :, 1], ALU.add))
                dve.tensor_scalar(dk[:], ps_f[0:DH, 0:2], L1_EPS, None, ALU.max)
                c.link(dve.tensor_scalar(dq[:], dq[:], L1_EPS, None, ALU.max))
                dve.reciprocal(dk[:], dk[:])
                c.link(dve.reciprocal(dq[:], dq[:]))
                for m in range(2):
                    ins = dve.tensor_tensor(stT[:, m, :], ps_a[0:DH, m * DH:(m + 1) * DH], blocks[:], ALU.mult)
                ins.then_inc(st_ready, 1)
                dve.wait_ge(m1_done, b + 1)
                for m in range(2):
                    ins = dve.tensor_scalar(m1[:, m, :], ps_g[0:DH, m * D:(m + 1) * D], dq[:, m:m + 1], dk[:, m:m + 1],
                                            ALU.mult, ALU.mult)
                ins.then_inc(m1_ready, 1)
                dve.wait_ge(y_done, b + 1)
                dve.wait_ge(h1_out, 16 * b + 16)
                for t in range(3):
                    ins = dve.tensor_tensor(h1[:, 2 * t:2 * t + 2, :],
                                            (ps_b, ps_c, ps_d)[t][0:T, 0:2 * D].rearrange("p (t d) -> p t d", d=D),
                                            x[:, 2 * t:2 * t + 2, :], ALU.add)
                ins.then_inc(h1_ready, 1)
                dve.wait_ge(h1_ready, b + 1)
                dve.wait_ge(x2_out, 16 * b + 16)
                layernorm(h1, x2, 1, x2_ready)
                dve.wait_ge(rms_ready, b + 1)
                c.link(dve.reciprocal(sumsq[:], sumsq[:]))
                dve.tensor_scalar(x2[:, :, D], sumsq[:], 2.0, None, ALU.mult).then_inc(norm_ready, 1)
                dve.wait_ge(x2_turned, b + 1)
                dve.tensor_copy(zT[:, 0, 0:G], ps_b[0:DH, 0:G])
                dve.tensor_copy(zT[:, 0, G:SEQ], ps_c[0:DH, 0:G]).then_inc(x2T_ready, 1)
                dve.wait_ge(logits_done, b + 1)
                logits = ps_f[0:T, 0:NT * E].rearrange("p (t e) -> p t e", e=E)
                c.link(dve.tensor_reduce(lmax[:], logits, AX_X, ALU.max))
                dve.tensor_tensor(prob[:], logits, lmax[:].unsqueeze(2).to_broadcast([T, NT, E]), ALU.subtract
                                  ).then_inc(shifted, 1)
                dve.wait_ge(exped, b + 1)
                c.link(dve.tensor_reduce(lmax[:], prob[:], AX_X, ALU.add))
                c.link(dve.reciprocal(lmax[:], lmax[:]))
                c.link(dve.tensor_tensor(prob[:], prob[:], lmax[:].unsqueeze(2).to_broadcast([T, NT, E]), ALU.mult))
                dve.sem_inc(passed, 1)
                for t in range(NT):
                    ins = dve.max(top[:, t, :], prob[:, t, :])
                c.link(ins)
                dve.sem_inc(passed, 1)
                for t in range(NT):
                    ins = dve.max_index(topi[:, t, :], top[:, t, :], prob[:, t, :])
                c.link(ins)
                c.link(dve.tensor_copy(topf[:], topi[:, :, 0:2]))
                for k in range(2):
                    ins = dve.tensor_tensor(hot[:, k], iota8[:].unsqueeze(1).to_broadcast([T, NT, E]),
                                            topf[:, :, k:k + 1].to_broadcast([T, NT, E]), ALU.is_equal)
                c.link(ins)
                c.link(dve.tensor_tensor(both[:], hot[:, 0], hot[:, 1], ALU.add))
                for t in range(NT):
                    ins = dve.tensor_tensor(earlier[:, t + 1, :], earlier[:, t, :], both[:, t, :], ALU.add)
                    if t < NT - 1:
                        c.link(ins)
                ins.then_inc(hot_ready, 1)
                dve.wait_ge(pos_done, b + 1)
                c.link(dve.tensor_copy(earlier[:, 0, :], earlier[:, NT, :]))
                counts = ps_g[0:T, 0:NT * E].rearrange("p (t e) -> p t e", e=E)
                for k in range(2):
                    ins = dve.tensor_tensor(tmp8[:, k], counts, hot[:, k], ALU.mult)
                c.link(ins)
                c.link(dve.tensor_reduce(pos[:], tmp8[:], AX_X, ALU.add))
                c.link(dve.tensor_scalar(keep[:], pos[:], float(cap), None, ALU.is_lt))
                c.link(dve.tensor_scalar(row[:], pos[:], float(cap - 1), None, ALU.min))
                for k in range(2):
                    ins = dve.scalar_tensor_tensor(out=row[:, k], in0=topf[:, :, k], scalar=float(cap), in1=row[:, k],
                                                   op0=ALU.mult, op1=ALU.add)
                c.link(ins)
                c.link(dve.tensor_scalar(slot[:], keep[:], -float(E * cap), float(E * cap), ALU.mult, ALU.add))
                c.link(dve.tensor_tensor(slot[:], slot[:], row[:], ALU.add))
                dve.tensor_scalar(tokid[:], tok_of_p[:], first_token[:, 0:1], None, ALU.add)
                c.link(dve.tensor_tensor(lmax[:], top[:, :, 0], top[:, :, 1], ALU.add))
                c.link(dve.reciprocal(lmax[:], lmax[:]))
                for k in range(2):
                    ins = dve.tensor_tensor(pos[:, k], top[:, :, k], lmax[:], ALU.mult)
                c.link(ins)
                c.link(dve.tensor_tensor(pos[:], pos[:], keep[:], ALU.mult))
                dve.tensor_copy(route[:, b, 0:2, :], row[:])
                c.link(dve.tensor_copy(route[:, b, 2:4, :], pos[:]))
                c.link(dve.tensor_scalar(first_token[:], first_token[:], float(SEQ), None, ALU.add))
                dve.wait_ge(lists_free, b + 1)
                dve.tensor_copy(tokid_i[:], tokid[:])
                dve.tensor_copy(slot_i[:], slot[:]).then_inc(slots_ready, 1)
                c.close()


def phase_experts(nc, a, n_img, cap, x2_dram, slot_dram, y_dram):
    steps = cap // G
    assert steps % 2 == 0 and cap % G == 0
    KT = HID // 128
    with ExitStack() as ctx:
        def sb(name, shape, dt=F32):
            return ctx.enter_context(nc.sbuf_tensor("b_" + name + "_t", shape, dt))

        def sem(name):
            return nc.alloc_semaphore("b_" + name)

        def bank(name):
            return ctx.enter_context(nc.psum_tensor("b_" + name, [128, 512], F32))

        slots = sb("slots", [T, E * 3 * steps + 3], I32)
        rows = sb("rows", [T, 2, 3], I32)
        xg = sb("xg", [T, 2, 3, D + 1])
        z = sb("z", [T, 3, D])
        zT = sb("zT", [DH, 2, G])
        w13 = sb("w13", [DH, 2, 2, 2 * HID])
        w2 = sb("w2", [128, 2, KT, D])
        norm = sb("norm", [DH, E, 2])
        gate = sb("gate", [128, 2, G])
        hidden = sb("hidden", [128, KT, G])
        y = sb("y", [T, 2, 3, D])
        ident = sb("ident", [128, 128])

        ps_z0, ps_z1, ps_g0, ps_g1, ps_u0, ps_u1, ps_y0, ps_y1 = (
            bank(n) for n in ("z0", "z1", "g0", "g1", "u0", "u1", "y0", "y1"))
        ps_g, ps_u = (ps_g0, ps_g1), (ps_u0, ps_u1)

        consts = sem("consts")
        norm_in = sem("norm_in")
        slots_in = sem("slots_in")
        w13_in = [sem("w13_in0"), sem("w13_in1")]
        w2_in = [sem("w2_in0"), sem("w2_in1")]
        w13_ready = sem("w13_ready")
        rows_ready = sem("rows_ready")
        gathered = [sem("gathered0"), sem("gathered1")]
        z_ready = sem("z_ready")
        z_turned = sem("z_turned")
        zT0_ready = sem("zT0_ready")
        zT1_ready = sem("zT1_ready")
        up_done = sem("up_done")
        gate_ready = sem("gate_ready")
        hidden_ready = sem("hidden_ready")
        y_done = sem("y_done")
        y_ready = sem("y_ready")
        y_out = [sem("y_out0"), sem("y_out1")]
        expert_done = sem("expert_done")
        passed = sem("passed")

        x_rows = x2_dram.rearrange("b p t d -> (b p t) d")
        y_steps = y_dram.rearrange("(e p g j) d -> e g p (j d)", e=E, p=T, j=3)

        block = ctx.enter_context(nc.Block())

        @block.sync
        def _(sp):
            def weights(e, k):
                sp.dma_start(w13[:, k], a["w13T"][e]).then_inc(w13_in[k], 16)
                sp.dma_start(w2[:, k], a["w2T"][e]).then_inc(w2_in[k], 16)

            def stores(e):
                with sp.Fori(0, steps // 2) as h:
                    for k in range(2):
                        sp.wait_ge(y_ready, steps * e + 2 * h + k + 2)
                        sp.dma_start(y_steps[e, 2 * h + k], y[:, k].rearrange("p j d -> p (j d)")).then_inc(y_out[k], 16)

            sp.dma_start(norm[:], a["norm_w"]).then_inc(norm_in, 16)
            sp.wait_ge(consts, 3)
            sp.dma_start(slots[:, 0:E * 3 * steps].rearrange("p (e k) -> p e k", e=E),
                         slot_dram.rearrange("(e p k) one -> p e (k one)", e=E, p=T)).then_inc(slots_in, 16)
            weights(0, 0)
            weights(1, 1)
            sp.sem_inc(y_out[0], 16)
            sp.sem_inc(y_out[1], 16)
            with sp.Fori(0, E // 2 - 1) as j:
                for k in range(2):
                    stores(2 * j + k)
                    sp.wait_ge(expert_done, 2 * j + k + 1)
                    weights(2 * j + k + 2, k)
            for k in range(2):
                stores(E - 2 + k)
            for k in range(2):
                sp.wait_ge(y_out[k], 16 * (E * steps // 2 + 1))

        @block.gpsimd
        def _(pool):
            identity(pool, ident[:], consts, 0)
            pool.memset(slots[:, E * 3 * steps:], 0).then_inc(consts, 1)
            pool.wait_ge(slots_in, 16)
            pool.wait_ge(norm_in, 16)

            def gather(s, k):
                pool.tensor_copy(rows[:, k, :], slots[:, bass.ds(3 * s, 3)]).then_inc(rows_ready, 1)
                pool.wait_ge(rows_ready, s + 1)
                pool.sem_inc(passed, 1)
                for i in range(3):
                    pool.indirect_dma_start(out=xg[:, k, i, :], out_offset=None, in_=x_rows,
                                            in_offset=bass.IndirectOffsetOnAxis(ap=rows[:, k, i:i + 1], axis=0),
                                            ).then_inc(gathered[k], 16)

            gather(0, 0)
            with pool.Fori(0, E // 2) as j:
                for ke in range(2):
                    e = 2 * j + ke
                    pool.wait_ge(w13_in[ke], 16 * j + 16)
                    pool.sem_inc(passed, 1)
                    for m in range(2):
                        ins = pool.tensor_tensor(w13[:, ke, m, :], w13[:, ke, m, :],
                                                 norm[:, bass.ds(e, 1), m].to_broadcast([DH, 2 * HID]), ALU.mult)
                    ins.then_inc(w13_ready, 1)
                    with pool.Fori(0, steps // 2) as h:
                        for k in range(2):
                            s = steps * e + 2 * h + k
                            pool.wait_ge(y_ready, s + 1)
                            pool.sem_inc(passed, 1)
                            gather(s + 1, 1 - k)
            pool.wait_ge(gathered[0], 48 * (E * steps // 2 + 1))
            pool.wait_ge(gathered[1], 48 * (E * steps // 2))

        @block.tensor
        def _(pe):
            pe.wait_ge(consts, 2)

            def turn(n):
                pe.wait_ge(z_ready, n)
                for m in range(2):
                    for t in range(3):
                        ins = pe.transpose((ps_z0, ps_z1)[m][0:DH, t * T:(t + 1) * T],
                                           z[:, t, m * DH:(m + 1) * DH], ident[0:T, 0:T])
                ins.then_inc(z_turned, 1)

            turn(1)
            with pe.Fori(0, E // 2) as j:
                for ke in range(2):
                    e = 2 * j + ke
                    pe.wait_ge(w13_ready, e + 1)
                    pe.wait_ge(w2_in[ke], 16 * j + 16)
                    pe.sem_inc(passed, 1)
                    with pe.Fori(0, steps) as h:
                        s = steps * e + h
                        pe.wait_ge(zT0_ready, s + 1)
                        pe.wait_ge(zT1_ready, s + 1)
                        for i in range(KT):
                            pe.wait_ge(hidden_ready, 4 * s + i + 1)
                            for ps, off in ((ps_g, 0), (ps_u, HID)):
                                for c in range(2):
                                    ins = pe.matmul(ps[i % 2][:, 0:G], w13[:, ke, c, off + i * 128:off + (i + 1) * 128],
                                                    zT[:, c, :], start=(c == 0), stop=(c == 1))
                            ins.then_inc(up_done, 1)
                        turn(s + 2)
                        pe.wait_ge(y_ready, s + 1)
                        for i in range(KT):
                            pe.wait_ge(hidden_ready, 4 * s + i + 3)
                            for t in range(3):
                                out = ps_y0[0:T, t * D:(t + 1) * D] if t < 2 else ps_y1[0:T, 0:D]
                                ins = pe.matmul(out, hidden[:, i, t * T:(t + 1) * T], w2[:, ke, i, :],
                                                start=(i == 0 and t != 1), stop=(i == KT - 1), skip_group_check=True)
                        ins.then_inc(y_done, 1)
                    pe.sem_inc(passed, 1)
                    pe.wait_ge(y_done, steps * (e + 1))
                    pe.sem_inc(expert_done, 1)

        @block.scalar
        def _(act):
            act.wait_ge(z_turned, 1)
            act.activation(zT[:, 1, :], ps_z1[0:DH, 0:G], ACT.Copy).then_inc(zT1_ready, 1)
            with act.Fori(0, E * steps) as s:
                for i in range(KT):
                    act.wait_ge(up_done, 4 * s + i + 1)
                    act.wait_ge(hidden_ready, 4 * s + i + 1)
                    act.activation(gate[:, i % 2, :], ps_g[i % 2][:, 0:G], ACT.Silu).then_inc(gate_ready, 1)
                act.wait_ge(z_turned, s + 2)
                act.activation(zT[:, 1, :], ps_z1[0:DH, 0:G], ACT.Copy).then_inc(zT1_ready, 1)

        @block.vector
        def _(dve):
            dve.sem_inc(hidden_ready, 2)
            dve.sem_inc(y_ready, 1)

            def normed(k, count):
                dve.wait_ge(gathered[k], count)
                dve.tensor_tensor(z[:], xg[:, k, :, 0:D], xg[:, k, :, D:D + 1].to_broadcast([T, 3, D]), ALU.mult
                                  ).then_inc(z_ready, 1)

            def turned(s):
                dve.wait_ge(z_turned, s + 1)
                dve.tensor_copy(zT[:, 0, :], ps_z0[0:DH, 0:G]).then_inc(zT0_ready, 1)

            normed(0, 48)
            turned(0)
            with dve.Fori(0, E * steps // 2) as h:
                for k in range(2):
                    s = 2 * h + k
                    for i in range(KT):
                        if i == 2:
                            normed(1 - k, 48 * (h + k) + 48)
                        dve.wait_ge(gate_ready, 4 * s + i + 1)
                        dve.tensor_tensor(hidden[:, i, :], gate[:, i % 2, :], ps_u[i % 2][:, 0:G], ALU.mult
                                          ).then_inc(hidden_ready, 1)
                    turned(s + 1)
                    dve.wait_ge(y_done, s + 1)
                    dve.wait_ge(y_out[k], 16 * h + 16)
                    dve.tensor_tensor(y[:, k, 0:2, :], ps_y0[0:T, 0:2 * D].rearrange("p (t d) -> p t d", d=D),
                                      xg[:, k, 0:2, 0:D], ALU.add)
                    dve.tensor_tensor(y[:, k, 2, :], ps_y1[0:T, 0:D], xg[:, k, 2, 0:D], ALU.add).then_inc(y_ready, 1)


def phase_prepare(nc, a, n_img, h1_dram, y_dram, route, h2_dram, u_dram, ak_dram, delta_dram, kq_dram, dx_dram, zs_dram):
    with ExitStack() as ctx:
        def sb(name, shape, dt=F32):
            return ctx.enter_context(nc.sbuf_tensor("c_" + name + "_t", shape, dt))

        def sem(name):
            return nc.alloc_semaphore("c_" + name)

        inT = sb("inT", [DH, 2, 2 * DI])
        xprojT = sb("xprojT", [128, M3, KR])
        dtheadT = sb("dtheadT", [KR, DI])
        conv_w = sb("conv_w", [128, M3, TAPS])
        conv_b = sb("conv_b", [128, M3])
        dt_b = sb("dt_b", [128, M3])
        d_skip = sb("d_skip", [128, M3])
        decay = sb("decay", [CH, 1])
        ck = sb("ck", [KR, NC, NS])
        ident = sb("ident", [128, 128])
        ones = sb("ones", [NS, 128])
        eps_col = sb("eps_col", [T, 1])
        rows = sb("rows", [T, 2, NT], I32)
        shares = sb("shares", [T, 2, NT])
        yg = sb("yg", [T, 2, NT, D])
        h = sb("h", [T, NT, D])
        h2 = sb("h2", [T, NT, D])
        stats = sb("stats", [T, NT, 6])
        mv = sb("mv", [T, NT, 2])
        rstd = sb("rstd", [T, NT])
        z = sb("z", [T, NT, D])
        zT = sb("zT", [DH, 2, SEQ])
        xpad = sb("xpad", [128, M3, SEQ + TAPS - 1])
        xc = sb("xc", [128, M3, SEQ])
        xs = sb("xs", [128, M3, SEQ])
        zs = sb("zs", [128, M3, SEQ])
        dx = sb("dx", [128, M3, SEQ])
        xd = sb("xd", [KR, SEQ])
        dts = sb("dts", [128, M3, SEQ])
        den = sb("den", [128, M3, SEQ])
        delta = sb("delta", [128, M3, SEQ])
        u = sb("u", [128, M3, SEQ])
        kq = sb("kq", [NS, 2, SEQ])
        rest = sb("rest", [NS, 2, SEQ])
        mid = sb("mid", [NS, 2, SEQ], BF16)
        split = sb("split", [80, 2, SEQ], BF16)
        uT = sb("uT", [KR, NC, DI])
        squares = sb("squares", [CH, 2, DI])
        u2 = sb("u2", [CH, NC])
        kT = sb("kT", [CH, NC, NS])
        kTsq = sb("kTsq", [CH, NC, NS])
        k2 = sb("k2", [CH, NC])
        g2 = sb("g2", [CH, NC])
        gn = sb("gn", [CH, NC])
        gr = sb("gr", [CH, NC])
        alpha = sb("alpha", [CH, NC])
        ak = sb("ak", [CH, NC, NS])

        ps = [ctx.enter_context(nc.psum_tensor(f"c_ps{n}", [128, 512], F32)) for n in range(8)]

        weights_in = sem("weights_in")
        consts = sem("consts")
        rows_ready = sem("rows_ready")
        rows_used = sem("rows_used")
        gathered = sem("gathered")
        h1_in = sem("h1_in")
        h1_used = sem("h1_used")
        h2_ready = sem("h2_ready")
        var_ready = sem("var_ready")
        std_ready = sem("std_ready")
        z_ready = sem("z_ready")
        z_turned = sem("z_turned")
        zT0_ready = sem("zT0_ready")
        zT1_ready = sem("zT1_ready")
        in_done = sem("in_done")
        x_copied = sem("x_copied")
        zs_ready = sem("zs_ready")
        conv_ready = sem("conv_ready")
        xs_ready = sem("xs_ready")
        xd_done = sem("xd_done")
        xd_ready = sem("xd_ready")
        dt_done = sem("dt_done")
        dts_ready = sem("dts_ready")
        ksq_ready = sem("ksq_ready")
        ksq_done = sem("ksq_done")
        den_mul = sem("den_mul")
        den_ready = sem("den_ready")
        delta_ready = sem("delta_ready")
        u_ready = sem("u_ready")
        u_turned = sem("u_turned")
        uT_copied = sem("uT_copied")
        u2_ready = sem("u2_ready")
        k_turned = sem("k_turned")
        g2_ready = sem("g2_ready")
        g_ready = sem("g_ready")
        ck_ready = sem("ck_ready")
        carry_done = sem("carry_done")
        carry_ready = sem("carry_ready")
        dx_ready = sem("dx_ready")
        split_ready = sem("split_ready")
        stored = {n: sem("stored_" + n) for n in ("h2", "u", "ak", "delta", "kq", "dx", "zs")}
        chain = sem("chain")
        pchain = sem("pchain")
        passed = sem("passed")
        V_PER = 31
        W_IN = 9 * 16

        y_rows = y_dram
        block = ctx.enter_context(nc.Block())

        @block.sync
        def _(sp):
            for dst, src in ((inT, "inT"), (xprojT, "xprojT"), (conv_w, "conv_w"), (conv_b, "conv_b"), (dt_b, "dt_b"),
                             (d_skip, "d_skip"), (decay, "decay")):
                sp.dma_start(dst[:], a[src]).then_inc(weights_in, 16)
            sp.dma_start(dtheadT[:], a["dtheadT"]).then_inc(weights_in, 16)
            sp.dma_start(ck[CARRY:, :, :], a["carry_decay"]).then_inc(weights_in, 16)
            for s in stored.values():
                sp.sem_inc(s, 16)
            with sp.Fori(0, n_img) as b:
                sp.wait_ge(h1_used, b + 1)
                sp.dma_start(h[:], h1_dram[b]).then_inc(h1_in, 16)
                sp.wait_ge(h2_ready, b + 1)
                sp.dma_start(h2_dram[b], h2[:]).then_inc(stored["h2"], 16)
                sp.wait_ge(zs_ready, 6 * b + 6)
                sp.dma_start(zs_dram[b], zs[:]).then_inc(stored["zs"], 16)
                sp.wait_ge(dx_ready, b + 1)
                sp.dma_start(dx_dram[b], dx[:]).then_inc(stored["dx"], 16)
                sp.wait_ge(delta_ready, b + 1)
                sp.dma_start(delta_dram[b], delta[:]).then_inc(stored["delta"], 16)
                sp.wait_ge(split_ready, 3 * b + 3)
                sp.dma_start(kq_dram[b], split[:]).then_inc(stored["kq"], 16)
                sp.wait_ge(ck_ready, b + 1)
                sp.dma_start(ak_dram[b], ak[:]).then_inc(stored["ak"], 16)
                sp.wait_ge(carry_ready, (NC - 1) * (b + 1))
                sp.dma_start(u_dram[b], uT[:]).then_inc(stored["u"], 16)
            for s in stored.values():
                sp.wait_ge(s, 16 * n_img + 16)

        @block.gpsimd
        def _(pool):
            identity(pool, ident[:], consts, 0)
            pool.memset(ones[:], 1.0)
            pool.memset(eps_col[:], LN_EPS)
            pool.memset(xpad[:], 0.0)
            pool.memset(split[:], 0.0)
            pool.memset(uT[:], 0.0)
            pool.memset(ck[0:CARRY], 0.0).then_inc(consts, 1)
            pool.sem_inc(rows_used, 1)
            with pool.Fori(0, n_img) as b:
                pool.wait_ge(rows_ready, b + 1)
                pool.sem_inc(passed, 1)
                for k in range(2):
                    for t in range(NT):
                        pool.indirect_dma_start(out=yg[:, k, t, :], out_offset=None, in_=y_rows,
                                                in_offset=bass.IndirectOffsetOnAxis(ap=rows[:, k, t:t + 1], axis=0),
                                                ).then_inc(gathered, 16)
                pool.wait_ge(delta_ready, b + 1)
                pool.sem_inc(passed, 1)
                pool.tensor_tensor(u[:], delta[:], xs[:], ALU.mult).then_inc(u_ready, 1)

        @block.tensor
        def _(pe):
            pe.wait_ge(weights_in, W_IN)
            pe.wait_ge(consts, 3)
            with pe.Fori(0, n_img) as b:
                pe.wait_ge(z_ready, b + 1)
                for m in range(2):
                    for g in range(2):
                        for t in range(3):
                            ins = pe.transpose(ps[2 * m + g][0:DH, t * T:(t + 1) * T],
                                               z[:, 3 * g + t, m * DH:(m + 1) * DH], ident[0:T, 0:T])
                ins.then_inc(z_turned, 1)
                pe.wait_ge(zT0_ready, b + 1)
                pe.wait_ge(zT1_ready, b + 1)
                for m in range(2 * M3):
                    for g in range(2):
                        n = 2 * m + g
                        if 4 <= n < 10:
                            pe.wait_ge(x_copied, 6 * b + n - 3)
                        elif n >= 10:
                            pe.wait_ge(zs_ready, 6 * b + n - 9)
                        for c in range(2):
                            ins = pe.matmul(ps[4 + n % 4][:, 0:G], inT[:, c, m * 128:(m + 1) * 128],
                                            zT[:, c, g * G:(g + 1) * G], start=(c == 0), stop=(c == 1))
                        ins.then_inc(in_done, 1)
                pe.wait_ge(xs_ready, M3 * b + M3)
                for g in range(2):
                    for m in range(M3):
                        ins = pe.matmul(ps[g][0:KR, 0:G], xprojT[:, m, :], xs[:, m, g * G:(g + 1) * G],
                                        start=(m == 0), stop=(m == M3 - 1))
                    ins.then_inc(xd_done, 1)
                pe.wait_ge(xd_ready, 2 * b + 2)
                for m in range(M3):
                    for g in range(2):
                        n = 2 * m + g
                        if n < 4:
                            pe.wait_ge(zs_ready, 6 * b + 6)
                        else:
                            pe.wait_ge(dts_ready, 6 * b + n - 3)
                        pe.matmul(ps[4 + n % 4][:, 0:G], dtheadT[:, m * 128:(m + 1) * 128],
                                  xd[:, g * G:(g + 1) * G], start=True, stop=True
                                  ).then_inc(dt_done, 1)
                pe.wait_ge(ksq_ready, b + 1)
                for g in range(2):
                    ins = pe.matmul(ps[2 + g][:, 0:G], ones[:, :], kq[:, 0, g * G:(g + 1) * G], start=True, stop=True)
                ins.then_inc(ksq_done, 1)
                for c in range(NC):
                    ins = pe.transpose(ps[0][0:CH, c * NS:(c + 1) * NS], xd[0:NS, c * CH:(c + 1) * CH], ident[0:NS, 0:NS])
                ins.then_inc(k_turned, 1)
                pe.wait_ge(u_ready, b + 1)
                pe.wait_ge(dts_ready, 6 * b + 6)
                for c in range(NC):
                    if c >= 4:
                        pe.wait_ge(uT_copied, NC * b + c - 3)
                    pe.sem_inc(passed, 1)
                    for m in range(M3):
                        ins = pe.transpose(ps[4 + c % 4][0:CH, m * 128:(m + 1) * 128], u[:, m, c * CH:(c + 1) * CH],
                                           ident[:])
                    ins.then_inc(u_turned, 1)
                pe.wait_ge(ck_ready, b + 1)
                pe.wait_ge(uT_copied, NC * b + NC)
                for c in range(NC - 1):
                    if c:
                        pe.wait_ge(carry_ready, (NC - 1) * b + c)
                    pe.matmul(ps[1][0:NS, 0:DI], ck[:, c, :], uT[:, c, :], start=True, stop=True).then_inc(carry_done, 1)

        @block.scalar
        def _(act):
            act.wait_ge(weights_in, W_IN)
            act.wait_ge(consts, 3)
            with act.Fori(0, n_img) as b:
                act.wait_ge(var_ready, b + 1)
                act.activation(rstd[:], mv[:, :, 1], ACT.Sqrt, bias=eps_col[:, 0:1]).then_inc(std_ready, 1)
                act.wait_ge(z_turned, b + 1)
                act.activation(zT[:, 1, 0:G], ps[2][0:DH, 0:G], ACT.Copy)
                act.activation(zT[:, 1, G:SEQ], ps[3][0:DH, 0:G], ACT.Copy).then_inc(zT1_ready, 1)
                act.wait_ge(stored["zs"], 16 * b + 16)
                for m in range(M3):
                    for g in range(2):
                        n = 2 * m + g
                        act.wait_ge(in_done, 12 * b + 6 + n + 1)
                        act.activation(zs[:, m, g * G:(g + 1) * G], ps[4 + (n + 6) % 4][:, 0:G], ACT.Silu
                                       ).then_inc(zs_ready, 1)
                for m in range(M3):
                    act.wait_ge(conv_ready, M3 * b + m + 1)
                    act.activation(xs[:, m, :], xc[:, m, :], ACT.Silu, bias=conv_b[:, m:m + 1]).then_inc(xs_ready, 1)
                for g in range(2):
                    act.wait_ge(xd_done, 2 * b + g + 1)
                    act.activation(xd[:, g * G:(g + 1) * G], ps[g][0:KR, 0:G], ACT.Copy).then_inc(xd_ready, 1)
                for m in range(M3):
                    for g in range(2):
                        n = 2 * m + g
                        act.wait_ge(dt_done, 6 * b + n + 1)
                        act.activation(dts[:, m, g * G:(g + 1) * G], ps[4 + n % 4][:, 0:G], ACT.Sigmoid,
                                       bias=dt_b[:, m:m + 1]).then_inc(dts_ready, 1)
                act.wait_ge(stored["dx"], 16 * b + 16)
                act.wait_ge(xs_ready, M3 * b + M3)
                for m in range(M3):
                    ins = act.activation(dx[:, m, :], xs[:, m, :], ACT.Copy, scale=d_skip[:, m:m + 1])
                ins.then_inc(dx_ready, 1)
                act.wait_ge(den_mul, b + 1)
                act.activation(den[:], den[:], ACT.Copy, bias=1.0).then_inc(den_ready, 1)
                for c in range(NC):
                    act.wait_ge(uT_copied, NC * b + c + 1)
                    if c >= 2:
                        act.wait_ge(u2_ready, NC * b + c - 1)
                    act.activation(squares[:, c % 2, :], uT[0:CH, c, :], ACT.Square, accum_out=u2[:, c:c + 1]
                                   ).then_inc(u2_ready, 1)
                act.wait_ge(g2_ready, b + 1)
                act.activation(gn[:], g2[:], ACT.Sqrt).then_inc(g_ready, 1)

        @block.vector
        def _(dve):
            dve.wait_ge(weights_in, W_IN)
            dve.wait_ge(consts, 3)
            dve.sem_inc(h1_used, 1)
            with dve.Fori(0, n_img) as b:
                c_ = Chain(dve, chain, V_PER * b, V_PER)
                dve.tensor_copy(rows[:], route[:, bass.ds(b, 1), 0:2, :].rearrange("p one k t -> p (one k) t")
                                ).then_inc(rows_ready, 1)
                c_.link(dve.tensor_copy(shares[:], route[:, bass.ds(b, 1), 2:4, :].rearrange("p one k t -> p (one k) t")))
                dve.wait_ge(gathered, 16 * 2 * NT * (b + 1))
                for k in range(2):
                    ins = dve.tensor_tensor(yg[:, k], yg[:, k], shares[:, k, :].unsqueeze(2).to_broadcast([T, NT, D]),
                                            ALU.mult)
                c_.link(ins)
                c_.link(dve.tensor_tensor(yg[:, 0], yg[:, 0], yg[:, 1], ALU.add))
                dve.wait_ge(h1_in, 16 * b + 16)
                dve.wait_ge(stored["h2"], 16 * b + 16)
                dve.tensor_tensor(h2[:], h[:], yg[:, 0], ALU.add).then_inc(h2_ready, 1)
                dve.sem_inc(passed, 1)
                dve.wait_ge(h2_ready, b + 1)
                dve.sem_inc(h1_used, 1)
                for t in range(NT):
                    ins = dve.bn_stats(stats[:, t, :], h2[:, t, :])
                c_.link(ins)
                dve.sem_inc(passed, 1)
                for t in range(NT):
                    ins = dve.bn_aggr(mv[:, t, :], stats[:, t, :])
                ins.then_inc(var_ready, 1)
                dve.wait_ge(std_ready, b + 1)
                c_.link(dve.reciprocal(rstd[:], rstd[:]))
                for t in range(NT):
                    ins = dve.tensor_scalar(z[:, t, :], h2[:, t, :], mv[:, t, 0:1], rstd[:, t:t + 1],
                                            ALU.subtract, ALU.mult)
                ins.then_inc(z_ready, 1)
                dve.wait_ge(z_turned, b + 1)
                dve.tensor_copy(zT[:, 0, 0:G], ps[0][0:DH, 0:G])
                dve.tensor_copy(zT[:, 0, G:SEQ], ps[1][0:DH, 0:G]).then_inc(zT0_ready, 1)
                for m in range(M3):
                    for g in range(2):
                        n = 2 * m + g
                        dve.wait_ge(in_done, 12 * b + n + 1)
                        dve.tensor_copy(xpad[:, m, TAPS - 1 + g * G:TAPS - 1 + (g + 1) * G], ps[4 + n % 4][:, 0:G]
                                        ).then_inc(x_copied, 1)
                    dve.wait_ge(x_copied, 6 * b + 2 * m + 2)
                    c_.link(dve.tensor_scalar(xc[:, m, :], xpad[:, m, 0:SEQ], conv_w[:, m, 0:1], None, ALU.mult))
                    for j in range(1, TAPS):
                        ins = dve.scalar_tensor_tensor(out=xc[:, m, :], in0=xpad[:, m, j:j + SEQ],
                                                       scalar=conv_w[:, m, j:j + 1], in1=xc[:, m, :],
                                                       op0=ALU.mult, op1=ALU.add)
                        if j < TAPS - 1:
                            c_.link(ins)
                    ins.then_inc(conv_ready, 1)
                dve.wait_ge(xd_ready, 2 * b + 2)
                dve.tensor_tensor(kq[:, 0, :], xd[0:NS, :], xd[0:NS, :], ALU.mult).then_inc(ksq_ready, 1)
                c_.link(dve.tensor_copy(kq[:, 1, :], xd[32:32 + NS, :]))
                dve.wait_ge(stored["kq"], 16 * b + 16)
                dve.tensor_copy(split[0:NS], kq[:]).then_inc(split_ready, 1)
                dve.wait_ge(split_ready, 3 * b + 1)
                c_.link(dve.tensor_tensor(rest[:], kq[:], split[0:NS], ALU.subtract))
                c_.link(dve.tensor_copy(mid[:], rest[:]))
                dve.tensor_copy(split[32:32 + NS], mid[:]).then_inc(split_ready, 1)
                c_.link(dve.tensor_tensor(rest[:], rest[:], mid[:], ALU.subtract))
                dve.tensor_copy(split[64:64 + NS], rest[:]).then_inc(split_ready, 1)
                dve.wait_ge(ksq_done, b + 1)
                dve.wait_ge(dts_ready, 6 * b + 6)
                for g in range(2):
                    ins = dve.tensor_tensor(den[:, :, g * G:(g + 1) * G], dts[:, :, g * G:(g + 1) * G],
                                            ps[2 + g][:, 0:G].unsqueeze(1).to_broadcast([128, M3, G]), ALU.mult)
                ins.then_inc(den_mul, 1)
                dve.wait_ge(k_turned, b + 1)
                c_.link(dve.tensor_copy(kT[:].rearrange("p c n -> p (c n)"), ps[0][0:CH, 0:NC * NS]))
                c_.link(dve.tensor_tensor(kTsq[:], kT[:], kT[:], ALU.mult))
                c_.link(dve.tensor_reduce(k2[:], kTsq[:], AX_X, ALU.add))
                dve.wait_ge(den_ready, b + 1)
                c_.link(dve.reciprocal(den[:], den[:]))
                dve.wait_ge(stored["delta"], 16 * b + 16)
                dve.tensor_tensor(delta[:], dts[:], den[:], ALU.mult).then_inc(delta_ready, 1)
                dve.wait_ge(stored["u"], 16 * b + 16)
                for c in range(NC):
                    dve.wait_ge(u_turned, NC * b + c + 1)
                    dve.tensor_copy(uT[0:CH, c, :], ps[4 + c % 4][0:CH, 0:DI]).then_inc(uT_copied, 1)
                dve.wait_ge(u2_ready, NC * b + NC)
                dve.tensor_tensor(g2[:], u2[:], k2[:], ALU.mult).then_inc(g2_ready, 1)
                dve.wait_ge(g_ready, b + 1)
                c_.link(dve.tensor_scalar(gn[:], gn[:], 1e-7, None, ALU.add))
                c_.link(dve.reciprocal(gn[:], gn[:]))
                c_.link(dve.tensor_tensor(gr[:], gn[:], gn[:], ALU.mult))
                c_.link(dve.tensor_tensor(gr[:], gr[:], g2[:], ALU.mult))
                c_.link(dve.tensor_scalar(alpha[:], gr[:], NS_C, NS_B, ALU.mult, ALU.add))
                c_.link(dve.tensor_tensor(alpha[:], alpha[:], gr[:], ALU.mult))
                c_.link(dve.tensor_scalar(alpha[:], alpha[:], NS_A, None, ALU.add))
                c_.link(dve.tensor_tensor(alpha[:], alpha[:], gn[:], ALU.mult))
                dve.wait_ge(stored["ak"], 16 * b + 16)
                c_.link(dve.tensor_tensor(ak[:], kT[:], alpha[:].unsqueeze(2).to_broadcast([CH, NC, NS]), ALU.mult))
                dve.tensor_scalar(ck[0:CH], ak[:], decay[:, 0:1], None, ALU.mult).then_inc(ck_ready, 1)
                for c in range(NC - 1):
                    dve.wait_ge(carry_done, (NC - 1) * b + c + 1)
                    dve.tensor_copy(uT[CARRY:CARRY + NS, c + 1, :], ps[1][0:NS, 0:DI]).then_inc(carry_ready, 1)
                c_.close()


def phase_scan(nc, a, n_img, u_dram, ak_dram, delta_dram, kq_dram, dx_dram, zs_dram, h2_dram, h3_dram):
    UNITS = NQ * M3
    PAIRS = NC // 2
    with ExitStack() as ctx:
        def sb(name, shape, dt=F32):
            return ctx.enter_context(nc.sbuf_tensor("d_" + name + "_t", shape, dt))

        def sem(name):
            return nc.alloc_semaphore("d_" + name)

        v = sb("v", [128, M3, Q4, SEQ])
        da = sb("da", [128, 2, Q4, SEQ])
        kb = sb("kb", [128, 2, Q4, SEQ])
        qb = sb("qb", [128, 2, Q4, SEQ])
        lk = sb("lk", [KR, 2, NC, Q4, CH])
        uT = sb("uT", [KR, NC, DI])
        ak = sb("ak", [CH, NC, NS])
        kq = sb("kq", [KR, 2, SEQ], BF16)
        delta = sb("delta", [128, M3, SEQ])
        y = sb("y", [128, M3, SEQ])
        zs = sb("zs", [128, M3, SEQ])
        h = sb("h", [T, NT, D])
        within = sb("within", [CH, CH])
        select = sb("select", [KR, NS, 128], BF16)
        outT = sb("outT", [128, M3, D])
        ident = sb("ident", [128, 128])

        ps_v = [ctx.enter_context(nc.psum_tensor(f"d_v{n}", [128, 512], F32)) for n in range(4)]
        ps_y = ctx.enter_context(nc.psum_tensor("d_y", [128, 2, 512], F32))
        ps_b = ctx.enter_context(nc.psum_tensor("d_b", [128, 2, 512], F32))

        QUARTER = M3 * PAIRS
        V0 = 2 * QUARTER
        W0 = 2 * M3
        weights_in = sem("weights_in")
        consts = sem("consts")
        u_in = [sem(f"u_in{m}") for m in range(M3)]
        ak_in = sem("ak_in")
        kq_in = sem("kq_in")
        delta_in = [sem(f"delta_in{m}") for m in range(M3)]
        dx_in = sem("dx_in")
        zs_in = sem("zs_in")
        h2_in = sem("h2_in")
        carried_in = [sem("carried_in0"), sem("carried_in1")]
        zeroed = sem("zeroed")
        lk_ready = sem("lk_ready")
        spread = sem("spread")
        spread_copied = sem("spread_copied")
        v_done = sem("v_done")
        v_ready = sem("v_ready")
        w_ready = sem("w_ready")
        da_ready = sem("da_ready")
        scanned = sem("scanned")
        hq_ready = sem("hq_ready")
        ysum_done = sem("ysum_done")
        y_added = sem("y_added")
        gated = sem("gated")
        out_done = sem("out_done")
        h3_ready = sem("h3_ready")
        h3_out = sem("h3_out")

        block = ctx.enter_context(nc.Block())

        def each_unit(eng, step):
            for u in range(3):
                step(0, u, False, True)
            with eng.Fori(0, n_img - 1) as b:
                for u in range(3, UNITS):
                    step(b, u, True, True)
                for u in range(3):
                    step(b + 1, u, True, True)
            for u in range(3, UNITS):
                step(n_img - 1, u, True, False)

        @block.sync
        def _(sp):
            sp.dma_start(within[:], a["within"]).then_inc(weights_in, 16)
            sp.dma_start(outT[:], a["outT"]).then_inc(weights_in, 16)
            sp.sem_inc(h3_out, 16)

            def load_carried(b, q):
                sp.wait_ge(v_done, QUARTER * (NQ * b + q + 1))
                sp.dma_start(lk[CARRY:CARRY + NS, q % 2].rearrange("p c n t -> p (c n t)"),
                             a["carried"][q % NQ].rearrange("p c n t -> p (c n t)")).then_inc(carried_in[q % 2], 16)

            def load_part(b, m):
                cols = slice(m * 128, (m + 1) * 128)
                sp.wait_ge(w_ready, W0 + UNITS * b - M3 + m + 1)
                sp.dma_start(delta[:, m, :], delta_dram[b][:, m, :]).then_inc(delta_in[m], 16)
                sp.wait_ge(v_done, V0 + PAIRS * (UNITS * b - M3 + m + 1))
                sp.dma_start(uT[0:CARRY + NS, :, cols], u_dram[b][0:CARRY + NS, :, cols]).then_inc(u_in[m], 16)

            def load_first(b):
                sp.wait_ge(lk_ready, NQ * b + 1)
                sp.dma_start(ak[:], ak_dram[b]).then_inc(ak_in, 16)
                sp.wait_ge(spread, 8 * NQ * b + 1)
                sp.dma_start(kq[0:80], kq_dram[b]).then_inc(kq_in, 16)

            def load_skip(b):
                sp.dma_start(y[:], dx_dram[b]).then_inc(dx_in, 16)

            def load_gates(b):
                sp.dma_start(zs[:], zs_dram[b]).then_inc(zs_in, 16)

            def load_residual(b):
                sp.wait_ge(h3_out, 16 * b + 16)
                sp.dma_start(h[:], h2_dram[b]).then_inc(h2_in, 16)

            sp.wait_ge(zeroed, 3)
            load_first(0)
            load_carried(0, 0)
            for m in range(M3):
                load_part(0, m)
            load_carried(0, 1)
            load_skip(0)
            load_gates(0)
            with sp.Fori(0, n_img - 1) as b:
                load_residual(b)
                load_carried(b, 2)
                load_carried(b, 3)
                load_first(b + 1)
                load_carried(b, 4)
                for m in range(M3):
                    load_part(b + 1, m)
                load_carried(b, 5)
                sp.wait_ge(gated, b + 1)
                load_skip(b + 1)
                sp.wait_ge(out_done, b + 1)
                load_gates(b + 1)
                sp.wait_ge(h3_ready, b + 2)
                sp.dma_start(h3_dram[b], h[:]).then_inc(h3_out, 16)
            load_residual(n_img - 1)
            load_carried(n_img - 1, 2)
            load_carried(n_img - 1, 3)
            sp.wait_ge(h3_ready, n_img + 1)
            sp.dma_start(h3_dram[n_img - 1], h[:]).then_inc(h3_out, 16)
            sp.wait_ge(h3_out, 16 * n_img + 16)

        @block.gpsimd
        def _(pool):
            identity(pool, ident[:], consts, 0)
            pool.memset(select[:], 0.0).then_inc(consts, 1)
            for part in range(3):
                pool.wait_ge(consts, part + 3)
                pool.affine_select(out=select[:], in_=select[:], compare_op=ALU.not_equal, fill=1.0, base=-32 * part,
                                   pattern=[[-1, NS], [0, 128]], channel_multiplier=1).then_inc(consts, 1)
            pool.wait_ge(consts, 6)
            pool.memset(kq[64:], 0.0).then_inc(zeroed, 1)
            pool.memset(uT[64:], 0.0).then_inc(zeroed, 1)
            pool.wait_ge(zeroed, 2)
            pool.memset(lk[:], 0.0).then_inc(zeroed, 1)
            pool.memset(da[:], 0.0).then_inc(consts, 1)
            pool.wait_ge(weights_in, 32)
            pool.wait_ge(consts, 7)
            pool.wait_ge(zeroed, 3)
            pool.sem_inc(hq_ready, W0)
            pool.sem_inc(lk_ready, 1)

            def powers(b, q):
                if q % NQ == 0:
                    pool.wait_ge(ak_in, 16 * (b + q // NQ) + 16)
                pool.wait_ge(v_done, QUARTER * (NQ * b + q + 1))
                q4 = q % NQ
                pool.tensor_tensor(lk[0:CH, q % 2], within[:].unsqueeze(1).unsqueeze(1).to_broadcast([CH, NC, Q4, CH]),
                                   ak[:, :, Q4 * q4:Q4 * q4 + Q4].unsqueeze(3).to_broadcast([CH, NC, Q4, CH]),
                                   ALU.mult).then_inc(lk_ready, 1)

            def step(b, u, behind, ahead):
                q, m = u // M3, u % M3
                pool.wait_ge(spread_copied, 8 * NQ * b + 8 * q + 9)
                pool.wait_ge(scanned, UNITS * b + u + 1)
                pool.tensor_tensor(v[:, m], v[:, m], qb[:, q % 2], ALU.mult).then_inc(hq_ready, 1)
                if m == 0 and (q + 1 < NQ or ahead):
                    powers(b, q + 1)

            powers(0, 0)
            each_unit(pool, step)

        @block.tensor
        def _(pe):
            pe.wait_ge(weights_in, 32)
            pe.wait_ge(consts, 7)
            pe.wait_ge(zeroed, 3)
            pe.sem_inc(ysum_done, 3)
            pe.sem_inc(v_done, V0)
            pe.sem_inc(spread, 1)

            def spread_rows(b, q, first, last):
                if q % NQ == 0 and first == 0:
                    pe.wait_ge(kq_in, 16 * (b + q // NQ) + 16)
                for i in range(first, last):
                    pe.wait_ge(spread_copied, 8 * NQ * b + 8 * q + i + 1)
                    for g in range(2):
                        ins = pe.matmul(ps_b[:, g, 0:G], select[:, Q4 * (q % NQ) + i % Q4, :],
                                        kq[:, i // Q4, g * G:(g + 1) * G], start=True, stop=True)
                    ins.then_inc(spread, 1)

            def momentum(b, u):
                q, m = u // M3, u % M3
                if m == 0:
                    pe.wait_ge(lk_ready, NQ * b + q + 2)
                    pe.wait_ge(carried_in[q % 2], 16 * (2 * b + q // 2 + 1))
                if q == 0:
                    pe.wait_ge(u_in[m], 16 * b + 16)
                for k in range(PAIRS):
                    n = PAIRS * u + k
                    pe.wait_ge(v_ready, UNITS * PAIRS * b + n + 1)
                    for c in range(2):
                        ins = pe.matmul(ps_v[n % 4][:, c * Q4 * CH:(c + 1) * Q4 * CH], uT[:, 2 * k + c, m * 128:(m + 1) * 128],
                                        lk[:, q % 2, 2 * k + c].rearrange("p n t -> p (n t)"), start=True, stop=True)
                    ins.then_inc(v_done, 1)

            def sum_states(b, u, g):
                m = u % M3
                if g == 0:
                    pe.wait_ge(hq_ready, W0 + UNITS * b + u + 1)
                    pe.wait_ge(y_added, UNITS * b + u + 1)
                for i in range(Q4):
                    ins = pe.matmul(ps_y[:, g, 0:G], ident[:], v[:, m, i, g * G:(g + 1) * G],
                                    start=(i == 0), stop=(i == Q4 - 1))
                if g:
                    ins.then_inc(ysum_done, 1)

            def project_out(b, copied):
                pe.wait_ge(gated, b + 1)
                pe.wait_ge(spread_copied, 8 * NQ * (b + 1) + copied + 1)
                for t in range(NT):
                    out = (ps_b[0:T, 0], ps_b[0:T, 1], ps_y[0:T, 0])[t // 2][:, (t % 2) * D:(t % 2 + 1) * D]
                    for m in range(M3):
                        ins = pe.matmul(out, zs[:, m, t * T:(t + 1) * T], outT[:, m, :], start=(m == 0), stop=(m == M3 - 1))
                ins.then_inc(out_done, 1)

            def step(b, u, behind, ahead):
                q, m = u // M3, u % M3
                rows = (0, 3, 6, 8)[m:m + 2]
                momentum(b, u)
                if u == 2 and behind:
                    project_out(b - 1, 8 + rows[0])
                    pe.wait_ge(h3_ready, b + 1)
                for g in range(3):
                    if rows[0] + g < rows[1] and (q + 1 < NQ or ahead):
                        spread_rows(b, q + 1, rows[0] + g, rows[0] + g + 1)
                    if g < 2 and u >= 2:
                        sum_states(b, u - 2, g)
                    elif g < 2 and behind:
                        sum_states(b - 1, UNITS + u - 2, g)

            def finish(b):
                for u in range(UNITS - 2, UNITS):
                    for g in range(2):
                        sum_states(b, u, g)
                project_out(b, 0)

            spread_rows(0, 0, 0, 8)
            each_unit(pe, step)
            finish(n_img - 1)

        @block.scalar
        def _(act):
            act.wait_ge(consts, 7)
            act.sem_inc(v_ready, 4)
            act.sem_inc(spread_copied, 1)

            def copy_spread(b, q, first, last):
                for i in range(first, last):
                    if i == 0:
                        act.wait_ge(w_ready, UNITS * b + M3 * (q + 1))
                    if i == Q4:
                        act.wait_ge(hq_ready, UNITS * b + M3 * (q + 1))
                    act.wait_ge(spread, 8 * NQ * b + 8 * q + i + 2)
                    act.activation((kb, qb)[i // Q4][:, q % 2, i % Q4, :].rearrange("p (g t) -> p g t", g=2),
                                   ps_b[:, :, 0:G], ACT.Copy).then_inc(spread_copied, 1)

            def step(b, u, behind, ahead):
                q, m = u // M3, u % M3
                act.wait_ge(w_ready, W0 + UNITS * b + u + 1)
                act.activation(da[:, u % 2, :, 1:SEQ], da[:, u % 2, :, 1:SEQ], ACT.Copy, scale=-1.0, bias=1.0
                               ).then_inc(da_ready, 1)
                act.wait_ge(ysum_done, UNITS * b + u + 1)
                for k in range(PAIRS):
                    n = PAIRS * u + k
                    act.wait_ge(v_done, V0 + UNITS * PAIRS * b + n + 1)
                    act.activation(v[:, m, :, k * T:(k + 1) * T].rearrange("p n (c t) -> p n c t", c=2),
                                   ps_v[n % 4][:, 0:2 * Q4 * CH].rearrange("p (c n t) -> p n c t", c=2, n=Q4),
                                   ACT.Copy).then_inc(v_ready, 1)
                if q + 1 < NQ or ahead:
                    rows = (0, 3, 6, 8)[m:m + 2]
                    copy_spread(b, q + 1, rows[0], rows[1])

            copy_spread(0, 0, 0, 8)
            each_unit(act, step)

        @block.vector
        def _(dve):
            dve.wait_ge(consts, 7)
            dve.sem_inc(w_ready, W0)
            dve.sem_inc(y_added, 1)
            dve.sem_inc(h3_ready, 1)

            def decays(b, u, started):
                q, m = u // M3, u % M3
                dve.wait_ge(spread_copied, 8 * NQ * b + 8 * q + 5)
                if q % NQ == 0:
                    dve.wait_ge(delta_in[m], 16 * (b + q // NQ) + 16)
                if started:
                    dve.wait_ge(scanned, UNITS * b + u - 1)
                dve.tensor_tensor(da[:, u % 2, :, 1:SEQ], kb[:, q % 2, :, 1:SEQ],
                                  delta[:, m, 1:SEQ].unsqueeze(1).to_broadcast([128, Q4, SEQ - 1]), ALU.mult
                                  ).then_inc(w_ready, 1)

            def add_states(b, u):
                m = u % M3
                dve.wait_ge(ysum_done, UNITS * b + u + 4)
                if u == 0:
                    dve.wait_ge(dx_in, 16 * b + 16)
                if u >= M3:
                    dve.wait_ge(y_added, UNITS * b + u - 1)
                dve.tensor_tensor(y[:, m, :].rearrange("p (g t) -> p g t", g=2), ps_y[:, :, 0:G],
                                  y[:, m, :].rearrange("p (g t) -> p g t", g=2), ALU.add).then_inc(y_added, 1)

            def gate(b):
                dve.wait_ge(zs_in, 16 * b + 16)
                dve.wait_ge(y_added, UNITS * (b + 1) + 1)
                dve.tensor_tensor(zs[:], y[:], zs[:], ALU.mult).then_inc(gated, 1)

            def residual(b):
                dve.wait_ge(h2_in, 16 * b + 16)
                dve.wait_ge(out_done, b + 1)
                for t in range(3):
                    src = (ps_b[0:T, 0], ps_b[0:T, 1], ps_y[0:T, 0])[t][:, 0:2 * D]
                    ins = dve.tensor_tensor(h[:, 2 * t:2 * t + 2, :], src.rearrange("p (t d) -> p t d", d=D),
                                            h[:, 2 * t:2 * t + 2, :], ALU.add)
                ins.then_inc(h3_ready, 1)

            def step(b, u, behind, ahead):
                if u + 1 < UNITS or ahead:
                    decays(b, u + 1, behind or u >= 1)
                dve.wait_ge(da_ready, UNITS * b + u + 1)
                dve.wait_ge(v_ready, UNITS * PAIRS * b + PAIRS * (u + 1) + 4)
                flat = v[:, u % M3].rearrange("p n t -> p (n t)")
                dve.tensor_tensor_scan(flat, da[:, u % 2].rearrange("p n t -> p (n t)"), flat, 0.0, ALU.mult, ALU.add
                                       ).then_inc(scanned, 1)
                if u == 2 and behind:
                    residual(b - 1)
                if u >= 2:
                    add_states(b, u - 2)
                elif behind:
                    add_states(b - 1, UNITS + u - 2)
                if u == 1 and behind:
                    gate(b - 1)

            def finish(b):
                add_states(b, UNITS - 2)
                add_states(b, UNITS - 1)
                gate(b)
                residual(b)

            decays(0, 0, False)
            each_unit(dve, step)
            finish(n_img - 1)


def phase_project(nc, a, half, n_img, h3_dram, hn_dram, qk_dram, v_dram):
    b0 = half * n_img
    P = "e%d_" % half
    with ExitStack() as ctx:
        def sb(name, shape, dt=F32):
            return ctx.enter_context(nc.sbuf_tensor(P + name + "_t", shape, dt))

        def sem(name):
            return nc.alloc_semaphore(P + name)

        w = sb("w", [DH, 2, 3 * D])
        gain = sb("gain", [DH, 2])
        shift = sb("shift", [DH, 2])
        gumbel = sb("gumbel", [T, 3])
        bias = sb("bias", [T, D])
        ident = sb("ident", [128, 128])
        eps_col = sb("eps_col", [T, 1])
        h = sb("h", [T, NT, D])
        hn = sb("hn", [T, NT, D])
        hb = sb("hb", [T, NT, D])
        z = sb("z", [T, NT, D])
        stats = sb("stats", [T, NT, 6])
        mv = sb("mv", [T, NT, 2])
        rstd = sb("rstd", [T, NT])
        zT = sb("zT", [DH, 2, SEQ])
        parts = sb("parts", [DH, 2, 3, 2, SEQ], BF16)
        rest = sb("rest", [DH, 4, G])
        va = sb("va", [T, NT, HEADS, 32])

        ps = [ctx.enter_context(nc.psum_tensor(f"{P}ps{n}", [128, 512], F32)) for n in range(8)]

        weights_in = sem("weights_in")
        consts = sem("consts")
        h_in = sem("h_in")
        h_used = sem("h_used")
        var_ready = sem("var_ready")
        std_ready = sem("std_ready")
        hn_ready = sem("hn_ready")
        hb_ready = sem("hb_ready")
        hb_out = sem("hb_out")
        z_ready = sem("z_ready")
        z_turned = sem("z_turned")
        zT0_ready = sem("zT0_ready")
        zT1_ready = sem("zT1_ready")
        qk_done = sem("qk_done")
        hi_ready = sem("hi_ready")
        rest_ready = sem("rest_ready")
        mid_ready = sem("mid_ready")
        lo_ready = sem("lo_ready")
        qk_out = sem("qk_out")
        v_done = sem("v_done")
        v_ready = sem("v_ready")
        v_out = sem("v_out")
        chain = sem("chain")
        passed = sem("passed")
        V_PER = 4

        block = ctx.enter_context(nc.Block())

        @block.sync
        def _(sp):
            names = ("n1s_g", "n1s_b") if half else ("n1l_g", "n1l_b")
            sp.dma_start(w[:], a["f_wqkv"]).then_inc(weights_in, 16)
            sp.dma_start(gain[:], a[names[0]]).then_inc(weights_in, 16)
            sp.dma_start(shift[:], a[names[1]]).then_inc(weights_in, 16)
            sp.dma_start(gumbel[:], a["gumbel"].partition_broadcast(T)).then_inc(weights_in, 16)
            sp.dma_start(bias[:], a["f_bproj"].partition_broadcast(T)).then_inc(weights_in, 16)
            sp.sem_inc(hb_out, 16)
            sp.sem_inc(qk_out, 64)
            sp.sem_inc(v_out, 16)
            with sp.Fori(0, n_img) as b:
                sp.wait_ge(h_used, b + 1)
                sp.dma_start(h[:], h3_dram[b + b0]).then_inc(h_in, 16)
                sp.wait_ge(hb_ready, b + 1)
                sp.dma_start(hn_dram[b + b0], hb[:]).then_inc(hb_out, 16)
                sp.wait_ge(v_ready, 3 * b + 3)
                sp.dma_start(v_dram[b + b0], va[:]).then_inc(v_out, 16)
                sp.wait_ge(lo_ready, 8 * b + 12)
                for m in range(2):
                    for x in range(2):
                        sp.dma_start(qk_dram[b + b0, x, :, m * DH:(m + 1) * DH, :].rearrange("p r t -> r p t"),
                                     parts[:, x, :, m, :]).then_inc(qk_out, 16)
            sp.wait_ge(hb_out, 16 * n_img + 16)
            sp.wait_ge(qk_out, 64 * n_img + 64)
            sp.wait_ge(v_out, 16 * n_img + 16)

        @block.gpsimd
        def _(pool):
            identity(pool, ident[:], consts, 0)
            pool.memset(eps_col[:], LN_EPS)
            pool.memset(va[:], 1.0).then_inc(consts, 1)
            pool.wait_ge(weights_in, 80)
            if half:
                pool.tensor_scalar(gumbel[:, 1:2], gumbel[:, 1:2], gumbel[:, 0:1], None, ALU.add).then_inc(consts, 1)
                pool.wait_ge(consts, 4)
                pool.tensor_scalar(gumbel[:, 2:3], gumbel[:, 2:3], gumbel[:, 1:2], None, ALU.add).then_inc(consts, 1)
                pool.wait_ge(consts, 5)
                for n, (lo, hi) in enumerate(((DH, D), (64, DH), (0, 64))):
                    ins = pool.tensor_scalar(bias[:, lo:hi], bias[:, lo:hi], gumbel[:, n:n + 1], None, ALU.mult)
                ins.then_inc(consts, 1)
                pool.wait_ge(consts, 6)
            pool.sem_inc(lo_ready, 4)
            with pool.Fori(0, n_img) as b:
                pool.wait_ge(hn_ready, b + 1)
                pool.wait_ge(hb_out, 16 * b + 16)
                pool.tensor_tensor(hb[:], hn[:], bias[:].unsqueeze(1).to_broadcast([T, NT, D]), ALU.add
                                   ).then_inc(hb_ready, 1)
                for n in range(8):
                    x, m, g = n // 4, n // 2 % 2, n % 2
                    pool.wait_ge(mid_ready, 8 * b + n + 1)
                    pool.tensor_tensor(parts[:, x, 2, m, g * G:(g + 1) * G], rest[:, n % 4, :],
                                       parts[:, x, 1, m, g * G:(g + 1) * G], ALU.subtract).then_inc(lo_ready, 1)

        @block.tensor
        def _(pe):
            pe.wait_ge(weights_in, 80)
            pe.wait_ge(consts, 3)
            with pe.Fori(0, n_img) as b:
                pe.wait_ge(z_ready, b + 1)
                for m in range(2):
                    for g in range(2):
                        for t in range(3):
                            ins = pe.transpose(ps[2 * m + g][0:DH, t * T:(t + 1) * T],
                                               z[:, 3 * g + t, m * DH:(m + 1) * DH], ident[0:T, 0:T])
                ins.then_inc(z_turned, 1)
                pe.wait_ge(zT0_ready, b + 1)
                pe.wait_ge(zT1_ready, b + 1)
                for n in range(8):
                    x, m, g = n // 4, n // 2 % 2, n % 2
                    if n >= 4:
                        pe.wait_ge(rest_ready, 8 * b + n - 3)
                    for c in range(2):
                        ins = pe.matmul(ps[4 + n % 4][0:DH, 0:G], w[:, c, x * D + m * DH:x * D + (m + 1) * DH],
                                        zT[:, c, g * G:(g + 1) * G], start=(c == 0), stop=(c == 1))
                    ins.then_inc(qk_done, 1)
                for t in range(NT):
                    for c in range(2):
                        ins = pe.matmul(ps[t // 2][0:T, (t % 2) * D:(t % 2 + 1) * D], zT[:, c, t * T:(t + 1) * T],
                                        w[:, c, 2 * D:3 * D], start=(c == 0), stop=(c == 1))
                    if t % 2:
                        ins.then_inc(v_done, 1)

        @block.scalar
        def _(act):
            act.wait_ge(weights_in, 80)
            act.wait_ge(consts, 3)
            with act.Fori(0, n_img) as b:
                for n in range(2):
                    act.wait_ge(var_ready, 2 * b + n + 1)
                    act.activation(rstd[:], mv[:, :, 1], ACT.Sqrt, bias=eps_col[:, 0:1]).then_inc(std_ready, 1)
                act.wait_ge(z_turned, b + 1)
                for g in range(2):
                    ins = act.activation(zT[:, 1, g * G:(g + 1) * G], ps[2 + g][0:DH, 0:G], ACT.Identity,
                                         scale=gain[:, 1:2], bias=shift[:, 1:2])
                ins.then_inc(zT1_ready, 1)
                act.wait_ge(qk_out, 64 * b + 64)

                def high(n):
                    x, m, g = n // 4, n // 2 % 2, n % 2
                    act.wait_ge(qk_done, 8 * b + n + 1)
                    act.activation(parts[:, x, 0, m, g * G:(g + 1) * G], ps[4 + n % 4][0:DH, 0:G], ACT.Copy
                                   ).then_inc(hi_ready, 1)

                high(0)
                for n in range(8):
                    x, m, g = n // 4, n // 2 % 2, n % 2
                    if n < 7:
                        high(n + 1)
                    act.wait_ge(rest_ready, 8 * b + n + 1)
                    act.activation(parts[:, x, 1, m, g * G:(g + 1) * G], rest[:, n % 4, :], ACT.Copy
                                   ).then_inc(mid_ready, 1)

        @block.vector
        def _(dve):
            dve.wait_ge(weights_in, 80)
            dve.wait_ge(consts, 3)
            dve.sem_inc(h_used, 1)
            with dve.Fori(0, n_img) as b:
                c_ = Chain(dve, chain, V_PER * b, V_PER)

                def layernorm(src, dst, n, done):
                    for t in range(NT):
                        ins = dve.bn_stats(stats[:, t, :], src[:, t, :])
                    c_.link(ins)
                    dve.sem_inc(passed, 1)
                    for t in range(NT):
                        ins = dve.bn_aggr(mv[:, t, :], stats[:, t, :])
                    ins.then_inc(var_ready, 1)
                    dve.wait_ge(std_ready, 2 * b + n + 1)
                    c_.link(dve.reciprocal(rstd[:], rstd[:]))
                    for t in range(NT):
                        ins = dve.tensor_scalar(dst[:, t, :], src[:, t, :], mv[:, t, 0:1], rstd[:, t:t + 1],
                                                ALU.subtract, ALU.mult)
                    ins.then_inc(done, 1)

                dve.wait_ge(h_in, 16 * b + 16)
                dve.wait_ge(h_used, b + 1)
                layernorm(h, hn, 0, hn_ready)
                dve.wait_ge(hn_ready, b + 1)
                layernorm(hn, z, 1, z_ready)
                dve.wait_ge(hb_ready, b + 1)
                dve.sem_inc(h_used, 1)
                dve.wait_ge(z_turned, b + 1)
                for g in range(2):
                    ins = dve.tensor_scalar(zT[:, 0, g * G:(g + 1) * G], ps[g][0:DH, 0:G], gain[:, 0:1], shift[:, 0:1],
                                            ALU.mult, ALU.add)
                ins.then_inc(zT0_ready, 1)
                for n in range(8):
                    x, m, g = n // 4, n // 2 % 2, n % 2
                    dve.wait_ge(hi_ready, 8 * b + n + 1)
                    dve.wait_ge(lo_ready, 8 * b + n + 1)
                    dve.tensor_tensor(rest[:, n % 4, :], ps[4 + n % 4][0:DH, 0:G], parts[:, x, 0, m, g * G:(g + 1) * G],
                                      ALU.subtract).then_inc(rest_ready, 1)
                dve.wait_ge(v_out, 16 * b + 16)
                for t in range(3):
                    dve.wait_ge(v_done, 3 * b + t + 1)
                    dve.tensor_copy(va[:, 2 * t:2 * t + 2, :, 0:HD],
                                    ps[t][0:T, 0:2 * D].rearrange("p (t h d) -> p t h d", t=2, h=HEADS)
                                    ).then_inc(v_ready, 1)
                c_.close()


def phase_attend(nc, a, n_img, hn_dram, qk_dram, v_dram, x1_dram):
    GR = HEADS // 4
    PER = 4
    QG = 4 * NT * 2
    RG = QG // PER
    R = GR * RG
    LEAD = RG + 6
    S = 8
    KR6 = QK_ROWS + 3
    MISC = 15
    SQ = GR * QG
    with ExitStack() as ctx:
        def sb(name, shape, dt=F32):
            return ctx.enter_context(nc.sbuf_tensor("f_" + name + "_t", shape, dt))

        def sem(name):
            return nc.alloc_semaphore("f_" + name)

        q6 = sb("q6", [KR6, GR, 4, SEQ], BF16)
        k6 = sb("k6", [KR6, GR, 4, SEQ], BF16)
        va = sb("va", [T, GR, NT, 4, 32])
        p = sb("p", [T, 2, 4, G])
        mx = sb("mx", [T, 4, NT, 2])
        nmx = sb("nmx", [T, NT, 4])
        negs = sb("negs", [T, NT, 3, 4])
        part = sb("part", [T, NT, 4], BF16)
        nrest = sb("nrest", [T, NT, 4])
        nparts = sb("nparts", [12, SEQ], BF16)
        sums = sb("sums", [36, T])
        inv = sb("inv", [36, T])
        oT = sb("oT", [128, 3, SEQ])
        wp = sb("wp", [128, 2, 3, D])
        gumbel = sb("gumbel", [128, 3])
        ident = sb("ident", [128, 128])
        sums_to = sb("sums_to", [36, 3, 3, 4, 32])
        hn = sb("hn", [T, NT, D])
        x1 = sb("x1", [T, NT, D])

        ps_s = [ctx.enter_context(nc.psum_tensor(f"f_s{n}", [128, 2, 512], F32)) for n in range(2)]
        ps_q = [ctx.enter_context(nc.psum_tensor(f"f_q{n}", [128, 512], F32)) for n in range(2)]
        ps_o = ctx.enter_context(nc.psum_tensor("f_o", [128, 512], F32))
        ps_m = ctx.enter_context(nc.psum_tensor("f_m", [128, 512], F32))

        weights_in = sem("weights_in")
        consts = sem("consts")
        w_chain = sem("w_chain")
        qk_in = [sem(f"qk_in{j}") for j in range(GR)]
        v_in = [sem(f"v_in{j}") for j in range(GR)]
        hn_in = sem("hn_in")
        q_done = sem("q_done")
        q_used = sem("q_used")
        nmx_ready = sem("nmx_ready")
        misc_done = sem("misc_done")
        misc_used = sem("misc_used")
        split = sem("split")
        mid_ready = sem("mid_ready")
        max_in = [sem(f"max_in{j}") for j in range(GR)]
        s_done = sem("s_done")
        p_ready = sem("p_ready")
        pv_done = sem("pv_done")
        o_ready = sem("o_ready")
        sums_in = sem("sums_in")
        inv_ready = sem("inv_ready")
        x1_out = sem("x1_out")
        chain = sem("chain")
        passed = sem("passed")

        block = ctx.enter_context(nc.Block())

        def each_image(eng, rounds, finish, spans):
            rounds(0, 0, S, False, True, 0)
            for half, (first, end) in enumerate(spans):
                with eng.Fori(first, end) as b:
                    rounds(b, S, R, True, True, half)
                    rounds(b + 1, 0, S, True, True, half)
            rounds(n_img - 1, S, R, True, False, 1)
            finish(n_img - 1)

        def queries_of(r, ahead):
            n = PER * (r + LEAD)
            return range(n, n + PER) if ahead or n < SQ else range(0)

        def group_before(r):
            return (r + LEAD) // RG - 1 if (r + LEAD) % RG == 0 else None

        USES = {(3, 0): ("inverses", 3, True), (3, 1): ("inverses", 4, True), (4, 0): ("inverses", 5, True),
                (5, 0): ("output", 0, True), (6, 0): ("output", 1, True), (7, 0): ("output", 2, True),
                (8, 0): ("maxima", 2, False), (9, 0): ("maxima", 3, False),
                (20, 0): ("maxima", 4, False), (21, 0): ("maxima", 5, False),
                (22, 0): ("inverses", 0, False), (23, 0): ("inverses", 1, False), (24, 0): ("inverses", 2, False),
                (32, 0): ("maxima", 6, False), (33, 0): ("maxima", 7, False)}
        OUTPUTS, MAXIMA_USE = 3, (None, 6, 8, 13)
        INVERT_ROUNDS = (20, 2)

        def misc_use(b, i):
            return MISC * b + i - 4

        def misc_in(b, r, slot, behind, ahead):
            if (r, slot) not in USES:
                return None
            what, n, previous = USES[r, slot]
            if (previous and not behind) or (what == "maxima" and n // 2 == GR and not ahead):
                return None
            return what, (b - 1 if previous else b), n, misc_use(b, list(USES).index((r, slot)))

        @block.sync
        def _(sp):
            for half in range(2):
                sp.dma_start(wp[:, half], a["f_wproj"]).then_inc(weights_in, 16)
            sp.dma_start(gumbel[:], a["gumbel"].partition_broadcast(128)).then_inc(weights_in, 16)
            sp.sem_inc(x1_out, 16)

            def load(b, j):
                for x, dst in enumerate((q6, k6)):
                    for n, pair in enumerate(PRODUCTS):
                        sp.dma_start(dst[HD * n:HD * n + HD, j, :, :],
                                     qk_dram[b, x, pair[x], 4 * HD * j:4 * HD * (j + 1), :].rearrange(
                                         "(i d) t -> d i t", d=HD)).then_inc(qk_in[j], 16)
                sp.dma_start(va[:, j], v_dram[b][:, :, 4 * j:4 * j + 4, :]).then_inc(v_in[j], 16)

            def load_next(b, j):
                sp.wait_ge(pv_done, R * b + RG * (j + 1) + 2)
                load(b + 1, j)

            def maxima(b, j, use):
                sp.wait_ge(misc_used, use + 3)
                for n in range(3):
                    sp.dma_start(q6[QK_ROWS + n:QK_ROWS + n + 1, j, :, :], nparts[4 * n:4 * n + 4, :]
                                 ).then_inc(max_in[j], 16)

            def take_sums(b, n):
                if n % 3 == 0:
                    sp.wait_ge(inv_ready, 2 * b + n // 3 + 1)
                    sp.sem_inc(passed, 1)
                sp.wait_ge(o_ready, 6 * b + n + 2)
                j, g = n // 2, n % 2
                for i in range(4):
                    row = 4 * (n % 3) + i
                    sp.dma_start(sums[row::12, :], oT[32 * i + HD:32 * i + HD + 1, j, g * G:(g + 1) * G].rearrange(
                        "one (t p) -> one t p", p=T)).then_inc(sums_in, 16)

            def store(b, use):
                sp.wait_ge(misc_used, use + 4)
                sp.dma_start(x1_dram[b], x1[:]).then_inc(x1_out, 16)

            def image(b, behind, ahead):
                if behind:
                    take_sums(b - 1, 5)
                    load_next(b - 1, 2)
                take_sums(b, 0)
                if behind:
                    store(b - 1, misc_use(b, OUTPUTS))
                sp.dma_start(hn[:], hn_dram[b]).then_inc(hn_in, 16)
                maxima(b, 1, misc_use(b, MAXIMA_USE[1]))
                take_sums(b, 1)
                if ahead:
                    load_next(b, 0)
                take_sums(b, 2)
                maxima(b, 2, misc_use(b, MAXIMA_USE[2]))
                take_sums(b, 3)
                if ahead:
                    load_next(b, 1)
                take_sums(b, 4)
                if ahead:
                    maxima(b + 1, 0, misc_use(b, MAXIMA_USE[3]))

            sp.sem_inc(inv_ready, 1)
            for j in range(GR):
                load(0, j)
            maxima(0, 0, 0)
            image(0, False, True)
            with sp.Fori(1, n_img - 1) as b:
                image(b, True, True)
            image(n_img - 1, True, False)
            take_sums(n_img - 1, 5)
            store(n_img - 1, misc_use(n_img, OUTPUTS) - 2)
            sp.wait_ge(x1_out, 16 * n_img + 16)

        @block.gpsimd
        def _(pool):
            identity(pool, ident[:], consts, 0)
            pool.memset(sums_to[:], 0.0).then_inc(consts, 1)
            pool.wait_ge(consts, 3)
            pool.affine_select(out=sums_to[:], in_=sums_to[:], compare_op=ALU.not_equal, fill=1.0, base=0,
                               pattern=[[-4, 3], [-12, 3], [-1, 4], [0, 32]], channel_multiplier=1).then_inc(consts, 1)
            pool.wait_ge(consts, 4)
            pool.memset(k6[QK_ROWS:], 1.0).then_inc(consts, 1)
            pool.wait_ge(consts, 5)
            pool.wait_ge(weights_in, 48)
            pool.tensor_scalar(gumbel[:, 1:2], gumbel[:, 1:2], gumbel[:, 0:1], None, ALU.add).then_inc(consts, 1)
            pool.wait_ge(consts, 6)
            pool.tensor_scalar(gumbel[:, 2:3], gumbel[:, 2:3], gumbel[:, 1:2], None, ALU.add).then_inc(consts, 1)
            pool.wait_ge(consts, 7)
            scaled = Chain(pool, w_chain)
            for rows, j, cols, n in ((slice(0, 128), 0, slice(0, 64), 3), (slice(0, 128), 0, slice(64, DH), 2),
                                     (slice(0, 128), 0, slice(DH, D), 1), (slice(0, 64), 1, slice(0, DH), 2),
                                     (slice(0, 64), 1, slice(DH, D), 1), (slice(64, 128), 1, slice(0, D), 1),
                                     (slice(0, 128), 2, slice(0, D), 1)):
                scaled.link(pool.tensor_scalar(wp[rows, 1, j, cols], wp[rows, 1, j, cols], gumbel[rows, n - 1:n], None,
                                               ALU.mult))
            pool.sem_inc(consts, 1)

            def split_maxima(n):
                pool.wait_ge(nmx_ready, n + 1)
                pool.sem_inc(passed, 1)
                c = Chain(pool, chain, 4 * n, 4)
                c.link(pool.tensor_copy(part[:], nmx[:]))
                pool.sem_inc(passed, 1)
                c.link(pool.tensor_copy(negs[:, :, 0, :], part[:]))
                c.link(pool.tensor_tensor(nrest[:], nmx[:], negs[:, :, 0, :], ALU.subtract))
                pool.sem_inc(passed, 1)
                c.link(pool.tensor_copy(part[:], nrest[:]))
                pool.sem_inc(passed, 1)
                pool.tensor_copy(negs[:, :, 1, :], part[:]).then_inc(mid_ready, 1)
                pool.wait_ge(mid_ready, n + 1)
                pool.tensor_tensor(negs[:, :, 2, :], nrest[:], negs[:, :, 1, :], ALU.subtract).then_inc(split, 1)
                c.close()

            with pool.Fori(0, GR * n_img) as n:
                split_maxima(n)

        @block.tensor
        def _(pe):
            pe.wait_ge(weights_in, 48)
            pe.wait_ge(consts, 8)
            pe.sem_inc(pv_done, 2)

            def by_queries(b, n):
                j, h, t, g = n // QG % GR, n // (2 * NT) % 4, n // 2 % NT, n % 2
                if n % QG == 0:
                    pe.wait_ge(qk_in[j], 192 * (b + n // SQ) + 192)
                pe.wait_ge(q_used, SQ * b + n + 1)
                pe.matmul(ps_q[n % 2][0:T, 0:G], q6[0:QK_ROWS, j, h, t * T:(t + 1) * T],
                          k6[0:QK_ROWS, j, h, g * G:(g + 1) * G], start=True, stop=True).then_inc(q_done, 1)

            def turn_maxima(b, j, g, use):
                pe.wait_ge(split, GR * b + j + 1)
                pe.wait_ge(misc_used, use + 1)
                pe.sem_inc(passed, 1)
                for t in range(3):
                    ins = pe.transpose(ps_m[0:12, t * T:(t + 1) * T],
                                       negs[:, 3 * g + t].rearrange("p n h -> p (n h)"), ident[0:T, 0:T])
                ins.then_inc(misc_done, 1)

            def weigh(b, r):
                j, t = r // RG, r % NT
                pe.wait_ge(p_ready, 2 * R * b + 2 * r + 4)
                if t == 0:
                    pe.wait_ge(o_ready, 6 * b + r // NT + 1)
                for i in range(4):
                    ins = pe.matmul(ps_o[32 * i:32 * i + 32, 0:G], va[:, j, t, i, :], p[:, r % 2, i, :],
                                    start=(t == 0), stop=(t == NT - 1))
                ins.then_inc(pv_done, 1)

            def spread_inverses(b, n, use):
                pe.wait_ge(inv_ready, 2 * b + n // 3 + 2)
                pe.wait_ge(misc_used, use + 1)
                for t in range(3):
                    ins = pe.matmul(ps_m[:, t * T:(t + 1) * T], sums_to[:, n % 3, t].rearrange("p i c -> p (i c)"), inv[:],
                                    start=True, stop=True)
                ins.then_inc(misc_done, 1)

            def project_out(b, n, use, half):
                pe.wait_ge(misc_used, use + 1)
                for t in range(2 * n, 2 * n + 2):
                    for j in range(GR):
                        ins = pe.matmul(ps_m[0:T, (t % 2) * D:(t % 2 + 1) * D], oT[:, j, t * T:(t + 1) * T],
                                        wp[:, half, j, :], start=(j == 0), stop=(j == GR - 1))
                ins.then_inc(misc_done, 1)

            def misc(use, half):
                if use is not None:
                    what, b, n, before = use
                    if what == "inverses":
                        spread_inverses(b, n, before)
                    elif what == "output":
                        project_out(b, n, before, half)
                    else:
                        turn_maxima(b, n // 2, n % 2, before)

            def rounds(b, first, last, behind, ahead, half):
                for r in range(first, last):
                    j, g, t = r // RG, r // NT % 2, r % NT
                    queries = queries_of(r, ahead)
                    if r % RG == 0:
                        pe.wait_ge(max_in[j], 48 * b + 48)
                        pe.wait_ge(v_in[j], 16 * b + 16)
                    for e in range(2):
                        pe.wait_ge(p_ready, 2 * R * b + 2 * r + e + 1)
                        for i in range(2):
                            ins = pe.matmul(ps_s[e][0:T, i, 0:G], k6[:, j, 2 * e + i, t * T:(t + 1) * T],
                                            q6[:, j, 2 * e + i, g * G:(g + 1) * G], start=True, stop=True)
                        ins.then_inc(s_done, 1)
                        for n in queries[e:e + 1]:
                            by_queries(b, n)
                    if r:
                        weigh(b, r - 1)
                    elif behind:
                        weigh(b - 1, R - 1)
                    misc(misc_in(b, r, 0, behind, ahead), half)
                    for n in queries[2:3]:
                        by_queries(b, n)
                    misc(misc_in(b, r, 1, behind, ahead), half)
                    for n in queries[3:4]:
                        by_queries(b, n)

            def finish(b):
                weigh(b, R - 1)
                for n in range(3):
                    spread_inverses(b, n + 3, misc_use(b + 1, n) - 2)
                for n in range(3):
                    project_out(b, n, misc_use(b + 1, OUTPUTS + n) - 2, 1)

            for n in range(QG):
                by_queries(0, n)
            for g in range(2):
                turn_maxima(0, 0, g, g)
            for n in range(QG, PER * LEAD):
                by_queries(0, n)
            each_image(pe, rounds, finish, ((0, n_img // 2), (n_img // 2, n_img - 1)))

        @block.scalar
        def _(act):
            act.wait_ge(consts, 8)
            act.sem_inc(p_ready, 2)
            act.sem_inc(o_ready, 1)

            def keep(b, n):
                act.wait_ge(pv_done, R * b + NT * n + 8)
                j, g = n // 2, n % 2
                if n < 2:
                    act.wait_ge(misc_done, misc_use(b, OUTPUTS + 2 + g))
                act.activation(oT[:, j, g * G:(g + 1) * G], ps_o[:, 0:G], ACT.Copy).then_inc(o_ready, 1)

            def rounds(b, first, last, behind, ahead, half):
                for r in range(first, last):
                    for e in range(2):
                        act.wait_ge(s_done, 2 * R * b + 2 * r + e + 1)
                        if e == 0:
                            act.wait_ge(pv_done, R * b + r + 1)
                        act.activation(p[:, r % 2, 2 * e:2 * e + 2, :], ps_s[e][0:T, :, 0:G], ACT.Exp, scale=HD ** -0.5
                                       ).then_inc(p_ready, 1)
                    if r and r % NT == 0:
                        keep(b, r // NT - 1)
                    elif r == 0 and behind:
                        keep(b - 1, 5)

            def finish(b):
                keep(b, 5)

            each_image(act, rounds, finish, ((0, n_img - 1),))

        @block.vector
        def _(dve):
            dve.wait_ge(consts, 8)
            dve.sem_inc(q_used, 2)
            dve.sem_inc(misc_used, 1)

            def maximum(b, n):
                h, t, g = n // (2 * NT) % 4, n // 2 % NT, n % 2
                dve.wait_ge(q_done, SQ * b + n + 1)
                dve.tensor_reduce(mx[:, h, t, g:g + 1], ps_q[n % 2][0:T, 0:G], AX_X, ALU.max).then_inc(q_used, 1)

            def negated(b, j):
                dve.wait_ge(q_used, SQ * b + QG * (j + 1) + 2)
                dve.tensor_reduce(nmx[:].rearrange("p t h -> p h t"), mx[:], AX_X, ALU.max, negate=True
                                  ).then_inc(nmx_ready, 1)
                dve.wait_ge(nmx_ready, GR * b + j + 1)

            def maxima_rows(b, j, g, use, first_group=False):
                if j:
                    dve.wait_ge(max_in[j - 1], 48 * b + 48)
                elif not first_group:
                    dve.wait_ge(max_in[GR - 1], 48 * b)
                dve.wait_ge(misc_done, use + 1)
                dve.tensor_copy(nparts[:, g * G:(g + 1) * G], ps_m[0:12, 0:G]).then_inc(misc_used, 1)

            def invert(b, batch, use):
                dve.wait_ge(sums_in, 192 * (2 * b + batch + 1))
                dve.wait_ge(misc_done, use)
                dve.reciprocal(inv[:], sums[:]).then_inc(inv_ready, 1)

            def normalize(b, n, use):
                j, g = n // 2, n % 2
                dve.wait_ge(misc_done, use + 1)
                dve.tensor_tensor(oT[:, j, g * G:(g + 1) * G], oT[:, j, g * G:(g + 1) * G], ps_m[:, 0:G], ALU.mult
                                  ).then_inc(misc_used, 1)

            def residual(b, n, use):
                if n == 0:
                    dve.wait_ge(hn_in, 16 * b + 16)
                    dve.wait_ge(x1_out, 16 * b + 16)
                dve.wait_ge(misc_done, use + 1)
                dve.tensor_tensor(x1[:, 2 * n:2 * n + 2, :], ps_m[0:T, 0:2 * D].rearrange("p (t d) -> p t d", d=D),
                                  hn[:, 2 * n:2 * n + 2, :], ALU.add).then_inc(misc_used, 1)

            def misc(use):
                if use is not None:
                    what, b, n, before = use
                    if what == "inverses":
                        normalize(b, n, before)
                    elif what == "output":
                        residual(b, n, before)
                    else:
                        maxima_rows(b, n // 2, n % 2, before)

            def rounds(b, first, last, behind, ahead, half):
                for r in range(first, last):
                    done = group_before(r)
                    if done is not None and (ahead or done < GR):
                        negated(b, done)
                    queries = queries_of(r, ahead)
                    for n in queries[:2]:
                        maximum(b, n)
                    misc(misc_in(b, r, 0, behind, ahead))
                    for n in queries[2:3]:
                        maximum(b, n)
                    misc(misc_in(b, r, 1, behind, ahead))
                    for n in queries[3:]:
                        maximum(b, n)
                    if r == INVERT_ROUNDS[0]:
                        invert(b, 0, misc_use(b, MAXIMA_USE[1]))
                    elif r == INVERT_ROUNDS[1] and behind:
                        invert(b - 1, 1, misc_use(b, 0) - 2)

            def finish(b):
                invert(b, 1, misc_use(b + 1, 0) - 2)
                for n in range(3):
                    normalize(b, n + 3, misc_use(b + 1, n) - 2)
                for n in range(3):
                    residual(b, n, misc_use(b + 1, OUTPUTS + n) - 2)

            for n in range(QG):
                maximum(0, n)
            negated(0, 0)
            for g in range(2):
                maxima_rows(0, 0, g, g, first_group=True)
            for n in range(QG, PER * LEAD):
                maximum(0, n)
            each_image(dve, rounds, finish, ((0, n_img - 1),))


def phase_mlp(nc, a, half, n_img, h3_dram, x1_dram, out_dram):
    b0 = half * n_img
    P = "g%d_" % half
    BR = 3 if half else 1
    KEEP = (D, DH, 64)
    MT = MLP // 128
    U = 2 * BR
    with ExitStack() as ctx:
        def sb(name, shape, dt=F32):
            return ctx.enter_context(nc.sbuf_tensor(P + name + "_t", shape, dt))

        def sem(name):
            return nc.alloc_semaphore(P + name)

        w1 = sb("w1", [DH, 2, MLP])
        w1c = sb("w1c", [DH, MLP])
        b1 = sb("b1", [128, MT])
        w2 = sb("w2", [128, BR, MT, D])
        gain = sb("gain", [DH, 2])
        shift = sb("shift", [DH, 2])
        gumbel = sb("gumbel", [128, 3])
        gsum = sb("gsum", [T, 3])
        bias = sb("bias", [T, D])
        ident = sb("ident", [128, 128])
        eps_col = sb("eps_col", [T, 1])
        x1 = sb("x1", [T, NT, D])
        h = sb("h", [T, NT, D])
        res = sb("res", [T, 2, NT, D])
        z = sb("z", [T, NT, D])
        stats = sb("stats", [T, NT, 6])
        mv = sb("mv", [T, NT, 2])
        rstd = sb("rstd", [T, NT])
        zT = sb("zT", [DH, 2, SEQ])
        hid = sb("hid", [128, 2, MT, G])
        o = sb("o", [T, NT, D])

        ps = [ctx.enter_context(nc.psum_tensor(f"{P}ps{n}", [128, 512], F32)) for n in range(8)]

        weights_in = sem("weights_in")
        consts = sem("consts")
        w_chain = sem("w_chain")
        x1_in = sem("x1_in")
        h_in = sem("h_in")
        var_ready = sem("var_ready")
        std_ready = sem("std_ready")
        z_ready = sem("z_ready")
        res1_ready = sem("res1_ready")
        res_ready = sem("res_ready")
        z_turned = sem("z_turned")
        zT0_ready = sem("zT0_ready")
        zT1_ready = sem("zT1_ready")
        up_done = sem("up_done")
        hid_ready = sem("hid_ready")
        down_done = sem("down_done")
        o_ready = sem("o_ready")
        o_out = sem("o_out")
        chain = sem("chain")
        passed = sem("passed")
        V_PER = 2
        W_IN = 8 * 16

        block = ctx.enter_context(nc.Block())

        def each_image(eng, body):
            if n_img > 2:
                with eng.Fori(0, n_img // 2 - 1) as j:
                    body(j, 0, True)
                    body(j, 1, True)
            body(n_img // 2 - 1, 0, True)
            body(n_img // 2 - 1, 1, False)

        @block.sync
        def _(sp):
            names = ("n2s_g", "n2s_b") if half else ("n2l_g", "n2l_b")
            sp.dma_start(w1[:], a["w_fc1"]).then_inc(weights_in, 16)
            sp.dma_start(w1c[0:64, :], a["w_fc1"][0:64, 0, :]).then_inc(weights_in, 16)
            sp.dma_start(b1[:], a["b_fc1"]).then_inc(weights_in, 16)
            sp.dma_start(w2[:, 0], a["w_fc2"]).then_inc(weights_in, 16)
            sp.dma_start(gain[:], a[names[0]]).then_inc(weights_in, 16)
            sp.dma_start(shift[:], a[names[1]]).then_inc(weights_in, 16)
            sp.dma_start(gumbel[:], a["gumbel"].partition_broadcast(128)).then_inc(weights_in, 16)
            sp.dma_start(bias[:], a["b_fc2"].partition_broadcast(T)).then_inc(weights_in, 16)
            sp.sem_inc(o_out, 16)

            def load(b):
                sp.dma_start(x1[:], x1_dram[b + b0]).then_inc(x1_in, 16)
                sp.dma_start(h[:], h3_dram[b + b0]).then_inc(h_in, 16)

            def image(j, k, ahead):
                b = 2 * j + k
                if ahead:
                    sp.wait_ge(z_ready, b + 1)
                    sp.wait_ge(res_ready, b + 1)
                    load(b + 1)
                sp.wait_ge(o_ready, 2 * b + 3)
                for t in range(NT):
                    sp.dma_start(out_dram[b + b0, t * T:(t + 1) * T, :], o[:, t, :]).then_inc(o_out, 16)

            load(0)
            each_image(sp, image)
            sp.wait_ge(o_out, 16 * NT * n_img + 16)

        @block.gpsimd
        def _(pool):
            identity(pool, ident[:], consts, 0)
            pool.memset(eps_col[:], LN_EPS).then_inc(consts, 1)
            pool.wait_ge(consts, 3)
            pool.memset(w1c[64:DH, :], 0.0).then_inc(consts, 1)
            pool.wait_ge(weights_in, W_IN)
            pool.wait_ge(consts, 4)
            if half:
                scaled = Chain(pool, w_chain)
                scaled.link(pool.tensor_copy(gsum[:, 0:1], gumbel[0:T, 0:1]))
                for n in range(1, 3):
                    scaled.link(pool.tensor_scalar(gsum[:, n:n + 1], gumbel[0:T, n:n + 1], gsum[:, n - 1:n], None, ALU.add))
                for n, (lo, hi) in enumerate(((DH, D), (64, DH), (0, 64))):
                    scaled.link(pool.tensor_scalar(bias[:, lo:hi], bias[:, lo:hi], gsum[:, n:n + 1], None, ALU.mult))
                for n in (2, 1, 0):
                    scaled.link(pool.tensor_scalar(w2[:, n], w2[:, 0], gumbel[:, n:n + 1], None, ALU.mult))
            pool.sem_inc(consts, 1)

            def residual(b, k):
                pool.wait_ge(x1_in, 16 * b + 16)
                pool.wait_ge(h_in, 16 * b + 16)
                pool.tensor_tensor(res[:, k], x1[:], h[:], ALU.add).then_inc(res1_ready, 1)
                pool.wait_ge(res1_ready, b + 1)
                pool.tensor_tensor(res[:, k], res[:, k], bias[:].unsqueeze(1).to_broadcast([T, NT, D]), ALU.add
                                   ).then_inc(res_ready, 1)

            def image(j, k, ahead):
                b = 2 * j + k
                if ahead:
                    pool.wait_ge(o_ready, 2 * b + 1)
                    residual(b + 1, 1 - k)

            residual(0, 0)
            each_image(pool, image)

        @block.tensor
        def _(pe):
            pe.wait_ge(weights_in, W_IN)
            pe.wait_ge(consts, 5)
            pe.sem_inc(down_done, 2)

            def turn(b):
                pe.wait_ge(z_ready, b + 1)
                for m in range(2):
                    for g in range(2):
                        pe.wait_ge((zT0_ready, zT1_ready)[m], 2 * b + g + 1)
                        pe.sem_inc(passed, 1)
                        for t in range(3):
                            ins = pe.transpose(ps[m][0:DH, t * T:(t + 1) * T], z[:, 3 * g + t, m * DH:(m + 1) * DH],
                                               ident[0:T, 0:T])
                        ins.then_inc(z_turned, 1)

            def up(b, u):
                g, br = u // BR, u % BR
                for i in range(MT):
                    n = MT * u + i
                    pe.wait_ge(hid_ready, MT * U * b + n + 1)
                    out = ps[2 + n % 4][:, 0:G]
                    for c in range(2 if br == 0 else 1):
                        w = w1c if br == 2 else w1[:, c, :]
                        ins = pe.matmul(out, w[:, i * 128:(i + 1) * 128], zT[:, c, g * G:(g + 1) * G],
                                        start=(c == 0), stop=(br > 0 or c == 1))
                    ins.then_inc(up_done, 1)

            def down(b, u):
                g, br = u // BR, u % BR
                pe.wait_ge(hid_ready, MT * U * b + MT * (u + 1) + 4)
                if br == 0:
                    pe.wait_ge(o_ready, 2 * b + g + 1)
                for t in range(3):
                    for i in range(MT):
                        out = (ps[6][0:T, t * D:t * D + KEEP[br]] if t < 2 else ps[7][0:T, 0:KEEP[br]])
                        ins = pe.matmul(out, hid[:, u % 2, i, t * T:(t + 1) * T], w2[:, br, i, 0:KEEP[br]],
                                        start=(br == 0 and i == 0 and t != 1), stop=(br == BR - 1 and i == MT - 1),
                                        skip_group_check=True)
                ins.then_inc(down_done, 1)

            def image(j, k, ahead):
                b = 2 * j + k
                pe.wait_ge(zT0_ready, 2 * b + 3)
                pe.wait_ge(zT1_ready, 2 * b + 3)
                for u in range(U):
                    up(b, u)
                    if u:
                        down(b, u - 1)
                if ahead:
                    turn(b + 1)
                down(b, U - 1)

            turn(0)
            each_image(pe, image)

        @block.scalar
        def _(act):
            act.wait_ge(weights_in, W_IN)
            act.wait_ge(consts, 5)
            act.sem_inc(hid_ready, 4)
            act.sem_inc(zT1_ready, 1)

            def root(b):
                act.wait_ge(var_ready, b + 1)
                act.activation(rstd[:], mv[:, :, 1], ACT.Sqrt, bias=eps_col[:, 0:1]).then_inc(std_ready, 1)

            def turned(b):
                for g in range(2):
                    act.wait_ge(z_turned, 4 * b + 3 + g)
                    act.activation(zT[:, 1, g * G:(g + 1) * G], ps[1][0:DH, 0:G], ACT.Identity,
                                   scale=gain[:, 1:2], bias=shift[:, 1:2]).then_inc(zT1_ready, 1)

            def image(j, k, ahead):
                b = 2 * j + k
                for u in range(U):
                    act.wait_ge(down_done, U * b + u + 1)
                    for i in range(MT):
                        n = MT * u + i
                        act.wait_ge(up_done, MT * U * b + n + 1)
                        act.activation(hid[:, u % 2, i, :], ps[2 + n % 4][:, 0:G], ACT.Gelu, bias=b1[:, i:i + 1]
                                       ).then_inc(hid_ready, 1)
                    if u == 0 and ahead:
                        root(b + 1)
                if ahead:
                    turned(b + 1)

            root(0)
            turned(0)
            each_image(act, image)

        @block.vector
        def _(dve):
            dve.wait_ge(weights_in, W_IN)
            dve.wait_ge(consts, 5)
            dve.sem_inc(zT0_ready, 1)
            dve.sem_inc(o_ready, 1)

            def layernorm(b):
                c_ = Chain(dve, chain, V_PER * b, V_PER)
                dve.wait_ge(x1_in, 16 * b + 16)
                for t in range(NT):
                    ins = dve.bn_stats(stats[:, t, :], x1[:, t, :])
                c_.link(ins)
                dve.sem_inc(passed, 1)
                for t in range(NT):
                    ins = dve.bn_aggr(mv[:, t, :], stats[:, t, :])
                ins.then_inc(var_ready, 1)
                dve.wait_ge(std_ready, b + 1)
                c_.link(dve.reciprocal(rstd[:], rstd[:]))
                for t in range(NT):
                    ins = dve.tensor_scalar(z[:, t, :], x1[:, t, :], mv[:, t, 0:1], rstd[:, t:t + 1],
                                            ALU.subtract, ALU.mult)
                ins.then_inc(z_ready, 1)
                c_.close()

            def turned(b):
                for g in range(2):
                    dve.wait_ge(z_turned, 4 * b + 1 + g)
                    dve.tensor_scalar(zT[:, 0, g * G:(g + 1) * G], ps[0][0:DH, 0:G], gain[:, 0:1], shift[:, 0:1],
                                      ALU.mult, ALU.add).then_inc(zT0_ready, 1)

            def image(j, k, ahead):
                b = 2 * j + k
                if ahead:
                    layernorm(b + 1)
                dve.wait_ge(res_ready, b + 1)
                dve.wait_ge(o_out, 16 * NT * b + 16)
                for g in range(2):
                    if g == 1 and ahead:
                        turned(b + 1)
                    dve.wait_ge(down_done, U * b + BR * (g + 1) + 2)
                    dve.tensor_tensor(o[:, 3 * g:3 * g + 2, :], ps[6][0:T, 0:2 * D].rearrange("p (t d) -> p t d", d=D),
                                      res[:, k, 3 * g:3 * g + 2, :], ALU.add)
                    dve.tensor_tensor(o[:, 3 * g + 2, :], ps[7][0:T, 0:D], res[:, k, 3 * g + 2, :], ALU.add
                                      ).then_inc(o_ready, 1)

            layernorm(0)
            turned(0)
            each_image(dve, image)


def build(nc, a, out):
    n_img = a["txt"].shape[0]
    cap = -(-5 * 2 * n_img * SEQ // (4 * E))

    def scratch(name, shape, dt=F32):
        return nc.dram_tensor(name, shape, dt, kind="Internal").ap()

    h1 = scratch("h1_scratch", (n_img, T, NT, D))
    x2 = scratch("x2_scratch", (n_img, T, NT, D + 1))
    slots = scratch("slots_scratch", (E * cap, 1), I32)
    y = scratch("y_scratch", (E * cap, D))
    h2 = scratch("h2_scratch", (n_img, T, NT, D))
    u = scratch("u_scratch", (n_img, KR, NC, DI))
    ak = scratch("ak_scratch", (n_img, CH, NC, NS))
    delta = scratch("delta_scratch", (n_img, 128, M3, SEQ))
    kq = scratch("kq_scratch", (n_img, 80, 2, SEQ), BF16)
    dx = scratch("dx_scratch", (n_img, 128, M3, SEQ))
    zs = scratch("zs_scratch", (n_img, 128, M3, SEQ))
    h3 = scratch("h3_scratch", (n_img, T, NT, D))
    hn = scratch("hn_scratch", (n_img, T, NT, D))
    qk = scratch("qk_scratch", (n_img, 2, 3, 192, SEQ), BF16)
    v = scratch("v_scratch", (n_img, T, NT, HEADS, 32))
    x1 = scratch("x1_scratch", (n_img, T, NT, D))

    with nc.sbuf_tensor("route", [T, n_img, 4, NT], F32) as route:
        with nc.cleanup_on_exit():
            phase_route(nc, a, n_img, cap, h1, x2, slots, route)
        with nc.cleanup_on_exit():
            phase_experts(nc, a, n_img, cap, x2, slots, y)
        with nc.cleanup_on_exit():
            phase_prepare(nc, a, n_img, h1, y, route, h2, u, ak, delta, kq, dx, zs)
    with nc.cleanup_on_exit():
        phase_scan(nc, a, n_img, u, ak, delta, kq, dx, zs, h2, h3)
    for half in range(2):
        with nc.cleanup_on_exit():
            phase_project(nc, a, half, n_img // 2, h3, hn, qk, v)
    with nc.cleanup_on_exit():
        phase_attend(nc, a, n_img, hn, qk, v, x1)
    for half in range(2):
        with nc.cleanup_on_exit():
            phase_mlp(nc, a, half, n_img // 2, h3, x1, out)


def lay_out(i):
    c = np.ascontiguousarray
    i = {k: np.asarray(v) for k, v in i.items()}
    n = i["x"].shape[0]
    o = {}
    p = i["x"].reshape(n, 14, 2, 8, 14, 2, 8, 3).transpose(0, 2, 5, 3, 6, 7, 1, 4).reshape(n, 8, 96, 196)
    o["patches"] = c(p.transpose(0, 2, 1, 3))
    w = i["L0_tok_W"].reshape(2, 8, 2, 8, 5, 3, 192).transpose(0, 2, 1, 3, 5, 4, 6).reshape(8, 96, 5, 192)
    o["tok_w"] = c(w.transpose(1, 0, 2, 3))
    o["tok_b"] = c(i["L0_tok_b"].reshape(2, 96).T)
    o["txt"] = c(i["txt"])
    halves = lambda m: c(m.reshape(2, 96, -1).transpose(1, 0, 2))
    o["a_wqkvT"] = halves(i["L0_attn_w_qkv"].T)
    o["a_wqkv"] = c(i["L0_attn_w_qkv"].reshape(6, 96, 192).transpose(1, 0, 2))
    o["a_wprojT"] = halves(i["L0_attn_w_proj"].T)
    o["a_bproj"] = c(i["L0_attn_b_proj"].reshape(1, 192))
    o["gateT"] = halves(i["L0_ffn_gate_w"].T)
    o["w13T"] = c(i["L0_ffn_w13"].transpose(0, 2, 1).reshape(8, 2, 96, 1024).transpose(0, 2, 1, 3))
    o["w2T"] = c(i["L0_ffn_w2"].transpose(0, 2, 1).reshape(8, 4, 128, 192).transpose(0, 2, 1, 3))
    o["norm_w"] = c(i["L0_ffn_norm_w"].reshape(8, 2, 96).transpose(2, 0, 1))
    thirds = lambda m: c(m.reshape(3, 128, -1).transpose(1, 0, 2))
    o["inT"] = halves(i["L1_attn_in_proj_w"].T)
    xp = i["L1_attn_x_proj_w"].T
    pad = np.zeros((384, 16), xp.dtype)
    o["xprojT"] = thirds(np.concatenate([xp[:, 12:28], pad, xp[:, 28:44], pad, xp[:, 0:12], pad[:, :4], pad], 1))
    o["dtheadT"] = np.zeros((96, 384), xp.dtype)
    o["dtheadT"][64:76] = i["L1_attn_dt_head_w"].T
    o["conv_w"] = thirds(i["L1_attn_conv_w"][:, 0, :])
    o["conv_b"] = c(i["L1_attn_conv_b"].reshape(3, 128).T)
    o["dt_b"] = c(i["L1_attn_dt_head_b"].reshape(3, 128).T)
    o["d_skip"] = c(i["L1_attn_D"].reshape(3, 128).T)
    o["outT"] = thirds(i["L1_attn_out_proj_w"].T)
    s = np.arange(59)
    p = np.float64(0.9) ** np.arange(60)
    o["decay"] = p[58 - s].astype(np.float32)[:, None]
    o["carry_decay"] = np.zeros((32, 12, 16), np.float32)
    o["carry_decay"][:16] = (p[59] * np.eye(16))[:, None, :]
    o["within"] = np.where(s[None, :] >= s[:, None], p[np.maximum(s[None, :] - s[:, None], 0)], 0).astype(np.float32)
    e = np.eye(16).reshape(16, 4, 1, 4, 1) * p[1:60]
    o["carried"] = c(np.broadcast_to(e, (16, 4, 12, 4, 59)).transpose(1, 0, 2, 3, 4).astype(np.float32))
    o["f_wqkv"] = halves(i["L1_ffn_w_qkv"])
    for n in ("n1l_g", "n1l_b", "n1s_g", "n1s_b", "n2l_g", "n2l_b", "n2s_g", "n2s_b"):
        o[n] = c(i["L1_ffn_" + n].reshape(2, 96).T)
    o["gumbel"] = c(i["L1_ffn_gumbel_weights"])
    o["w_fc1"] = halves(i["L1_ffn_w_fc1"])
    o["b_fc1"] = c(i["L1_ffn_b_fc1"].reshape(6, 128).T)
    o["w_fc2"] = c(i["L1_ffn_w_fc2"].reshape(6, 128, 192).transpose(1, 0, 2))
    o["b_fc2"] = c(i["L1_ffn_b_fc2"])
    o["f_bproj"] = c(i["L1_ffn_b_proj"])
    wp = np.zeros((4, 32, 3, 192), np.float32)
    wp[:, :16] = i["L1_ffn_w_proj"].reshape(3, 4, 16, 192).transpose(1, 2, 0, 3)
    o["f_wproj"] = c(wp.reshape(128, 3, 192))
    return o


def kernel(**inputs):
    import concourse.bacc as bacc
    from concourse.bass_utils import run_bass_kernel_spmd

    arrays = lay_out(inputs)
    nc = bacc.Bacc("TRN2", target_bir_lowering=False, num_devices=1)
    a = {name: nc.dram_tensor(name, v.shape, mybir.dt.from_np(v.dtype), kind="ExternalInput").ap()
         for name, v in arrays.items()}
    n_img = inputs["txt"].shape[0]
    out = nc.dram_tensor("out", (n_img, SEQ, D), F32, kind="ExternalOutput").ap()
    build(nc, a, out)
    r = run_bass_kernel_spmd(nc, [arrays], core_ids=[0])
    return r.results[0]["out"]
```

```python
from contextlib import ExitStack

import numpy as np
import concourse.bass as bass
from concourse import mybir

F32 = mybir.dt.float32
I32 = mybir.dt.int32
U32 = mybir.dt.uint32
ALU = mybir.AluOpType
ACT = mybir.ActivationFunctionType
AX_X = mybir.AxisListType.X

D = 192
DH = 96
N_TXT = 512
GRID = 14
N_PATCH = GRID * GRID
SEQ = N_PATCH + N_TXT
T = 118
NT = SEQ // T
G = 3 * T
QUAD_K = 8
E = 8
HID = 512
HEADS = 12
HD = 16
LN_EPS = 1e-5
MOE_EPS = 1e-6
L1_EPS = 1e-12


class Chain:

    def __init__(self, eng, sem, start=0, per=None):
        self.eng, self.sem, self.start, self.per, self.count = eng, sem, start, per, 0

    def link(self, ins):
        self.count += 1
        ins.then_inc(self.sem, 1)
        self.eng.wait_ge(self.sem, self.start + self.count)

    def close(self):
        assert self.count == self.per, (self.count, self.per)


def identity(pool, ident, sem, n):
    pool.memset(ident, 0.0).then_inc(sem, 1)
    pool.wait_ge(sem, n + 1)
    pool.affine_select(out=ident, in_=ident, compare_op=ALU.not_equal, fill=1.0, base=0,
                       pattern=[[-1, ident.shape[1]]], channel_multiplier=1).then_inc(sem, 1)


def region(q, c):
    a, b = q // 2, q % 2
    inner = [slice(1, GRID), slice(0, GRID - 1)]
    edge = [slice(0, 1), slice(GRID - 1, GRID)]
    return (edge if c & 1 else inner)[a], (edge if c & 2 else inner)[b]


DI = 384
M3 = DI // 128
NS = 16
RANK = 12
TAPS = 4
CH = 59
NC = SEQ // CH
CARRY = 64
KR = 96
Q4 = 4
NQ = NS // Q4
BETA = 0.9
NS_A, NS_B, NS_C = 3.4445, -4.775, 2.0315
BF16 = mybir.dt.bfloat16

MLP = 768
PRODUCTS = ((0, 0), (0, 1), (1, 0), (1, 1), (0, 2), (2, 0))
QK_ROWS = HD * len(PRODUCTS)


def phase_route(nc, a, n_img, cap, h1_dram, x2_dram, slot_dram, route):
    with ExitStack() as ctx:
        def sb(name, shape, dt=F32):
            return ctx.enter_context(nc.sbuf_tensor("ra_" + name, shape, dt))

        def sem(name):
            return nc.alloc_semaphore("ra_" + name)

        def bank(name):
            return ctx.enter_context(nc.psum_tensor("ra_" + name, [128, 512], F32))

        w_copies = sb("w_copies", [DH, QUAD_K, 5, D])
        w_class = sb("w_class", [DH, QUAD_K, 4, D])
        b_tok = sb("b_tok", [DH, 2])
        wqkvT = sb("wqkvT", [DH, 2, 3 * D])
        wq = sb("wq", [DH, 2, D])
        wprojT = sb("wprojT", [DH, 2, D])
        gateT = sb("gateT", [DH, 2, E])
        b_proj = sb("b_proj", [1, D])
        ident = sb("ident", [128, 128])
        blocks = sb("blocks", [DH, DH])
        before = sb("before", [T, T])
        ones = sb("ones", [T, T])
        zero_rows = sb("zero_rows", [T, E * cap // T], I32)
        iota8 = sb("iota8", [T, E])
        tok_of_p = sb("tok_of_p", [T, NT])
        patches = sb("patches", [DH, QUAD_K, N_PATCH])
        tokT = sb("tokT", [DH, 2, N_PATCH])
        x = sb("x", [T, NT, D])
        stats = sb("stats", [T, NT, 6])
        mv = sb("mv", [T, NT, 2])
        rstd = sb("rstd", [T, NT])
        z = sb("z", [T, NT, D])
        zT = sb("zT", [DH, 2, SEQ])
        x2T = sb("x2T", [DH, 2, SEQ])
        scratch = sb("scratch", [DH, 4, G])
        qsum = sb("qsum", [DH, 2, 2])
        dq = sb("dq", [DH, 2])
        dk = sb("dk", [DH, 2])
        kv = sb("kv", [T, NT, 2 * D])
        kabs = sb("kabs", [T, NT, D])
        stT = sb("stT", [DH, 2, DH])
        m1 = sb("m1", [DH, 2, D])
        m2 = sb("m2", [DH, 2, D])
        h1 = sb("h1", [T, NT, D])
        x2 = sb("x2", [T, NT, D + 1])
        squares = sb("squares", [T, NT, D])
        sumsq = sb("sumsq", [T, NT])
        moe_eps = sb("moe_eps", [T, 1])
        lmax = sb("lmax", [T, NT])
        prob = sb("prob", [T, NT, E])
        top = sb("top", [T, NT, E])
        topi = sb("topi", [T, NT, E], U32)
        topf = sb("topf", [T, NT, 2])
        hot = sb("hot", [T, 2, NT, E])
        both = sb("both", [T, NT, E])
        earlier = sb("earlier", [T, NT + 1, E])
        pos = sb("pos", [T, 2, NT])
        keep = sb("keep", [T, 2, NT])
        row = sb("row", [T, 2, NT])
        slot = sb("slot", [T, 2, NT])
        slot_i = sb("slot_i", [T, 2, NT], I32)
        first_token = sb("first_token", [T, 1])
        tokid = sb("tokid", [T, NT])
        tokid_i = sb("tokid_i", [T, NT], I32)
        tmp8 = sb("tmp8", [T, 2, NT, E])
        eps_col = sb("eps_col", [T, 1])

        ps_tok, ps_a, ps_b, ps_c, ps_d, ps_e, ps_f, ps_g = (
            bank(n) for n in ("tok", "a", "b", "c", "d", "e", "f", "g"))

        weights_in = sem("weights_in")
        consts = sem("consts")
        w_chain = sem("w_chain")
        w_summed = sem("w_summed")
        table_clear = sem("table_clear")
        patches_in = sem("patches_in")
        txt_in = sem("txt_in")
        tok_done = sem("tok_done")
        tok_biased = sem("tok_biased")
        tok_turned = sem("tok_turned")
        z_turned = sem("z_turned")
        zT_ready = sem("zT_ready")
        var_ready = [sem("var_ready1"), sem("var_ready2")]
        std_ready = [sem("std_ready1"), sem("std_ready2")]
        z_ready = sem("z_ready")
        q_done = sem("q_done")
        q_summed = sem("q_summed")
        kv_done = sem("kv_done")
        kv_ready = sem("kv_ready")
        kabs_ready = sem("kabs_ready")
        st_done = sem("st_done")
        st_ready = sem("st_ready")
        m1_done = sem("m1_done")
        m1_ready = sem("m1_ready")
        m2_done = sem("m2_done")
        m2_ready = sem("m2_ready")
        y_done = sem("y_done")
        h1_ready = sem("h1_ready")
        h1_out = sem("h1_out")
        x2_ready = sem("x2_ready")
        sumsq_ready = sem("sumsq_ready")
        rms_ready = sem("rms_ready")
        norm_ready = sem("norm_ready")
        x2_out = sem("x2_out")
        x2_turned = sem("x2_turned")
        x2T_ready = sem("x2T_ready")
        logits_done = sem("logits_done")
        shifted = sem("shifted")
        exped = sem("exped")
        hot_ready = sem("hot_ready")
        pos_done = sem("pos_done")
        slots_ready = sem("slots_ready")
        scattered = sem("scattered")
        lists_free = sem("lists_free")
        passed = sem("passed")
        tok_chain = sem("tok_chain")
        chain1 = sem("chain1")
        chain2 = sem("chain2")
        chain3 = sem("chain3")

        V1_PER, V2_PER, V3_PER = 2, 3, 31
        W_IN = 7 * 16

        block = ctx.enter_context(nc.Block())

        def each_image(eng, body):
            body(-2, True, False, False, False)
            body(-1, True, True, False, False)
            body(0, True, True, True, False)
            with eng.Fori(1, n_img - 2) as b:
                body(b, True, True, True, True)
            body(n_img - 2, False, True, True, True)
            body(n_img - 1, False, False, True, True)
            body(n_img, False, False, False, True)

        @block.sync
        def _(sp):
            sp.dma_start(w_copies[:], a["tok_w"]).then_inc(weights_in, 16)
            sp.dma_start(b_tok[:], a["tok_b"]).then_inc(weights_in, 16)
            sp.dma_start(wqkvT[:], a["a_wqkvT"]).then_inc(weights_in, 16)
            sp.dma_start(wq[:], a["a_wqkv"][:, 0:2, :]).then_inc(weights_in, 16)
            sp.dma_start(wprojT[:], a["a_wprojT"]).then_inc(weights_in, 16)
            sp.dma_start(gateT[:], a["gateT"]).then_inc(weights_in, 16)
            sp.dma_start(b_proj[:], a["a_bproj"]).then_inc(weights_in, 16)
            sp.wait_ge(consts, 12)
            sp.dma_start(slot_dram.rearrange("(p k) one -> p (k one)", p=T), zero_rows[:]).then_inc(table_clear, 16)
            first_text = 2 * T - N_PATCH

            def load_patches(b):
                sp.dma_start(patches[:], a["patches"][b]).then_inc(patches_in, 16)

            def load_text(b):
                sp.dma_start(x[N_PATCH - T:T, 1, :], a["txt"][b, 0:first_text, :]).then_inc(txt_in, 16)
                sp.dma_start(x[:, 2:NT, :], a["txt"][b, first_text:N_TXT, :].rearrange("(t p) d -> p t d", p=T)
                             ).then_inc(txt_in, 16)

            def body(b, ahead, first, second, third):
                if ahead:
                    if not isinstance(b, int) or b > -2:
                        sp.wait_ge(tok_done, b + 2)
                    load_patches(b + 2)
                if third:
                    sp.wait_ge(norm_ready, b)
                    sp.dma_start(x2_dram[b - 1], x2[:]).then_inc(x2_out, 16)
                if second:
                    sp.wait_ge(h1_ready, b + 1)
                    sp.dma_start(h1_dram[b], h1[:]).then_inc(h1_out, 16)
                    if first:
                        load_text(b + 1)

            sp.sem_inc(h1_out, 16)
            sp.sem_inc(x2_out, 16)
            load_text(0)
            each_image(sp, body)
            sp.wait_ge(h1_out, 16 * n_img + 16)
            sp.wait_ge(x2_out, 16 * n_img + 16)

        @block.gpsimd
        def _(pool):
            identity(pool, ident[:], consts, 0)
            pool.wait_ge(consts, 2)
            pool.memset(ones[:], 1.0).then_inc(consts, 1)
            pool.memset(blocks[:], 1.0).then_inc(consts, 1)
            pool.memset(zero_rows[:], 0).then_inc(consts, 1)
            pool.memset(eps_col[:], LN_EPS)
            pool.memset(first_token[:], 0.0).then_inc(consts, 1)
            pool.iota(iota8[:], pattern=[[1, E]], base=0, channel_multiplier=0,
                      allow_small_or_imprecise_dtypes=True).then_inc(consts, 1)
            pool.memset(moe_eps[:], MOE_EPS)
            pool.iota(tok_of_p[:], pattern=[[1, NT]], base=0, channel_multiplier=NT,
                      allow_small_or_imprecise_dtypes=True).then_inc(consts, 1)
            pool.wait_ge(consts, 8)
            pool.affine_select(out=before[:], in_=ones[:], compare_op=ALU.is_gt, fill=0.0, base=0,
                               pattern=[[1, T]], channel_multiplier=-1).then_inc(consts, 1)
            heads = blocks[:].rearrange("e (h d) -> e h d", d=HD)
            pool.affine_select(out=heads, in_=heads, compare_op=ALU.is_ge, fill=0.0, base=0,
                               pattern=[[-HD, DH // HD], [0, HD]], channel_multiplier=1).then_inc(consts, 1)
            pool.wait_ge(consts, 10)
            pool.affine_select(out=heads, in_=heads, compare_op=ALU.is_ge, fill=0.0, base=HD - 1,
                               pattern=[[HD, DH // HD], [0, HD]], channel_multiplier=-1).then_inc(consts, 1)
            pool.memset(earlier[:], 0.0).then_inc(consts, 1)
            pool.wait_ge(table_clear, 16)
            pool.sem_inc(lists_free, 1)
            with pool.Fori(0, n_img) as b:
                pool.wait_ge(slots_ready, b + 1)
                pool.sem_inc(passed, 1)
                for k in range(2):
                    for t in range(NT):
                        pool.indirect_dma_start(
                            out=slot_dram, out_offset=bass.IndirectOffsetOnAxis(ap=slot_i[:, k, t:t + 1], axis=0),
                            in_=tokid_i[:, t:t + 1], in_offset=None, bounds_check=E * cap - 1,
                            oob_is_err=False).then_inc(scattered, 16)
                pool.wait_ge(scattered, 16 * 2 * NT * (b + 1))
                pool.sem_inc(lists_free, 1)

        @block.tensor
        def _(pe):
            pe.wait_ge(weights_in, W_IN)
            pe.wait_ge(consts, 12)
            pe.wait_ge(w_summed, 1)

            def tokens(b, m):
                if m == 0:
                    pe.wait_ge(patches_in, 16 * b + 16)
                o = ps_tok[0:DH, m * 256:m * 256 + N_PATCH].rearrange("p (y x) -> p y x", x=GRID)
                for c in range(4):
                    for kt in range(QUAD_K):
                        ys, xs = region(kt // 2, c)
                        mv_ = patches[:, kt, :].rearrange("p (y x) -> p y x", x=GRID)
                        ins = pe.matmul(o[:, ys, xs], w_class[:, kt, c, m * DH:(m + 1) * DH], mv_[:, ys, xs],
                                        start=(m == 0 and c == 0 and kt == 0), stop=(c == 3 and kt == QUAD_K - 1),
                                        skip_group_check=True)
                if m == 1:
                    ins.then_inc(tok_done, 1)

            def turn_tokens(b):
                pe.wait_ge(tok_biased, b + 1)
                for m in range(2):
                    pe.transpose(ps_a[0:T, m * DH:(m + 1) * DH], tokT[:, m, 0:T], ident[0:DH, 0:DH])
                    ins = pe.transpose(ps_a[0:N_PATCH - T, D + m * DH:D + (m + 1) * DH],
                                       tokT[:, m, T:N_PATCH], ident[0:DH, 0:DH])
                ins.then_inc(tok_turned, 1)

            def turn(src, done):
                for m in range(2):
                    for g in range(2):
                        out = (ps_b, ps_c, ps_d, ps_e)[2 * m + g]
                        for t in range(3):
                            ins = pe.transpose(out[0:DH, t * T:(t + 1) * T],
                                               src[:, 3 * g + t, m * DH:(m + 1) * DH], ident[0:T, 0:T])
                ins.then_inc(done, 1)

            def queries_keys_values(b, tokens_ahead):
                if tokens_ahead:
                    pe.wait_ge(tok_biased, b + 2)
                pe.wait_ge(zT_ready, 2 * b + 2)
                for m in range(2):
                    for g in range(2):
                        out = (ps_a, ps_tok)[m][0:DH, 0:G] if g == 0 else (ps_f, ps_g)[m][0:DH, 0:G]
                        for c in range(2):
                            ins = pe.matmul(out, wqkvT[:, c, m * DH:(m + 1) * DH], zT[:, c, g * G:(g + 1) * G],
                                            start=(c == 0), stop=(c == 1))
                ins.then_inc(q_done, 1)
                for t in range(NT):
                    out = (ps_b, ps_c, ps_d, ps_e)[t % 4]
                    if t >= 4:
                        pe.wait_ge(kv_ready, NT * b + t - 3)
                    for c in range(2):
                        ins = pe.matmul(out[0:T, 0:2 * D], zT[:, c, t * T:(t + 1) * T], wqkvT[:, c, D:3 * D],
                                        start=(c == 0), stop=(c == 1))
                    ins.then_inc(kv_done, 1)

            def logits(b, behind):
                pe.wait_ge(x2_ready, b + 1)
                if behind:
                    pe.wait_ge(kv_ready, NT * (b + 2))
                    pe.wait_ge(q_summed, 4 * (b + 2))
                turn(x2, x2_turned)
                pe.wait_ge(x2T_ready, 2 * b + 2)
                for t in range(NT):
                    for c in range(2):
                        ins = pe.matmul(ps_f[0:T, t * E:(t + 1) * E], x2T[:, c, t * T:(t + 1) * T], gateT[:, c, :],
                                        start=(c == 0), stop=(c == 1))
                ins.then_inc(logits_done, 1)

            def attention(b):
                pe.wait_ge(q_summed, 4 * b + 4)
                pe.wait_ge(kabs_ready, NT * b + NT)
                pe.wait_ge(kv_ready, NT * b + NT)
                for m in range(2):
                    for t in range(NT):
                        pe.matmul(ps_a[0:DH, m * DH:(m + 1) * DH], kv[:, t, D + m * DH:D + (m + 1) * DH],
                                  kv[:, t, m * DH:(m + 1) * DH], start=(t == 0), stop=(t == NT - 1))
                for m in range(2):
                    for t in range(NT):
                        ins = pe.matmul(ps_a[0:DH, 2 * D + m:2 * D + m + 1], kabs[:, t, m * DH:(m + 1) * DH],
                                        ones[0:T, 0:1], start=(t == 0), stop=(t == NT - 1))
                ins.then_inc(st_done, 1)
                pe.wait_ge(st_ready, b + 1)
                for m in range(2):
                    ins = pe.matmul(ps_g[0:DH, m * D:(m + 1) * D], stT[:, m, :], wprojT[:, m, :],
                                    start=True, stop=True)
                ins.then_inc(m1_done, 1)
                pe.wait_ge(m1_ready, b + 1)
                for c in range(2):
                    for m in range(2):
                        ins = pe.matmul(ps_a[0:DH, c * D:(c + 1) * D], wq[:, m, c * DH:(c + 1) * DH], m1[:, m, :],
                                        start=(m == 0), stop=(m == 1))
                ins.then_inc(m2_done, 1)
                pe.wait_ge(m2_ready, b + 1)
                for t in range(NT):
                    out = (ps_b, ps_c, ps_d)[t // 2][0:T, (t % 2) * D:(t % 2 + 1) * D]
                    for c in range(2):
                        pe.matmul(out, zT[:, c, t * T:(t + 1) * T], m2[:, c, :], start=(c == 0), stop=False)
                    ins = pe.matmul(out, ones[0:1, 0:T], b_proj[0:1, :], start=False, stop=True)
                ins.then_inc(y_done, 1)

            def positions(b):
                pe.wait_ge(hot_ready, b + 1)
                flat = ps_f[0:T, 256:256 + NT * E]
                pe.matmul(flat, before[:], both[:].rearrange("p t e -> p (t e)"), start=True, stop=False)
                pe.matmul(flat, ones[:], earlier[:, 0:NT, :].rearrange("p t e -> p (t e)"),
                          start=False, stop=True).then_inc(pos_done, 1)

            def body(b, ahead, first, second, third):
                if second:
                    queries_keys_values(b, first)
                if third:
                    logits(b - 1, second)
                if second:
                    attention(b)
                if first:
                    turn_tokens(b + 1)
                if ahead:
                    tokens(b + 2, 0)
                if third:
                    positions(b - 1)
                if first:
                    pe.wait_ge(z_ready, b + 2)
                    turn(z, z_turned)
                if ahead:
                    tokens(b + 2, 1)

            each_image(pe, body)

        @block.scalar
        def _(act):
            act.wait_ge(weights_in, W_IN)
            act.wait_ge(consts, 12)

            def root(b, n):
                act.wait_ge(var_ready[n], b + 1)
                act.activation(rstd[:], mv[:, :, 1], ACT.Sqrt, bias=eps_col[:, 0:1]).then_inc(std_ready[n], 1)

            def body(b, ahead, first, second, third):
                if third:
                    root(b - 1, 1)
                    act.wait_ge(x2_ready, b)
                    for t in range(NT):
                        ins = act.activation(squares[:, t, :], x2[:, t, 0:D], ACT.Square, scale=2.0,
                                             accum_out=sumsq[:, t:t + 1])
                    ins.then_inc(sumsq_ready, 1)
                    act.wait_ge(sumsq_ready, b)
                    act.activation(sumsq[:], sumsq[:], ACT.Sqrt, bias=moe_eps[:, 0:1], scale=1.0 / D).then_inc(rms_ready, 1)
                if second:
                    act.wait_ge(q_done, b + 1)
                    for m in range(2):
                        for g in range(2):
                            src = (ps_a, ps_tok)[m] if g == 0 else (ps_f, ps_g)[m]
                            act.activation(scratch[:, 2 * m + g, :], src[0:DH, 0:G], ACT.Abs,
                                           accum_out=qsum[:, m, g:g + 1]).then_inc(q_summed, 1)
                    for t in range(NT):
                        act.wait_ge(kv_ready, NT * b + t + 1)
                        act.activation(kabs[:, t, :], kv[:, t, 0:D], ACT.Abs).then_inc(kabs_ready, 1)
                if third:
                    act.wait_ge(x2_turned, b)
                    act.activation(x2T[:, 1, 0:G], ps_d[0:DH, 0:G], ACT.Copy)
                    act.activation(x2T[:, 1, G:SEQ], ps_e[0:DH, 0:G], ACT.Copy).then_inc(x2T_ready, 1)
                if second:
                    act.wait_ge(m2_done, b + 1)
                    act.activation(m2[:].rearrange("p c d -> p (c d)"), ps_a[0:DH, 0:2 * D], ACT.Copy).then_inc(m2_ready, 1)
                if third:
                    act.wait_ge(shifted, b)
                    act.activation(prob[:], prob[:], ACT.Exp).then_inc(exped, 1)
                if first:
                    root(b + 1, 0)
                    act.wait_ge(z_turned, b + 2)
                    act.activation(zT[:, 1, 0:G], ps_d[0:DH, 0:G], ACT.Copy)
                    act.activation(zT[:, 1, G:SEQ], ps_e[0:DH, 0:G], ACT.Copy).then_inc(zT_ready, 1)
                if ahead:
                    act.wait_ge(tok_done, b + 3)
                    for m in range(2):
                        ins = act.activation(tokT[:, m, :], ps_tok[0:DH, m * 256:m * 256 + N_PATCH], ACT.Identity,
                                             bias=b_tok[:, m:m + 1])
                    ins.then_inc(tok_biased, 1)

            each_image(act, body)

        @block.vector
        def _(dve):
            dve.wait_ge(weights_in, W_IN)
            dve.wait_ge(consts, 12)
            w = Chain(dve, w_chain)
            for q in range(4):
                qa, qb = q // 2, q % 2
                ks = slice(2 * q, 2 * q + 2)
                own_y, own_x, other_y, other_x = qa, 2 * qb, 1 - qa, 2 * (1 - qb)
                w.link(dve.tensor_tensor(w_class[:, ks, 3, :], w_copies[:, ks, 0, :],
                                         w_copies[:, ks, 1 + own_y + own_x, :], ALU.add))
                w.link(dve.tensor_tensor(w_class[:, ks, 1, :], w_class[:, ks, 3, :],
                                         w_copies[:, ks, 1 + own_y + other_x, :], ALU.add))
                w.link(dve.tensor_tensor(w_class[:, ks, 2, :], w_class[:, ks, 3, :],
                                         w_copies[:, ks, 1 + other_y + own_x, :], ALU.add))
                w.link(dve.tensor_tensor(w_class[:, ks, 0, :], w_class[:, ks, 1, :],
                                         w_copies[:, ks, 1 + other_y + own_x, :], ALU.add))
                w.link(dve.tensor_tensor(w_class[:, ks, 0, :], w_class[:, ks, 0, :],
                                         w_copies[:, ks, 1 + other_y + other_x, :], ALU.add))
            dve.sem_inc(w_summed, 1)

            def layernorm(c, src, dst, b, n, done):
                for t in range(NT):
                    ins = dve.bn_stats(stats[:, t, :], src[:, t, :])
                c.link(ins)
                dve.sem_inc(passed, 1)
                for t in range(NT):
                    ins = dve.bn_aggr(mv[:, t, :], stats[:, t, :])
                ins.then_inc(var_ready[n], 1)
                dve.wait_ge(std_ready[n], b + 1)
                c.link(dve.reciprocal(rstd[:], rstd[:]))
                for t in range(NT):
                    ins = dve.tensor_scalar(dst[:, t, 0:D], src[:, t, :], mv[:, t, 0:1], rstd[:, t:t + 1],
                                            ALU.subtract, ALU.mult)
                ins.then_inc(done, 1)

            def patch_tokens(b):
                dve.wait_ge(tok_turned, b + 1)
                dve.wait_ge(txt_in, 32 * b + 32)
                dve.tensor_copy(x[:, 0, :], ps_a[0:T, 0:D])
                dve.tensor_copy(x[0:N_PATCH - T, 1, :], ps_a[0:N_PATCH - T, D:2 * D]).then_inc(tok_chain, 1)
                dve.wait_ge(tok_chain, b + 1)

            def attention(b, c):
                dve.wait_ge(st_done, b + 1)
                dve.wait_ge(q_summed, 4 * b + 4)
                c.link(dve.tensor_tensor(dq[:], qsum[:, :, 0], qsum[:, :, 1], ALU.add))
                dve.tensor_scalar(dk[:], ps_a[0:DH, 2 * D:2 * D + 2], L1_EPS, None, ALU.max)
                c.link(dve.tensor_scalar(dq[:], dq[:], L1_EPS, None, ALU.max))
                dve.reciprocal(dk[:], dk[:])
                c.link(dve.reciprocal(dq[:], dq[:]))
                for m in range(2):
                    ins = dve.tensor_tensor(stT[:, m, :], ps_a[0:DH, m * DH:(m + 1) * DH], blocks[:], ALU.mult)
                ins.then_inc(st_ready, 1)
                dve.wait_ge(m1_done, b + 1)
                for m in range(2):
                    ins = dve.tensor_scalar(m1[:, m, :], ps_g[0:DH, m * D:(m + 1) * D], dq[:, m:m + 1], dk[:, m:m + 1],
                                            ALU.mult, ALU.mult)
                ins.then_inc(m1_ready, 1)
                dve.wait_ge(y_done, b + 1)
                dve.wait_ge(h1_out, 16 * b + 16)
                for t in range(3):
                    ins = dve.tensor_tensor(h1[:, 2 * t:2 * t + 2, :],
                                            (ps_b, ps_c, ps_d)[t][0:T, 0:2 * D].rearrange("p (t d) -> p t d", d=D),
                                            x[:, 2 * t:2 * t + 2, :], ALU.add)
                ins.then_inc(h1_ready, 1)

            def choices(b, c):
                dve.wait_ge(rms_ready, b + 1)
                c.link(dve.reciprocal(sumsq[:], sumsq[:]))
                dve.tensor_scalar(x2[:, :, D], sumsq[:], 2.0, None, ALU.mult).then_inc(norm_ready, 1)
                dve.wait_ge(logits_done, b + 1)
                logits = ps_f[0:T, 0:NT * E].rearrange("p (t e) -> p t e", e=E)
                c.link(dve.tensor_reduce(lmax[:], logits, AX_X, ALU.max))
                dve.tensor_tensor(prob[:], logits, lmax[:].unsqueeze(2).to_broadcast([T, NT, E]), ALU.subtract
                                  ).then_inc(shifted, 1)
                dve.wait_ge(exped, b + 1)
                c.link(dve.tensor_reduce(lmax[:], prob[:], AX_X, ALU.add))
                c.link(dve.reciprocal(lmax[:], lmax[:]))
                c.link(dve.tensor_tensor(prob[:], prob[:], lmax[:].unsqueeze(2).to_broadcast([T, NT, E]), ALU.mult))
                dve.sem_inc(passed, 1)
                for t in range(NT):
                    ins = dve.max(top[:, t, :], prob[:, t, :])
                c.link(ins)
                dve.sem_inc(passed, 1)
                for t in range(NT):
                    ins = dve.max_index(topi[:, t, :], top[:, t, :], prob[:, t, :])
                c.link(ins)
                c.link(dve.tensor_copy(topf[:], topi[:, :, 0:2]))
                for k in range(2):
                    ins = dve.tensor_tensor(hot[:, k], iota8[:].unsqueeze(1).to_broadcast([T, NT, E]),
                                            topf[:, :, k:k + 1].to_broadcast([T, NT, E]), ALU.is_equal)
                c.link(ins)
                c.link(dve.tensor_tensor(both[:], hot[:, 0], hot[:, 1], ALU.add))
                for t in range(NT):
                    ins = dve.tensor_tensor(earlier[:, t + 1, :], earlier[:, t, :], both[:, t, :], ALU.add)
                    if t < NT - 1:
                        c.link(ins)
                ins.then_inc(hot_ready, 1)

            def slots(b, c):
                dve.wait_ge(pos_done, b + 1)
                c.link(dve.tensor_copy(earlier[:, 0, :], earlier[:, NT, :]))
                counts = ps_f[0:T, 256:256 + NT * E].rearrange("p (t e) -> p t e", e=E)
                for k in range(2):
                    ins = dve.tensor_tensor(tmp8[:, k], counts, hot[:, k], ALU.mult)
                c.link(ins)
                c.link(dve.tensor_reduce(pos[:], tmp8[:], AX_X, ALU.add))
                c.link(dve.tensor_scalar(keep[:], pos[:], float(cap), None, ALU.is_lt))
                c.link(dve.tensor_scalar(row[:], pos[:], float(cap - 1), None, ALU.min))
                for k in range(2):
                    ins = dve.scalar_tensor_tensor(out=row[:, k], in0=topf[:, :, k], scalar=float(cap), in1=row[:, k],
                                                   op0=ALU.mult, op1=ALU.add)
                c.link(ins)
                c.link(dve.tensor_scalar(slot[:], keep[:], -float(E * cap), float(E * cap), ALU.mult, ALU.add))
                c.link(dve.tensor_tensor(slot[:], slot[:], row[:], ALU.add))
                dve.tensor_scalar(tokid[:], tok_of_p[:], first_token[:, 0:1], None, ALU.add)
                c.link(dve.tensor_tensor(lmax[:], top[:, :, 0], top[:, :, 1], ALU.add))
                c.link(dve.reciprocal(lmax[:], lmax[:]))
                for k in range(2):
                    ins = dve.tensor_tensor(pos[:, k], top[:, :, k], lmax[:], ALU.mult)
                c.link(ins)
                c.link(dve.tensor_tensor(pos[:], pos[:], keep[:], ALU.mult))
                at = b if isinstance(b, int) else bass.ds(b, 1)
                dve.tensor_copy(route[:, at, 0:2, :], row[:])
                c.link(dve.tensor_copy(route[:, at, 2:4, :], pos[:]))
                c.link(dve.tensor_scalar(first_token[:], first_token[:], float(SEQ), None, ALU.add))
                dve.wait_ge(lists_free, b + 1)
                dve.tensor_copy(tokid_i[:], tokid[:])
                dve.tensor_copy(slot_i[:], slot[:]).then_inc(slots_ready, 1)

            def body(b, ahead, first, second, third):
                if third:
                    c3 = Chain(dve, chain3, V3_PER * (b - 1), V3_PER)
                    dve.wait_ge(h1_ready, b)
                    dve.wait_ge(x2_out, 16 * b)
                    layernorm(c3, h1, x2, b - 1, 1, x2_ready)
                if second:
                    for t in range(NT):
                        dve.wait_ge(kv_done, NT * b + t + 1)
                        dve.tensor_copy(kv[:, t, :], (ps_b, ps_c, ps_d, ps_e)[t % 4][0:T, 0:2 * D]).then_inc(kv_ready, 1)
                if third:
                    dve.wait_ge(x2_turned, b)
                    dve.tensor_copy(x2T[:, 0, 0:G], ps_b[0:DH, 0:G])
                    dve.tensor_copy(x2T[:, 0, G:SEQ], ps_c[0:DH, 0:G]).then_inc(x2T_ready, 1)
                if second:
                    c2 = Chain(dve, chain2, V2_PER * b, V2_PER)
                    attention(b, c2)
                    c2.close()
                if third:
                    choices(b - 1, c3)
                if first:
                    patch_tokens(b + 1)
                    c1 = Chain(dve, chain1, V1_PER * (b + 1), V1_PER)
                    layernorm(c1, x, z, b + 1, 0, z_ready)
                    c1.close()
                if third:
                    slots(b - 1, c3)
                    c3.close()
                if first:
                    dve.wait_ge(z_turned, b + 2)
                    dve.tensor_copy(zT[:, 0, 0:G], ps_b[0:DH, 0:G])
                    dve.tensor_copy(zT[:, 0, G:SEQ], ps_c[0:DH, 0:G]).then_inc(zT_ready, 1)

            each_image(dve, body)


def phase_experts(nc, a, n_img, cap, x2_dram, slot_dram, y_dram):
    steps = cap // G
    assert steps % 2 == 0 and cap % G == 0
    KT = HID // 128
    with ExitStack() as ctx:
        def sb(name, shape, dt=F32):
            return ctx.enter_context(nc.sbuf_tensor("b_" + name + "_t", shape, dt))

        def sem(name):
            return nc.alloc_semaphore("b_" + name)

        def bank(name):
            return ctx.enter_context(nc.psum_tensor("b_" + name, [128, 512], F32))

        slots = sb("slots", [T, E * 3 * steps + 3], I32)
        rows = sb("rows", [T, 2, 3], I32)
        xg = sb("xg", [T, 2, 3, D + 1])
        z = sb("z", [T, 3, D])
        zT = sb("zT", [DH, 2, G])
        w13 = sb("w13", [DH, 2, 2, 2 * HID])
        w2 = sb("w2", [128, 2, KT, D])
        norm = sb("norm", [DH, E, 2])
        gate = sb("gate", [128, 2, G])
        hidden = sb("hidden", [128, KT, G])
        y = sb("y", [T, 2, 3, D])
        ident = sb("ident", [128, 128])

        ps_z0, ps_z1, ps_g0, ps_g1, ps_u0, ps_u1, ps_y0, ps_y1 = (
            bank(n) for n in ("z0", "z1", "g0", "g1", "u0", "u1", "y0", "y1"))
        ps_g, ps_u = (ps_g0, ps_g1), (ps_u0, ps_u1)

        consts = sem("consts")
        norm_in = sem("norm_in")
        slots_in = sem("slots_in")
        w13_in = [sem("w13_in0"), sem("w13_in1")]
        w2_in = [sem("w2_in0"), sem("w2_in1")]
        w13_ready = sem("w13_ready")
        rows_ready = sem("rows_ready")
        gathered = [sem("gathered0"), sem("gathered1")]
        z_ready = sem("z_ready")
        z_turned = sem("z_turned")
        zT0_ready = sem("zT0_ready")
        zT1_ready = sem("zT1_ready")
        up_done = sem("up_done")
        gate_ready = sem("gate_ready")
        hidden_ready = sem("hidden_ready")
        y_done = sem("y_done")
        y_ready = sem("y_ready")
        y_out = [sem("y_out0"), sem("y_out1")]
        expert_done = sem("expert_done")
        passed = sem("passed")

        x_rows = x2_dram.rearrange("b p t d -> (b p t) d")
        y_steps = y_dram.rearrange("(e p g j) d -> e g p (j d)", e=E, p=T, j=3)

        block = ctx.enter_context(nc.Block())

        @block.sync
        def _(sp):
            def weights(e, k):
                sp.dma_start(w13[:, k], a["w13T"][e]).then_inc(w13_in[k], 16)
                sp.dma_start(w2[:, k], a["w2T"][e]).then_inc(w2_in[k], 16)

            def stores(e):
                with sp.Fori(0, steps // 2) as h:
                    for k in range(2):
                        sp.wait_ge(y_ready, steps * e + 2 * h + k + 2)
                        sp.dma_start(y_steps[e, 2 * h + k], y[:, k].rearrange("p j d -> p (j d)")).then_inc(y_out[k], 16)

            sp.dma_start(norm[:], a["norm_w"]).then_inc(norm_in, 16)
            sp.wait_ge(consts, 3)
            sp.dma_start(slots[:, 0:E * 3 * steps].rearrange("p (e k) -> p e k", e=E),
                         slot_dram.rearrange("(e p k) one -> p e (k one)", e=E, p=T)).then_inc(slots_in, 16)
            weights(0, 0)
            weights(1, 1)
            sp.sem_inc(y_out[0], 16)
            sp.sem_inc(y_out[1], 16)
            with sp.Fori(0, E // 2 - 1) as j:
                for k in range(2):
                    stores(2 * j + k)
                    sp.wait_ge(expert_done, 2 * j + k + 1)
                    weights(2 * j + k + 2, k)
            for k in range(2):
                stores(E - 2 + k)
            for k in range(2):
                sp.wait_ge(y_out[k], 16 * (E * steps // 2 + 1))

        @block.gpsimd
        def _(pool):
            identity(pool, ident[:], consts, 0)
            pool.memset(slots[:, E * 3 * steps:], 0).then_inc(consts, 1)
            pool.wait_ge(slots_in, 16)
            pool.wait_ge(norm_in, 16)

            def gather(s, k):
                pool.tensor_copy(rows[:, k, :], slots[:, bass.ds(3 * s, 3)]).then_inc(rows_ready, 1)
                pool.wait_ge(rows_ready, s + 1)
                pool.sem_inc(passed, 1)
                for i in range(3):
                    pool.indirect_dma_start(out=xg[:, k, i, :], out_offset=None, in_=x_rows,
                                            in_offset=bass.IndirectOffsetOnAxis(ap=rows[:, k, i:i + 1], axis=0),
                                            ).then_inc(gathered[k], 16)

            gather(0, 0)
            with pool.Fori(0, E // 2) as j:
                for ke in range(2):
                    e = 2 * j + ke
                    pool.wait_ge(w13_in[ke], 16 * j + 16)
                    pool.sem_inc(passed, 1)
                    for m in range(2):
                        ins = pool.tensor_tensor(w13[:, ke, m, :], w13[:, ke, m, :],
                                                 norm[:, bass.ds(e, 1), m].to_broadcast([DH, 2 * HID]), ALU.mult)
                    ins.then_inc(w13_ready, 1)
                    with pool.Fori(0, steps // 2) as h:
                        for k in range(2):
                            s = steps * e + 2 * h + k
                            pool.wait_ge(y_ready, s + 1)
                            pool.sem_inc(passed, 1)
                            gather(s + 1, 1 - k)
            pool.wait_ge(gathered[0], 48 * (E * steps // 2 + 1))
            pool.wait_ge(gathered[1], 48 * (E * steps // 2))

        @block.tensor
        def _(pe):
            pe.wait_ge(consts, 2)

            def turn(n):
                pe.wait_ge(z_ready, n)
                for m in range(2):
                    for t in range(3):
                        ins = pe.transpose((ps_z0, ps_z1)[m][0:DH, t * T:(t + 1) * T],
                                           z[:, t, m * DH:(m + 1) * DH], ident[0:T, 0:T])
                ins.then_inc(z_turned, 1)

            turn(1)
            with pe.Fori(0, E // 2) as j:
                for ke in range(2):
                    e = 2 * j + ke
                    pe.wait_ge(w13_ready, e + 1)
                    pe.wait_ge(w2_in[ke], 16 * j + 16)
                    pe.sem_inc(passed, 1)
                    with pe.Fori(0, steps) as h:
                        s = steps * e + h
                        pe.wait_ge(zT0_ready, s + 1)
                        pe.wait_ge(zT1_ready, s + 1)
                        for i in range(KT):
                            pe.wait_ge(hidden_ready, 4 * s + i + 1)
                            for ps, off in ((ps_g, 0), (ps_u, HID)):
                                for c in range(2):
                                    ins = pe.matmul(ps[i % 2][:, 0:G], w13[:, ke, c, off + i * 128:off + (i + 1) * 128],
                                                    zT[:, c, :], start=(c == 0), stop=(c == 1))
                            ins.then_inc(up_done, 1)
                        turn(s + 2)
                        pe.wait_ge(y_ready, s + 1)
                        for i in range(KT):
                            pe.wait_ge(hidden_ready, 4 * s + i + 3)
                            for t in range(3):
                                out = ps_y0[0:T, t * D:(t + 1) * D] if t < 2 else ps_y1[0:T, 0:D]
                                ins = pe.matmul(out, hidden[:, i, t * T:(t + 1) * T], w2[:, ke, i, :],
                                                start=(i == 0 and t != 1), stop=(i == KT - 1), skip_group_check=True)
                        ins.then_inc(y_done, 1)
                    pe.sem_inc(passed, 1)
                    pe.wait_ge(y_done, steps * (e + 1))
                    pe.sem_inc(expert_done, 1)

        @block.scalar
        def _(act):
            act.wait_ge(z_turned, 1)
            act.activation(zT[:, 1, :], ps_z1[0:DH, 0:G], ACT.Copy).then_inc(zT1_ready, 1)
            with act.Fori(0, E * steps) as s:
                for i in range(KT):
                    act.wait_ge(up_done, 4 * s + i + 1)
                    act.wait_ge(hidden_ready, 4 * s + i + 1)
                    act.activation(gate[:, i % 2, :], ps_g[i % 2][:, 0:G], ACT.Silu).then_inc(gate_ready, 1)
                act.wait_ge(z_turned, s + 2)
                act.activation(zT[:, 1, :], ps_z1[0:DH, 0:G], ACT.Copy).then_inc(zT1_ready, 1)

        @block.vector
        def _(dve):
            dve.sem_inc(hidden_ready, 2)
            dve.sem_inc(y_ready, 1)

            def normed(k, count):
                dve.wait_ge(gathered[k], count)
                dve.tensor_tensor(z[:], xg[:, k, :, 0:D], xg[:, k, :, D:D + 1].to_broadcast([T, 3, D]), ALU.mult
                                  ).then_inc(z_ready, 1)

            def turned(s):
                dve.wait_ge(z_turned, s + 1)
                dve.tensor_copy(zT[:, 0, :], ps_z0[0:DH, 0:G]).then_inc(zT0_ready, 1)

            normed(0, 48)
            turned(0)
            with dve.Fori(0, E * steps // 2) as h:
                for k in range(2):
                    s = 2 * h + k
                    for i in range(KT):
                        if i == 2:
                            normed(1 - k, 48 * (h + k) + 48)
                        dve.wait_ge(gate_ready, 4 * s + i + 1)
                        dve.tensor_tensor(hidden[:, i, :], gate[:, i % 2, :], ps_u[i % 2][:, 0:G], ALU.mult
                                          ).then_inc(hidden_ready, 1)
                    turned(s + 1)
                    dve.wait_ge(y_done, s + 1)
                    dve.wait_ge(y_out[k], 16 * h + 16)
                    dve.tensor_tensor(y[:, k, 0:2, :], ps_y0[0:T, 0:2 * D].rearrange("p (t d) -> p t d", d=D),
                                      xg[:, k, 0:2, 0:D], ALU.add)
                    dve.tensor_tensor(y[:, k, 2, :], ps_y1[0:T, 0:D], xg[:, k, 2, 0:D], ALU.add).then_inc(y_ready, 1)


def phase_prepare(nc, a, n_img, h1_dram, y_dram, route, h2_dram, u_dram, ak_dram, delta_dram, kq_dram, dx_dram, zs_dram):
    with ExitStack() as ctx:
        def sb(name, shape, dt=F32):
            return ctx.enter_context(nc.sbuf_tensor("c_" + name + "_t", shape, dt))

        def sem(name):
            return nc.alloc_semaphore("c_" + name)

        inT = sb("inT", [DH, 2, 2 * DI])
        xprojT = sb("xprojT", [128, M3, KR])
        dtheadT = sb("dtheadT", [KR, DI])
        conv_w = sb("conv_w", [128, M3, TAPS])
        conv_b = sb("conv_b", [128, M3])
        dt_b = sb("dt_b", [128, M3])
        d_skip = sb("d_skip", [128, M3])
        decay = sb("decay", [CH, 1])
        ck = sb("ck", [KR, NC, NS])
        ident = sb("ident", [128, 128])
        ones = sb("ones", [NS, 128])
        eps_col = sb("eps_col", [T, 1])
        rows = sb("rows", [T, 2, NT], I32)
        shares = sb("shares", [T, 2, NT])
        yg = sb("yg", [T, 2, NT, D])
        h = sb("h", [T, NT, D])
        h2 = sb("h2", [T, NT, D])
        stats = sb("stats", [T, NT, 6])
        mv = sb("mv", [T, NT, 2])
        rstd = sb("rstd", [T, NT])
        z = sb("z", [T, NT, D])
        zT = sb("zT", [DH, 2, SEQ])
        xpad = sb("xpad", [128, M3, SEQ + TAPS - 1])
        xc = sb("xc", [128, M3, SEQ])
        xs = sb("xs", [128, M3, SEQ])
        zs = sb("zs", [128, M3, SEQ])
        dx = sb("dx", [128, M3, SEQ])
        xd = sb("xd", [KR, SEQ])
        dts = sb("dts", [128, M3, SEQ])
        den = sb("den", [128, M3, SEQ])
        delta = sb("delta", [128, M3, SEQ])
        u = sb("u", [128, M3, SEQ])
        kq = sb("kq", [NS, 2, SEQ])
        rest = sb("rest", [NS, 2, SEQ])
        mid = sb("mid", [NS, 2, SEQ], BF16)
        split = sb("split", [80, 2, SEQ], BF16)
        uT = sb("uT", [KR, NC, DI])
        squares = sb("squares", [CH, 2, DI])
        u2 = sb("u2", [CH, NC])
        kT = sb("kT", [CH, NC, NS])
        kTsq = sb("kTsq", [CH, NC, NS])
        k2 = sb("k2", [CH, NC])
        g2 = sb("g2", [CH, NC])
        gn = sb("gn", [CH, NC])
        gr = sb("gr", [CH, NC])
        alpha = sb("alpha", [CH, NC])
        ak = sb("ak", [CH, NC, NS])

        ps = [ctx.enter_context(nc.psum_tensor(f"c_ps{n}", [128, 512], F32)) for n in range(8)]

        weights_in = sem("weights_in")
        consts = sem("consts")
        rows_ready = sem("rows_ready")
        gathered = sem("gathered")
        h1_in = sem("h1_in")
        h2_ready = sem("h2_ready")
        var_ready = sem("var_ready")
        std_ready = sem("std_ready")
        z_ready = sem("z_ready")
        z_turned = sem("z_turned")
        zT0_ready = sem("zT0_ready")
        zT1_ready = sem("zT1_ready")
        in_done = sem("in_done")
        x_copied = sem("x_copied")
        zs_ready = sem("zs_ready")
        conv_ready = sem("conv_ready")
        xs_ready = sem("xs_ready")
        xd_done = sem("xd_done")
        xd_ready = sem("xd_ready")
        dt_done = sem("dt_done")
        dts_ready = sem("dts_ready")
        ksq_ready = sem("ksq_ready")
        ksq_done = sem("ksq_done")
        den_mul = sem("den_mul")
        den_ready = sem("den_ready")
        inverse_ready = sem("inverse_ready")
        delta_ready = sem("delta_ready")
        u_ready = sem("u_ready")
        u_turned = sem("u_turned")
        uT_copied = sem("uT_copied")
        u2_ready = sem("u2_ready")
        k_turned = sem("k_turned")
        kT_ready = sem("kT_ready")
        g2_ready = sem("g2_ready")
        g_ready = sem("g_ready")
        ck_ready = sem("ck_ready")
        carry_done = sem("carry_done")
        carry_ready = sem("carry_ready")
        dx_ready = sem("dx_ready")
        split_ready = sem("split_ready")
        stored = {n: sem("stored_" + n) for n in ("h2", "u", "carried", "ak", "delta", "kq", "dx", "zs")}
        chain_a = sem("chain_a")
        chain_b = sem("chain_b")
        conv_chain = sem("conv_chain")
        pchain = sem("pchain")
        passed = sem("passed")
        A_PER, CONV_PER, B_PER, P_PER = 2, 9, 15, 3
        W_IN = 9 * 16
        C1 = NC - 1

        block = ctx.enter_context(nc.Block())

        def each_image(eng, body):
            body(-2, True, False, False, False)
            body(-1, True, True, False, False)
            body(0, True, True, True, False)
            with eng.Fori(1, n_img - 2) as b:
                body(b, True, True, True, True)
            body(n_img - 2, False, True, True, True)
            body(n_img - 1, False, False, True, True)
            body(n_img, False, False, False, True)

        @block.sync
        def _(sp):
            for dst, src in ((inT, "inT"), (xprojT, "xprojT"), (conv_w, "conv_w"), (conv_b, "conv_b"), (dt_b, "dt_b"),
                             (d_skip, "d_skip"), (decay, "decay"), (dtheadT, "dtheadT")):
                sp.dma_start(dst[:], a[src]).then_inc(weights_in, 16)
            sp.dma_start(ck[CARRY:, :, :], a["carry_decay"]).then_inc(weights_in, 16)
            for s in stored.values():
                sp.sem_inc(s, 16)

            def store(name, dst, src, ready, count):
                sp.wait_ge(ready, count)
                sp.dma_start(dst, src).then_inc(stored[name], 16)

            def body(b, fetch, first, second, third):
                if first:
                    store("h2", h2_dram[b + 1], h2[:], h2_ready, b + 3)
                if fetch:
                    sp.wait_ge(h2_ready, b + 3)
                    sp.dma_start(h[:], h1_dram[b + 2]).then_inc(h1_in, 16)
                if second:
                    store("kq", kq_dram[b], split[:], split_ready, 3 * b + 3)
                    store("dx", dx_dram[b], dx[:], dx_ready, b + 1)
                    store("delta", delta_dram[b], delta[:], delta_ready, M3 * b + M3)
                if third:
                    store("carried", u_dram[b - 1][CARRY:CARRY + NS], uT[CARRY:CARRY + NS], carry_ready,
                          C1 * (b + 2))
                if second:
                    store("u", u_dram[b][0:CH], uT[0:CH], uT_copied, NC * b + NC)
                    store("ak", ak_dram[b], ak[:], ck_ready, b + 1)
                if first:
                    store("zs", zs_dram[b + 1], zs[:], zs_ready, 6 * b + 12)

            each_image(sp, body)
            for s in stored.values():
                sp.wait_ge(s, 16 * n_img + 16)

        @block.gpsimd
        def _(pool):
            identity(pool, ident[:], consts, 0)
            pool.memset(ones[:], 1.0)
            pool.memset(eps_col[:], LN_EPS)
            pool.memset(xpad[:], 0.0)
            pool.memset(split[:], 0.0)
            pool.memset(uT[:], 0.0)
            pool.memset(ck[0:CARRY], 0.0).then_inc(consts, 1)
            pool.sem_inc(h2_ready, 1)
            pool.sem_inc(u_ready, M3)

            def combine(b):
                c_ = Chain(pool, pchain, P_PER * b, P_PER)
                at = slice(b, b + 1) if isinstance(b, int) else bass.ds(b, 1)
                pool.tensor_copy(rows[:], route[:, at, 0:2, :].rearrange("p one k t -> p (one k) t")).then_inc(rows_ready, 1)
                c_.link(pool.tensor_copy(shares[:], route[:, at, 2:4, :].rearrange("p one k t -> p (one k) t")))
                pool.wait_ge(rows_ready, b + 1)
                pool.sem_inc(passed, 1)
                for k in range(2):
                    for t in range(NT):
                        pool.indirect_dma_start(out=yg[:, k, t, :], out_offset=None, in_=y_dram,
                                                in_offset=bass.IndirectOffsetOnAxis(ap=rows[:, k, t:t + 1], axis=0),
                                                ).then_inc(gathered, 16)
                pool.wait_ge(gathered, 16 * 2 * NT * (b + 1))
                pool.sem_inc(passed, 1)
                for k in range(2):
                    ins = pool.tensor_tensor(yg[:, k], yg[:, k], shares[:, k, :].unsqueeze(2).to_broadcast([T, NT, D]),
                                             ALU.mult)
                c_.link(ins)
                pool.sem_inc(passed, 1)
                c_.link(pool.tensor_tensor(yg[:, 0], yg[:, 0], yg[:, 1], ALU.add))
                pool.wait_ge(h1_in, 16 * b + 16)
                pool.wait_ge(z_ready, b + 1)
                pool.wait_ge(stored["h2"], 16 * b + 16)
                pool.tensor_tensor(h2[:], h[:], yg[:, 0], ALU.add).then_inc(h2_ready, 1)
                c_.close()

            def body(b, fetch, first, second, third):
                if fetch:
                    combine(b + 2)
                if second:
                    pool.wait_ge(u2_ready, NC * b + NC)
                    pool.wait_ge(stored["delta"], 16 * b + 16)
                    for m in range(M3):
                        pool.wait_ge(inverse_ready, M3 * b + m + 1)
                        pool.tensor_tensor(delta[:, m], dts[:, m], den[:, m], ALU.mult).then_inc(delta_ready, 1)
                        pool.wait_ge(delta_ready, M3 * b + m + 1)
                        pool.tensor_tensor(u[:, m], delta[:, m], xs[:, m], ALU.mult).then_inc(u_ready, 1)

            each_image(pool, body)

        @block.tensor
        def _(pe):
            pe.wait_ge(weights_in, W_IN)
            pe.wait_ge(consts, 3)
            pe.sem_inc(carry_done, C1)

            def step_sizes(b):
                pe.wait_ge(xs_ready, M3 * b + 2 * M3)
                pe.wait_ge(kT_ready, b + 1)
                pe.wait_ge(carry_ready, C1 * (b + 1))
                for g in range(2):
                    for m in range(M3):
                        ins = pe.matmul(ps[g][0:KR, 0:G], xprojT[:, m, :], xs[:, m, g * G:(g + 1) * G],
                                        start=(m == 0), stop=(m == M3 - 1))
                    ins.then_inc(xd_done, 1)
                pe.wait_ge(xd_ready, 2 * b + 2)
                for m in range(M3):
                    for g in range(2):
                        n = 2 * m + g
                        if n < 4:
                            pe.wait_ge(zs_ready, 6 * b + 6)
                        else:
                            pe.wait_ge(dts_ready, 6 * b + n - 3)
                        pe.matmul(ps[4 + n % 4][:, 0:G], dtheadT[:, m * 128:(m + 1) * 128],
                                  xd[:, g * G:(g + 1) * G], start=True, stop=True).then_inc(dt_done, 1)
                pe.wait_ge(ksq_ready, b + 1)
                pe.wait_ge(u2_ready, NC * b + NC)
                for g in range(2):
                    ins = pe.matmul(ps[2 + g][:, 0:G], ones[:], kq[:, 0, g * G:(g + 1) * G], start=True, stop=True)
                ins.then_inc(ksq_done, 1)
                for c in range(NC):
                    ins = pe.transpose(ps[0][0:CH, c * NS:(c + 1) * NS], xd[0:NS, c * CH:(c + 1) * CH], ident[0:NS, 0:NS])
                ins.then_inc(k_turned, 1)

            def turn(b, behind):
                pe.wait_ge(z_ready, b + 2)
                if behind:
                    pe.wait_ge(dts_ready, 6 * b)
                for m in range(2):
                    for g in range(2):
                        for t in range(3):
                            ins = pe.transpose(ps[4 + 2 * m + g][0:DH, t * T:(t + 1) * T],
                                               z[:, 3 * g + t, m * DH:(m + 1) * DH], ident[0:T, 0:T])
                ins.then_inc(z_turned, 1)

            def in_projection(b, first, last):
                for n in range(first, last):
                    m, g = n // 2, n % 2
                    if n == 0:
                        pe.wait_ge(zT0_ready, b + 1)
                        pe.wait_ge(zT1_ready, b + 1)
                    elif 4 <= n < 10:
                        pe.wait_ge(x_copied, 6 * b + n - 3)
                    elif n >= 10:
                        pe.wait_ge(zs_ready, 6 * b + n - 9)
                    for c in range(2):
                        ins = pe.matmul(ps[4 + n % 4][:, 0:G], inT[:, c, m * 128:(m + 1) * 128],
                                        zT[:, c, g * G:(g + 1) * G], start=(c == 0), stop=(c == 1))
                    ins.then_inc(in_done, 1)

            def carry(b, c):
                if c == 0:
                    pe.wait_ge(ck_ready, b + 1)
                    pe.wait_ge(uT_copied, NC * b + NC)
                pe.wait_ge(carry_ready, C1 * (b + 2) + c)
                pe.matmul(ps[1][0:NS, 0:DI], ck[:, c, :], uT[:, c, :], start=True, stop=True).then_inc(carry_done, 1)

            def turn_updates(b):
                pe.wait_ge(u_ready, M3 * b + 2 * M3)
                pe.wait_ge(ksq_done, b + 1)
                pe.wait_ge(den_mul, M3 * b + M3)
                for c in range(NC):
                    if c >= 2:
                        pe.wait_ge(u2_ready, NC * b + NC + c - 1)
                    pe.sem_inc(passed, 1)
                    for m in range(M3):
                        ins = pe.transpose(ps[2 + c % 2][0:CH, m * 128:(m + 1) * 128], u[:, m, c * CH:(c + 1) * CH],
                                           ident[:])
                    ins.then_inc(u_turned, 1)

            def body(b, fetch, first, second, third):
                if second:
                    step_sizes(b)
                if first:
                    turn(b + 1, second)
                for c in range(C1):
                    if first and c < 4:
                        in_projection(b + 1, c, c + 1)
                    if third:
                        carry(b - 1, c)
                if first:
                    in_projection(b + 1, 4, 6)
                if second:
                    turn_updates(b)
                if first:
                    in_projection(b + 1, 6, 12)

            each_image(pe, body)

        @block.scalar
        def _(act):
            act.wait_ge(weights_in, W_IN)
            act.wait_ge(consts, 3)
            act.sem_inc(u2_ready, NC)
            act.sem_inc(xs_ready, M3)
            act.sem_inc(carry_ready, 2 * C1)

            def updates(b):
                act.wait_ge(stored["u"], 16 * b + 16)
                act.wait_ge(carry_done, C1 * (b + 1))
                for c in range(NC):
                    act.wait_ge(u_turned, NC * b + c + 1)
                    act.activation(uT[0:CH, c, :], ps[2 + c % 2][0:CH, 0:DI], ACT.Copy).then_inc(uT_copied, 1)
                    if c >= 2:
                        act.wait_ge(u2_ready, NC * b + NC + c - 1)
                    act.activation(squares[:, c % 2, :], ps[2 + c % 2][0:CH, 0:DI], ACT.Square, accum_out=u2[:, c:c + 1]
                                   ).then_inc(u2_ready, 1)

            def body(b, fetch, first, second, third):
                if first:
                    act.wait_ge(var_ready, b + 2)
                    act.activation(rstd[:], mv[:, :, 1], ACT.Sqrt, bias=eps_col[:, 0:1]).then_inc(std_ready, 1)
                if second:
                    for g in range(2):
                        act.wait_ge(xd_done, 2 * b + g + 1)
                        act.activation(xd[:, g * G:(g + 1) * G], ps[g][0:KR, 0:G], ACT.Copy).then_inc(xd_ready, 1)
                    for m in range(M3):
                        for g in range(2):
                            n = 2 * m + g
                            act.wait_ge(dt_done, 6 * b + n + 1)
                            act.activation(dts[:, m, g * G:(g + 1) * G], ps[4 + n % 4][:, 0:G], ACT.Sigmoid,
                                           bias=dt_b[:, m:m + 1]).then_inc(dts_ready, 1)
                    for m in range(M3):
                        act.wait_ge(den_mul, M3 * b + m + 1)
                        act.activation(den[:, m], den[:, m], ACT.Copy, bias=1.0).then_inc(den_ready, 1)
                if first:
                    act.wait_ge(z_turned, b + 2)
                    act.activation(zT[:, 1, 0:G], ps[6][0:DH, 0:G], ACT.Copy)
                    act.activation(zT[:, 1, G:SEQ], ps[7][0:DH, 0:G], ACT.Copy).then_inc(zT1_ready, 1)
                if second:
                    act.wait_ge(stored["dx"], 16 * b + 16)
                    act.wait_ge(xs_ready, M3 * b + 2 * M3)
                    for m in range(M3):
                        ins = act.activation(dx[:, m, :], xs[:, m, :], ACT.Copy, scale=d_skip[:, m:m + 1])
                    ins.then_inc(dx_ready, 1)
                if third:
                    act.wait_ge(stored["carried"], 16 * (b - 1) + 16)
                    for c in range(C1):
                        act.wait_ge(carry_done, C1 * b + c + 1)
                        act.activation(uT[CARRY:CARRY + NS, c + 1, :], ps[1][0:NS, 0:DI], ACT.Copy).then_inc(carry_ready, 1)
                if second:
                    updates(b)
                    act.wait_ge(g2_ready, b + 1)
                    act.activation(gn[:], g2[:], ACT.Sqrt).then_inc(g_ready, 1)
                if first:
                    act.wait_ge(u_ready, M3 * (b + 2))
                    for m in range(M3):
                        act.wait_ge(conv_ready, M3 * (b + 1) + m + 1)
                        act.activation(xs[:, m, :], xc[:, m, :], ACT.Silu, bias=conv_b[:, m:m + 1]).then_inc(xs_ready, 1)
                    act.wait_ge(stored["zs"], 16 * (b + 1) + 16)
                    for n in range(6):
                        m, g = n // 2, n % 2
                        act.wait_ge(in_done, 12 * (b + 1) + 6 + n + 1)
                        act.activation(zs[:, m, g * G:(g + 1) * G], ps[4 + (n + 6) % 4][:, 0:G], ACT.Silu
                                       ).then_inc(zs_ready, 1)

            each_image(act, body)

        @block.vector
        def _(dve):
            dve.wait_ge(weights_in, W_IN)
            dve.wait_ge(consts, 3)
            dve.sem_inc(z_ready, 1)
            dve.sem_inc(kT_ready, 1)

            def layernorm(b):
                c_ = Chain(dve, chain_a, A_PER * b, A_PER)
                dve.wait_ge(h2_ready, b + 2)
                for t in range(NT):
                    ins = dve.bn_stats(stats[:, t, :], h2[:, t, :])
                c_.link(ins)
                dve.sem_inc(passed, 1)
                for t in range(NT):
                    ins = dve.bn_aggr(mv[:, t, :], stats[:, t, :])
                ins.then_inc(var_ready, 1)
                dve.wait_ge(std_ready, b + 1)
                c_.link(dve.reciprocal(rstd[:], rstd[:]))
                for t in range(NT):
                    ins = dve.tensor_scalar(z[:, t, :], h2[:, t, :], mv[:, t, 0:1], rstd[:, t:t + 1],
                                            ALU.subtract, ALU.mult)
                ins.then_inc(z_ready, 1)
                c_.close()

            def turned(b):
                dve.wait_ge(z_turned, b + 1)
                dve.tensor_copy(zT[:, 0, 0:G], ps[4][0:DH, 0:G])
                dve.tensor_copy(zT[:, 0, G:SEQ], ps[5][0:DH, 0:G]).then_inc(zT0_ready, 1)

            def convolve(b, m):
                c_ = Chain(dve, conv_chain, CONV_PER * b + M3 * m)
                for g in range(2):
                    n = 2 * m + g
                    dve.wait_ge(in_done, 12 * b + n + 1)
                    dve.tensor_copy(xpad[:, m, TAPS - 1 + g * G:TAPS - 1 + (g + 1) * G], ps[4 + n % 4][:, 0:G]
                                    ).then_inc(x_copied, 1)
                dve.wait_ge(x_copied, 6 * b + 2 * m + 2)
                dve.wait_ge(xs_ready, M3 * b + m + 1)
                c_.link(dve.tensor_scalar(xc[:, m, :], xpad[:, m, 0:SEQ], conv_w[:, m, 0:1], None, ALU.mult))
                for j in range(1, TAPS):
                    ins = dve.scalar_tensor_tensor(out=xc[:, m, :], in0=xpad[:, m, j:j + SEQ],
                                                   scalar=conv_w[:, m, j:j + 1], in1=xc[:, m, :],
                                                   op0=ALU.mult, op1=ALU.add)
                    if j < TAPS - 1:
                        c_.link(ins)
                ins.then_inc(conv_ready, 1)

            def parts(b, c_):
                dve.wait_ge(xd_ready, 2 * b + 2)
                dve.tensor_tensor(kq[:, 0, :], xd[0:NS, :], xd[0:NS, :], ALU.mult).then_inc(ksq_ready, 1)
                c_.link(dve.tensor_copy(kq[:, 1, :], xd[32:32 + NS, :]))
                dve.wait_ge(stored["kq"], 16 * b + 16)
                dve.tensor_copy(split[0:NS], kq[:]).then_inc(split_ready, 1)
                dve.wait_ge(split_ready, 3 * b + 1)
                c_.link(dve.tensor_tensor(rest[:], kq[:], split[0:NS], ALU.subtract))
                c_.link(dve.tensor_copy(mid[:], rest[:]))
                dve.tensor_copy(split[32:32 + NS], mid[:]).then_inc(split_ready, 1)
                c_.link(dve.tensor_tensor(rest[:], rest[:], mid[:], ALU.subtract))
                dve.tensor_copy(split[64:64 + NS], rest[:]).then_inc(split_ready, 1)

            def step_sizes(b):
                dve.wait_ge(ksq_done, b + 1)
                dve.wait_ge(dts_ready, 6 * b + 6)
                for m in range(M3):
                    for g in range(2):
                        ins = dve.tensor_tensor(den[:, m, g * G:(g + 1) * G], dts[:, m, g * G:(g + 1) * G],
                                                ps[2 + g][:, 0:G], ALU.mult)
                    ins.then_inc(den_mul, 1)

            def invert(b):
                for m in range(M3):
                    dve.wait_ge(den_ready, M3 * b + m + 1)
                    dve.reciprocal(den[:, m], den[:, m]).then_inc(inverse_ready, 1)

            def keys(b, c_):
                dve.wait_ge(k_turned, b + 1)
                dve.tensor_copy(kT[:].rearrange("p c n -> p (c n)"), ps[0][0:CH, 0:NC * NS]).then_inc(kT_ready, 1)
                dve.wait_ge(kT_ready, b + 2)
                c_.link(dve.tensor_tensor(kTsq[:], kT[:], kT[:], ALU.mult))
                c_.link(dve.tensor_reduce(k2[:], kTsq[:], AX_X, ALU.add))

            def scale(b, c_):
                dve.wait_ge(u2_ready, NC * b + 2 * NC)
                dve.tensor_tensor(g2[:], u2[:], k2[:], ALU.mult).then_inc(g2_ready, 1)
                dve.wait_ge(g_ready, b + 1)
                c_.link(dve.tensor_scalar(gn[:], gn[:], 1e-7, None, ALU.add))
                c_.link(dve.reciprocal(gn[:], gn[:]))
                c_.link(dve.tensor_tensor(gr[:], gn[:], gn[:], ALU.mult))
                c_.link(dve.tensor_tensor(gr[:], gr[:], g2[:], ALU.mult))
                c_.link(dve.tensor_scalar(alpha[:], gr[:], NS_C, NS_B, ALU.mult, ALU.add))
                c_.link(dve.tensor_tensor(alpha[:], alpha[:], gr[:], ALU.mult))
                c_.link(dve.tensor_scalar(alpha[:], alpha[:], NS_A, None, ALU.add))
                c_.link(dve.tensor_tensor(alpha[:], alpha[:], gn[:], ALU.mult))
                dve.wait_ge(stored["ak"], 16 * b + 16)
                c_.link(dve.tensor_tensor(ak[:], kT[:], alpha[:].unsqueeze(2).to_broadcast([CH, NC, NS]), ALU.mult))
                dve.tensor_scalar(ck[0:CH], ak[:], decay[:, 0:1], None, ALU.mult).then_inc(ck_ready, 1)

            def body(b, fetch, first, second, third):
                if first:
                    layernorm(b + 1)
                if second:
                    c_ = Chain(dve, chain_b, B_PER * b, B_PER)
                    parts(b, c_)
                    step_sizes(b)
                if first:
                    turned(b + 1)
                if second:
                    invert(b)
                    keys(b, c_)
                if first:
                    convolve(b + 1, 0)
                    convolve(b + 1, 1)
                    convolve(b + 1, 2)
                if second:
                    scale(b, c_)
                    c_.close()

            each_image(dve, body)


def phase_scan(nc, a, n_img, u_dram, ak_dram, delta_dram, kq_dram, dx_dram, zs_dram, h2_dram, h3_dram):
    UNITS = NQ * M3
    PAIRS = NC // 2
    with ExitStack() as ctx:
        def sb(name, shape, dt=F32):
            return ctx.enter_context(nc.sbuf_tensor("d_" + name + "_t", shape, dt))

        def sem(name):
            return nc.alloc_semaphore("d_" + name)

        v = sb("v", [128, M3, Q4, SEQ])
        da = sb("da", [128, 2, Q4, SEQ])
        kb = sb("kb", [128, 2, Q4, SEQ])
        qb = sb("qb", [128, 2, Q4, SEQ])
        lk = sb("lk", [KR, 2, NC, Q4, CH])
        uT = sb("uT", [KR, NC, DI])
        ak = sb("ak", [CH, NC, NS])
        kq = sb("kq", [KR, 2, SEQ], BF16)
        delta = sb("delta", [128, M3, SEQ])
        y = sb("y", [128, M3, SEQ])
        zs = sb("zs", [128, M3, SEQ])
        h = sb("h", [T, NT, D])
        within = sb("within", [CH, CH])
        select = sb("select", [KR, NS, 128], BF16)
        outT = sb("outT", [128, M3, D])
        ident = sb("ident", [128, 128])

        ps_v = [ctx.enter_context(nc.psum_tensor(f"d_v{n}", [128, 512], F32)) for n in range(4)]
        ps_y = ctx.enter_context(nc.psum_tensor("d_y", [128, 2, 512], F32))
        ps_b = ctx.enter_context(nc.psum_tensor("d_b", [128, 2, 512], F32))

        QUARTER = M3 * PAIRS
        V0 = 2 * QUARTER
        W0 = 2 * M3
        weights_in = sem("weights_in")
        consts = sem("consts")
        u_in = [sem(f"u_in{m}") for m in range(M3)]
        ak_in = sem("ak_in")
        kq_in = sem("kq_in")
        delta_in = [sem(f"delta_in{m}") for m in range(M3)]
        dx_in = sem("dx_in")
        zs_in = sem("zs_in")
        h2_in = sem("h2_in")
        carried_in = [sem("carried_in0"), sem("carried_in1")]
        zeroed = sem("zeroed")
        lk_ready = sem("lk_ready")
        spread = sem("spread")
        spread_copied = sem("spread_copied")
        v_done = sem("v_done")
        v_ready = sem("v_ready")
        w_ready = sem("w_ready")
        da_ready = sem("da_ready")
        scanned = sem("scanned")
        hq_ready = sem("hq_ready")
        paired = sem("paired")
        ysum_done = sem("ysum_done")
        y_added = sem("y_added")
        gated = sem("gated")
        out_done = sem("out_done")
        h3_ready = sem("h3_ready")
        h3_out = sem("h3_out")

        block = ctx.enter_context(nc.Block())

        def each_unit(eng, step):
            for u in range(3):
                step(0, u, False, True)
            with eng.Fori(0, n_img - 1) as b:
                for u in range(3, UNITS):
                    step(b, u, True, True)
                for u in range(3):
                    step(b + 1, u, True, True)
            for u in range(3, UNITS):
                step(n_img - 1, u, True, False)

        @block.sync
        def _(sp):
            sp.dma_start(within[:], a["within"]).then_inc(weights_in, 16)
            sp.dma_start(outT[:], a["outT"]).then_inc(weights_in, 16)
            sp.sem_inc(h3_out, 16)

            def load_carried(b, q):
                sp.wait_ge(v_done, QUARTER * (NQ * b + q + 1))
                sp.dma_start(lk[CARRY:CARRY + NS, q % 2].rearrange("p c n t -> p (c n t)"),
                             a["carried"][q % NQ].rearrange("p c n t -> p (c n t)")).then_inc(carried_in[q % 2], 16)

            def load_part(b, m):
                cols = slice(m * 128, (m + 1) * 128)
                sp.wait_ge(w_ready, W0 + UNITS * b - M3 + m + 1)
                sp.dma_start(delta[:, m, :], delta_dram[b][:, m, :]).then_inc(delta_in[m], 16)
                sp.wait_ge(v_done, V0 + PAIRS * (UNITS * b - M3 + m + 1))
                for rows in (slice(0, CH), slice(CARRY, CARRY + NS)):
                    sp.dma_start(uT[rows, :, cols], u_dram[b][rows, :, cols]).then_inc(u_in[m], 16)

            def load_first(b):
                sp.wait_ge(lk_ready, NQ * b + 1)
                sp.dma_start(ak[:], ak_dram[b]).then_inc(ak_in, 16)
                sp.wait_ge(spread, 8 * NQ * b + 1)
                sp.dma_start(kq[0:80], kq_dram[b]).then_inc(kq_in, 16)

            def load_skip(b):
                sp.dma_start(y[:], dx_dram[b]).then_inc(dx_in, 16)

            def load_gates(b):
                sp.dma_start(zs[:], zs_dram[b]).then_inc(zs_in, 16)

            def load_residual(b):
                sp.wait_ge(h3_out, 16 * b + 16)
                sp.dma_start(h[:], h2_dram[b]).then_inc(h2_in, 16)

            sp.wait_ge(zeroed, 3)
            load_first(0)
            load_carried(0, 0)
            for m in range(M3):
                load_part(0, m)
            load_carried(0, 1)
            load_skip(0)
            load_gates(0)
            with sp.Fori(0, n_img - 1) as b:
                load_residual(b)
                load_carried(b, 2)
                load_carried(b, 3)
                load_first(b + 1)
                load_carried(b, 4)
                for m in range(M3):
                    load_part(b + 1, m)
                load_carried(b, 5)
                sp.wait_ge(gated, b + 1)
                load_skip(b + 1)
                sp.wait_ge(out_done, b + 1)
                load_gates(b + 1)
                sp.wait_ge(h3_ready, b + 2)
                sp.dma_start(h3_dram[b], h[:]).then_inc(h3_out, 16)
            load_residual(n_img - 1)
            load_carried(n_img - 1, 2)
            load_carried(n_img - 1, 3)
            sp.wait_ge(h3_ready, n_img + 1)
            sp.dma_start(h3_dram[n_img - 1], h[:]).then_inc(h3_out, 16)
            sp.wait_ge(h3_out, 16 * n_img + 16)

        @block.gpsimd
        def _(pool):
            identity(pool, ident[:], consts, 0)
            pool.memset(select[:], 0.0).then_inc(consts, 1)
            for part in range(3):
                pool.wait_ge(consts, part + 3)
                pool.affine_select(out=select[:], in_=select[:], compare_op=ALU.not_equal, fill=1.0, base=-32 * part,
                                   pattern=[[-1, NS], [0, 128]], channel_multiplier=1).then_inc(consts, 1)
            pool.wait_ge(consts, 6)
            pool.memset(kq[64:], 0.0).then_inc(zeroed, 1)
            pool.wait_ge(zeroed, 1)
            pool.memset(uT[:], 0.0).then_inc(zeroed, 1)
            pool.wait_ge(zeroed, 2)
            pool.memset(lk[:], 0.0).then_inc(zeroed, 1)
            pool.memset(da[:], 0.0).then_inc(consts, 1)
            pool.wait_ge(weights_in, 32)
            pool.wait_ge(consts, 7)
            pool.wait_ge(zeroed, 3)
            pool.sem_inc(hq_ready, W0)
            pool.sem_inc(lk_ready, 1)

            def powers(b, q):
                if q % NQ == 0:
                    pool.wait_ge(ak_in, 16 * (b + q // NQ) + 16)
                pool.wait_ge(v_done, QUARTER * (NQ * b + q + 1))
                q4 = q % NQ
                pool.tensor_tensor(lk[0:CH, q % 2], within[:].unsqueeze(1).unsqueeze(1).to_broadcast([CH, NC, Q4, CH]),
                                   ak[:, :, Q4 * q4:Q4 * q4 + Q4].unsqueeze(3).to_broadcast([CH, NC, Q4, CH]),
                                   ALU.mult).then_inc(lk_ready, 1)

            def step(b, u, behind, ahead):
                q, m = u // M3, u % M3
                pool.wait_ge(spread_copied, 8 * NQ * b + 8 * q + 9)
                pool.wait_ge(scanned, UNITS * b + u + 1)
                pool.tensor_tensor(v[:, m], v[:, m], qb[:, q % 2], ALU.mult).then_inc(hq_ready, 1)
                if m == 0 and (q + 1 < NQ or ahead):
                    powers(b, q + 1)

            powers(0, 0)
            each_unit(pool, step)

        @block.tensor
        def _(pe):
            pe.wait_ge(weights_in, 32)
            pe.wait_ge(consts, 7)
            pe.wait_ge(zeroed, 3)
            pe.sem_inc(ysum_done, 3)
            pe.sem_inc(v_done, V0)
            pe.sem_inc(spread, 1)

            def spread_rows(b, q, first, last):
                if q % NQ == 0 and first == 0:
                    pe.wait_ge(kq_in, 16 * (b + q // NQ) + 16)
                for i in range(first, last):
                    pe.wait_ge(spread_copied, 8 * NQ * b + 8 * q + i + 1)
                    for g in range(2):
                        ins = pe.matmul(ps_b[:, g, 0:G], select[:, Q4 * (q % NQ) + i % Q4, :],
                                        kq[:, i // Q4, g * G:(g + 1) * G], start=True, stop=True)
                    ins.then_inc(spread, 1)

            def momentum(b, u):
                q, m = u // M3, u % M3
                if m == 0:
                    pe.wait_ge(lk_ready, NQ * b + q + 2)
                    pe.wait_ge(carried_in[q % 2], 16 * (2 * b + q // 2 + 1))
                if q == 0:
                    pe.wait_ge(u_in[m], 32 * b + 32)
                for k in range(PAIRS):
                    n = PAIRS * u + k
                    pe.wait_ge(v_ready, UNITS * PAIRS * b + n + 1)
                    for c in range(2):
                        ins = pe.matmul(ps_v[n % 4][:, c * Q4 * CH:(c + 1) * Q4 * CH], uT[:, 2 * k + c, m * 128:(m + 1) * 128],
                                        lk[:, q % 2, 2 * k + c].rearrange("p n t -> p (n t)"), start=True, stop=True)
                    ins.then_inc(v_done, 1)

            def sum_states(b, u, g):
                m = u % M3
                if g == 0:
                    pe.wait_ge(paired, UNITS * b + u + 1)
                    pe.wait_ge(y_added, UNITS * b + u + 1)
                for i in range(2):
                    ins = pe.matmul(ps_y[:, g, 0:G], ident[:], v[:, m, i, g * G:(g + 1) * G],
                                    start=(i == 0), stop=(i == 1))
                if g:
                    ins.then_inc(ysum_done, 1)

            def project_out(b, copied):
                pe.wait_ge(gated, b + 1)
                pe.wait_ge(spread_copied, 8 * NQ * (b + 1) + copied + 1)
                for t in range(NT):
                    out = (ps_b[0:T, 0], ps_b[0:T, 1], ps_y[0:T, 0])[t // 2][:, (t % 2) * D:(t % 2 + 1) * D]
                    for m in range(M3):
                        ins = pe.matmul(out, zs[:, m, t * T:(t + 1) * T], outT[:, m, :], start=(m == 0), stop=(m == M3 - 1))
                ins.then_inc(out_done, 1)

            def step(b, u, behind, ahead):
                q, m = u // M3, u % M3
                rows = (0, 3, 6, 8)[m:m + 2]
                momentum(b, u)
                if u == 2 and behind:
                    project_out(b - 1, 8 + rows[0])
                    pe.wait_ge(h3_ready, b + 1)
                for g in range(3):
                    if rows[0] + g < rows[1] and (q + 1 < NQ or ahead):
                        spread_rows(b, q + 1, rows[0] + g, rows[0] + g + 1)
                    if g < 2 and u >= 2:
                        sum_states(b, u - 2, g)
                    elif g < 2 and behind:
                        sum_states(b - 1, UNITS + u - 2, g)

            def finish(b):
                for u in range(UNITS - 2, UNITS):
                    for g in range(2):
                        sum_states(b, u, g)
                project_out(b, 0)

            spread_rows(0, 0, 0, 8)
            each_unit(pe, step)
            finish(n_img - 1)

        @block.scalar
        def _(act):
            act.wait_ge(consts, 7)
            act.sem_inc(v_ready, 4)
            act.sem_inc(spread_copied, 1)

            def copy_spread(b, q, first, last):
                for i in range(first, last):
                    if i == 0:
                        act.wait_ge(w_ready, UNITS * b + M3 * (q + 1))
                    if i == Q4:
                        act.wait_ge(hq_ready, UNITS * b + M3 * (q + 1))
                    act.wait_ge(spread, 8 * NQ * b + 8 * q + i + 2)
                    act.activation((kb, qb)[i // Q4][:, q % 2, i % Q4, :].rearrange("p (g t) -> p g t", g=2),
                                   ps_b[:, :, 0:G], ACT.Copy).then_inc(spread_copied, 1)

            def step(b, u, behind, ahead):
                q, m = u // M3, u % M3
                act.wait_ge(w_ready, W0 + UNITS * b + u + 1)
                act.activation(da[:, u % 2, :, 1:SEQ], da[:, u % 2, :, 1:SEQ], ACT.Copy, scale=-1.0, bias=1.0
                               ).then_inc(da_ready, 1)
                act.wait_ge(ysum_done, UNITS * b + u + 1)
                for k in range(PAIRS):
                    n = PAIRS * u + k
                    act.wait_ge(v_done, V0 + UNITS * PAIRS * b + n + 1)
                    act.activation(v[:, m, :, k * T:(k + 1) * T].rearrange("p n (c t) -> p n c t", c=2),
                                   ps_v[n % 4][:, 0:2 * Q4 * CH].rearrange("p (c n t) -> p n c t", c=2, n=Q4),
                                   ACT.Copy).then_inc(v_ready, 1)
                if q + 1 < NQ or ahead:
                    rows = (0, 3, 6, 8)[m:m + 2]
                    copy_spread(b, q + 1, rows[0], rows[1])

            copy_spread(0, 0, 0, 8)
            each_unit(act, step)

        @block.vector
        def _(dve):
            dve.wait_ge(consts, 7)
            dve.sem_inc(w_ready, W0)
            dve.sem_inc(y_added, 1)
            dve.sem_inc(h3_ready, 1)

            def decays(b, u, started):
                q, m = u // M3, u % M3
                dve.wait_ge(spread_copied, 8 * NQ * b + 8 * q + 5)
                if q % NQ == 0:
                    dve.wait_ge(delta_in[m], 16 * (b + q // NQ) + 16)
                if started:
                    dve.wait_ge(scanned, UNITS * b + u - 1)
                dve.tensor_tensor(da[:, u % 2, :, 1:SEQ], kb[:, q % 2, :, 1:SEQ],
                                  delta[:, m, 1:SEQ].unsqueeze(1).to_broadcast([128, Q4, SEQ - 1]), ALU.mult
                                  ).then_inc(w_ready, 1)

            def pair_states(b, u):
                m = u % M3
                dve.wait_ge(hq_ready, W0 + UNITS * b + u + 1)
                dve.tensor_tensor(v[:, m, 0:2, :], v[:, m, 0:2, :], v[:, m, 2:4, :], ALU.add).then_inc(paired, 1)

            def add_states(b, u):
                m = u % M3
                dve.wait_ge(ysum_done, UNITS * b + u + 4)
                if u == 0:
                    dve.wait_ge(dx_in, 16 * b + 16)
                if u >= M3:
                    dve.wait_ge(y_added, UNITS * b + u - 1)
                dve.tensor_tensor(y[:, m, :].rearrange("p (g t) -> p g t", g=2), ps_y[:, :, 0:G],
                                  y[:, m, :].rearrange("p (g t) -> p g t", g=2), ALU.add).then_inc(y_added, 1)

            def gate(b):
                dve.wait_ge(zs_in, 16 * b + 16)
                dve.wait_ge(y_added, UNITS * (b + 1) + 1)
                dve.tensor_tensor(zs[:], y[:], zs[:], ALU.mult).then_inc(gated, 1)

            def residual(b):
                dve.wait_ge(h2_in, 16 * b + 16)
                dve.wait_ge(out_done, b + 1)
                for t in range(3):
                    src = (ps_b[0:T, 0], ps_b[0:T, 1], ps_y[0:T, 0])[t][:, 0:2 * D]
                    ins = dve.tensor_tensor(h[:, 2 * t:2 * t + 2, :], src.rearrange("p (t d) -> p t d", d=D),
                                            h[:, 2 * t:2 * t + 2, :], ALU.add)
                ins.then_inc(h3_ready, 1)

            def step(b, u, behind, ahead):
                if u >= 2:
                    pair_states(b, u - 2)
                elif behind:
                    pair_states(b - 1, UNITS + u - 2)
                if u + 1 < UNITS or ahead:
                    decays(b, u + 1, behind or u >= 1)
                dve.wait_ge(da_ready, UNITS * b + u + 1)
                dve.wait_ge(v_ready, UNITS * PAIRS * b + PAIRS * (u + 1) + 4)
                flat = v[:, u % M3].rearrange("p n t -> p (n t)")
                dve.tensor_tensor_scan(flat, da[:, u % 2].rearrange("p n t -> p (n t)"), flat, 0.0, ALU.mult, ALU.add
                                       ).then_inc(scanned, 1)
                if u == 2 and behind:
                    residual(b - 1)
                if u >= 2:
                    add_states(b, u - 2)
                elif behind:
                    add_states(b - 1, UNITS + u - 2)
                if u == 1 and behind:
                    gate(b - 1)

            def finish(b):
                pair_states(b, UNITS - 2)
                pair_states(b, UNITS - 1)
                add_states(b, UNITS - 2)
                add_states(b, UNITS - 1)
                gate(b)
                residual(b)

            decays(0, 0, False)
            each_unit(dve, step)
            finish(n_img - 1)


def phase_project(nc, a, half, n_img, h3_dram, hn_dram, qk_dram, v_dram):
    b0 = half * n_img
    P = "e%d_" % half
    with ExitStack() as ctx:
        def sb(name, shape, dt=F32):
            return ctx.enter_context(nc.sbuf_tensor(P + name + "_t", shape, dt))

        def sem(name):
            return nc.alloc_semaphore(P + name)

        w = sb("w", [DH, 2, 3 * D])
        gain = sb("gain", [DH, 2])
        shift = sb("shift", [DH, 2])
        gumbel = sb("gumbel", [T, 3])
        bias = sb("bias", [T, D])
        ident = sb("ident", [128, 128])
        eps_col = sb("eps_col", [T, 1])
        h = sb("h", [T, NT, D])
        hn = sb("hn", [T, NT, D])
        hb = sb("hb", [T, NT, D])
        z = sb("z", [T, NT, D])
        stats = sb("stats", [T, NT, 6])
        mv = sb("mv", [T, NT, 2])
        rstd = sb("rstd", [T, NT])
        zT = sb("zT", [DH, 2, SEQ])
        parts = sb("parts", [DH, 2, 3, 2, SEQ], BF16)
        rest = sb("rest", [DH, 4, G])
        va = sb("va", [T, NT, HEADS, 32])

        ps = [ctx.enter_context(nc.psum_tensor(f"{P}ps{n}", [128, 512], F32)) for n in range(8)]

        weights_in = sem("weights_in")
        consts = sem("consts")
        h_in = sem("h_in")
        h_used = sem("h_used")
        var_ready = [sem("var_ready1"), sem("var_ready2")]
        std_ready = [sem("std_ready1"), sem("std_ready2")]
        hn_ready = sem("hn_ready")
        hb_ready = sem("hb_ready")
        hb_out = sem("hb_out")
        z_ready = sem("z_ready")
        z_turned = sem("z_turned")
        zT0_ready = sem("zT0_ready")
        zT1_ready = sem("zT1_ready")
        qk_done = sem("qk_done")
        hi_ready = sem("hi_ready")
        rest_ready = sem("rest_ready")
        mid_ready = sem("mid_ready")
        lo_ready = sem("lo_ready")
        qk_out = [sem("q_out"), sem("k_out")]
        v_done = sem("v_done")
        v_ready = sem("v_ready")
        v_out = sem("v_out")
        chain = sem("chain")
        passed = sem("passed")
        V_PER = 4

        block = ctx.enter_context(nc.Block())

        def each_image(eng, body):
            with eng.Fori(0, n_img - 1) as b:
                body(b, True)
            body(n_img - 1, False)

        @block.sync
        def _(sp):
            names = ("n1s_g", "n1s_b") if half else ("n1l_g", "n1l_b")
            sp.dma_start(w[:], a["f_wqkv"]).then_inc(weights_in, 16)
            sp.dma_start(gain[:], a[names[0]]).then_inc(weights_in, 16)
            sp.dma_start(shift[:], a[names[1]]).then_inc(weights_in, 16)
            sp.dma_start(gumbel[:], a["gumbel"].partition_broadcast(T)).then_inc(weights_in, 16)
            sp.dma_start(bias[:], a["f_bproj"].partition_broadcast(T)).then_inc(weights_in, 16)
            sp.sem_inc(hb_out, 16)
            sp.sem_inc(qk_out[0], 32)
            sp.sem_inc(qk_out[1], 32)
            sp.sem_inc(v_out, 16)
            def load(b):
                sp.wait_ge(h_used, b + 1)
                sp.dma_start(h[:], h3_dram[b + b0]).then_inc(h_in, 16)

            def body(b, first):
                if first:
                    load(b + 1)
                sp.wait_ge(hb_ready, b + 2)
                sp.dma_start(hn_dram[b + b0], hb[:]).then_inc(hb_out, 16)
                for x in range(2):
                    sp.wait_ge(lo_ready, 8 * b + 4 * x + 8)
                    for m in range(2):
                        sp.dma_start(qk_dram[b + b0, x, :, m * DH:(m + 1) * DH, :].rearrange("p r t -> r p t"),
                                     parts[:, x, :, m, :]).then_inc(qk_out[x], 16)
                sp.wait_ge(v_ready, 3 * b + 3)
                sp.dma_start(v_dram[b + b0], va[:]).then_inc(v_out, 16)

            load(0)
            each_image(sp, body)
            sp.wait_ge(hb_out, 16 * n_img + 16)
            sp.wait_ge(qk_out[0], 32 * n_img + 32)
            sp.wait_ge(qk_out[1], 32 * n_img + 32)
            sp.wait_ge(v_out, 16 * n_img + 16)

        @block.gpsimd
        def _(pool):
            identity(pool, ident[:], consts, 0)
            pool.memset(eps_col[:], LN_EPS)
            pool.memset(va[:], 1.0).then_inc(consts, 1)
            pool.wait_ge(weights_in, 80)
            if half:
                pool.tensor_scalar(gumbel[:, 1:2], gumbel[:, 1:2], gumbel[:, 0:1], None, ALU.add).then_inc(consts, 1)
                pool.wait_ge(consts, 4)
                pool.tensor_scalar(gumbel[:, 2:3], gumbel[:, 2:3], gumbel[:, 1:2], None, ALU.add).then_inc(consts, 1)
                pool.wait_ge(consts, 5)
                for n, (lo, hi) in enumerate(((DH, D), (64, DH), (0, 64))):
                    ins = pool.tensor_scalar(bias[:, lo:hi], bias[:, lo:hi], gumbel[:, n:n + 1], None, ALU.mult)
                ins.then_inc(consts, 1)
                pool.wait_ge(consts, 6)
            pool.sem_inc(lo_ready, 4)
            pool.sem_inc(hb_ready, 1)
            with pool.Fori(0, n_img) as b:
                pool.wait_ge(hn_ready, b + 1)
                pool.wait_ge(hb_out, 16 * b + 16)
                pool.tensor_tensor(hb[:], hn[:], bias[:].unsqueeze(1).to_broadcast([T, NT, D]), ALU.add
                                   ).then_inc(hb_ready, 1)
                for n in range(8):
                    x, m, g = n // 4, n // 2 % 2, n % 2
                    pool.wait_ge(mid_ready, 8 * b + n + 1)
                    pool.tensor_tensor(parts[:, x, 2, m, g * G:(g + 1) * G], rest[:, n % 4, :],
                                       parts[:, x, 1, m, g * G:(g + 1) * G], ALU.subtract).then_inc(lo_ready, 1)

        @block.tensor
        def _(pe):
            pe.wait_ge(weights_in, 80)
            pe.wait_ge(consts, 3)
            with pe.Fori(0, n_img) as b:
                pe.wait_ge(z_ready, b + 1)
                for m in range(2):
                    for g in range(2):
                        for t in range(3):
                            ins = pe.transpose(ps[2 * m + g][0:DH, t * T:(t + 1) * T],
                                               z[:, 3 * g + t, m * DH:(m + 1) * DH], ident[0:T, 0:T])
                ins.then_inc(z_turned, 1)
                pe.wait_ge(zT0_ready, b + 1)
                pe.wait_ge(zT1_ready, b + 1)
                for n in range(8):
                    x, m, g = n // 4, n // 2 % 2, n % 2
                    if n >= 4:
                        pe.wait_ge(rest_ready, 8 * b + n - 3)
                    for c in range(2):
                        ins = pe.matmul(ps[4 + n % 4][0:DH, 0:G], w[:, c, x * D + m * DH:x * D + (m + 1) * DH],
                                        zT[:, c, g * G:(g + 1) * G], start=(c == 0), stop=(c == 1))
                    ins.then_inc(qk_done, 1)
                for t in range(NT):
                    for c in range(2):
                        ins = pe.matmul(ps[t // 2][0:T, (t % 2) * D:(t % 2 + 1) * D], zT[:, c, t * T:(t + 1) * T],
                                        w[:, c, 2 * D:3 * D], start=(c == 0), stop=(c == 1))
                    if t % 2:
                        ins.then_inc(v_done, 1)

        @block.scalar
        def _(act):
            act.wait_ge(weights_in, 80)
            act.wait_ge(consts, 3)

            def root(b, n):
                act.wait_ge(var_ready[n], b + 1)
                act.activation(rstd[:], mv[:, :, 1], ACT.Sqrt, bias=eps_col[:, 0:1]).then_inc(std_ready[n], 1)

            def body(b, first):
                act.wait_ge(z_turned, b + 1)
                for g in range(2):
                    ins = act.activation(zT[:, 1, g * G:(g + 1) * G], ps[2 + g][0:DH, 0:G], ACT.Identity,
                                         scale=gain[:, 1:2], bias=shift[:, 1:2])
                ins.then_inc(zT1_ready, 1)

                def high(n):
                    x, m, g = n // 4, n // 2 % 2, n % 2
                    if n % 4 == 0:
                        act.wait_ge(qk_out[x], 32 * b + 32)
                    act.wait_ge(qk_done, 8 * b + n + 1)
                    act.activation(parts[:, x, 0, m, g * G:(g + 1) * G], ps[4 + n % 4][0:DH, 0:G], ACT.Copy
                                   ).then_inc(hi_ready, 1)

                high(0)
                for n in range(8):
                    x, m, g = n // 4, n // 2 % 2, n % 2
                    if n < 7:
                        high(n + 1)
                    act.wait_ge(rest_ready, 8 * b + n + 1)
                    act.activation(parts[:, x, 1, m, g * G:(g + 1) * G], rest[:, n % 4, :], ACT.Copy
                                   ).then_inc(mid_ready, 1)
                    if n == 3 and first:
                        root(b + 1, 0)
                if first:
                    root(b + 1, 1)

            root(0, 0)
            root(0, 1)
            each_image(act, body)

        @block.vector
        def _(dve):
            dve.wait_ge(weights_in, 80)
            dve.wait_ge(consts, 3)
            dve.sem_inc(h_used, 1)

            def layernorm(src, dst, b, n, done):
                c_ = Chain(dve, chain, V_PER * b + 2 * n)
                for t in range(NT):
                    ins = dve.bn_stats(stats[:, t, :], src[:, t, :])
                c_.link(ins)
                dve.sem_inc(passed, 1)
                for t in range(NT):
                    ins = dve.bn_aggr(mv[:, t, :], stats[:, t, :])
                ins.then_inc(var_ready[n], 1)
                dve.wait_ge(std_ready[n], b + 1)
                c_.link(dve.reciprocal(rstd[:], rstd[:]))
                for t in range(NT):
                    ins = dve.tensor_scalar(dst[:, t, :], src[:, t, :], mv[:, t, 0:1], rstd[:, t:t + 1],
                                            ALU.subtract, ALU.mult)
                ins.then_inc(done, 1)

            def norm(b):
                dve.wait_ge(h_in, 16 * b + 16)
                dve.wait_ge(hb_ready, b + 1)
                layernorm(h, hn, b, 0, hn_ready)
                dve.wait_ge(hn_ready, b + 1)
                dve.sem_inc(h_used, 1)

            def rests(b, first, last):
                for n in range(first, last):
                    x, m, g = n // 4, n // 2 % 2, n % 2
                    dve.wait_ge(hi_ready, 8 * b + n + 1)
                    dve.wait_ge(lo_ready, 8 * b + n + 1)
                    dve.tensor_tensor(rest[:, n % 4, :], ps[4 + n % 4][0:DH, 0:G], parts[:, x, 0, m, g * G:(g + 1) * G],
                                      ALU.subtract).then_inc(rest_ready, 1)

            def body(b, first):
                dve.wait_ge(z_turned, b + 1)
                for g in range(2):
                    ins = dve.tensor_scalar(zT[:, 0, g * G:(g + 1) * G], ps[g][0:DH, 0:G], gain[:, 0:1], shift[:, 0:1],
                                            ALU.mult, ALU.add)
                ins.then_inc(zT0_ready, 1)
                rests(b, 0, 4)
                if first:
                    norm(b + 1)
                rests(b, 4, 8)
                dve.wait_ge(v_out, 16 * b + 16)
                for t in range(3):
                    dve.wait_ge(v_done, 3 * b + t + 1)
                    dve.tensor_copy(va[:, 2 * t:2 * t + 2, :, 0:HD],
                                    ps[t][0:T, 0:2 * D].rearrange("p (t h d) -> p t h d", t=2, h=HEADS)
                                    ).then_inc(v_ready, 1)
                if first:
                    layernorm(hn, z, b + 1, 1, z_ready)

            norm(0)
            layernorm(hn, z, 0, 1, z_ready)
            each_image(dve, body)


def phase_attend(nc, a, n_img, hn_dram, qk_dram, v_dram, x1_dram):
    GR = HEADS // 4
    PER = 4
    QG = 4 * NT * 2
    RG = QG // PER
    R = GR * RG
    LEAD = RG + 6
    S = 8
    KR6 = QK_ROWS + 3
    MISC = 15
    SQ = GR * QG
    with ExitStack() as ctx:
        def sb(name, shape, dt=F32):
            return ctx.enter_context(nc.sbuf_tensor("f_" + name + "_t", shape, dt))

        def sem(name):
            return nc.alloc_semaphore("f_" + name)

        q6 = sb("q6", [KR6, GR, 4, SEQ], BF16)
        k6 = sb("k6", [KR6, GR, 4, SEQ], BF16)
        va = sb("va", [T, GR, NT, 4, 32])
        p = sb("p", [T, 2, 4, G])
        mx = sb("mx", [T, 4, NT, 2])
        nmx = sb("nmx", [T, NT, 4])
        negs = sb("negs", [T, NT, 3, 4])
        part = sb("part", [T, NT, 4], BF16)
        nrest = sb("nrest", [T, NT, 4])
        nparts = sb("nparts", [12, SEQ], BF16)
        sums = sb("sums", [36, T])
        inv = sb("inv", [36, T])
        oT = sb("oT", [128, 3, SEQ])
        wp = sb("wp", [128, 2, 3, D])
        gumbel = sb("gumbel", [128, 3])
        ident = sb("ident", [128, 128])
        sums_to = sb("sums_to", [36, 3, 3, 4, 32])
        hn = sb("hn", [T, NT, D])
        x1 = sb("x1", [T, NT, D])

        ps_s = [ctx.enter_context(nc.psum_tensor(f"f_s{n}", [128, 2, 512], F32)) for n in range(2)]
        ps_q = [ctx.enter_context(nc.psum_tensor(f"f_q{n}", [128, 512], F32)) for n in range(2)]
        ps_o = ctx.enter_context(nc.psum_tensor("f_o", [128, 512], F32))
        ps_m = ctx.enter_context(nc.psum_tensor("f_m", [128, 512], F32))

        weights_in = sem("weights_in")
        consts = sem("consts")
        w_chain = sem("w_chain")
        qk_in = [sem(f"qk_in{j}") for j in range(GR)]
        v_in = [sem(f"v_in{j}") for j in range(GR)]
        hn_in = sem("hn_in")
        q_done = sem("q_done")
        q_used = sem("q_used")
        nmx_ready = sem("nmx_ready")
        misc_done = sem("misc_done")
        misc_used = sem("misc_used")
        split = sem("split")
        mid_ready = sem("mid_ready")
        max_in = [sem(f"max_in{j}") for j in range(GR)]
        s_done = sem("s_done")
        p_ready = sem("p_ready")
        pv_done = sem("pv_done")
        o_ready = sem("o_ready")
        sums_in = sem("sums_in")
        inv_ready = sem("inv_ready")
        x1_out = sem("x1_out")
        chain = sem("chain")
        passed = sem("passed")

        block = ctx.enter_context(nc.Block())

        def each_image(eng, rounds, finish, spans):
            rounds(0, 0, S, False, True, 0)
            for half, (first, end) in enumerate(spans):
                with eng.Fori(first, end) as b:
                    rounds(b, S, R, True, True, half)
                    rounds(b + 1, 0, S, True, True, half)
            rounds(n_img - 1, S, R, True, False, 1)
            finish(n_img - 1)

        def queries_of(r, ahead):
            n = PER * (r + LEAD)
            return range(n, n + PER) if ahead or n < SQ else range(0)

        def group_before(r):
            return (r + LEAD) // RG - 1 if (r + LEAD) % RG == 0 else None

        USES = {(3, 0): ("inverses", 3, True), (3, 1): ("inverses", 4, True), (4, 0): ("inverses", 5, True),
                (5, 0): ("output", 0, True), (6, 0): ("output", 1, True), (7, 0): ("output", 2, True),
                (8, 0): ("maxima", 2, False), (9, 0): ("maxima", 3, False),
                (20, 0): ("maxima", 4, False), (21, 0): ("maxima", 5, False),
                (22, 0): ("inverses", 0, False), (23, 0): ("inverses", 1, False), (24, 0): ("inverses", 2, False),
                (32, 0): ("maxima", 6, False), (33, 0): ("maxima", 7, False)}
        OUTPUTS, MAXIMA_USE = 3, (None, 6, 8, 13)
        INVERT_ROUNDS = (20, 2)

        def misc_use(b, i):
            return MISC * b + i - 4

        def misc_in(b, r, slot, behind, ahead):
            if (r, slot) not in USES:
                return None
            what, n, previous = USES[r, slot]
            if (previous and not behind) or (what == "maxima" and n // 2 == GR and not ahead):
                return None
            return what, (b - 1 if previous else b), n, misc_use(b, list(USES).index((r, slot)))

        @block.sync
        def _(sp):
            for half in range(2):
                sp.dma_start(wp[:, half], a["f_wproj"]).then_inc(weights_in, 16)
            sp.dma_start(gumbel[:], a["gumbel"].partition_broadcast(128)).then_inc(weights_in, 16)
            sp.sem_inc(x1_out, 16)

            def load(b, j):
                for x, dst in enumerate((q6, k6)):
                    for n, pair in enumerate(PRODUCTS):
                        sp.dma_start(dst[HD * n:HD * n + HD, j, :, :],
                                     qk_dram[b, x, pair[x], 4 * HD * j:4 * HD * (j + 1), :].rearrange(
                                         "(i d) t -> d i t", d=HD)).then_inc(qk_in[j], 16)
                sp.dma_start(va[:, j], v_dram[b][:, :, 4 * j:4 * j + 4, :]).then_inc(v_in[j], 16)

            def load_next(b, j):
                sp.wait_ge(pv_done, R * b + RG * (j + 1) + 2)
                load(b + 1, j)

            def maxima(b, j, use):
                sp.wait_ge(misc_used, use + 3)
                for n in range(3):
                    sp.dma_start(q6[QK_ROWS + n:QK_ROWS + n + 1, j, :, :], nparts[4 * n:4 * n + 4, :]
                                 ).then_inc(max_in[j], 16)

            def take_sums(b, n):
                if n % 3 == 0:
                    sp.wait_ge(inv_ready, 2 * b + n // 3 + 1)
                    sp.sem_inc(passed, 1)
                sp.wait_ge(o_ready, 6 * b + n + 2)
                j, g = n // 2, n % 2
                for i in range(4):
                    row = 4 * (n % 3) + i
                    sp.dma_start(sums[row::12, :], oT[32 * i + HD:32 * i + HD + 1, j, g * G:(g + 1) * G].rearrange(
                        "one (t p) -> one t p", p=T)).then_inc(sums_in, 16)

            def store(b, use):
                sp.wait_ge(misc_used, use + 4)
                sp.dma_start(x1_dram[b], x1[:]).then_inc(x1_out, 16)

            def image(b, behind, ahead):
                if behind:
                    take_sums(b - 1, 5)
                    load_next(b - 1, 2)
                take_sums(b, 0)
                if behind:
                    store(b - 1, misc_use(b, OUTPUTS))
                sp.dma_start(hn[:], hn_dram[b]).then_inc(hn_in, 16)
                maxima(b, 1, misc_use(b, MAXIMA_USE[1]))
                take_sums(b, 1)
                if ahead:
                    load_next(b, 0)
                take_sums(b, 2)
                maxima(b, 2, misc_use(b, MAXIMA_USE[2]))
                take_sums(b, 3)
                if ahead:
                    load_next(b, 1)
                take_sums(b, 4)
                if ahead:
                    maxima(b + 1, 0, misc_use(b, MAXIMA_USE[3]))

            sp.sem_inc(inv_ready, 1)
            for j in range(GR):
                load(0, j)
            maxima(0, 0, 0)
            image(0, False, True)
            with sp.Fori(1, n_img - 1) as b:
                image(b, True, True)
            image(n_img - 1, True, False)
            take_sums(n_img - 1, 5)
            store(n_img - 1, misc_use(n_img, OUTPUTS) - 2)
            sp.wait_ge(x1_out, 16 * n_img + 16)

        @block.gpsimd
        def _(pool):
            identity(pool, ident[:], consts, 0)
            pool.memset(sums_to[:], 0.0).then_inc(consts, 1)
            pool.wait_ge(consts, 3)
            pool.affine_select(out=sums_to[:], in_=sums_to[:], compare_op=ALU.not_equal, fill=1.0, base=0,
                               pattern=[[-4, 3], [-12, 3], [-1, 4], [0, 32]], channel_multiplier=1).then_inc(consts, 1)
            pool.wait_ge(consts, 4)
            pool.memset(k6[QK_ROWS:], 1.0).then_inc(consts, 1)
            pool.wait_ge(consts, 5)
            pool.wait_ge(weights_in, 48)
            pool.tensor_scalar(gumbel[:, 1:2], gumbel[:, 1:2], gumbel[:, 0:1], None, ALU.add).then_inc(consts, 1)
            pool.wait_ge(consts, 6)
            pool.tensor_scalar(gumbel[:, 2:3], gumbel[:, 2:3], gumbel[:, 1:2], None, ALU.add).then_inc(consts, 1)
            pool.wait_ge(consts, 7)
            scaled = Chain(pool, w_chain)
            for rows, j, cols, n in ((slice(0, 128), 0, slice(0, 64), 3), (slice(0, 128), 0, slice(64, DH), 2),
                                     (slice(0, 128), 0, slice(DH, D), 1), (slice(0, 64), 1, slice(0, DH), 2),
                                     (slice(0, 64), 1, slice(DH, D), 1), (slice(64, 128), 1, slice(0, D), 1),
                                     (slice(0, 128), 2, slice(0, D), 1)):
                scaled.link(pool.tensor_scalar(wp[rows, 1, j, cols], wp[rows, 1, j, cols], gumbel[rows, n - 1:n], None,
                                               ALU.mult))
            pool.sem_inc(consts, 1)

            def split_maxima(n):
                pool.wait_ge(nmx_ready, n + 1)
                pool.sem_inc(passed, 1)
                c = Chain(pool, chain, 4 * n, 4)
                c.link(pool.tensor_copy(part[:], nmx[:]))
                pool.sem_inc(passed, 1)
                c.link(pool.tensor_copy(negs[:, :, 0, :], part[:]))
                c.link(pool.tensor_tensor(nrest[:], nmx[:], negs[:, :, 0, :], ALU.subtract))
                pool.sem_inc(passed, 1)
                c.link(pool.tensor_copy(part[:], nrest[:]))
                pool.sem_inc(passed, 1)
                pool.tensor_copy(negs[:, :, 1, :], part[:]).then_inc(mid_ready, 1)
                pool.wait_ge(mid_ready, n + 1)
                pool.tensor_tensor(negs[:, :, 2, :], nrest[:], negs[:, :, 1, :], ALU.subtract).then_inc(split, 1)
                c.close()

            with pool.Fori(0, GR * n_img) as n:
                split_maxima(n)

        @block.tensor
        def _(pe):
            pe.wait_ge(weights_in, 48)
            pe.wait_ge(consts, 8)
            pe.sem_inc(pv_done, 2)

            def by_queries(b, n):
                j, h, t, g = n // QG % GR, n // (2 * NT) % 4, n // 2 % NT, n % 2
                if n % QG == 0:
                    pe.wait_ge(qk_in[j], 192 * (b + n // SQ) + 192)
                pe.wait_ge(q_used, SQ * b + n + 1)
                pe.matmul(ps_q[n % 2][0:T, 0:G], q6[0:QK_ROWS, j, h, t * T:(t + 1) * T],
                          k6[0:QK_ROWS, j, h, g * G:(g + 1) * G], start=True, stop=True).then_inc(q_done, 1)

            def turn_maxima(b, j, g, use):
                pe.wait_ge(split, GR * b + j + 1)
                pe.wait_ge(misc_used, use + 1)
                pe.sem_inc(passed, 1)
                for t in range(3):
                    ins = pe.transpose(ps_m[0:12, t * T:(t + 1) * T],
                                       negs[:, 3 * g + t].rearrange("p n h -> p (n h)"), ident[0:T, 0:T])
                ins.then_inc(misc_done, 1)

            def weigh(b, r):
                j, t = r // RG, r % NT
                pe.wait_ge(p_ready, 2 * R * b + 2 * r + 4)
                if t == 0:
                    pe.wait_ge(o_ready, 6 * b + r // NT + 1)
                for i in range(4):
                    ins = pe.matmul(ps_o[32 * i:32 * i + 32, 0:G], va[:, j, t, i, :], p[:, r % 2, i, :],
                                    start=(t == 0), stop=(t == NT - 1))
                ins.then_inc(pv_done, 1)

            def spread_inverses(b, n, use):
                pe.wait_ge(inv_ready, 2 * b + n // 3 + 2)
                pe.wait_ge(misc_used, use + 1)
                for t in range(3):
                    ins = pe.matmul(ps_m[:, t * T:(t + 1) * T], sums_to[:, n % 3, t].rearrange("p i c -> p (i c)"), inv[:],
                                    start=True, stop=True)
                ins.then_inc(misc_done, 1)

            def project_out(b, n, use, half):
                pe.wait_ge(misc_used, use + 1)
                for t in range(2 * n, 2 * n + 2):
                    for j in range(GR):
                        ins = pe.matmul(ps_m[0:T, (t % 2) * D:(t % 2 + 1) * D], oT[:, j, t * T:(t + 1) * T],
                                        wp[:, half, j, :], start=(j == 0), stop=(j == GR - 1))
                ins.then_inc(misc_done, 1)

            def misc(use, half):
                if use is not None:
                    what, b, n, before = use
                    if what == "inverses":
                        spread_inverses(b, n, before)
                    elif what == "output":
                        project_out(b, n, before, half)
                    else:
                        turn_maxima(b, n // 2, n % 2, before)

            def rounds(b, first, last, behind, ahead, half):
                for r in range(first, last):
                    j, g, t = r // RG, r // NT % 2, r % NT
                    queries = queries_of(r, ahead)
                    if r % RG == 0:
                        pe.wait_ge(max_in[j], 48 * b + 48)
                        pe.wait_ge(v_in[j], 16 * b + 16)
                    for e in range(2):
                        pe.wait_ge(p_ready, 2 * R * b + 2 * r + e + 1)
                        for i in range(2):
                            ins = pe.matmul(ps_s[e][0:T, i, 0:G], k6[:, j, 2 * e + i, t * T:(t + 1) * T],
                                            q6[:, j, 2 * e + i, g * G:(g + 1) * G], start=True, stop=True)
                        ins.then_inc(s_done, 1)
                        for n in queries[e:e + 1]:
                            by_queries(b, n)
                    if r:
                        weigh(b, r - 1)
                    elif behind:
                        weigh(b - 1, R - 1)
                    misc(misc_in(b, r, 0, behind, ahead), half)
                    for n in queries[2:3]:
                        by_queries(b, n)
                    misc(misc_in(b, r, 1, behind, ahead), half)
                    for n in queries[3:4]:
                        by_queries(b, n)

            def finish(b):
                weigh(b, R - 1)
                for n in range(3):
                    spread_inverses(b, n + 3, misc_use(b + 1, n) - 2)
                for n in range(3):
                    project_out(b, n, misc_use(b + 1, OUTPUTS + n) - 2, 1)

            for n in range(QG):
                by_queries(0, n)
            for g in range(2):
                turn_maxima(0, 0, g, g)
            for n in range(QG, PER * LEAD):
                by_queries(0, n)
            each_image(pe, rounds, finish, ((0, n_img // 2), (n_img // 2, n_img - 1)))

        @block.scalar
        def _(act):
            act.wait_ge(consts, 8)
            act.sem_inc(p_ready, 2)
            act.sem_inc(o_ready, 1)

            def keep(b, n):
                act.wait_ge(pv_done, R * b + NT * n + 8)
                j, g = n // 2, n % 2
                if n < 2:
                    act.wait_ge(misc_done, misc_use(b, OUTPUTS + 2 + g))
                act.activation(oT[:, j, g * G:(g + 1) * G], ps_o[:, 0:G], ACT.Copy).then_inc(o_ready, 1)

            def rounds(b, first, last, behind, ahead, half):
                for r in range(first, last):
                    for e in range(2):
                        act.wait_ge(s_done, 2 * R * b + 2 * r + e + 1)
                        if e == 0:
                            act.wait_ge(pv_done, R * b + r + 1)
                        act.activation(p[:, r % 2, 2 * e:2 * e + 2, :], ps_s[e][0:T, :, 0:G], ACT.Exp, scale=HD ** -0.5
                                       ).then_inc(p_ready, 1)
                    if r and r % NT == 0:
                        keep(b, r // NT - 1)
                    elif r == 0 and behind:
                        keep(b - 1, 5)

            def finish(b):
                keep(b, 5)

            each_image(act, rounds, finish, ((0, n_img - 1),))

        @block.vector
        def _(dve):
            dve.wait_ge(consts, 8)
            dve.sem_inc(q_used, 2)
            dve.sem_inc(misc_used, 1)

            def maximum(b, n):
                h, t, g = n // (2 * NT) % 4, n // 2 % NT, n % 2
                dve.wait_ge(q_done, SQ * b + n + 1)
                dve.tensor_reduce(mx[:, h, t, g:g + 1], ps_q[n % 2][0:T, 0:G], AX_X, ALU.max).then_inc(q_used, 1)

            def negated(b, j):
                dve.wait_ge(q_used, SQ * b + QG * (j + 1) + 2)
                dve.tensor_reduce(nmx[:].rearrange("p t h -> p h t"), mx[:], AX_X, ALU.max, negate=True
                                  ).then_inc(nmx_ready, 1)
                dve.wait_ge(nmx_ready, GR * b + j + 1)

            def maxima_rows(b, j, g, use, first_group=False):
                if j:
                    dve.wait_ge(max_in[j - 1], 48 * b + 48)
                elif not first_group:
                    dve.wait_ge(max_in[GR - 1], 48 * b)
                dve.wait_ge(misc_done, use + 1)
                dve.tensor_copy(nparts[:, g * G:(g + 1) * G], ps_m[0:12, 0:G]).then_inc(misc_used, 1)

            def invert(b, batch, use):
                dve.wait_ge(sums_in, 192 * (2 * b + batch + 1))
                dve.wait_ge(misc_done, use)
                dve.reciprocal(inv[:], sums[:]).then_inc(inv_ready, 1)

            def normalize(b, n, use):
                j, g = n // 2, n % 2
                dve.wait_ge(misc_done, use + 1)
                dve.tensor_tensor(oT[:, j, g * G:(g + 1) * G], oT[:, j, g * G:(g + 1) * G], ps_m[:, 0:G], ALU.mult
                                  ).then_inc(misc_used, 1)

            def residual(b, n, use):
                if n == 0:
                    dve.wait_ge(hn_in, 16 * b + 16)
                    dve.wait_ge(x1_out, 16 * b + 16)
                dve.wait_ge(misc_done, use + 1)
                dve.tensor_tensor(x1[:, 2 * n:2 * n + 2, :], ps_m[0:T, 0:2 * D].rearrange("p (t d) -> p t d", d=D),
                                  hn[:, 2 * n:2 * n + 2, :], ALU.add).then_inc(misc_used, 1)

            def misc(use):
                if use is not None:
                    what, b, n, before = use
                    if what == "inverses":
                        normalize(b, n, before)
                    elif what == "output":
                        residual(b, n, before)
                    else:
                        maxima_rows(b, n // 2, n % 2, before)

            def rounds(b, first, last, behind, ahead, half):
                for r in range(first, last):
                    done = group_before(r)
                    if done is not None and (ahead or done < GR):
                        negated(b, done)
                    queries = queries_of(r, ahead)
                    for n in queries[:2]:
                        maximum(b, n)
                    misc(misc_in(b, r, 0, behind, ahead))
                    for n in queries[2:3]:
                        maximum(b, n)
                    misc(misc_in(b, r, 1, behind, ahead))
                    for n in queries[3:]:
                        maximum(b, n)
                    if r == INVERT_ROUNDS[0]:
                        invert(b, 0, misc_use(b, MAXIMA_USE[1]))
                    elif r == INVERT_ROUNDS[1] and behind:
                        invert(b - 1, 1, misc_use(b, 0) - 2)

            def finish(b):
                invert(b, 1, misc_use(b + 1, 0) - 2)
                for n in range(3):
                    normalize(b, n + 3, misc_use(b + 1, n) - 2)
                for n in range(3):
                    residual(b, n, misc_use(b + 1, OUTPUTS + n) - 2)

            for n in range(QG):
                maximum(0, n)
            negated(0, 0)
            for g in range(2):
                maxima_rows(0, 0, g, g, first_group=True)
            for n in range(QG, PER * LEAD):
                maximum(0, n)
            each_image(dve, rounds, finish, ((0, n_img - 1),))


def phase_mlp(nc, a, half, n_img, h3_dram, x1_dram, out_dram):
    b0 = half * n_img
    P = "g%d_" % half
    BR = 3 if half else 1
    KEEP = (D, DH, 64)
    MT = MLP // 128
    U = 2 * BR
    with ExitStack() as ctx:
        def sb(name, shape, dt=F32):
            return ctx.enter_context(nc.sbuf_tensor(P + name + "_t", shape, dt))

        def sem(name):
            return nc.alloc_semaphore(P + name)

        w1 = sb("w1", [DH, 2, MLP])
        w1c = sb("w1c", [DH, MLP])
        b1 = sb("b1", [128, MT])
        w2 = sb("w2", [128, BR, MT, D])
        gain = sb("gain", [DH, 2])
        shift = sb("shift", [DH, 2])
        gumbel = sb("gumbel", [128, 3])
        gsum = sb("gsum", [T, 3])
        bias = sb("bias", [T, D])
        ident = sb("ident", [128, 128])
        eps_col = sb("eps_col", [T, 1])
        x1 = sb("x1", [T, NT, D])
        h = sb("h", [T, NT, D])
        res = sb("res", [T, 2, NT, D])
        z = sb("z", [T, NT, D])
        stats = sb("stats", [T, NT, 6])
        mv = sb("mv", [T, NT, 2])
        rstd = sb("rstd", [T, NT])
        zT = sb("zT", [DH, 2, SEQ])
        hid = sb("hid", [128, 2, MT, G])
        o = sb("o", [T, NT, D])

        ps = [ctx.enter_context(nc.psum_tensor(f"{P}ps{n}", [128, 512], F32)) for n in range(8)]

        weights_in = sem("weights_in")
        consts = sem("consts")
        w_chain = sem("w_chain")
        x1_in = sem("x1_in")
        h_in = sem("h_in")
        var_ready = sem("var_ready")
        std_ready = sem("std_ready")
        z_ready = sem("z_ready")
        res1_ready = sem("res1_ready")
        res_ready = sem("res_ready")
        z_turned = sem("z_turned")
        zT0_ready = sem("zT0_ready")
        zT1_ready = sem("zT1_ready")
        up_done = sem("up_done")
        hid_ready = sem("hid_ready")
        down_done = sem("down_done")
        o_ready = sem("o_ready")
        o_out = sem("o_out")
        chain = sem("chain")
        passed = sem("passed")
        V_PER = 2
        W_IN = 8 * 16

        block = ctx.enter_context(nc.Block())

        def each_image(eng, body):
            if n_img > 2:
                with eng.Fori(0, n_img // 2 - 1) as j:
                    body(j, 0, True)
                    body(j, 1, True)
            body(n_img // 2 - 1, 0, True)
            body(n_img // 2 - 1, 1, False)

        @block.sync
        def _(sp):
            names = ("n2s_g", "n2s_b") if half else ("n2l_g", "n2l_b")
            sp.dma_start(w1[:], a["w_fc1"]).then_inc(weights_in, 16)
            sp.dma_start(w1c[0:64, :], a["w_fc1"][0:64, 0, :]).then_inc(weights_in, 16)
            sp.dma_start(b1[:], a["b_fc1"]).then_inc(weights_in, 16)
            sp.dma_start(w2[:, 0], a["w_fc2"]).then_inc(weights_in, 16)
            sp.dma_start(gain[:], a[names[0]]).then_inc(weights_in, 16)
            sp.dma_start(shift[:], a[names[1]]).then_inc(weights_in, 16)
            sp.dma_start(gumbel[:], a["gumbel"].partition_broadcast(128)).then_inc(weights_in, 16)
            sp.dma_start(bias[:], a["b_fc2"].partition_broadcast(T)).then_inc(weights_in, 16)
            sp.sem_inc(o_out, 16)

            def load(b):
                sp.dma_start(x1[:], x1_dram[b + b0]).then_inc(x1_in, 16)
                sp.dma_start(h[:], h3_dram[b + b0]).then_inc(h_in, 16)

            def image(j, k, ahead):
                b = 2 * j + k
                if ahead:
                    sp.wait_ge(z_ready, b + 1)
                    sp.wait_ge(res_ready, b + 1)
                    load(b + 1)
                sp.wait_ge(o_ready, 2 * b + 3)
                for t in range(NT):
                    sp.dma_start(out_dram[b + b0, t * T:(t + 1) * T, :], o[:, t, :]).then_inc(o_out, 16)

            load(0)
            each_image(sp, image)
            sp.wait_ge(o_out, 16 * NT * n_img + 16)

        @block.gpsimd
        def _(pool):
            identity(pool, ident[:], consts, 0)
            pool.memset(eps_col[:], LN_EPS).then_inc(consts, 1)
            pool.wait_ge(consts, 3)
            pool.memset(w1c[64:DH, :], 0.0).then_inc(consts, 1)
            pool.wait_ge(weights_in, W_IN)
            pool.wait_ge(consts, 4)
            if half:
                scaled = Chain(pool, w_chain)
                scaled.link(pool.tensor_copy(gsum[:, 0:1], gumbel[0:T, 0:1]))
                for n in range(1, 3):
                    scaled.link(pool.tensor_scalar(gsum[:, n:n + 1], gumbel[0:T, n:n + 1], gsum[:, n - 1:n], None, ALU.add))
                for n, (lo, hi) in enumerate(((DH, D), (64, DH), (0, 64))):
                    scaled.link(pool.tensor_scalar(bias[:, lo:hi], bias[:, lo:hi], gsum[:, n:n + 1], None, ALU.mult))
                for n in (2, 1, 0):
                    scaled.link(pool.tensor_scalar(w2[:, n], w2[:, 0], gumbel[:, n:n + 1], None, ALU.mult))
            pool.sem_inc(consts, 1)

            def residual(b, k):
                pool.wait_ge(x1_in, 16 * b + 16)
                pool.wait_ge(h_in, 16 * b + 16)
                pool.tensor_tensor(res[:, k], x1[:], h[:], ALU.add).then_inc(res1_ready, 1)
                pool.wait_ge(res1_ready, b + 1)
                pool.tensor_tensor(res[:, k], res[:, k], bias[:].unsqueeze(1).to_broadcast([T, NT, D]), ALU.add
                                   ).then_inc(res_ready, 1)

            def image(j, k, ahead):
                b = 2 * j + k
                if ahead:
                    pool.wait_ge(o_ready, 2 * b + 1)
                    residual(b + 1, 1 - k)

            residual(0, 0)
            each_image(pool, image)

        @block.tensor
        def _(pe):
            pe.wait_ge(weights_in, W_IN)
            pe.wait_ge(consts, 5)
            pe.sem_inc(down_done, 2)

            def turn(b):
                pe.wait_ge(z_ready, b + 1)
                for m in range(2):
                    for g in range(2):
                        pe.wait_ge((zT0_ready, zT1_ready)[m], 2 * b + g + 1)
                        pe.sem_inc(passed, 1)
                        for t in range(3):
                            ins = pe.transpose(ps[m][0:DH, t * T:(t + 1) * T], z[:, 3 * g + t, m * DH:(m + 1) * DH],
                                               ident[0:T, 0:T])
                        ins.then_inc(z_turned, 1)

            def up(b, u):
                g, br = u // BR, u % BR
                for i in range(MT):
                    n = MT * u + i
                    pe.wait_ge(hid_ready, MT * U * b + n + 1)
                    out = ps[2 + n % 4][:, 0:G]
                    for c in range(2 if br == 0 else 1):
                        w = w1c if br == 2 else w1[:, c, :]
                        ins = pe.matmul(out, w[:, i * 128:(i + 1) * 128], zT[:, c, g * G:(g + 1) * G],
                                        start=(c == 0), stop=(br > 0 or c == 1))
                    ins.then_inc(up_done, 1)

            def down(b, u):
                g, br = u // BR, u % BR
                pe.wait_ge(hid_ready, MT * U * b + MT * (u + 1) + 4)
                if br == 0:
                    pe.wait_ge(o_ready, 2 * b + g + 1)
                for t in range(3):
                    for i in range(MT):
                        out = (ps[6][0:T, t * D:t * D + KEEP[br]] if t < 2 else ps[7][0:T, 0:KEEP[br]])
                        ins = pe.matmul(out, hid[:, u % 2, i, t * T:(t + 1) * T], w2[:, br, i, 0:KEEP[br]],
                                        start=(br == 0 and i == 0 and t != 1), stop=(br == BR - 1 and i == MT - 1),
                                        skip_group_check=True)
                ins.then_inc(down_done, 1)

            def image(j, k, ahead):
                b = 2 * j + k
                pe.wait_ge(zT0_ready, 2 * b + 3)
                pe.wait_ge(zT1_ready, 2 * b + 3)
                for u in range(U):
                    up(b, u)
                    if u:
                        down(b, u - 1)
                if ahead:
                    turn(b + 1)
                down(b, U - 1)

            turn(0)
            each_image(pe, image)

        @block.scalar
        def _(act):
            act.wait_ge(weights_in, W_IN)
            act.wait_ge(consts, 5)
            act.sem_inc(hid_ready, 4)
            act.sem_inc(zT1_ready, 1)

            def root(b):
                act.wait_ge(var_ready, b + 1)
                act.activation(rstd[:], mv[:, :, 1], ACT.Sqrt, bias=eps_col[:, 0:1]).then_inc(std_ready, 1)

            def turned(b):
                for g in range(2):
                    act.wait_ge(z_turned, 4 * b + 3 + g)
                    act.activation(zT[:, 1, g * G:(g + 1) * G], ps[1][0:DH, 0:G], ACT.Identity,
                                   scale=gain[:, 1:2], bias=shift[:, 1:2]).then_inc(zT1_ready, 1)

            def image(j, k, ahead):
                b = 2 * j + k
                for u in range(U):
                    act.wait_ge(down_done, U * b + u + 1)
                    for i in range(MT):
                        n = MT * u + i
                        act.wait_ge(up_done, MT * U * b + n + 1)
                        act.activation(hid[:, u % 2, i, :], ps[2 + n % 4][:, 0:G], ACT.Gelu, bias=b1[:, i:i + 1]
                                       ).then_inc(hid_ready, 1)
                    if u == 0 and ahead:
                        root(b + 1)
                if ahead:
                    turned(b + 1)

            root(0)
            turned(0)
            each_image(act, image)

        @block.vector
        def _(dve):
            dve.wait_ge(weights_in, W_IN)
            dve.wait_ge(consts, 5)
            dve.sem_inc(zT0_ready, 1)
            dve.sem_inc(o_ready, 1)

            def layernorm(b):
                c_ = Chain(dve, chain, V_PER * b, V_PER)
                dve.wait_ge(x1_in, 16 * b + 16)
                for t in range(NT):
                    ins = dve.bn_stats(stats[:, t, :], x1[:, t, :])
                c_.link(ins)
                dve.sem_inc(passed, 1)
                for t in range(NT):
                    ins = dve.bn_aggr(mv[:, t, :], stats[:, t, :])
                ins.then_inc(var_ready, 1)
                dve.wait_ge(std_ready, b + 1)
                c_.link(dve.reciprocal(rstd[:], rstd[:]))
                for t in range(NT):
                    ins = dve.tensor_scalar(z[:, t, :], x1[:, t, :], mv[:, t, 0:1], rstd[:, t:t + 1],
                                            ALU.subtract, ALU.mult)
                ins.then_inc(z_ready, 1)
                c_.close()

            def turned(b):
                for g in range(2):
                    dve.wait_ge(z_turned, 4 * b + 1 + g)
                    dve.tensor_scalar(zT[:, 0, g * G:(g + 1) * G], ps[0][0:DH, 0:G], gain[:, 0:1], shift[:, 0:1],
                                      ALU.mult, ALU.add).then_inc(zT0_ready, 1)

            def image(j, k, ahead):
                b = 2 * j + k
                if ahead:
                    layernorm(b + 1)
                dve.wait_ge(res_ready, b + 1)
                dve.wait_ge(o_out, 16 * NT * b + 16)
                for g in range(2):
                    if g == 1 and ahead:
                        turned(b + 1)
                    dve.wait_ge(down_done, U * b + BR * (g + 1) + 2)
                    dve.tensor_tensor(o[:, 3 * g:3 * g + 2, :], ps[6][0:T, 0:2 * D].rearrange("p (t d) -> p t d", d=D),
                                      res[:, k, 3 * g:3 * g + 2, :], ALU.add)
                    dve.tensor_tensor(o[:, 3 * g + 2, :], ps[7][0:T, 0:D], res[:, k, 3 * g + 2, :], ALU.add
                                      ).then_inc(o_ready, 1)

            layernorm(0)
            turned(0)
            each_image(dve, image)


def build(nc, a, out):
    n_img = a["txt"].shape[0]
    cap = -(-5 * 2 * n_img * SEQ // (4 * E))

    def scratch(name, shape, dt=F32):
        return nc.dram_tensor(name, shape, dt, kind="Internal").ap()

    h1 = scratch("h1_scratch", (n_img, T, NT, D))
    x2 = scratch("x2_scratch", (n_img, T, NT, D + 1))
    slots = scratch("slots_scratch", (E * cap, 1), I32)
    y = scratch("y_scratch", (E * cap, D))
    h2 = scratch("h2_scratch", (n_img, T, NT, D))
    u = scratch("u_scratch", (n_img, KR, NC, DI))
    ak = scratch("ak_scratch", (n_img, CH, NC, NS))
    delta = scratch("delta_scratch", (n_img, 128, M3, SEQ))
    kq = scratch("kq_scratch", (n_img, 80, 2, SEQ), BF16)
    dx = scratch("dx_scratch", (n_img, 128, M3, SEQ))
    zs = scratch("zs_scratch", (n_img, 128, M3, SEQ))
    h3 = scratch("h3_scratch", (n_img, T, NT, D))
    hn = scratch("hn_scratch", (n_img, T, NT, D))
    qk = scratch("qk_scratch", (n_img, 2, 3, 192, SEQ), BF16)
    v = scratch("v_scratch", (n_img, T, NT, HEADS, 32))
    x1 = scratch("x1_scratch", (n_img, T, NT, D))

    with nc.sbuf_tensor("route", [T, n_img, 4, NT], F32) as route:
        with nc.cleanup_on_exit():
            phase_route(nc, a, n_img, cap, h1, x2, slots, route)
        with nc.cleanup_on_exit():
            phase_experts(nc, a, n_img, cap, x2, slots, y)
        with nc.cleanup_on_exit():
            phase_prepare(nc, a, n_img, h1, y, route, h2, u, ak, delta, kq, dx, zs)
    with nc.cleanup_on_exit():
        phase_scan(nc, a, n_img, u, ak, delta, kq, dx, zs, h2, h3)
    for half in range(2):
        with nc.cleanup_on_exit():
            phase_project(nc, a, half, n_img // 2, h3, hn, qk, v)
    with nc.cleanup_on_exit():
        phase_attend(nc, a, n_img, hn, qk, v, x1)
    for half in range(2):
        with nc.cleanup_on_exit():
            phase_mlp(nc, a, half, n_img // 2, h3, x1, out)


def lay_out(i):
    c = np.ascontiguousarray
    i = {k: np.asarray(v) for k, v in i.items()}
    n = i["x"].shape[0]
    o = {}
    p = i["x"].reshape(n, 14, 2, 8, 14, 2, 8, 3).transpose(0, 2, 5, 3, 6, 7, 1, 4).reshape(n, 8, 96, 196)
    o["patches"] = c(p.transpose(0, 2, 1, 3))
    w = i["L0_tok_W"].reshape(2, 8, 2, 8, 5, 3, 192).transpose(0, 2, 1, 3, 5, 4, 6).reshape(8, 96, 5, 192)
    o["tok_w"] = c(w.transpose(1, 0, 2, 3))
    o["tok_b"] = c(i["L0_tok_b"].reshape(2, 96).T)
    o["txt"] = c(i["txt"])
    halves = lambda m: c(m.reshape(2, 96, -1).transpose(1, 0, 2))
    o["a_wqkvT"] = halves(i["L0_attn_w_qkv"].T)
    o["a_wqkv"] = c(i["L0_attn_w_qkv"].reshape(6, 96, 192).transpose(1, 0, 2))
    o["a_wprojT"] = halves(i["L0_attn_w_proj"].T)
    o["a_bproj"] = c(i["L0_attn_b_proj"].reshape(1, 192))
    o["gateT"] = halves(i["L0_ffn_gate_w"].T)
    o["w13T"] = c(i["L0_ffn_w13"].transpose(0, 2, 1).reshape(8, 2, 96, 1024).transpose(0, 2, 1, 3))
    o["w2T"] = c(i["L0_ffn_w2"].transpose(0, 2, 1).reshape(8, 4, 128, 192).transpose(0, 2, 1, 3))
    o["norm_w"] = c(i["L0_ffn_norm_w"].reshape(8, 2, 96).transpose(2, 0, 1))
    thirds = lambda m: c(m.reshape(3, 128, -1).transpose(1, 0, 2))
    o["inT"] = halves(i["L1_attn_in_proj_w"].T)
    xp = i["L1_attn_x_proj_w"].T
    pad = np.zeros((384, 16), xp.dtype)
    o["xprojT"] = thirds(np.concatenate([xp[:, 12:28], pad, xp[:, 28:44], pad, xp[:, 0:12], pad[:, :4], pad], 1))
    o["dtheadT"] = np.zeros((96, 384), xp.dtype)
    o["dtheadT"][64:76] = i["L1_attn_dt_head_w"].T
    o["conv_w"] = thirds(i["L1_attn_conv_w"][:, 0, :])
    o["conv_b"] = c(i["L1_attn_conv_b"].reshape(3, 128).T)
    o["dt_b"] = c(i["L1_attn_dt_head_b"].reshape(3, 128).T)
    o["d_skip"] = c(i["L1_attn_D"].reshape(3, 128).T)
    o["outT"] = thirds(i["L1_attn_out_proj_w"].T)
    s = np.arange(59)
    p = np.float64(0.9) ** np.arange(60)
    o["decay"] = p[58 - s].astype(np.float32)[:, None]
    o["carry_decay"] = np.zeros((32, 12, 16), np.float32)
    o["carry_decay"][:16] = (p[59] * np.eye(16))[:, None, :]
    o["within"] = np.where(s[None, :] >= s[:, None], p[np.maximum(s[None, :] - s[:, None], 0)], 0).astype(np.float32)
    e = np.eye(16).reshape(16, 4, 1, 4, 1) * p[1:60]
    o["carried"] = c(np.broadcast_to(e, (16, 4, 12, 4, 59)).transpose(1, 0, 2, 3, 4).astype(np.float32))
    o["f_wqkv"] = halves(i["L1_ffn_w_qkv"])
    for n in ("n1l_g", "n1l_b", "n1s_g", "n1s_b", "n2l_g", "n2l_b", "n2s_g", "n2s_b"):
        o[n] = c(i["L1_ffn_" + n].reshape(2, 96).T)
    o["gumbel"] = c(i["L1_ffn_gumbel_weights"])
    o["w_fc1"] = halves(i["L1_ffn_w_fc1"])
    o["b_fc1"] = c(i["L1_ffn_b_fc1"].reshape(6, 128).T)
    o["w_fc2"] = c(i["L1_ffn_w_fc2"].reshape(6, 128, 192).transpose(1, 0, 2))
    o["b_fc2"] = c(i["L1_ffn_b_fc2"])
    o["f_bproj"] = c(i["L1_ffn_b_proj"])
    wp = np.zeros((4, 32, 3, 192), np.float32)
    wp[:, :16] = i["L1_ffn_w_proj"].reshape(3, 4, 16, 192).transpose(1, 2, 0, 3)
    o["f_wproj"] = c(wp.reshape(128, 3, 192))
    return o


def kernel(**inputs):
    import concourse.bacc as bacc
    from concourse.bass_utils import run_bass_kernel_spmd

    arrays = lay_out(inputs)
    nc = bacc.Bacc("TRN2", target_bir_lowering=False, num_devices=1)
    a = {name: nc.dram_tensor(name, v.shape, mybir.dt.from_np(v.dtype), kind="ExternalInput").ap()
         for name, v in arrays.items()}
    n_img = inputs["txt"].shape[0]
    out = nc.dram_tensor("out", (n_img, SEQ, D), F32, kind="ExternalOutput").ap()
    build(nc, a, out)
    r = run_bass_kernel_spmd(nc, [arrays], core_ids=[0])
    return r.results[0]["out"]
```
